# Optimizing a Trainium2 kernel written in Bass

```python
import numpy as np
import jax
import jax.numpy as jnp

def _softmax(x, axis=-1):
    return jax.nn.softmax(x, axis=axis)

def _gelu(x):
    return jax.nn.gelu(x, approximate=True)

def _silu(x):
    return jax.nn.silu(x)

def _sigmoid(x):
    return jax.nn.sigmoid(x)

def _layernorm(x, axis=-1, eps=1e-05):
    m = jnp.mean(x, axis=axis, keepdims=True)
    v = jnp.var(x, axis=axis, keepdims=True)
    return (x - m) / jnp.sqrt(v + eps)

def _scatter_add(tgt, idx, src, axis=0):
    return tgt.at[idx].add(src)

def _segment_sum(src, seg, n):
    return jax.ops.segment_sum(src, seg, n)
kernel_name = 'mk_flamingo_gated_d4_seqx_r4_5e9b32'

def setup_inputs(seed: int=0):
    np.random.seed(seed)
    _w = jnp.asarray

    def _rec_inputs():
        import jax
        import jax.numpy as jnp
        _rk = jax.random.key(seed)
        x = 7.22e-05 + 1 * jax.random.normal(jax.random.fold_in(_rk, 1), (2, 1024, 256), jnp.float32)
        _lenS = 1024 - jax.random.randint(jax.random.fold_in(_rk, 7), (2,), 0, max(1, 1024 // 4) + 1, jnp.int32)
        _lenS2 = 77 - jax.random.randint(jax.random.fold_in(_rk, 8), (2,), 0, max(1, 77 // 4) + 1, jnp.int32)
        _ctx_1024P = jax.random.normal(jax.random.fold_in(_rk, 11), (2, 16, 256), jnp.float32)
        _ctx_1024c = jax.random.dirichlet(jax.random.fold_in(_rk, 511), 0.3 * jnp.ones((16,), jnp.float32), (2, 77))
        _ctx_1024t = jnp.einsum('bsk,bkd->bsd', _ctx_1024c, _ctx_1024P)
        _ctx_1024t = _ctx_1024t * jax.lax.rsqrt(jnp.mean(jnp.square(_ctx_1024t)) + 1e-12) * 0.953939
        ctx_1024 = -0.000514642 + 1.00011 * (_ctx_1024t + 0.3 * jax.random.normal(jax.random.fold_in(_rk, 611), (2, 77, 256), jnp.float32))
        _g = jax.random.normal(jax.random.fold_in(_rk, 9001), (2, 4), jnp.float32)
        _g = jnp.sign(_g) * jnp.maximum(jnp.abs(_g), 1.0) + (_g == 0) * 1.0
        g_xattn = _g[0]
        g_ffn = _g[1]
        return (x, ctx_1024, g_xattn, g_ffn)
    x, ctx_1024, g_xattn, g_ffn = _rec_inputs()

    def _L0_xattn_setup():
        import jax, jax.numpy as jnp
        import numpy as np
        B, S, E, H = (4, 512, 128, 256)
        key = jax.random.key(seed)
        ks = jax.random.split(key, 8)
        s = 1.0 / np.sqrt(H)
        return {'hidden_states': jax.random.normal(ks[0], (B, S, H), jnp.float32), 'external_embeddings': jax.random.normal(ks[1], (B, E, H), jnp.float32), 'Wq': jax.random.normal(ks[2], (H, H), jnp.float32) * s, 'bq': jax.random.normal(ks[3], (H,), jnp.float32) * 0.02, 'Wk': jax.random.normal(ks[4], (H, H), jnp.float32) * s, 'bk': jax.random.normal(ks[5], (H,), jnp.float32) * 0.02, 'Wv': jax.random.normal(ks[6], (H, H), jnp.float32) * s, 'bv': jax.random.normal(ks[7], (H,), jnp.float32) * 0.02}
    _L0_xattn_all = _L0_xattn_setup()
    _L0_xattn_in = {k: v for k, v in _L0_xattn_all.items() if k in ('Wq', 'bq', 'Wk', 'bk', 'Wv', 'bv')}
    del _L0_xattn_all

    def _L0_ffn_setup():
        import jax, jax.numpy as jnp
        import numpy as np
        BLOCK = 32
        W_BITS = 4
        ACT_BITS = 16

        def act_qdq(x):
            qmax = 2.0 ** (ACT_BITS - 1) - 1.0
            scale = jnp.maximum(jnp.max(jnp.abs(x)) / qmax, 1e-12)
            return jnp.clip(jnp.round(x / scale), -qmax - 1.0, qmax) * scale

        def fixed_qdq_u16(x):
            scale = 1.0 / 65536.0
            return jnp.clip(jnp.round(x / scale), 0.0, 65535.0) * scale

        def lpbq_dequant(w):
            O, I = w.shape
            qmax = 2.0 ** (W_BITS - 1) - 1.0
            wb = w.reshape(O, I // BLOCK, BLOCK)
            s = jnp.maximum(jnp.max(jnp.abs(wb), axis=-1, keepdims=True) / qmax, 1e-12)
            wq = jnp.clip(jnp.round(wb / s), -qmax - 1.0, qmax) * s
            return wq.reshape(O, I)
        key = jax.random.key(seed)
        k1, k2, k3, k4 = jax.random.split(key, 4)
        B, S, H, I = (2, 1024, 256, 768)
        x = jax.random.normal(k1, (B, S, H), jnp.float32)
        w_gate = jax.random.normal(k2, (I, H), jnp.float32) * 0.02
        w_up = jax.random.normal(k3, (I, H), jnp.float32) * 0.02
        w_down = jax.random.normal(k4, (H, I), jnp.float32) * 0.02
        return {'x': x, 'w_gate': w_gate, 'w_up': w_up, 'w_down': w_down}
    _L0_ffn_all = _L0_ffn_setup()
    _L0_ffn_in = {k: v for k, v in _L0_ffn_all.items() if k in ('w_gate', 'w_up', 'w_down')}
    del _L0_ffn_all

    def _L1_xattn_setup():
        import jax, jax.numpy as jnp
        import numpy as np
        DIM = 256
        key = jax.random.key(seed)
        ks = jax.random.split(key, 8)
        B, S, D = (8, 512, DIM)
        scale = 1.0 / np.sqrt(D)
        x1 = jax.random.normal(ks[0], (B, S, D), dtype=jnp.float32)
        x2 = jax.random.normal(ks[1], (B, S, D), dtype=jnp.float32)
        Wq = jax.random.normal(ks[2], (D, D), dtype=jnp.float32) * scale
        bq = jnp.zeros((D,), dtype=jnp.float32)
        Wk = jax.random.normal(ks[3], (D, D), dtype=jnp.float32) * scale
        bk = jnp.zeros((D,), dtype=jnp.float32)
        Wv = jax.random.normal(ks[4], (D, D), dtype=jnp.float32) * scale
        bv = jnp.zeros((D,), dtype=jnp.float32)
        return {'x1': x1, 'x2': x2, 'Wq': Wq, 'bq': bq, 'Wk': Wk, 'bk': bk, 'Wv': Wv, 'bv': bv}
    _L1_xattn_all = _L1_xattn_setup()
    _L1_xattn_in = {k: v for k, v in _L1_xattn_all.items() if k in ('Wq', 'bq', 'Wk', 'bk', 'Wv', 'bv')}
    del _L1_xattn_all

    def _L1_ffn_setup():
        import jax, jax.numpy as jnp
        import numpy as np
        EPS = 1e-05
        LN_EPS = 1e-05
        NUM_EXPERTS = 8
        TOP_K = 2
        HIDDEN = 256
        INTER = 512

        def _swiglu(x, wg, wu, wd):
            return jax.nn.silu(x @ wg) * (x @ wu) @ wd
        key = jax.random.key(seed)
        ks = jax.random.split(key, 10)
        B, S, H, I, E = (8, 1024, HIDDEN, INTER, NUM_EXPERTS)
        std_h = 1.0 / np.sqrt(H)
        std_i = 1.0 / np.sqrt(I)
        return {'x': jax.random.normal(ks[0], (B, S, H), dtype=jnp.float32), 'ln_scale': jnp.ones((H,), dtype=jnp.float32), 'ln_bias': jnp.zeros((H,), dtype=jnp.float32), 'gate_w': jax.random.normal(ks[1], (E, H), dtype=jnp.float32) * 0.01, 'Wg': jax.random.normal(ks[2], (E, H, I), dtype=jnp.float32) * std_h, 'Wu': jax.random.normal(ks[3], (E, H, I), dtype=jnp.float32) * std_h, 'Wd': jax.random.normal(ks[4], (E, I, H), dtype=jnp.float32) * std_i, 'sWg': jax.random.normal(ks[5], (H, I), dtype=jnp.float32) * std_h, 'sWu': jax.random.normal(ks[6], (H, I), dtype=jnp.float32) * std_h, 'sWd': jax.random.normal(ks[7], (I, H), dtype=jnp.float32) * std_i}
    _L1_ffn_all = _L1_ffn_setup()
    _L1_ffn_in = {k: v for k, v in _L1_ffn_all.items() if k in ('ln_scale', 'ln_bias', 'gate_w', 'Wg', 'Wu', 'Wd', 'sWg', 'sWu', 'sWd')}
    del _L1_ffn_all

    def _L2_xattn_setup():
        import jax, jax.numpy as jnp
        import numpy as np
        EMBED_DIM = 256
        N_HEADS = 16
        HEAD_DIM = EMBED_DIM // N_HEADS
        key = jax.random.key(seed)
        ks = jax.random.split(key, 8)
        B, Tq, Tk, C = (2, 512, 512, EMBED_DIM)
        s = 1.0 / np.sqrt(C)
        return {'query': jax.random.normal(ks[0], (B, Tq, C), jnp.float32), 'context': jax.random.normal(ks[1], (B, Tk, C), jnp.float32), 'Wq': jax.random.normal(ks[2], (C, C), jnp.float32) * s, 'bq': jnp.zeros((C,), jnp.float32), 'Wkv': jax.random.normal(ks[3], (C, 2 * C), jnp.float32) * s, 'bkv': jnp.zeros((2 * C,), jnp.float32), 'Wo': jax.random.normal(ks[4], (C, C), jnp.float32) * s, 'bo': jnp.zeros((C,), jnp.float32)}
    _L2_xattn_all = _L2_xattn_setup()
    _L2_xattn_in = {k: v for k, v in _L2_xattn_all.items() if k in ('Wq', 'bq', 'Wkv', 'bkv', 'Wo', 'bo')}
    del _L2_xattn_all

    def _L2_ffn_setup():
        import jax, jax.numpy as jnp
        import numpy as np
        B, S, D_MODEL, D_HIDDEN = (4, 512, 256, 1024)

        def act_quant(x):
            scale = 127.0 / jnp.clip(jnp.max(jnp.abs(x), axis=-1, keepdims=True), 1e-05)
            return jnp.clip(jnp.round(x * scale), -128, 127) / scale

        def weight_quant(w):
            scale = 1.0 / jnp.clip(jnp.mean(jnp.abs(w)), 1e-05)
            return jnp.clip(jnp.round(w * scale), -1, 1) / scale

        def bit_linear(x, w):
            xq = x + jax.lax.stop_gradient(act_quant(x) - x)
            wq = w + jax.lax.stop_gradient(weight_quant(w) - w)
            return jnp.einsum('bsd,hd->bsh', xq, wq)

        def depthwise_conv1d(x_bcl, w, b):
            y = jax.lax.conv_general_dilated(x_bcl, w, window_strides=(1,), padding=[(1, 1)], dimension_numbers=('NCH', 'OIH', 'NCH'), feature_group_count=x_bcl.shape[1])
            return y + b[None, :, None]
        key = jax.random.key(seed)
        ks = jax.random.split(key, 5)
        lim1 = 1.0 / np.sqrt(D_MODEL)
        lim2 = 1.0 / np.sqrt(D_HIDDEN)
        limc = 1.0 / np.sqrt(3.0)
        return {'x': jax.random.normal(ks[0], (B, S, D_MODEL), dtype=jnp.float32), 'w1': jax.random.uniform(ks[1], (D_HIDDEN, D_MODEL), jnp.float32, -lim1, lim1), 'conv_w': jax.random.uniform(ks[2], (D_HIDDEN, 1, 3), jnp.float32, -limc, limc), 'conv_b': jax.random.uniform(ks[3], (D_HIDDEN,), jnp.float32, -limc, limc), 'w2': jax.random.uniform(ks[4], (D_MODEL, D_HIDDEN), jnp.float32, -lim2, lim2)}
    _L2_ffn_all = _L2_ffn_setup()
    _L2_ffn_in = {k: v for k, v in _L2_ffn_all.items() if k in ('w1', 'conv_w', 'conv_b', 'w2')}
    del _L2_ffn_all

    def _L3_xattn_setup():
        import jax, jax.numpy as jnp
        import numpy as np
        HID = 256
        HEADS = 16
        HEAD_DIM = HID // HEADS
        MAX_REL = 2

        def _rel_embeddings(table, length_q, length_k):
            dist = jnp.arange(length_k)[None, :] - jnp.arange(length_q)[:, None]
            idx = jnp.clip(dist, -MAX_REL, MAX_REL) + MAX_REL
            return table[idx]
        key = jax.random.key(seed)
        ks = jax.random.split(key, 16)
        B, L = (2, 512)
        s = 1.0 / np.sqrt(HID)
        inp = {'query': jax.random.normal(ks[0], (B, L, HID), jnp.float32), 'key': jax.random.normal(ks[1], (B, L, HID), jnp.float32), 'value': jax.random.normal(ks[2], (B, L, HID), jnp.float32), 'Wq': jax.random.normal(ks[3], (HID, HID), jnp.float32) * s, 'bq': jnp.zeros((HID,), jnp.float32), 'Wk': jax.random.normal(ks[4], (HID, HID), jnp.float32) * s, 'bk': jnp.zeros((HID,), jnp.float32), 'Wv': jax.random.normal(ks[5], (HID, HID), jnp.float32) * s, 'bv': jnp.zeros((HID,), jnp.float32), 'Wo': jax.random.normal(ks[6], (HID, HID), jnp.float32) * s, 'bo': jnp.zeros((HID,), jnp.float32), 'rel_k': jax.random.normal(ks[7], (2 * MAX_REL + 1, HEAD_DIM), jnp.float32) * 0.1, 'rel_v': jax.random.normal(ks[8], (2 * MAX_REL + 1, HEAD_DIM), jnp.float32) * 0.1}
        return inp
    _L3_xattn_all = _L3_xattn_setup()
    _L3_xattn_in = {k: v for k, v in _L3_xattn_all.items() if k in ('Wq', 'bq', 'Wk', 'bk', 'Wv', 'bv', 'Wo', 'bo', 'rel_k', 'rel_v')}
    del _L3_xattn_all

    def _L3_ffn_setup():
        import jax, jax.numpy as jnp
        import numpy as np
        DIM = 256
        DEPTH = 6
        HEADS = 16
        DIM_HEAD = 64
        WINDOW = 64
        INNER = HEADS * DIM_HEAD
        DIM_INNER = int(DIM * 4 * 2 / 3)
        QK_SCALE = 8.0

        def shift_tokens(t):
            a, s = jnp.split(t, 2, -1)
            s = jnp.pad(s, ((0, 0), (1, 0), (0, 0)))[:, :-1]
            return jnp.concatenate([a, s], -1)

        def l2norm(t):
            return t / jnp.maximum(jnp.linalg.norm(t, axis=-1, keepdims=True), 1e-12)

        def rotate_half(x):
            x1, x2 = jnp.split(x, 2, -1)
            return jnp.concatenate([-x2, x1], -1)

        def rotary_tables(n):
            half = jnp.arange(0, DIM_HEAD, 2, dtype=jnp.float32)
            inv_freq = 1.0 / 10000.0 ** (half / DIM_HEAD)
            t = jnp.arange(n, dtype=jnp.float32)
            freqs = t[:, None] * inv_freq[None, :]
            freqs = jnp.concatenate([freqs, freqs], -1)
            base_scale = (half + 0.4 * DIM_HEAD) / (1.4 * DIM_HEAD)
            power = (t - n // 2) / (WINDOW // 2)
            scale = base_scale[None, :] ** power[:, None]
            scale = jnp.concatenate([scale, scale], -1)
            return (freqs, scale)

        def local_attention(q, k, v):
            b, h, n, d = q.shape
            w = WINDOW
            nw = n // w
            bq = q.reshape(b, h, nw, w, d)
            bk = k.reshape(b, h, nw, w, d)
            bv = v.reshape(b, h, nw, w, d)

            def look(t):
                p = jnp.pad(t, ((0, 0), (0, 0), (1, 0), (0, 0), (0, 0)))
                return jnp.concatenate([p[:, :, :nw], p[:, :, 1:]], axis=3)
            bk2, bv2 = (look(bk), look(bv))
            seq = jnp.arange(n).reshape(nw, w)
            seq_p = jnp.pad(seq, ((1, 0), (0, 0)), constant_values=-1)
            jt = jnp.concatenate([seq_p[:nw], seq_p[1:]], axis=1)
            it = seq[:, :, None]
            jb = jt[:, None, :]
            mask = (it < jb) | (it > jb + w) | (jb == -1)
            sim = jnp.einsum('bhwie,bhwje->bhwij', bq, bk2) * QK_SCALE
            sim = jnp.where(mask, -jnp.finfo(sim.dtype).max, sim)
            attn = jax.nn.softmax(sim, -1)
            out = jnp.einsum('bhwij,bhwje->bhwie', attn, bv2)
            return out.reshape(b, h, n, d)

        def attn_layer(x, Wqkv, qs, ksc, Wo):
            b, n, _ = x.shape
            qkv = x @ Wqkv
            q, k, v = jnp.split(qkv, 3, -1)
            sh = lambda t: t.reshape(b, n, HEADS, DIM_HEAD).transpose(0, 2, 1, 3)
            q, k, v = (sh(q), sh(k), sh(v))
            q = l2norm(q) * qs
            k = l2norm(k) * ksc
            freqs, scale = rotary_tables(n)
            cos, sin = (jnp.cos(freqs), jnp.sin(freqs))
            q = q * cos * scale + rotate_half(q) * sin * scale
            inv = 1.0 / scale
            k = k * cos * inv + rotate_half(k) * sin * inv
            out = local_attention(q, k, v)
            out = out.transpose(0, 2, 1, 3).reshape(b, n, INNER)
            return out @ Wo

        def ffn_layer(x, g, bln, W1, b1, W2, b2):
            mu = x.mean(-1, keepdims=True)
            var = ((x - mu) ** 2).mean(-1, keepdims=True)
            xn = (x - mu) / jnp.sqrt(var + 1e-05) * g + bln
            hg = xn @ W1 + b1
            a, gate = jnp.split(hg, 2, -1)
            return a * jax.nn.gelu(gate, approximate=False) @ W2 + b2
        key = jax.random.key(seed)
        ks = jax.random.split(key, 8)
        B, N = (2, 512)
        init = lambda k, shape: jax.random.normal(k, shape, jnp.float32) * 0.02
        return {'x': jax.random.normal(ks[0], (B, N, DIM), jnp.float32), 'Wqkv': init(ks[1], (DEPTH, DIM, 3 * INNER)), 'q_scale': jnp.ones((DEPTH, DIM_HEAD), jnp.float32), 'k_scale': jnp.ones((DEPTH, DIM_HEAD), jnp.float32), 'Wo': init(ks[2], (DEPTH, INNER, DIM)), 'ln_g': jnp.ones((DEPTH, DIM), jnp.float32), 'ln_b': jnp.zeros((DEPTH, DIM), jnp.float32), 'W1': init(ks[3], (DEPTH, DIM, 2 * DIM_INNER)), 'b1': jnp.zeros((DEPTH, 2 * DIM_INNER), jnp.float32), 'W2': init(ks[4], (DEPTH, DIM_INNER, DIM)), 'b2': jnp.zeros((DEPTH, DIM), jnp.float32)}
    _L3_ffn_all = _L3_ffn_setup()
    _L3_ffn_in = {k: v for k, v in _L3_ffn_all.items() if k in ('Wqkv', 'q_scale', 'k_scale', 'Wo', 'ln_g', 'ln_b', 'W1', 'b1', 'W2', 'b2')}
    del _L3_ffn_all
    return {'x': x, 'ctx_1024': ctx_1024, 'g_xattn': g_xattn, 'g_ffn': g_ffn, 'L0_xattn_Wq': _L0_xattn_in['Wq'], 'L0_xattn_bq': _L0_xattn_in['bq'], 'L0_xattn_Wk': _L0_xattn_in['Wk'], 'L0_xattn_bk': _L0_xattn_in['bk'], 'L0_xattn_Wv': _L0_xattn_in['Wv'], 'L0_xattn_bv': _L0_xattn_in['bv'], 'L0_ffn_w_gate': _L0_ffn_in['w_gate'], 'L0_ffn_w_up': _L0_ffn_in['w_up'], 'L0_ffn_w_down': _L0_ffn_in['w_down'], 'L1_xattn_Wq': _L1_xattn_in['Wq'], 'L1_xattn_bq': _L1_xattn_in['bq'], 'L1_xattn_Wk': _L1_xattn_in['Wk'], 'L1_xattn_bk': _L1_xattn_in['bk'], 'L1_xattn_Wv': _L1_xattn_in['Wv'], 'L1_xattn_bv': _L1_xattn_in['bv'], 'L1_ffn_ln_scale': _L1_ffn_in['ln_scale'], 'L1_ffn_ln_bias': _L1_ffn_in['ln_bias'], 'L1_ffn_gate_w': _L1_ffn_in['gate_w'], 'L1_ffn_Wg': _L1_ffn_in['Wg'], 'L1_ffn_Wu': _L1_ffn_in['Wu'], 'L1_ffn_Wd': _L1_ffn_in['Wd'], 'L1_ffn_sWg': _L1_ffn_in['sWg'], 'L1_ffn_sWu': _L1_ffn_in['sWu'], 'L1_ffn_sWd': _L1_ffn_in['sWd'], 'L2_xattn_Wq': _L2_xattn_in['Wq'], 'L2_xattn_bq': _L2_xattn_in['bq'], 'L2_xattn_Wkv': _L2_xattn_in['Wkv'], 'L2_xattn_bkv': _L2_xattn_in['bkv'], 'L2_xattn_Wo': _L2_xattn_in['Wo'], 'L2_xattn_bo': _L2_xattn_in['bo'], 'L2_ffn_w1': _L2_ffn_in['w1'], 'L2_ffn_conv_w': _L2_ffn_in['conv_w'], 'L2_ffn_conv_b': _L2_ffn_in['conv_b'], 'L2_ffn_w2': _L2_ffn_in['w2'], 'L3_xattn_Wq': _L3_xattn_in['Wq'], 'L3_xattn_bq': _L3_xattn_in['bq'], 'L3_xattn_Wk': _L3_xattn_in['Wk'], 'L3_xattn_bk': _L3_xattn_in['bk'], 'L3_xattn_Wv': _L3_xattn_in['Wv'], 'L3_xattn_bv': _L3_xattn_in['bv'], 'L3_xattn_Wo': _L3_xattn_in['Wo'], 'L3_xattn_bo': _L3_xattn_in['bo'], 'L3_xattn_rel_k': _L3_xattn_in['rel_k'], 'L3_xattn_rel_v': _L3_xattn_in['rel_v'], 'L3_ffn_Wqkv': _L3_ffn_in['Wqkv'], 'L3_ffn_q_scale': _L3_ffn_in['q_scale'], 'L3_ffn_k_scale': _L3_ffn_in['k_scale'], 'L3_ffn_Wo': _L3_ffn_in['Wo'], 'L3_ffn_ln_g': _L3_ffn_in['ln_g'], 'L3_ffn_ln_b': _L3_ffn_in['ln_b'], 'L3_ffn_W1': _L3_ffn_in['W1'], 'L3_ffn_b1': _L3_ffn_in['b1'], 'L3_ffn_W2': _L3_ffn_in['W2'], 'L3_ffn_b2': _L3_ffn_in['b2']}

def reference(x, ctx_1024, g_xattn, g_ffn, L0_xattn_Wq, L0_xattn_bq, L0_xattn_Wk, L0_xattn_bk, L0_xattn_Wv, L0_xattn_bv, L0_ffn_w_gate, L0_ffn_w_up, L0_ffn_w_down, L1_xattn_Wq, L1_xattn_bq, L1_xattn_Wk, L1_xattn_bk, L1_xattn_Wv, L1_xattn_bv, L1_ffn_ln_scale, L1_ffn_ln_bias, L1_ffn_gate_w, L1_ffn_Wg, L1_ffn_Wu, L1_ffn_Wd, L1_ffn_sWg, L1_ffn_sWu, L1_ffn_sWd, L2_xattn_Wq, L2_xattn_bq, L2_xattn_Wkv, L2_xattn_bkv, L2_xattn_Wo, L2_xattn_bo, L2_ffn_w1, L2_ffn_conv_w, L2_ffn_conv_b, L2_ffn_w2, L3_xattn_Wq, L3_xattn_bq, L3_xattn_Wk, L3_xattn_bk, L3_xattn_Wv, L3_xattn_bv, L3_xattn_Wo, L3_xattn_bo, L3_xattn_rel_k, L3_xattn_rel_v, L3_ffn_Wqkv, L3_ffn_q_scale, L3_ffn_k_scale, L3_ffn_Wo, L3_ffn_ln_g, L3_ffn_ln_b, L3_ffn_W1, L3_ffn_b1, L3_ffn_W2, L3_ffn_b2):
    import jax
    import jax.numpy as jnp

    def _L0_xattn_ref(hidden_states, external_embeddings, Wq, bq, Wk, bk, Wv, bv):
        import jax, jax.numpy as jnp
        import numpy as np
        B, S, E, H = (4, 512, 128, 256)
        q = hidden_states @ Wq + bq
        k_tok = hidden_states @ Wk + bk
        v_tok = hidden_states @ Wv + bv
        k_ext = external_embeddings @ Wk + bk
        v_ext = external_embeddings @ Wv + bv
        s_self = jnp.einsum('bsh,bsh->bs', q, k_tok)[..., None]
        s_ext = jnp.einsum('bsh,beh->bse', q, k_ext)
        scores = jnp.concatenate([s_self, s_ext], axis=-1)
        probs = jax.nn.softmax(scores, axis=-1)
        ctx = probs[..., :1] * v_tok + jnp.einsum('bse,beh->bsh', probs[..., 1:], v_ext)
        return ctx

    def _L0_ffn_ref(x, w_gate, w_up, w_down):
        import jax, jax.numpy as jnp
        import numpy as np
        BLOCK = 32
        W_BITS = 4
        ACT_BITS = 16

        def act_qdq(x):
            qmax = 2.0 ** (ACT_BITS - 1) - 1.0
            scale = jnp.maximum(jnp.max(jnp.abs(x)) / qmax, 1e-12)
            return jnp.clip(jnp.round(x / scale), -qmax - 1.0, qmax) * scale

        def fixed_qdq_u16(x):
            scale = 1.0 / 65536.0
            return jnp.clip(jnp.round(x / scale), 0.0, 65535.0) * scale

        def lpbq_dequant(w):
            O, I = w.shape
            qmax = 2.0 ** (W_BITS - 1) - 1.0
            wb = w.reshape(O, I // BLOCK, BLOCK)
            s = jnp.maximum(jnp.max(jnp.abs(wb), axis=-1, keepdims=True) / qmax, 1e-12)
            wq = jnp.clip(jnp.round(wb / s), -qmax - 1.0, qmax) * s
            return wq.reshape(O, I)
        x = act_qdq(x)
        up = act_qdq(x @ lpbq_dequant(w_up).T)
        gate = act_qdq(x @ lpbq_dequant(w_gate).T)
        sig = fixed_qdq_u16(jax.nn.sigmoid(gate))
        gate = act_qdq(gate * sig)
        o = act_qdq(gate * up)
        return o @ lpbq_dequant(w_down).T

    def _L1_xattn_ref(x1, x2, Wq, bq, Wk, bk, Wv, bv):
        import jax, jax.numpy as jnp
        import numpy as np
        DIM = 256
        q = jnp.einsum('bsd,ed->bse', x1, Wq) + bq
        k = jnp.einsum('bsd,ed->bse', x2, Wk) + bk
        v = jnp.einsum('bsd,ed->bse', x2, Wv) + bv
        scale = jnp.asarray(q.shape[-1], q.dtype) ** (-0.5)
        attn = jnp.einsum('bqd,bkd->bqk', q, k) * scale
        attn = jax.nn.softmax(attn, axis=-1)
        return jnp.einsum('bqk,bkd->bqd', attn, v)

    def _L1_ffn_ref(x, ln_scale, ln_bias, gate_w, Wg, Wu, Wd, sWg, sWu, sWd):
        import jax, jax.numpy as jnp
        import numpy as np
        EPS = 1e-05
        LN_EPS = 1e-05
        NUM_EXPERTS = 8
        TOP_K = 2
        HIDDEN = 256
        INTER = 512

        def _swiglu(x, wg, wu, wd):
            return jax.nn.silu(x @ wg) * (x @ wu) @ wd
        B, S, H = x.shape
        xf = x.reshape(-1, H)
        mu = jnp.mean(xf, axis=-1, keepdims=True)
        var = jnp.var(xf, axis=-1, keepdims=True)
        xn = (xf - mu) * jax.lax.rsqrt(var + LN_EPS) * ln_scale + ln_bias
        logits = xn @ gate_w.T
        probs = jax.nn.softmax(logits, axis=-1)
        tk_probs, tk_idx = jax.lax.top_k(probs, TOP_K)
        tk_probs = tk_probs / (jnp.sum(tk_probs, axis=-1, keepdims=True) + EPS)
        onehot = tk_idx[..., None] == jnp.arange(NUM_EXPERTS)[None, None, :]
        w = jnp.sum(tk_probs[..., None] * onehot.astype(tk_probs.dtype), axis=1)
        out = _swiglu(xf, sWg, sWu, sWd)
        for e in range(NUM_EXPERTS):
            out = out + w[:, e:e + 1] * _swiglu(xf, Wg[e], Wu[e], Wd[e])
        return out.reshape(B, S, H)

    def _L2_xattn_ref(query, context, Wq, bq, Wkv, bkv, Wo, bo):
        import jax, jax.numpy as jnp
        import numpy as np
        EMBED_DIM = 256
        N_HEADS = 16
        HEAD_DIM = EMBED_DIM // N_HEADS
        B, Tq, C = query.shape
        Tk = context.shape[1]
        H, D = (N_HEADS, HEAD_DIM)
        q = (query @ Wq + bq).reshape(B, Tq, H, D)
        kv = (context @ Wkv + bkv).reshape(B, Tk, 2, H, D)
        k = kv[:, :, 0]
        v = kv[:, :, 1]
        scale = D ** (-0.5)
        attn = jnp.einsum('bqhd,bkhd->bhqk', q, k) * scale
        attn = jax.nn.softmax(attn, axis=-1)
        out = jnp.einsum('bhqk,bkhd->bqhd', attn, v).reshape(B, Tq, C)
        return out @ Wo + bo

    def _L2_ffn_ref(x, w1, conv_w, conv_b, w2):
        import jax, jax.numpy as jnp
        import numpy as np
        B, S, D_MODEL, D_HIDDEN = (4, 512, 256, 1024)

        def act_quant(x):
            scale = 127.0 / jnp.clip(jnp.max(jnp.abs(x), axis=-1, keepdims=True), 1e-05)
            return jnp.clip(jnp.round(x * scale), -128, 127) / scale

        def weight_quant(w):
            scale = 1.0 / jnp.clip(jnp.mean(jnp.abs(w)), 1e-05)
            return jnp.clip(jnp.round(w * scale), -1, 1) / scale

        def bit_linear(x, w):
            xq = x + jax.lax.stop_gradient(act_quant(x) - x)
            wq = w + jax.lax.stop_gradient(weight_quant(w) - w)
            return jnp.einsum('bsd,hd->bsh', xq, wq)

        def depthwise_conv1d(x_bcl, w, b):
            y = jax.lax.conv_general_dilated(x_bcl, w, window_strides=(1,), padding=[(1, 1)], dimension_numbers=('NCH', 'OIH', 'NCH'), feature_group_count=x_bcl.shape[1])
            return y + b[None, :, None]
        h = bit_linear(x, w1)
        h = depthwise_conv1d(h.transpose(0, 2, 1), conv_w, conv_b)
        h = h.transpose(0, 2, 1)
        h = jax.nn.silu(h)
        return bit_linear(h, w2)

    def _L3_xattn_ref(query, key, value, Wq, bq, Wk, bk, Wv, bv, Wo, bo, rel_k, rel_v):
        import jax, jax.numpy as jnp
        import numpy as np
        HID = 256
        HEADS = 16
        HEAD_DIM = HID // HEADS
        MAX_REL = 2

        def _rel_embeddings(table, length_q, length_k):
            dist = jnp.arange(length_k)[None, :] - jnp.arange(length_q)[:, None]
            idx = jnp.clip(dist, -MAX_REL, MAX_REL) + MAX_REL
            return table[idx]
        B, Lq, _ = query.shape
        Lk = key.shape[1]
        q = query @ Wq + bq
        k = key @ Wk + bk
        v = value @ Wv + bv
        qh = q.reshape(B, Lq, HEADS, HEAD_DIM).transpose(0, 2, 1, 3)
        kh = k.reshape(B, Lk, HEADS, HEAD_DIM).transpose(0, 2, 1, 3)
        vh = v.reshape(B, Lk, HEADS, HEAD_DIM).transpose(0, 2, 1, 3)
        attn1 = jnp.einsum('bhqd,bhkd->bhqk', qh, kh)
        rk = _rel_embeddings(rel_k, Lq, Lk)
        attn2 = jnp.einsum('bhqd,qkd->bhqk', qh, rk)
        scale = jnp.sqrt(jnp.asarray(HEAD_DIM, query.dtype))
        attn = jax.nn.softmax((attn1 + attn2) / scale, axis=-1)
        w1 = jnp.einsum('bhqk,bhkd->bhqd', attn, vh)
        rv = _rel_embeddings(rel_v, Lq, Lk)
        w2 = jnp.einsum('bhqk,qkd->bhqd', attn, rv)
        x = (w1 + w2).transpose(0, 2, 1, 3).reshape(B, Lq, HID)
        return x @ Wo + bo

    def _L3_ffn_ref(x, Wqkv, q_scale, k_scale, Wo, ln_g, ln_b, W1, b1, W2, b2):
        import jax, jax.numpy as jnp
        import numpy as np
        DIM = 256
        DEPTH = 6
        HEADS = 16
        DIM_HEAD = 64
        WINDOW = 64
        INNER = HEADS * DIM_HEAD
        DIM_INNER = int(DIM * 4 * 2 / 3)
        QK_SCALE = 8.0

        def shift_tokens(t):
            a, s = jnp.split(t, 2, -1)
            s = jnp.pad(s, ((0, 0), (1, 0), (0, 0)))[:, :-1]
            return jnp.concatenate([a, s], -1)

        def l2norm(t):
            return t / jnp.maximum(jnp.linalg.norm(t, axis=-1, keepdims=True), 1e-12)

        def rotate_half(x):
            x1, x2 = jnp.split(x, 2, -1)
            return jnp.concatenate([-x2, x1], -1)

        def rotary_tables(n):
            half = jnp.arange(0, DIM_HEAD, 2, dtype=jnp.float32)
            inv_freq = 1.0 / 10000.0 ** (half / DIM_HEAD)
            t = jnp.arange(n, dtype=jnp.float32)
            freqs = t[:, None] * inv_freq[None, :]
            freqs = jnp.concatenate([freqs, freqs], -1)
            base_scale = (half + 0.4 * DIM_HEAD) / (1.4 * DIM_HEAD)
            power = (t - n // 2) / (WINDOW // 2)
            scale = base_scale[None, :] ** power[:, None]
            scale = jnp.concatenate([scale, scale], -1)
            return (freqs, scale)

        def local_attention(q, k, v):
            b, h, n, d = q.shape
            w = WINDOW
            nw = n // w
            bq = q.reshape(b, h, nw, w, d)
            bk = k.reshape(b, h, nw, w, d)
            bv = v.reshape(b, h, nw, w, d)

            def look(t):
                p = jnp.pad(t, ((0, 0), (0, 0), (1, 0), (0, 0), (0, 0)))
                return jnp.concatenate([p[:, :, :nw], p[:, :, 1:]], axis=3)
            bk2, bv2 = (look(bk), look(bv))
            seq = jnp.arange(n).reshape(nw, w)
            seq_p = jnp.pad(seq, ((1, 0), (0, 0)), constant_values=-1)
            jt = jnp.concatenate([seq_p[:nw], seq_p[1:]], axis=1)
            it = seq[:, :, None]
            jb = jt[:, None, :]
            mask = (it < jb) | (it > jb + w) | (jb == -1)
            sim = jnp.einsum('bhwie,bhwje->bhwij', bq, bk2) * QK_SCALE
            sim = jnp.where(mask, -jnp.finfo(sim.dtype).max, sim)
            attn = jax.nn.softmax(sim, -1)
            out = jnp.einsum('bhwij,bhwje->bhwie', attn, bv2)
            return out.reshape(b, h, n, d)

        def attn_layer(x, Wqkv, qs, ksc, Wo):
            b, n, _ = x.shape
            qkv = x @ Wqkv
            q, k, v = jnp.split(qkv, 3, -1)
            sh = lambda t: t.reshape(b, n, HEADS, DIM_HEAD).transpose(0, 2, 1, 3)
            q, k, v = (sh(q), sh(k), sh(v))
            q = l2norm(q) * qs
            k = l2norm(k) * ksc
            freqs, scale = rotary_tables(n)
            cos, sin = (jnp.cos(freqs), jnp.sin(freqs))
            q = q * cos * scale + rotate_half(q) * sin * scale
            inv = 1.0 / scale
            k = k * cos * inv + rotate_half(k) * sin * inv
            out = local_attention(q, k, v)
            out = out.transpose(0, 2, 1, 3).reshape(b, n, INNER)
            return out @ Wo

        def ffn_layer(x, g, bln, W1, b1, W2, b2):
            mu = x.mean(-1, keepdims=True)
            var = ((x - mu) ** 2).mean(-1, keepdims=True)
            xn = (x - mu) / jnp.sqrt(var + 1e-05) * g + bln
            hg = xn @ W1 + b1
            a, gate = jnp.split(hg, 2, -1)
            return a * jax.nn.gelu(gate, approximate=False) @ W2 + b2
        for i in range(DEPTH):
            x = attn_layer(shift_tokens(x), Wqkv[i], q_scale[i], k_scale[i], Wo[i]) + x
            x = ffn_layer(shift_tokens(x), ln_g[i], ln_b[i], W1[i], b1[i], W2[i], b2[i]) + x
        return x
    x = x + jnp.tanh(g_xattn[0]) * _L0_xattn_ref(_layernorm(x, axis=-1), ctx_1024, L0_xattn_Wq, L0_xattn_bq, L0_xattn_Wk, L0_xattn_bk, L0_xattn_Wv, L0_xattn_bv)
    x = x + jnp.tanh(g_ffn[0]) * _L0_ffn_ref(_layernorm(x, axis=-1), L0_ffn_w_gate, L0_ffn_w_up, L0_ffn_w_down)
    x = x + jnp.tanh(g_xattn[1]) * _L1_xattn_ref(_layernorm(x, axis=-1), ctx_1024, L1_xattn_Wq, L1_xattn_bq, L1_xattn_Wk, L1_xattn_bk, L1_xattn_Wv, L1_xattn_bv)
    x = x + jnp.tanh(g_ffn[1]) * _L1_ffn_ref(_layernorm(x, axis=-1), L1_ffn_ln_scale, L1_ffn_ln_bias, L1_ffn_gate_w, L1_ffn_Wg, L1_ffn_Wu, L1_ffn_Wd, L1_ffn_sWg, L1_ffn_sWu, L1_ffn_sWd)
    x = x + jnp.tanh(g_xattn[2]) * _L2_xattn_ref(_layernorm(x, axis=-1), ctx_1024, L2_xattn_Wq, L2_xattn_bq, L2_xattn_Wkv, L2_xattn_bkv, L2_xattn_Wo, L2_xattn_bo)
    x = x + jnp.tanh(g_ffn[2]) * _L2_ffn_ref(_layernorm(x, axis=-1), L2_ffn_w1, L2_ffn_conv_w, L2_ffn_conv_b, L2_ffn_w2)
    x = x + jnp.tanh(g_xattn[3]) * _L3_xattn_ref(_layernorm(x, axis=-1), ctx_1024, ctx_1024, L3_xattn_Wq, L3_xattn_bq, L3_xattn_Wk, L3_xattn_bk, L3_xattn_Wv, L3_xattn_bv, L3_xattn_Wo, L3_xattn_bo, L3_xattn_rel_k, L3_xattn_rel_v)
    x = x + jnp.tanh(g_ffn[3]) * _L3_ffn_ref(_layernorm(x, axis=-1), L3_ffn_Wqkv, L3_ffn_q_scale, L3_ffn_k_scale, L3_ffn_Wo, L3_ffn_ln_g, L3_ffn_ln_b, L3_ffn_W1, L3_ffn_b1, L3_ffn_W2, L3_ffn_b2)
    return x

_drawn_inputs = setup_inputs


def setup_inputs(seed=0):
    import zlib

    import numpy as np

    out = dict(_drawn_inputs(seed))
    spreads = {'L1_xattn_bq': (0.0, 0.1),
     'L1_xattn_bk': (0.0, 2.0),
     'L1_xattn_bv': (0.0, 0.1),
     'L1_ffn_ln_scale': (1.0, 0.2),
     'L1_ffn_ln_bias': (0.0, 0.1),
     'L2_xattn_bq': (0.0, 0.751),
     'L2_xattn_bkv': (0.0, 0.1),
     'L2_xattn_bo': (0.0, 0.1),
     'L3_xattn_bq': (0.0, 0.671),
     'L3_xattn_bk': (0.0, 2.0),
     'L3_xattn_bv': (0.0, 0.1),
     'L3_xattn_bo': (0.0, 0.1),
     'L3_ffn_q_scale': (1.0, 0.6),
     'L3_ffn_k_scale': (1.0, 0.6),
     'L3_ffn_ln_g': (1.0, 0.6),
     'L3_ffn_ln_b': (0.0, 0.8),
     'L3_ffn_b1': (0.0, 0.699),
     'L3_ffn_b2': (0.0, 0.1)}
    factors = {'g_ffn': 23.88, 'L0_xattn_bk': 64.0, 'L3_xattn_rel_k': 34.616}
    for name, (base, spread) in spreads.items():
        noise = np.random.default_rng([zlib.crc32(name.encode()), seed]).standard_normal(out[name].shape)
        drawn = base * np.exp(spread * noise) if base else spread * noise
        out[name] = jnp.asarray(drawn.astype(out[name].dtype))
    for name, factor in factors.items():
        out[name] = (out[name] * factor).astype(out[name].dtype)
    return out
```

```python
from contextlib import ExitStack, contextmanager

import numpy as np
import concourse.bass as bass
from concourse import mybir

ALU = mybir.AluOpType
ACT = mybir.ActivationFunctionType
AX = mybir.AxisListType
F32 = mybir.dt.float32
BF16 = mybir.dt.bfloat16
F32R = mybir.dt.float32r
ABSMAX = bass.bass_isa.ReduceOp.absmax
RADD = bass.bass_isa.ReduceOp.add
ds = bass.ds

P = 128
B, S, D = 2, 1024, 256
C = D // P
T = B * S
G = 512
NG = T // G
GB = S // G
TG = G // P
E = 77
SP1 = S + 1
MAGIC = 12582912.0
EPS = 1e-5


@contextmanager
def semaphores(nc, stage, *names):
    with ExitStack() as s:
        sems = [s.enter_context(nc.semaphore(f"{stage}_{n}")) for n in names]
        yield sems
        with nc.Block(no_gpsimd_drain=True) as block:
            @block.sync
            def _(sp):
                for sem in sems:
                    sp.sem_clear(sem)


class Own:

    def __init__(self, eng, sem):
        self.eng, self.sem, self.n = eng, sem, 0

    def __call__(self, ins):
        self.n += 1
        ins.then_inc(self.sem, 1)
        self.eng.wait_ge(self.sem, self.n)


class Constants:

    def __init__(self, sb, A):
        self.ident, self.mean_w, self.ones = sb("ident", [P, P]), sb("mean_w", [P, P]), sb("ones", [P, P])
        self.last_row, self.eps = sb("last_row", [P, P]), sb("eps", [P, 1])
        self.head_of, self.head_cols, self.rel_mask = A["head_of"], A["head_cols"], A["rel_mask"]
        self.expert_iota = A["expert_iota"]


def bc(ap, axis, shape):
    return ap.unsqueeze(axis).to_broadcast(shape)


def layer_norm(nc, K, src, XN, tag, affine=None):
    with ExitStack() as s:
        sb = lambda n, sh: s.enter_context(nc.sbuf_tensor(f"{tag}_{n}", sh, F32))
        xsum = sb("xsum", [P, 2, G])
        sq = sb("sq", [P, 2, C, G])
        sqsum = sb("sqsum", [P, 2, G])
        lnv = sb("lnv", [P, 2, G])
        rstd = sb("rstd", [P, 2, G])
        mean_ps = s.enter_context(nc.psum_tensor(f"{tag}_mean", [P, 2, G], F32))
        var_ps = s.enter_context(nc.psum_tensor(f"{tag}_var", [P, 2, G], F32))
        with semaphores(nc, tag, "xsum", "mean", "centred", "squares", "sqsum", "var",
                        "lnv", "rstd", "scaled") as (
                xsum_ready, mean_ready, centred, squares, sqsum_ready, var_ready,
                lnv_ready, rstd_ready, scaled), nc.Block(no_gpsimd_drain=True) as block:

            @block.gpsimd
            def _(pool):
                for g in range(NG):
                    if g >= 2:
                        pool.wait_ge(mean_ready, g - 1)
                    nc.gpsimd.tensor_tensor(xsum[:, g % 2], src(0, g), src(1, g),
                                            ALU.add).then_inc(xsum_ready, 1)

            @block.tensor
            def _(pe):
                def mean(g):
                    pe.wait_ge(xsum_ready, g + 1)
                    if g >= 2:
                        pe.wait_ge(centred, g - 1)
                    nc.tensor.matmul(mean_ps[:, g % 2], K.mean_w[:, :], xsum[:, g % 2],
                                     start=True, stop=True).then_inc(mean_ready, 1)

                def var(g):
                    pe.wait_ge(sqsum_ready, g + 1)
                    if g >= 2:
                        pe.wait_ge(lnv_ready, g - 1)
                    nc.tensor.matmul(var_ps[:, g % 2], K.mean_w[:, :], sqsum[:, g % 2],
                                     start=True, stop=True).then_inc(var_ready, 1)
                for g in range(NG):
                    mean(g)
                    if g:
                        var(g - 1)
                var(NG - 1)

            @block.vector
            def _(dve):
                def centre(g):
                    dve.wait_ge(mean_ready, g + 1)
                    for c in range(C):
                        last = nc.vector.tensor_tensor(XN[:, c, g * G:(g + 1) * G], src(c, g),
                                                       mean_ps[:, g % 2], ALU.subtract)
                    last.then_inc(centred, 1)

                def sum_squares(g):
                    dve.wait_ge(squares, g + 1)
                    if g >= 2:
                        dve.wait_ge(var_ready, g - 1)
                    nc.vector.tensor_tensor(sqsum[:, g % 2], sq[:, g % 2, 0], sq[:, g % 2, 1],
                                            ALU.add).then_inc(sqsum_ready, 1)

                def scale(g):
                    dve.wait_ge(rstd_ready, g + 1)
                    for c in range(C):
                        view = XN[:, c, g * G:(g + 1) * G]
                        last = nc.vector.tensor_tensor(view, view, rstd[:, g % 2], ALU.mult)
                        last.then_inc(scaled, 1)
                    if affine is not None:
                        dve.wait_ge(scaled, C * (g + 1))
                        for c in range(C):
                            view = XN[:, c, g * G:(g + 1) * G]
                            nc.vector.tensor_scalar(view, view, affine[0][:, c:c + 1],
                                                    affine[1][:, c:c + 1], ALU.mult, ALU.add)
                for g in range(NG + 2):
                    if g < NG:
                        centre(g)
                    if 1 <= g <= NG:
                        sum_squares(g - 1)
                    if g >= 2:
                        scale(g - 2)

            @block.scalar
            def _(act):
                def square(g):
                    act.wait_ge(centred, g + 1)
                    if g >= 2:
                        act.wait_ge(sqsum_ready, g - 1)
                    nc.scalar.activation(sq[:, g % 2], XN[:, :, g * G:(g + 1) * G],
                                         ACT.Square).then_inc(squares, 1)

                def inverse_std(g):
                    act.wait_ge(var_ready, g + 1)
                    nc.scalar.activation(lnv[:, g % 2], var_ps[:, g % 2], ACT.Ln,
                                         bias=K.eps[:, 0:1]).then_inc(lnv_ready, 1)
                    act.wait_ge(lnv_ready, g + 1)
                    if g >= 2:
                        act.wait_ge(scaled, C * (g - 1))
                    nc.scalar.activation(rstd[:, g % 2], lnv[:, g % 2], ACT.Exp,
                                         scale=-0.5).then_inc(rstd_ready, 1)
                for g in range(NG + 1):
                    if g < NG:
                        square(g)
                    if g:
                        inverse_std(g - 1)


def wide_attention(nc, K, X, XN, ctxT, W, gate, tag, self_key, scale):
    M = E + 1 if self_key else E
    names = ("q", "k", "v")
    with ExitStack() as s:
        sb = lambda n, sh: s.enter_context(nc.sbuf_tensor(f"{tag}_{n}", sh, F32))
        w = {n: sb(f"w{n}", [P, C, D]) for n in names}
        b_col = {n: sb(f"b{n}", [P, C]) for n in names}
        bv_row = sb("bv_row", [P, D])
        kxT = sb("kxT", [P, C, B, E])
        vx = sb("vx", [P, B, D])

        with ExitStack() as s2:
            kx_ps = s2.enter_context(nc.psum_tensor(f"{tag}_kx_ps", [P, C, G], F32))
            vx_ps = s2.enter_context(nc.psum_tensor(f"{tag}_vx_ps", [P, B, G], F32))
            with semaphores(nc, f"{tag}_ctx", "loaded", "zeroed", "products") as (
                    loaded, zeroed, products), \
                    nc.Block(no_gpsimd_drain=True) as block:
                @block.sync
                def _(sp):
                    n = 0
                    for a in names:
                        sp.dma_start(w[a][:, :, :], W[f"w{a}"]).then_inc(loaded, 16)
                        sp.dma_start(b_col[a][:, :], W[f"b{a}"]).then_inc(loaded, 16)
                        n += 32
                    sp.dma_start(bv_row[:, :], W["bv_row"]).then_inc(loaded, 16)
                    sp.wait_ge(loaded, n + 16)

                @block.tensor
                def _(pe):
                    pe.wait_ge(loaded, 16 * 7)
                    for m in range(C):
                        for c in range(C):
                            nc.tensor.matmul(kx_ps[:, m, 0:B * E], w["k"][:, c, m * P:(m + 1) * P],
                                             ctxT[:, c, :], start=(c == 0), stop=(c == C - 1))
                    for b in range(B):
                        for c in range(C):
                            last = nc.tensor.matmul(vx_ps[0:E, b, 0:D], ctxT[:, c, b * E:(b + 1) * E],
                                                    w["v"][:, c, :], start=(c == 0), stop=(c == C - 1))
                    last.then_inc(products, 1)

                @block.vector
                def _(dve):
                    nc.vector.memset(vx[:, :, :], 0.0).then_inc(zeroed, 1)
                    dve.wait_ge(products, 1)
                    dve.wait_ge(zeroed, 1)
                    for m in range(C):
                        nc.vector.tensor_scalar(kxT[:, m].rearrange("p b e -> p (b e)"),
                                                kx_ps[:, m, 0:B * E], b_col["k"][:, m:m + 1], None,
                                                ALU.add)
                    for b in range(B):
                        nc.vector.tensor_tensor(vx[0:E, b], vx_ps[0:E, b, 0:D], bv_row[0:E, :],
                                                ALU.add)

        kg = sb("kg", [P, C, E])
        vg = sb("vg", [P, D])
        q_sb = sb("q", [P, C, G])
        qk_sb = sb("qk", [P, C, G])
        v_sb = sb("v", [P, C, G])
        t_sb = sb("t", [P, C, G])
        prob = sb("prob", [P, TG, M])
        stat = sb("stat", [P, 3, TG])
        pT = sb("pT", [P, G])
        proj_ps = s.enter_context(nc.psum_tensor(f"{tag}_proj", [P, 2, G], F32))
        s_ps = s.enter_context(nc.psum_tensor(f"{tag}_s", [P, TG, P], F32))
        pT_ps = s.enter_context(nc.psum_tensor(f"{tag}_pT_ps", [P, G], F32))
        o_ps = s.enter_context(nc.psum_tensor(f"{tag}_o", [P, C, G], F32))
        p0_ps = s.enter_context(nc.psum_tensor(f"{tag}_p0", [P, G], F32))
        which = [(n, m) for n in (names if self_key else ("q",)) for m in range(C)]

        with nc.Fori(0, B) as b, nc.Fori(0, GB) as h:
            cols = lambda c: X[:, c, ds(b * SP1 + h * G + 1, G)]
            xn = lambda c: XN[:, c, ds(b * S + h * G, G)]
            with semaphores(nc, tag, "staged", "proj", "taken", "scores", "maxed", "exped",
                            "prob", "probT", "pT", "out", "dve", "act") as (
                    staged, proj, taken, scores, maxed, exped, prob_ready, probT, pT_ready,
                    out_ready, dve_own, act_own), nc.Block(no_gpsimd_drain=True) as block:

                @block.tensor
                def _(pe):
                    for i, (n, m) in enumerate(which):
                        if i >= 2:
                            pe.wait_ge(taken, i - 1)
                        for c in range(C):
                            last = nc.tensor.matmul(proj_ps[:, i % 2], w[n][:, c, m * P:(m + 1) * P],
                                                    xn(c), start=(c == 0), stop=(c == C - 1))
                        last.then_inc(proj, 1)
                    pe.wait_ge(taken, len(which))
                    pe.wait_ge(staged, 2)
                    for t in range(TG):
                        tok = slice(t * P, (t + 1) * P)
                        for c in range(C):
                            last = nc.tensor.matmul(s_ps[:, t, 0:E], q_sb[:, c, tok], kg[:, c, :],
                                                    start=(c == 0), stop=(c == C - 1))
                        if self_key:
                            for c in range(C):
                                last = nc.tensor.matmul(s_ps[:, t, E:M], qk_sb[:, c, tok],
                                                        K.ones[:, 0:1], start=(c == 0), stop=(c == C - 1))
                    last.then_inc(scores, 1)
                    for t in range(TG):
                        pe.wait_ge(prob_ready, t + 1)
                        last = nc.tensor.transpose(pT_ps[0:M, t * P:(t + 1) * P], prob[:, t, :],
                                                   K.ident[:, :])
                    last.then_inc(probT, 1)
                    pe.wait_ge(pT_ready, 1)
                    if self_key:
                        nc.tensor.matmul(p0_ps[:, :], K.last_row[0:M, :], pT[0:M, :],
                                         start=True, stop=True)
                    for m in range(C):
                        last = nc.tensor.matmul(o_ps[:, m], vg[0:M, m * P:(m + 1) * P], pT[0:M, :],
                                                start=True, stop=True)
                    last.then_inc(out_ready, 1)

                @block.vector
                def _(dve):
                    own = Own(dve, dve_own)
                    nc.vector.tensor_copy(kg[:, :, :], kxT[:, :, ds(b, 1), :].rearrange(
                        "p c o e -> p (c o) e")).then_inc(staged, 1)
                    nc.vector.tensor_copy(vg[:, :], vx[:, ds(b, 1), :].rearrange(
                        "p o d -> p (o d)")).then_inc(staged, 1)
                    for i, (n, m) in enumerate(which):
                        dve.wait_ge(proj, i + 1)
                        src, bias = proj_ps[:, i % 2], b_col[n][:, m:m + 1]
                        if n == "q":
                            nc.vector.tensor_scalar(q_sb[:, m], src, bias, None, ALU.add).then_inc(taken, 1)
                            dve.wait_ge(taken, i + 1)
                        elif n == "k":
                            nc.vector.scalar_tensor_tensor(out=qk_sb[:, m], in0=src, scalar=bias,
                                                           in1=q_sb[:, m], op0=ALU.add,
                                                           op1=ALU.mult).then_inc(taken, 1)
                        else:
                            nc.vector.tensor_scalar(v_sb[:, m], src, bias, None, ALU.add).then_inc(taken, 1)
                    dve.wait_ge(scores, 1)
                    own(nc.vector.tensor_reduce(stat[:, 0, :], s_ps[:, :, 0:M], AX.X, ALU.max))
                    nc.vector.tensor_scalar(stat[:, 0, :], stat[:, 0, :], -scale, None,
                                            ALU.mult).then_inc(maxed, 1)
                    dve.wait_ge(exped, TG)
                    own(nc.vector.reciprocal(stat[:, 2, :], stat[:, 1, :]))
                    for t in range(TG):
                        nc.vector.tensor_scalar(prob[:, t, :], prob[:, t, :], stat[:, 2, t:t + 1], None,
                                                ALU.mult).then_inc(prob_ready, 1)
                    dve.wait_ge(probT, 1)
                    nc.vector.tensor_copy(pT[0:M, :], pT_ps[0:M, :]).then_inc(pT_ready, 1)
                    dve.wait_ge(out_ready, 1)
                    for m in range(C):
                        src = o_ps[:, m]
                        if self_key:
                            own(nc.vector.tensor_tensor(t_sb[:, m], v_sb[:, m], p0_ps[:, :], ALU.mult))
                            own(nc.vector.tensor_tensor(t_sb[:, m], t_sb[:, m], o_ps[:, m], ALU.add))
                            src = t_sb[:, m]
                        nc.vector.scalar_tensor_tensor(out=cols(m), in0=src, scalar=gate, in1=cols(m),
                                                       op0=ALU.mult, op1=ALU.add)

                @block.scalar
                def _(act):
                    act.wait_ge(maxed, 1)
                    for t in range(TG):
                        nc.scalar.activation(prob[:, t, :], s_ps[:, t, 0:M], ACT.Exp,
                                             bias=stat[:, 0, t:t + 1], scale=scale,
                                             accum_out=stat[:, 1, t:t + 1]).then_inc(exped, 1)


NE, TOPK, FE = 8, 2, 512
FC = FE // P
WE = 2 * C * FE + FC * D


def router(nc, K, XN2, gate_w, w_dram, tag):
    NT = T // P
    with ExitStack() as s:
        sb = lambda n, sh: s.enter_context(nc.sbuf_tensor(f"{tag}_{n}", sh, F32))
        gw = sb("gw", [P, C, NE])
        iota = sb("iota", [P, NE])
        prob = sb("prob", [P, NT, NE])
        rest = sb("rest", [P, NT, NE])
        pick = sb("pick", [P, 2, NT, NE])
        tmp = sb("tmp", [P, NT, NE])
        col = sb("col", [P, 6, NT])
        w9 = sb("w9", [P, NT, NE + 1])
        wT = sb("wT", [P, T])
        lg_ps = s.enter_context(nc.psum_tensor(f"{tag}_lg", [P, NT, NE], F32))
        wT_ps = s.enter_context(nc.psum_tensor(f"{tag}_wT_ps", [P, T], F32))
        full = [P, NT, NE]
        with semaphores(nc, tag, "loaded", "logits", "exped", "maxed", "weights", "turned", "copied",
                        "stored", "own") as (loaded, logits, exped, maxed, weighted, turned, copied,
                                             stored, dve_own), \
                nc.Block(no_gpsimd_drain=True) as block:
            @block.sync
            def _(sp):
                sp.dma_start(gw[:, :, :], gate_w).then_inc(loaded, 16)
                sp.dma_start(iota[:, :], K.expert_iota).then_inc(loaded, 16)
                sp.wait_ge(copied, 1)
                sp.dma_start(w_dram, wT[0:NE + 1, :]).then_inc(stored, 16)
                sp.wait_ge(stored, 16)

            @block.tensor
            def _(pe):
                pe.wait_ge(loaded, 32)
                for t in range(NT):
                    for c in range(C):
                        last = nc.tensor.matmul(lg_ps[:, t, :], XN2[:, c, t * P:(t + 1) * P], gw[:, c, :],
                                                start=(c == 0), stop=(c == C - 1))
                last.then_inc(logits, 1)
                pe.wait_ge(weighted, 1)
                for t in range(NT):
                    last = nc.tensor.transpose(wT_ps[0:NE + 1, t * P:(t + 1) * P], w9[:, t, :],
                                               K.ident[:, :])
                last.then_inc(turned, 1)

            @block.scalar
            def _(act):
                act.wait_ge(maxed, 1)
                nc.scalar.activation(prob[:, :, :], rest[:, :, :], ACT.Exp).then_inc(exped, 1)

            @block.vector
            def _(dve):
                own = Own(dve, dve_own)
                tt, tr, ts = nc.vector.tensor_tensor, nc.vector.tensor_reduce, nc.vector.tensor_scalar
                wide = lambda n: bc(col[:, n, :], 2, full)
                numbers = bc(iota[:, :], 1, full)
                dve.wait_ge(loaded, 32)
                dve.wait_ge(logits, 1)
                own(tr(col[:, 0, :], lg_ps[:, :, :], AX.X, ALU.max))
                tt(rest[:, :, :], lg_ps[:, :, :], wide(0), ALU.subtract).then_inc(maxed, 1)
                dve.wait_ge(exped, 1)
                own(tr(col[:, 1, :], prob[:, :, :], AX.X, ALU.add))
                own(nc.vector.reciprocal(col[:, 1, :], col[:, 1, :]))
                own(tt(prob[:, :, :], prob[:, :, :], wide(1), ALU.mult))
                left = prob
                for n in range(TOPK):
                    own(tr(col[:, 2 + n, :], left[:, :, :], AX.X, ALU.max))
                    own(tt(tmp[:, :, :], left[:, :, :], wide(2 + n), ALU.is_equal))
                    own(tt(tmp[:, :, :], tmp[:, :, :], numbers, ALU.mult))
                    own(tr(col[:, 4, :], tmp[:, :, :], AX.X, ALU.min))
                    own(tt(pick[:, n], numbers, wide(4), ALU.is_equal))
                    if n == 0:
                        own(nc.vector.scalar_tensor_tensor(
                            out=rest[:, :, :], in0=pick[:, 0], scalar=-2.0, in1=prob[:, :, :],
                            op0=ALU.mult, op1=ALU.add))
                        left = rest
                own(tt(col[:, 5, :], col[:, 2, :], col[:, 3, :], ALU.add))
                own(ts(col[:, 5, :], col[:, 5, :], EPS, None, ALU.add))
                own(nc.vector.reciprocal(col[:, 5, :], col[:, 5, :]))
                own(tt(tmp[:, :, :], pick[:, 0], pick[:, 1], ALU.add))
                own(tt(tmp[:, :, :], tmp[:, :, :], prob[:, :, :], ALU.mult))
                own(nc.vector.memset(w9[:, :, NE:NE + 1], 1.0))
                tt(w9[:, :, 0:NE], tmp[:, :, :], wide(5), ALU.mult).then_inc(weighted, 1)
                dve.wait_ge(turned, 1)
                nc.vector.tensor_copy(wT[0:NE + 1, :], wT_ps[0:NE + 1, :]).then_inc(copied, 1)


def split_tokens(nc, XN, XH, XL, tag, n=4):
    size = XN.shape[1] * XN.shape[2] // n
    flat = lambda x: x[:, :, :].rearrange("p c t -> p (c t)")
    with semaphores(nc, tag, "high") as (high,), nc.Block(no_gpsimd_drain=True) as block:
        @block.scalar
        def _(act):
            for i in range(n):
                part = slice(i * size, (i + 1) * size)
                nc.scalar.activation(flat(XH)[:, part], flat(XN)[:, part], ACT.Copy).then_inc(high, 1)

        @block.vector
        def _(dve):
            for i in range(n):
                part = slice(i * size, (i + 1) * size)
                dve.wait_ge(high, i + 1)
                nc.vector.tensor_tensor(flat(XL)[:, part], flat(XN)[:, part],
                                        flat(XH)[:, part].bitcast(F32), ALU.subtract)


def experts(nc, K, X, XH, XL, w_dram, we_dram, gate, tag):
    with ExitStack() as s:
        sb = lambda n, sh, dt=F32: s.enter_context(nc.sbuf_tensor(f"{tag}_{n}", sh, dt))
        raw = sb("raw", [P, 2, WE])
        wh = [sb(f"wh{j}", [P, WE], F32R) for j in range(2)]
        wl = [sb(f"wl{j}", [P, WE], F32R) for j in range(2)]
        share = sb("share", [P, 2, T])
        hg = sb("hg", [P, 2, G])
        hgw = sb("hgw", [P, 2, G])
        hid = sb("hid", [P, 2, G])
        hh = sb("hh", [P, 2, G], F32R)
        hl = sb("hl", [P, 2, G], F32R)
        gu_ps = s.enter_context(nc.psum_tensor(f"{tag}_gu", [P, 2, 2, G], F32))
        y_ps = s.enter_context(nc.psum_tensor(f"{tag}_y", [P, 2, C, G], F32))
        QW = 4
        piece = lambda q: slice(q * WE // QW, (q + 1) * WE // QW)

        def up_w(w, u, c, i):
            first = u * C * FE + c * FE + i * P
            return w[:, first:first + P]

        def down_w(w, i, m):
            first = 2 * C * FE + i * D + m * P
            return w[:, first:first + P]

        with semaphores(nc, f"{tag}_first", "loaded", "high") as (loaded, high), \
                nc.Block(no_gpsimd_drain=True) as block:
            @block.sync
            def _(sp):
                sp.dma_start(share[:, 0, :], w_dram[0:1, :].to_broadcast([P, T])).then_inc(loaded, 16)
                sp.dma_start(raw[:, 0, :], we_dram[0]).then_inc(loaded, 16)
                sp.wait_ge(loaded, 32)

            @block.scalar
            def _(act):
                act.wait_ge(loaded, 32)
                for q in range(QW):
                    nc.scalar.activation(wh[0][:, piece(q)], raw[:, 0, piece(q)], ACT.Copy).then_inc(high, 1)

            @block.vector
            def _(dve):
                for q in range(QW):
                    dve.wait_ge(high, q + 1)
                    nc.vector.tensor_tensor(wl[0][:, piece(q)], raw[:, 0, piece(q)],
                                            wh[0][:, piece(q)].bitcast(F32), ALU.subtract)

        def one_pass(e, both):
            half = NG * FC
            N = half * (2 if both else 1)
            where = lambda k: (k // half, (k % half) // FC, k % FC)
            second_at = {4 + q: q for q in range(QW)}
            next_at = {half + 4 + q: q for q in range(QW)}
            with semaphores(nc, tag, "raw1", "raw0", "share1", "share0", "gu", "silu", "shared", "prod",
                            "high", "low", "y", "added", "wh1", "wl1", "wh0", "down") as (
                    raw1, raw0, share1, share0, gu_ready, silu_ready, shared, prod, high, low,
                    y_ready, added, wh1, wl1, wh0, down_done), \
                    nc.Block(no_gpsimd_drain=True) as block:

                @block.sync
                def _(sp):
                    if not both:
                        return
                    sp.dma_start(raw[:, 1, :], we_dram[ds(e + 1, 1)].rearrange("o p w -> p (o w)")
                                 ).then_inc(raw1, 16)
                    sp.dma_start(share[:, 1, :], w_dram[ds(e + 1, 1), :].to_broadcast([P, T])
                                 ).then_inc(share1, 16)
                    sp.dma_start(raw[:, 0, :], we_dram[ds(e + 2, 1)].rearrange("o p w -> p (o w)")
                                 ).then_inc(raw0, 16)
                    sp.wait_ge(shared, half)
                    sp.dma_start(share[:, 0, :], w_dram[ds(e + 2, 1), :].to_broadcast([P, T])
                                 ).then_inc(share0, 16)
                    sp.wait_ge(share0, 16)
                    sp.wait_ge(raw0, 16)

                @block.tensor
                def _(pe):
                    def up(k):
                        j, g, i = where(k)
                        if k == half:
                            pe.wait_ge(wl1, QW)
                        if k >= 2:
                            pe.wait_ge(prod, k - 1)
                        tok = slice(g * G, (g + 1) * G)
                        for u in range(2):
                            for c in range(C):
                                a = (up_w(wh[j], u, c, i), up_w(wl[j], u, c, i))
                                x = (XH[:, c, tok], XL[:, c, tok])
                                for n, (p, q) in enumerate(((0, 0), (0, 1), (1, 0))):
                                    last = nc.tensor.matmul(gu_ps[:, k % 2, u], a[p], x[q],
                                                            start=(c == 0 and n == 0),
                                                            stop=(c == C - 1 and n == 2))
                        last.then_inc(gu_ready, 1)

                    def down(k):
                        j, g, i = where(k)
                        gg = j * NG + g
                        pe.wait_ge(low, k + 1)
                        if i == 0 and gg >= 2:
                            pe.wait_ge(added, gg - 1)
                        for m in range(C):
                            a = (down_w(wh[j], i, m), down_w(wl[j], i, m))
                            x = (hh[:, k % 2], hl[:, k % 2])
                            for n, (p, q) in enumerate(((0, 0), (0, 1), (1, 0))):
                                last = nc.tensor.matmul(y_ps[:, gg % 2, m], a[p], x[q],
                                                        start=(i == 0 and n == 0),
                                                        stop=(i == FC - 1 and n == 2))
                        last.then_inc(down_done, 1)
                    for k in range(N + 2):
                        if k < N:
                            up(k)
                        if k >= 2:
                            down(k - 2)

                @block.scalar
                def _(act):
                    def silu(k):
                        act.wait_ge(gu_ready, k + 1)
                        if k >= 2:
                            act.wait_ge(shared, k - 1)
                        nc.scalar.activation(hg[:, k % 2], gu_ps[:, k % 2, 0], ACT.Silu).then_inc(silu_ready, 1)

                    def take_high(k):
                        act.wait_ge(prod, k + 1)
                        if k >= 2:
                            act.wait_ge(down_done, k - 1)
                        nc.scalar.activation(hh[:, k % 2], hid[:, k % 2], ACT.Copy).then_inc(high, 1)
                    for k in range(N + 1):
                        if k < N:
                            silu(k)
                        if k:
                            take_high(k - 1)
                        if both and k in second_at:
                            act.wait_ge(raw1, 16)
                            q = piece(second_at[k])
                            nc.scalar.activation(wh[1][:, q], raw[:, 1, q], ACT.Copy).then_inc(wh1, 1)
                        if both and k in next_at:
                            act.wait_ge(raw0, 16)
                            act.wait_ge(down_done, half)
                            q = piece(next_at[k])
                            nc.scalar.activation(wh[0][:, q], raw[:, 0, q], ACT.Copy).then_inc(wh0, 1)

                @block.gpsimd
                def _(pool):
                    for k in range(N):
                        j, g, i = where(k)
                        if k == half:
                            pool.wait_ge(share1, 16)
                        pool.wait_ge(silu_ready, k + 1)
                        if k >= 2:
                            pool.wait_ge(prod, k - 1)
                        nc.gpsimd.tensor_tensor(hgw[:, k % 2], hg[:, k % 2],
                                                share[:, j, g * G:(g + 1) * G], ALU.mult
                                                ).then_inc(shared, 1)

                @block.vector
                def _(dve):
                    def product(k):
                        dve.wait_ge(shared, k + 1)
                        if k >= 2:
                            dve.wait_ge(low, k - 1)
                        nc.vector.tensor_tensor(hid[:, k % 2], gu_ps[:, k % 2, 1], hgw[:, k % 2],
                                                ALU.mult).then_inc(prod, 1)

                    def take_low(k):
                        dve.wait_ge(high, k + 1)
                        if k >= 2:
                            dve.wait_ge(down_done, k - 1)
                        nc.vector.tensor_tensor(hl[:, k % 2], hid[:, k % 2], hh[:, k % 2].bitcast(F32),
                                                ALU.subtract).then_inc(low, 1)

                    def add(gg):
                        dve.wait_ge(down_done, FC * (gg + 1))
                        if gg >= NG:
                            dve.wait_ge(added, gg - NG + 1)
                        g = gg % NG
                        for c in range(C):
                            view = X[:, c, (g // GB) * SP1 + 1 + (g % GB) * G:][:, 0:G]
                            last = nc.vector.scalar_tensor_tensor(out=view, in0=y_ps[:, gg % 2, c],
                                                                  scalar=gate, in1=view,
                                                                  op0=ALU.mult, op1=ALU.add)
                        last.then_inc(added, 1)
                    for k in range(N + 3):
                        if k < N:
                            product(k)
                        if 1 <= k <= N:
                            take_low(k - 1)
                        if k >= 3 and (k - 3) % FC == FC - 1:
                            add((k - 3) // FC)
                        if both and k in second_at:
                            dve.wait_ge(wh1, second_at[k] + 1)
                            q = piece(second_at[k])
                            nc.vector.tensor_tensor(wl[1][:, q], raw[:, 1, q], wh[1][:, q].bitcast(F32),
                                                    ALU.subtract).then_inc(wl1, 1)
                        if both and k in next_at:
                            dve.wait_ge(wh0, next_at[k] + 1)
                            q = piece(next_at[k])
                            nc.vector.tensor_tensor(wl[0][:, q], raw[:, 0, q], wh[0][:, q].bitcast(F32),
                                                    ALU.subtract)

        with nc.Fori(0, NE // 2) as pair:
            one_pass(pair * 2, True)
        one_pass(NE, False)


NH, HD = 16, 16
HC = NH // C
R = 4
MA = E + R
BANK_HEADS = G // E


def head_attention(nc, K, X, XN, ctxT, W, gate, tag, relative):
    with ExitStack() as s:
        sb = lambda n, sh: s.enter_context(nc.sbuf_tensor(f"{tag}_{n}", sh, F32))
        w = {n: sb(f"w{n}", [P, C, D]) for n in "qkvo"}
        b_col = {n: sb(f"b{n}", [P, C]) for n in "qko"}
        bv_row = sb("bv_row", [P, D])
        head_of = sb("head_of", [P, HC])
        head_cols = sb("head_cols", [P, HC, P])
        kT = sb("kT", [P, C, B * E])
        vx = sb("vx", [P, B, D])
        kblk = sb("kblk", [P, C, HC, E])
        vblk = sb("vblk", [P, NH, P])
        if relative:
            rel_k = sb("rel_k", [P, 1 + R])
            rel_v = sb("rel_v", [1 + R, D])
            rel_v0 = sb("rel_v0", [P, D])
            rel_mask = sb("rel_mask", [P, R, E])
            rblk = sb("rblk", [P, HC, R])
            corr = sb("corr", [P, NH, R])
            tmp = sb("tmp", [P, NH, E])

        loads = [(w[n][:, :, :], W[f"w{n}"]) for n in "qkvo"] + [(b_col[n][:, :], W[f"b{n}"]) for n in "qko"]
        loads += [(bv_row[:, :], W["bv_row"]), (head_of[:, :], K.head_of), (head_cols[:, :, :], K.head_cols)]
        if relative:
            loads += [(rel_k[:, :], W["rel_k"]), (rel_v[:, :], W["rel_v"]), (rel_v0[:, :], W["rel_v0"]),
                      (rel_mask[:, :, :], K.rel_mask)]

        with ExitStack() as s2:
            k_ps = s2.enter_context(nc.psum_tensor(f"{tag}_k_ps", [P, C, G], F32))
            v_ps = s2.enter_context(nc.psum_tensor(f"{tag}_v_ps", [P, B, G], F32))
            with semaphores(nc, f"{tag}_ctx", "loaded", "products", "own") as (
                    loaded, products, dve_own), \
                    nc.Block(no_gpsimd_drain=True) as block:
                @block.sync
                def _(sp):
                    for dst, src in loads:
                        sp.dma_start(dst, src).then_inc(loaded, 16)
                    sp.wait_ge(loaded, 16 * len(loads))

                @block.tensor
                def _(pe):
                    pe.wait_ge(loaded, 16 * len(loads))
                    for m in range(C):
                        for c in range(C):
                            nc.tensor.matmul(k_ps[:, m, 0:B * E], w["k"][:, c, m * P:(m + 1) * P],
                                             ctxT[:, c, :], start=(c == 0), stop=(c == C - 1))
                    for b in range(B):
                        for c in range(C):
                            last = nc.tensor.matmul(v_ps[0:E, b, 0:D], ctxT[:, c, b * E:(b + 1) * E],
                                                    w["v"][:, c, :], start=(c == 0), stop=(c == C - 1))
                    last.then_inc(products, 1)

                @block.vector
                def _(dve):
                    own = Own(dve, dve_own)
                    dve.wait_ge(loaded, 16 * len(loads))
                    if relative:
                        own(nc.vector.tensor_scalar(rel_k[:, 1:], rel_k[:, 1:], rel_k[:, 0:1], None,
                                                    ALU.subtract))
                        nc.vector.tensor_tensor(rblk[:, :, :], bc(rel_k[:, 1:], 1, [P, HC, R]),
                                                bc(head_of[:, :], 2, [P, HC, R]), ALU.mult)
                        own(nc.vector.tensor_tensor(rel_v[:, :], rel_v[:, :], rel_v0[0:1 + R, :],
                                                    ALU.subtract))
                        own(nc.vector.tensor_tensor(bv_row[:, :], bv_row[:, :], rel_v0[:, :], ALU.add))
                        for m in range(C):
                            own(nc.vector.tensor_scalar(b_col["k"][:, m:m + 1], b_col["k"][:, m:m + 1],
                                                        rel_k[:, 0:1], None, ALU.add))
                    dve.wait_ge(products, 1)
                    for m in range(C):
                        nc.vector.tensor_scalar(kT[:, m], k_ps[:, m, 0:B * E], b_col["k"][:, m:m + 1],
                                                None, ALU.add)
                    for b in range(B):
                        nc.vector.tensor_tensor(vx[0:E, b], v_ps[0:E, b, 0:D], bv_row[0:E, :], ALU.add)
            if relative:
                with semaphores(nc, f"{tag}_rel", "moved") as (moved,), \
                        nc.Block(no_gpsimd_drain=True) as block:
                    @block.sync
                    def _(sp):
                        for b in range(B):
                            sp.dma_start(vx[E:MA, b, :], rel_v[1:1 + R, :]).then_inc(moved, 16)
                        sp.wait_ge(moved, 16 * B)

        MK = MA if relative else E
        q_sb = sb("q", [P, C, G])
        ctx_sb = sb("ctx", [P, C, G])
        y_sb = sb("y", [P, C, G])
        ex = sb("ex", [P, 2, NH, E])
        prob = sb("prob", [P, 2, NH, MK])
        stat = sb("stat", [P, 2, 3, NH])
        pT = sb("pT", [P, NH, G])
        o_ps = s.enter_context(nc.psum_tensor(f"{tag}_o", [P, C, G], F32))
        s_ps = s.enter_context(nc.psum_tensor(f"{tag}_s", [P, 3, G], F32))
        pT_ps = s.enter_context(nc.psum_tensor(f"{tag}_pT_ps", [P, 2, TG, P], F32))
        pieces = []
        for h0 in range(0, NH, BANK_HEADS):
            h1 = min(h0 + BANK_HEADS, NH)
            for c in range(C):
                a, z = max(h0, c * HC), min(h1, (c + 1) * HC)
                if a < z:
                    pieces.append((h0 // BANK_HEADS, a - h0, a, z - a))
        banks = [(k, h0, min(BANK_HEADS, NH - h0)) for k, h0 in enumerate(range(0, NH, BANK_HEADS))]
        sview = lambda k, n: s_ps[:, k, 0:n * E].rearrange("p (h e) -> p h e", e=E)
        HB = TG
        NB = NH // HB

        with nc.Fori(0, B) as b:
            with nc.Block(no_gpsimd_drain=True) as block:
                @block.vector
                def _(dve):
                    for c in range(C):
                        nc.vector.tensor_tensor(
                            kblk[:, c], kT[:, c, ds(b * E, E)].unsqueeze(1).to_broadcast([P, HC, E]),
                            bc(head_of[:, :], 2, [P, HC, E]), ALU.mult)
                        nc.vector.tensor_tensor(
                            vblk[0:MK, c * HC:(c + 1) * HC, :],
                            vx[0:MK, ds(b, 1), c * P:(c + 1) * P].to_broadcast([MK, HC, P]),
                            head_cols[0:MK, :, :], ALU.mult)
            for h in range(GB):
                first = lambda t: relative and h == 0 and t == 0
                cols = lambda c: X[:, c, ds(b * SP1 + h * G + 1, G)]
                xn = lambda c: XN[:, c, ds(b * S + h * G, G)]
                with semaphores(nc, f"{tag}{h}", "q", "q_taken", "scores", "s_free", "less", "exped",
                                "prob", "zeroed", "turned", "copied", "mixed", "ctx", "y", "corr",
                                "own") as (
                        q_ready, q_taken, scores, s_free, less, exped, prob_ready, zeroed, turned,
                        copied, mixed, ctx_ready, y_ready, corr_ready, dve_own), \
                        nc.Block(no_gpsimd_drain=True) as block:

                    @block.tensor
                    def _(pe):
                        for m in range(C):
                            for c in range(C):
                                last = nc.tensor.matmul(o_ps[:, m], w["q"][:, c, m * P:(m + 1) * P], xn(c),
                                                        start=(c == 0), stop=(c == C - 1))
                            last.then_inc(q_ready, 1)
                        pe.wait_ge(q_taken, C)

                        def score(t):
                            if t:
                                pe.wait_ge(s_free, t)
                            tok = slice(t * P, (t + 1) * P)
                            if first(t):
                                for c in range(C):
                                    last = nc.tensor.matmul(
                                        pT_ps[:, 0, c, 0:HC * R], q_sb[:, c, tok],
                                        rblk[:, :, :].rearrange("p h r -> p (h r)"), start=True, stop=True)
                                last.then_inc(corr_ready, 1)
                            for k, off, h0, n in pieces:
                                c = h0 // HC
                                last = nc.tensor.matmul(
                                    s_ps[:, k, off * E:(off + n) * E], q_sb[:, c, tok],
                                    kblk[:, c, h0 - c * HC:h0 - c * HC + n, :].rearrange("p h e -> p (h e)"),
                                    start=True, stop=True)
                            last.then_inc(scores, 1)

                        def turn(t):
                            pe.wait_ge(prob_ready, t + 1)
                            for n in range(NB):
                                i = t * NB + n
                                if i >= 2:
                                    pe.wait_ge(copied, i - 1)
                                if first(t):
                                    pe.wait_ge(corr_ready, 2)
                                for j in range(HB):
                                    last = nc.tensor.transpose(pT_ps[0:MK, i % 2, j, :],
                                                               prob[:, t % 2, n * HB + j, :], K.ident[:, :])
                                last.then_inc(turned, 1)
                        score(0)
                        for t in range(TG):
                            if t + 1 < TG:
                                score(t + 1)
                            turn(t)
                        pe.wait_ge(copied, TG * NB)
                        for c in range(C):
                            for j in range(HC):
                                last = nc.tensor.matmul(o_ps[:, c], vblk[0:MK, c * HC + j, :],
                                                        pT[0:MK, c * HC + j, :],
                                                        start=(j == 0), stop=(j == HC - 1))
                            last.then_inc(mixed, 1)
                        pe.wait_ge(ctx_ready, C)
                        for m in range(C):
                            for c in range(C):
                                last = nc.tensor.matmul(s_ps[:, m], w["o"][:, c, m * P:(m + 1) * P],
                                                        ctx_sb[:, c], start=(c == 0), stop=(c == C - 1))
                            last.then_inc(y_ready, 1)

                    @block.vector
                    def _(dve):
                        own = Own(dve, dve_own)
                        for m in range(C):
                            dve.wait_ge(q_ready, m + 1)
                            nc.vector.tensor_scalar(q_sb[:, m], o_ps[:, m], b_col["q"][:, m:m + 1],
                                                    HD ** -0.5, ALU.add, ALU.mult).then_inc(q_taken, 1)

                        def less_max(t):
                            dve.wait_ge(scores, t + 1)
                            if first(t):
                                nc.vector.tensor_copy(
                                    corr[:, :, :].rearrange("p (c h) r -> p c (h r)", c=C),
                                    pT_ps[:, 0, 0:C, 0:HC * R]).then_inc(corr_ready, 1)
                                for k, h0, n in banks:
                                    last = nc.vector.tensor_copy(ex[:, 0, h0:h0 + n, :], sview(k, n))
                                last.then_inc(s_free, 1)
                                dve.wait_ge(corr_ready, 2)
                                dve.wait_ge(s_free, 1)
                                for r in range(R):
                                    own(nc.vector.tensor_tensor(
                                        tmp[:, :, :], bc(rel_mask[:, r, :], 1, [P, NH, E]),
                                        corr[:, :, r:r + 1].to_broadcast([P, NH, E]), ALU.mult))
                                    own(nc.vector.tensor_tensor(ex[:, 0], ex[:, 0], tmp[:, :, :], ALU.add))
                                own(nc.vector.tensor_reduce(stat[:, 0, 0, :], ex[:, 0], AX.X, ALU.max))
                                nc.vector.tensor_tensor(ex[:, 0], ex[:, 0],
                                                        bc(stat[:, 0, 0, :], 2, [P, NH, E]),
                                                        ALU.subtract).then_inc(less, 1)
                                return
                            for k, h0, n in banks:
                                last = nc.vector.tensor_reduce(stat[:, t % 2, 0, h0:h0 + n], sview(k, n),
                                                               AX.X, ALU.max)
                            own(last)
                            if t >= 2:
                                dve.wait_ge(exped, t - 1)
                            for k, h0, n in banks:
                                last = nc.vector.tensor_tensor(
                                    ex[:, t % 2, h0:h0 + n, :], sview(k, n),
                                    bc(stat[:, t % 2, 0, h0:h0 + n], 2, [P, n, E]), ALU.subtract)
                            last.then_inc(s_free, 1)
                            dve.wait_ge(s_free, t + 1)
                            nc.vector.nop().then_inc(less, 1)

                        def normalise(t):
                            dve.wait_ge(exped, t + 1)
                            own(nc.vector.tensor_reduce(stat[:, t % 2, 1, :], ex[:, t % 2], AX.X, ALU.add))
                            own(nc.vector.reciprocal(stat[:, t % 2, 2, :], stat[:, t % 2, 1, :]))
                            if t >= 2:
                                dve.wait_ge(turned, NB * (t - 1))
                            out = prob[:, t % 2, :, 0:E]
                            ins = nc.vector.tensor_tensor(out, ex[:, t % 2],
                                                          bc(stat[:, t % 2, 2, :], 2, [P, NH, E]), ALU.mult)
                            if first(t):
                                own(ins)
                                for r in range(R):
                                    own(nc.vector.tensor_tensor(
                                        tmp[:, :, :], bc(rel_mask[:, r, :], 1, [P, NH, E]), out, ALU.mult))
                                    ins = nc.vector.tensor_reduce(prob[:, 0, :, E + r:E + r + 1],
                                                                  tmp[:, :, :], AX.X, ALU.add)
                                    own(ins)
                                nc.vector.nop().then_inc(prob_ready, 1)
                            elif relative:
                                own(ins)
                                nc.vector.memset(prob[:, t % 2, :, E:MA], 0.0).then_inc(prob_ready, 1)
                            else:
                                ins.then_inc(prob_ready, 1)
                        less_max(0)
                        for t in range(TG):
                            if t + 1 < TG:
                                less_max(t + 1)
                            normalise(t)
                        for c in range(C):
                            dve.wait_ge(mixed, c + 1)
                            nc.vector.tensor_copy(ctx_sb[:, c], o_ps[:, c]).then_inc(ctx_ready, 1)
                        for m in range(C):
                            dve.wait_ge(y_ready, m + 1)
                            own(nc.vector.tensor_scalar(y_sb[:, m], s_ps[:, m], b_col["o"][:, m:m + 1],
                                                        gate, ALU.add, ALU.mult))
                            nc.vector.tensor_tensor(cols(m), y_sb[:, m], cols(m), ALU.add)

                    @block.scalar
                    def _(act):
                        def copies(t):
                            for n in range(NB):
                                i = t * NB + n
                                act.wait_ge(turned, i + 1)
                                nc.scalar.activation(
                                    pT[0:MK, n * HB:(n + 1) * HB, t * P:(t + 1) * P],
                                    pT_ps[0:MK, i % 2], ACT.Copy).then_inc(copied, 1)
                        for t in range(TG):
                            act.wait_ge(less, t + 1)
                            nc.scalar.activation(ex[:, t % 2], ex[:, t % 2], ACT.Exp).then_inc(exped, 1)
                            if t:
                                copies(t - 1)
                        copies(TG - 1)


FQ = 768
FQC = FQ // P
QB = 32
ACT_QMAX, ACT_QMIN = 32767.0, -32768.0
W_QMAX, W_QMIN = 7.0, -8.0
U16 = 65536.0
LEAST = 1e-12


def quantised_ffn(nc, K, X, XN, W, gate, tag):
    with ExitStack() as s:
        sb = lambda n, sh: s.enter_context(nc.sbuf_tensor(f"{tag}_{n}", sh, F32))
        wT = [sb("guT", [P, 2, C, FQ]), sb("dT", [P, FQC, D])]
        UP = sb("up", [P, FQC, T])
        GATE = sb("gate", [P, FQC, T])
        sig = sb("sig", [P, 2, T])
        peak = sb("peak", [P, 2, NG * FQC])
        peak_x = sb("peak_x", [P, 1])
        top = sb("top", [P, 4, 2])
        sc = sb("sc", [P, 12])
        SX, RX, SU, RU, SG, RG, SS, RS, SO, RO, SUS, SY = [sc[:, i:i + 1] for i in range(12)]

        with ExitStack() as s2:
            rows_of = (("g", FQC, D), ("u", FQC, D), ("d", C, FQ))
            t = lambda n, sh: s2.enter_context(nc.sbuf_tensor(f"{tag}_{n}", sh, F32))
            raw = [t(f"raw{n}", [P, k * m]) for n, k, m in rows_of]
            NBLK = FQC * D // QB
            wpeak = [t(f"wpeak{n}", [P, 2, NBLK]) for n, _, _ in rows_of]
            t_ps = s2.enter_context(nc.psum_tensor(f"{tag}_t_ps", [P, 4, TG, P], F32))
            turns = []
            for n, (name, k, m) in enumerate(rows_of):
                for j in range(k):
                    for c in range(m // P):
                        dst = (wT[0][:, n, c, j * P:(j + 1) * P] if n < 2 else
                               wT[1][:, c, j * P:(j + 1) * P])
                        turns.append((n, slice(j * m + c * P, j * m + (c + 1) * P), dst))
            with semaphores(nc, f"{tag}_w", "loaded", "quant", "turned", "own", "copied") as (
                    loaded, quant, turned, dve_own, copied), nc.Block(no_gpsimd_drain=True) as block:
                @block.sync
                def _(sp):
                    for n, (name, k, m) in enumerate(rows_of):
                        sp.dma_start(raw[n][:, :], W[f"w{name}"]).then_inc(loaded, 16)
                    sp.wait_ge(loaded, 16 * 3)

                @block.vector
                def _(dve):
                    own = Own(dve, dve_own)
                    dve.wait_ge(loaded, 16 * 3)
                    for n in range(3):
                        blocks = raw[n][:, :].rearrange("p (k w) -> p k w", w=QB)
                        scale, inv = wpeak[n][:, 0, :], wpeak[n][:, 1, :]
                        full = [P, NBLK, QB]
                        own(nc.vector.tensor_reduce(scale, blocks, AX.X, ALU.max, apply_absolute_value=True))
                        own(nc.vector.tensor_scalar(scale, scale, 1.0 / W_QMAX, LEAST, ALU.mult, ALU.max))
                        own(nc.vector.reciprocal(inv, scale))
                        own(nc.vector.tensor_tensor(blocks, blocks, bc(inv, 2, full), ALU.mult))
                        own(nc.vector.tensor_scalar(raw[n][:, :], raw[n][:, :], MAGIC, MAGIC, ALU.add,
                                                    ALU.subtract))
                        own(nc.vector.tensor_scalar(raw[n][:, :], raw[n][:, :], W_QMAX, W_QMIN, ALU.min,
                                                    ALU.max))
                        nc.vector.tensor_tensor(blocks, blocks, bc(scale, 2, full), ALU.mult
                                                ).then_inc(quant, 1)

                @block.tensor
                def _(pe):
                    for i, (n, src, dst) in enumerate(turns):
                        pe.wait_ge(quant, n + 1)
                        if i % TG == 0 and i // TG >= 4:
                            pe.wait_ge(copied, i - 4 * TG + TG)
                        nc.tensor.transpose(t_ps[:, (i // TG) % 4, i % TG, :], raw[n][:, src],
                                            K.ident[:, :]).then_inc(turned, 1)

                @block.scalar
                def _(act):
                    for i, (n, src, dst) in enumerate(turns):
                        act.wait_ge(turned, min((i // TG + 1) * TG, len(turns)))
                        nc.scalar.activation(dst, t_ps[:, (i // TG) % 4, i % TG, :], ACT.Copy
                                             ).then_inc(copied, 1)

        def scale_of(dve, own, dst, inv, peak_ap, least=LEAST):
            own(nc.vector.tensor_scalar(dst, peak_ap, 1.0 / ACT_QMAX, least, ALU.mult, ALU.max))
            own(nc.vector.reciprocal(inv, dst))

        with semaphores(nc, f"{tag}_x", "peaked", "reduced", "own") as (peaked, reduced, dve_own), \
                nc.Block(no_gpsimd_drain=True) as block:
            @block.gpsimd
            def _(pool):
                pool.wait_ge(peaked, 1)
                nc.gpsimd.partition_all_reduce(top[:, 0, 0:1], peak_x[:, :], P, ABSMAX).then_inc(reduced, 1)

            @block.vector
            def _(dve):
                own = Own(dve, dve_own)
                x = XN[:, :, :].rearrange("p c t -> p (c t)")
                nc.vector.tensor_reduce(peak_x[:, :], x, AX.X, ALU.max,
                                        apply_absolute_value=True).then_inc(peaked, 1)
                dve.wait_ge(reduced, 1)
                scale_of(dve, own, SX, RX, top[:, 0, 0:1])
                own(nc.vector.tensor_scalar(x, x, RX, ACT_QMAX, ALU.mult, ALU.min))
                own(nc.vector.tensor_scalar(x, x, ACT_QMIN, MAGIC, ALU.max, ALU.add))
                nc.vector.tensor_scalar(x, x, MAGIC, None, ALU.subtract)

        with ExitStack() as s2:
            gu_ps = s2.enter_context(nc.psum_tensor(f"{tag}_gu_ps", [P, 4, G], F32))
            with nc.Fori(0, NG) as g:
                with semaphores(nc, f"{tag}_gu", "ready", "scaled", "peaked") as (ready, scaled, peaked), \
                        nc.Block(no_gpsimd_drain=True) as block:
                    steps = [(u, i) for i in range(FQC) for u in range(2)]
                    dst = lambda u, i: (GATE, UP)[u][:, i, ds(g * G, G)]

                    @block.tensor
                    def _(pe):
                        for k, (u, i) in enumerate(steps):
                            if k >= 4:
                                pe.wait_ge(scaled, k - 3)
                            for c in range(C):
                                last = nc.tensor.matmul(gu_ps[:, k % 4], wT[0][:, u, c, i * P:(i + 1) * P],
                                                        XN[:, c, ds(g * G, G)], start=(c == 0),
                                                        stop=(c == C - 1))
                            last.then_inc(ready, 1)

                    @block.scalar
                    def _(act):
                        for k, (u, i) in enumerate(steps):
                            act.wait_ge(ready, k + 1)
                            nc.scalar.activation(dst(u, i), gu_ps[:, k % 4], ACT.Copy, scale=SX
                                                 ).then_inc(scaled, 1)

                    @block.vector
                    def _(dve):
                        for k, (u, i) in enumerate(steps):
                            dve.wait_ge(scaled, k + 1)
                            nc.vector.tensor_reduce(peak[:, 1 - u, ds(g * FQC + i, 1)], dst(u, i), AX.X,
                                                    ALU.max, apply_absolute_value=True)

        with semaphores(nc, f"{tag}_e", "peaked", "reduced", "own", "scales", "up", "gateq", "sig",
                        "gated", "pool") as (
                peaked, reduced, dve_own, scales, up_ready, gate_ready, sig_ready, gated, pool_own), \
                nc.Block(no_gpsimd_drain=True) as block:

            @block.gpsimd
            def _(pool):
                own = Own(pool, pool_own)
                for n, w in ((1, 2), (2, 1), (3, 1)):
                    pool.wait_ge(peaked, n)
                    nc.gpsimd.partition_all_reduce(top[:, n, 0:w], (peak[:, :, 0] if n == 1 else
                                                                    peak[:, 0, n:n + 1]),
                                                   P, ABSMAX).then_inc(reduced, 1)
                    if n == 1:
                        pool.wait_ge(scales, 1)
                        for i in range(FQC):
                            u = UP[:, i, :]
                            own(nc.gpsimd.tensor_scalar(u, u, RU, ACT_QMAX, ALU.mult, ALU.min))
                            own(nc.gpsimd.tensor_scalar(u, u, ACT_QMIN, MAGIC, ALU.max, ALU.add))
                            nc.gpsimd.tensor_scalar(u, u, MAGIC, None, ALU.subtract).then_inc(up_ready, 1)

            @block.scalar
            def _(act):
                for i in range(FQC):
                    act.wait_ge(gate_ready, i + 1)
                    if i >= 2:
                        act.wait_ge(gated, i - 1)
                    nc.scalar.activation(sig[:, i % 2], GATE[:, i, :], ACT.Sigmoid).then_inc(sig_ready, 1)

            @block.vector
            def _(dve):
                own = Own(dve, dve_own)
                ts = nc.vector.tensor_scalar
                own(nc.vector.tensor_reduce(sc[:, 0:2], peak[:, :, :], AX.X, ALU.max))
                nc.vector.tensor_copy(peak[:, :, 0], sc[:, 0:2]).then_inc(peaked, 1)
                dve.wait_ge(reduced, 1)
                scale_of(dve, own, SU, RU, top[:, 1, 0:1])
                scale_of(dve, own, SG, RG, top[:, 1, 1:2])
                nc.vector.nop().then_inc(scales, 1)

                def gate_numbers(i):
                    v = GATE[:, i, :]
                    own(ts(v, v, RG, ACT_QMAX, ALU.mult, ALU.min))
                    own(ts(v, v, ACT_QMIN, MAGIC, ALU.max, ALU.add))
                    ts(v, v, MAGIC, SG, ALU.subtract, ALU.mult).then_inc(gate_ready, 1)

                def times_sigmoid(i):
                    v = sig[:, i % 2]
                    dve.wait_ge(sig_ready, i + 1)
                    own(ts(v, v, U16, U16 - 1, ALU.mult, ALU.min))
                    own(ts(v, v, 0.0, MAGIC, ALU.max, ALU.add))
                    own(nc.vector.scalar_tensor_tensor(out=GATE[:, i, :], in0=v, scalar=MAGIC,
                                                       in1=GATE[:, i, :], op0=ALU.subtract, op1=ALU.mult))
                    nc.vector.tensor_reduce(peak[:, 1, 1 + i:2 + i], GATE[:, i, :], AX.X, ALU.max,
                                            apply_absolute_value=True).then_inc(gated, 1)
                gate_numbers(0)
                for i in range(FQC):
                    if i + 1 < FQC:
                        gate_numbers(i + 1)
                    times_sigmoid(i)
                dve.wait_ge(gated, FQC)
                nc.vector.tensor_reduce(peak[:, 0, 2:3], peak[:, 1, 1:1 + FQC], AX.X, ALU.max).then_inc(peaked, 1)
                dve.wait_ge(reduced, 2)
                scale_of(dve, own, SS, RS, top[:, 2, 0:1], LEAST * U16)
                for i in range(FQC):
                    v = GATE[:, i, :]
                    own(ts(v, v, RS, ACT_QMAX, ALU.mult, ALU.min))
                    own(ts(v, v, ACT_QMIN, MAGIC, ALU.max, ALU.add))
                    dve.wait_ge(up_ready, i + 1)
                    own(nc.vector.scalar_tensor_tensor(out=v, in0=v, scalar=MAGIC, in1=UP[:, i, :],
                                                       op0=ALU.subtract, op1=ALU.mult))
                    own(nc.vector.tensor_reduce(peak[:, 1, 1 + i:2 + i], v, AX.X, ALU.max,
                                                apply_absolute_value=True))
                nc.vector.tensor_reduce(peak[:, 0, 3:4], peak[:, 1, 1:1 + FQC], AX.X, ALU.max).then_inc(peaked, 1)
                own(ts(SUS, SS, SU, 1.0 / U16, ALU.mult, ALU.mult))
                dve.wait_ge(reduced, 3)
                own(ts(RO, top[:, 3, 0:1], SUS, None, ALU.mult))
                scale_of(dve, own, SO, RO, RO)
                own(ts(RO, RO, SUS, None, ALU.mult))
                ts(SY, SO, gate, None, ALU.mult)
                for i in range(FQC):
                    v = GATE[:, i, :]
                    own(ts(v, v, RO, ACT_QMAX, ALU.mult, ALU.min))
                    own(ts(v, v, ACT_QMIN, MAGIC, ALU.max, ALU.add))
                    ts(v, v, MAGIC, None, ALU.subtract)

        with ExitStack() as s2:
            y_ps = s2.enter_context(nc.psum_tensor(f"{tag}_y_ps", [P, C, G], F32))
            for b in range(B):
                with nc.Fori(0, GB) as h:
                    with semaphores(nc, f"{tag}_d{b}", "ready") as (ready,), \
                            nc.Block(no_gpsimd_drain=True) as block:
                        @block.tensor
                        def _(pe):
                            for m in range(C):
                                for i in range(FQC):
                                    last = nc.tensor.matmul(y_ps[:, m], wT[1][:, i, m * P:(m + 1) * P],
                                                            GATE[:, i, ds(h * G + b * S, G)],
                                                            start=(i == 0), stop=(i == FQC - 1))
                                last.then_inc(ready, 1)

                        @block.vector
                        def _(dve):
                            for m in range(C):
                                view = X[:, m, ds(h * G + (b * SP1 + 1), G)]
                                dve.wait_ge(ready, m + 1)
                                nc.vector.scalar_tensor_tensor(out=view, in0=y_ps[:, m], scalar=SY, in1=view,
                                                               op0=ALU.mult, op1=ALU.add)


FB = 1024
FBC = FB // P
SPAD = S + 2


def bit_ffn(nc, K, X, XN, W, gate, tag):
    with ExitStack() as s:
        sb = lambda n, sh, dt=F32: s.enter_context(nc.sbuf_tensor(f"{tag}_{n}", sh, dt))
        w_int = [sb("w1i", [P, C * FB], BF16), sb("w2i", [P, FBC * D], BF16)]
        wstat = sb("wstat", [P, 2, 4])
        sy = sb("sy", [P, 1])
        conv = sb("conv", [P, FBC, 3])
        conv_b = sb("conv_b", [P, FBC])
        H = sb("h", [P, FBC, B * SPAD])
        with ExitStack() as s2:
            raw = [s2.enter_context(nc.sbuf_tensor(f"{tag}_raw{n}", [P, C * FB], F32)) for n in range(2)]
            with semaphores(nc, f"{tag}_w", "loaded", "summed", "reduced", "own") as (
                    loaded, summed, reduced, dve_own), nc.Block(no_gpsimd_drain=True) as block:
                @block.sync
                def _(sp):
                    for dst, src in ((raw[0][:, :], W["w1"]), (raw[1][:, :], W["w2"]),
                                     (conv[:, :, :], W["conv_w"]), (conv_b[:, :], W["conv_b"])):
                        sp.dma_start(dst, src).then_inc(loaded, 16)
                    sp.wait_ge(loaded, 64)

                @block.gpsimd
                def _(pool):
                    for n in range(2):
                        pool.wait_ge(summed, n + 1)
                        nc.gpsimd.partition_all_reduce(wstat[:, n, 1:2], wstat[:, n, 0:1], P, RADD
                                                       ).then_inc(reduced, 1)

                @block.vector
                def _(dve):
                    own = Own(dve, dve_own)
                    ts = nc.vector.tensor_scalar
                    dve.wait_ge(loaded, 64)
                    for b in range(B):
                        for side in (0, SPAD - 1):
                            nc.vector.memset(H[:, :, b * SPAD + side:b * SPAD + side + 1], 0.0)
                    for n in range(2):
                        nc.vector.tensor_reduce(wstat[:, n, 0:1], raw[n][:, :], AX.X, ALU.add,
                                                apply_absolute_value=True).then_inc(summed, 1)
                    for n in range(2):
                        dve.wait_ge(reduced, n + 1)
                        own(ts(wstat[:, n, 2:3], wstat[:, n, 1:2], 1.0 / (FB * D), EPS, ALU.mult, ALU.max))
                        own(nc.vector.reciprocal(wstat[:, n, 3:4], wstat[:, n, 2:3]))
                        own(ts(raw[n][:, :], raw[n][:, :], wstat[:, n, 3:4], MAGIC, ALU.mult, ALU.add))
                        own(ts(raw[n][:, :], raw[n][:, :], MAGIC, 1.0, ALU.subtract, ALU.min))
                        own(ts(w_int[n][:, :], raw[n][:, :], -1.0, None, ALU.max))
                    ts(sy[:, :], wstat[:, 1, 2:3], gate, None, ALU.mult)

        peak = sb("peak", [P, G])
        top = sb("top", [P, G])
        scale = sb("scale", [P, G])
        back = sb("back", [P, G])

        def token_scales(own):
            own(nc.vector.tensor_scalar(top[:, :], top[:, :], EPS, None, ALU.max))
            own(nc.vector.reciprocal(scale[:, :], top[:, :]))
            own(nc.vector.tensor_scalar(scale[:, :], scale[:, :], 127.0, None, ALU.mult))
            own(nc.vector.tensor_scalar(back[:, :], top[:, :], 1.0 / 127.0, None, ALU.mult))

        def whole_numbers(own, dst, src, tmp):
            own(nc.vector.tensor_tensor(tmp, src, scale[:, :], ALU.mult))
            own(nc.vector.tensor_scalar(tmp, tmp, MAGIC, MAGIC, ALU.add, ALU.subtract))
            return nc.vector.tensor_scalar(dst, tmp, 127.0, -128.0, ALU.min, ALU.max)

        with ExitStack() as s2:
            x_int = s2.enter_context(nc.sbuf_tensor(f"{tag}_x_int", [P, C, G], BF16))
            tmp = s2.enter_context(nc.sbuf_tensor(f"{tag}_tmp", [P, C, G], F32))
            h_ps = s2.enter_context(nc.psum_tensor(f"{tag}_h_ps", [P, 4, G], F32))
            with nc.Fori(0, B) as b, nc.Fori(0, GB) as h:
                xn = lambda c: XN[:, c, ds(b * S + h * G, G)]
                with semaphores(nc, f"{tag}_1", "sizes", "peaked", "reduced", "x", "h", "taken", "own") as (
                        sizes, peaked, reduced, x_ready, h_ready, taken, dve_own), \
                        nc.Block(no_gpsimd_drain=True) as block:
                    @block.scalar
                    def _(act):
                        for c in range(C):
                            nc.scalar.activation(tmp[:, c], xn(c), ACT.Abs).then_inc(sizes, 1)

                    @block.gpsimd
                    def _(pool):
                        pool.wait_ge(peaked, 1)
                        nc.gpsimd.partition_all_reduce(top[:, :], peak[:, :], P, ABSMAX).then_inc(reduced, 1)

                    @block.vector
                    def _(dve):
                        own = Own(dve, dve_own)
                        dve.wait_ge(sizes, C)
                        nc.vector.tensor_tensor(peak[:, :], tmp[:, 0], tmp[:, 1], ALU.max).then_inc(peaked, 1)
                        dve.wait_ge(reduced, 1)
                        token_scales(own)
                        for c in range(C):
                            whole_numbers(own, x_int[:, c], xn(c), tmp[:, c]).then_inc(x_ready, 1)
                        for i in range(FBC):
                            dve.wait_ge(h_ready, i + 1)
                            nc.vector.scalar_tensor_tensor(out=H[:, i, ds(b * SPAD + h * G + 1, G)],
                                                           in0=h_ps[:, i % 4], scalar=wstat[:, 0, 2:3],
                                                           in1=back[:, :], op0=ALU.mult,
                                                           op1=ALU.mult).then_inc(taken, 1)

                    @block.tensor
                    def _(pe):
                        pe.wait_ge(x_ready, C)
                        for i in range(FBC):
                            if i >= 4:
                                pe.wait_ge(taken, i - 3)
                            for c in range(C):
                                last = nc.tensor.matmul(h_ps[:, i % 4],
                                                        w_int[0][:, c * FB + i * P:c * FB + (i + 1) * P],
                                                        x_int[:, c], start=(c == 0), stop=(c == C - 1))
                            last.then_inc(h_ready, 1)

        with ExitStack() as s2:
            act_sb = s2.enter_context(nc.sbuf_tensor(f"{tag}_act", [P, FBC, G], F32))
            size = s2.enter_context(nc.sbuf_tensor(f"{tag}_size", [P, 2, G], F32))
            a_int = s2.enter_context(nc.sbuf_tensor(f"{tag}_a_int", [P, FBC, G], BF16))
            y_sb = s2.enter_context(nc.sbuf_tensor(f"{tag}_y", [P, C, G], F32))
            y_ps = s2.enter_context(nc.psum_tensor(f"{tag}_y_ps", [P, C, G], F32))
            with nc.Fori(0, B) as b, nc.Fori(0, GB) as h:
                tap = lambda i, j: H[:, i, ds(b * SPAD + h * G + j, G)]
                with semaphores(nc, f"{tag}_2", "conv", "silu", "sizes", "peaked", "reduced", "a", "y", "own") as (
                        conv_ready, silu, sizes, peaked, reduced, a_ready, y_ready, dve_own), \
                        nc.Block(no_gpsimd_drain=True) as block:
                    @block.vector
                    def _(dve):
                        own = Own(dve, dve_own)

                        def widen(i):
                            dve.wait_ge(sizes, i + 1)
                            if i:
                                dve.wait_ge(peaked, i)
                                nc.vector.tensor_tensor(peak[:, :], peak[:, :], size[:, i % 2],
                                                        ALU.max).then_inc(peaked, 1)
                            else:
                                nc.vector.tensor_copy(peak[:, :], size[:, 0]).then_inc(peaked, 1)
                        for i in range(FBC):
                            v = act_sb[:, i]
                            own(nc.vector.tensor_scalar(v, tap(i, 1), conv[:, i, 1:2], conv_b[:, i:i + 1],
                                                        ALU.mult, ALU.add))
                            own(nc.vector.scalar_tensor_tensor(out=v, in0=tap(i, 0), scalar=conv[:, i, 0:1],
                                                               in1=v, op0=ALU.mult, op1=ALU.add))
                            nc.vector.scalar_tensor_tensor(out=v, in0=tap(i, 2), scalar=conv[:, i, 2:3],
                                                           in1=v, op0=ALU.mult, op1=ALU.add
                                                           ).then_inc(conv_ready, 1)
                            if i:
                                widen(i - 1)
                        widen(FBC - 1)
                        dve.wait_ge(reduced, 1)
                        token_scales(own)
                        for i in range(FBC):
                            whole_numbers(own, a_int[:, i], act_sb[:, i], act_sb[:, i]).then_inc(a_ready, 1)
                        for m in range(C):
                            dve.wait_ge(y_ready, m + 1)
                            own(nc.vector.scalar_tensor_tensor(out=y_sb[:, m], in0=y_ps[:, m],
                                                               scalar=sy[:, :], in1=back[:, :],
                                                               op0=ALU.mult, op1=ALU.mult))
                            view = X[:, m, ds(b * SP1 + h * G + 1, G)]
                            nc.vector.tensor_tensor(view, view, y_sb[:, m], ALU.add)

                    @block.scalar
                    def _(act):
                        for i in range(FBC):
                            act.wait_ge(conv_ready, i + 1)
                            nc.scalar.activation(act_sb[:, i], act_sb[:, i], ACT.Silu).then_inc(silu, 1)
                            act.wait_ge(silu, i + 1)
                            if i >= 2:
                                act.wait_ge(peaked, i - 1)
                            nc.scalar.activation(size[:, i % 2], act_sb[:, i], ACT.Abs).then_inc(sizes, 1)

                    @block.gpsimd
                    def _(pool):
                        pool.wait_ge(peaked, FBC)
                        nc.gpsimd.partition_all_reduce(top[:, :], peak[:, :], P, ABSMAX).then_inc(reduced, 1)

                    @block.tensor
                    def _(pe):
                        for m in range(C):
                            for i in range(FBC):
                                if m == 0:
                                    pe.wait_ge(a_ready, i + 1)
                                last = nc.tensor.matmul(y_ps[:, m],
                                                        w_int[1][:, i * D + m * P:i * D + (m + 1) * P],
                                                        a_int[:, i], start=(i == 0), stop=(i == FBC - 1))
                            last.then_inc(y_ready, 1)


DEPTH, LH, LD = 6, 16, 64
INNER = LH * LD
WIN = 64
KEYS = WIN + P
NT = S // P
PAIRS = LH // 2
QK_SCALE = 8.0
MASKED = -1e30
FI = 682
FIC = -(-FI // P)
FIP = FIC * P
WQKV, WO = C * 3 * INNER, PAIRS * D
W1, W2 = C * 2 * FIP, FIC * D
PIECE = (2, 3, 0, 1, 4, 5)
HILO = ((0, 0), (0, 1), (1, 0))


def local_attention(nc, K, Z, A, layer, tag):
    with ExitStack() as s:
        sb = lambda n, sh, dt=F32: s.enter_context(nc.sbuf_tensor(f"{tag}_{n}", sh, dt))
        wq = [sb(f"wqkv{n}", [P, C, 3 * INNER], F32R) for n in range(2)]
        wo = [sb(f"wo{n}", [P, PAIRS, D], F32R) for n in range(2)]
        tabs = sb("tabs", [P, 4, NT, LD])
        mask = sb("mask", [P, KEYS])
        NJOB = 4
        with ExitStack() as s2:
            raw = s2.enter_context(nc.sbuf_tensor(f"{tag}_raw", [P, WQKV + WO], F32))
            qk = s2.enter_context(nc.sbuf_tensor(f"{tag}_qk", [P, 4, LD], F32))
            step = WQKV // NJOB
            flat = [w[:, :, :].rearrange("p c n -> p (c n)") for w in wq + wo]
            dram = lambda a, lo, n: a[ds(layer, 1), :, lo:lo + n].rearrange("o p n -> p (o n)")
            jobs = [(raw[:, j * step:(j + 1) * step], dram(A["l_wqkv"], j * step, step),
                     flat[0][:, j * step:(j + 1) * step], flat[1][:, j * step:(j + 1) * step])
                    for j in range(NJOB)]
            jobs.append((raw[:, WQKV:], dram(A["l_wo"], 0, WO), flat[2], flat[3]))
            with semaphores(nc, f"{tag}_w", "loaded", "tabled", "high", "scaled") as (
                    loaded, tabled, high, scaled), \
                    nc.Block(no_gpsimd_drain=True) as block:
                @block.sync
                def _(sp):
                    sp.dma_start(tabs[:, :, :, :], A["rotary"]).then_inc(tabled, 16)
                    sp.dma_start(mask[:, :], A["band_mask"]).then_inc(tabled, 16)
                    sp.dma_start(qk[:, :, :], A["l_qk_scale"][ds(layer, 1)].rearrange(
                        "o p a d -> p (o a) d")).then_inc(tabled, 16)
                    for n, (dst, src, _h, _l) in enumerate(jobs):
                        if n:
                            sp.wait_ge(loaded, 16 * n)
                        sp.dma_start(dst, src).then_inc(loaded, 16)
                    sp.wait_ge(tabled, 48)
                    sp.wait_ge(loaded, 16 * len(jobs))

                @block.scalar
                def _(act):
                    for n, (src, _, hi, lo) in enumerate(jobs):
                        act.wait_ge(loaded, 16 * (n + 1))
                        nc.scalar.activation(hi, src, ACT.Copy).then_inc(high, 1)

                @block.vector
                def _(dve):
                    for n, (src, _, hi, lo) in enumerate(jobs):
                        dve.wait_ge(high, n + 1)
                        nc.vector.tensor_tensor(lo, src, hi.bitcast(F32), ALU.subtract)

                @block.gpsimd
                def _(pool):
                    pool.wait_ge(tabled, 48)
                    for n in range(4):
                        nc.gpsimd.tensor_tensor(tabs[:, n], tabs[:, n], bc(qk[:, n, :], 1, [P, NT, LD]),
                                                ALU.mult).then_inc(scaled, 1)
                    pool.wait_ge(scaled, 4)

        xs = [sb(f"xs{n}", [P, 2, C, P], F32R) for n in range(2)]
        sq = sb("sq", [P, 2, 512])
        ra = sb("ra", [P, 2, 512])
        rb = sb("rb", [P, 2, 512])
        rot = sb("rot", [P, 2, INNER])
        ssq = sb("ssq", [P, 2, 2 * LH])
        rn = sb("rn", [P, 2, LH])
        minus_half = sb("minus_half", [P, 2 * LH])
        sc8 = sb("sc8", [P, 2, LH])
        qT = sb("qT", [P, 2, PAIRS, P])
        kT = sb("kT", [P, 2, PAIRS, KEYS])
        vt = sb("vt", [P, 2, INNER])
        vp = sb("vp", [WIN, 2, INNER])
        sm = sb("sm", [P, 2, 4, KEYS])
        pr = sb("pr", [P, 2, 4, KEYS])
        mx = sb("mx", [P, 2, LH])
        nb = sb("nb", [P, 2, LH])
        sums = sb("sums", [P, 2, LH])
        rs = sb("rs", [P, 2, LH])
        pTa = sb("pTa", [WIN, 2, 4, P])
        pTb = sb("pTb", [P, 2, 4, P])
        o_sb = sb("o", [P, INNER])
        oT = [sb(f"oT{n}", [P, PAIRS, 2 * P], F32R) for n in range(2)]
        ps = lambda n, sh: s.enter_context(nc.psum_tensor(f"{tag}_{n}", sh, F32))
        proj_ps, s_ps = ps("proj_ps", [P, 2, 512]), ps("s_ps", [P, 2, 512])
        pTa_ps, pTb_ps = ps("pTa_ps", [P, 4, P]), ps("pTb_ps", [P, 4, P])
        o_ps, t_ps = ps("o_ps", [P, 512]), ps("t_ps", [P, 4, P])

        def steps(t):
            p, n = t - 1, t + 1
            y = p % 2 == 1
            seq = [("S", t, 0), ("TQ", t, 1), ("less", t, 0), ("xh", n + 1, 0), ("tq", t, 1), ("PT", p, 3),
                   ("copy", p, 3), ("exp", t, 0), ("J", n, 0), ("sq", n, 0), ("PV", p, 3), ("exp", t, 1),
                   ("rot", n, 0), ("xl", n + 1, 0), ("J", n, 1), ("out", p, 1),
                   ("S", t, 1), ("TO", p, 1), ("sq", n, 1), ("less", t, 1), ("to", p, 1), ("PT", t, 0),
                   ("copy", t, 0), ("exp", t, 2), ("rot", n, 1), ("J", n, 2), ("sq", n, 2), ("PV", t, 0),
                   ("exp", t, 3), ("rot", n, 2), ("J", n, 3),
                   ("S", t, 2), ("sq", n, 3), ("less", t, 2), ("PT", t, 1)]
            seq += [("Y", p, 0)] * y
            seq += [("copy", t, 1), ("exp", t, 4), ("rot", n, 3), ("J", n, 4), ("PV", t, 1)] \
                + [("yadd", p, 0)] * y
            seq += [("v", n, 4), ("exp", t, 5), ("out", t, 0), ("J", n, 5)]
            seq += [("Y", p, 1)] * y
            seq += [("S", t, 3), ("v", n, 5)] + [("yadd", p, 1)] * y
            return seq + [("less", t, 3), ("TK", n, 0), ("tk", n, 0), ("PT", t, 2), ("copy", t, 2),
                          ("exp", t, 6), ("TK", n, 1), ("tk", n, 1), ("PV", t, 2), ("exp", t, 7), ("TO", t, 0),
                          ("to", t, 0), ("TQ", n, 0), ("tq", n, 0)]
        order = [x for t in range(-1, NT + 1) for x in steps(t) if 0 <= x[1] < NT]
        turns = [x for x in order if x[0] in ("TQ", "TK", "TO", "Y")]
        turn_no = {x: n for n, x in enumerate(turns)}
        by_act = {x: sum(y[0] != "Y" for y in turns[:n + 1]) for x, n in turn_no.items()}
        by_dve = {x: sum(y[0] in ("TO", "Y") for y in turns[:n + 1]) for x, n in turn_no.items()}

        def follow(do):
            for name, t, i in order:
                if name in do:
                    do[name](t, i)

        with nc.Fori(0, B) as b:
            ztok = lambda c, first, n, shift=0: Z[:, c, ds(b * SP1 + (first + 1 - shift), n)]
            with semaphores(nc, tag, "xh", "xl", "proj", "sq", "rot", "v", "ssq", "norm", "pow", "rsum",
                            "kmul", "scores", "less", "exped", "turned", "copied", "pv", "out", "turn",
                            "t_act", "t_dve", "vp", "set", "own") as (
                    xh_ok, xl_ok, proj_ok, sq_ok, rot_ok, v_ok, ssq_ok, norm_ok, pow_ok, sum_ok,
                    kmul_ok, scores_ok, less_ok, exp_ok, turned_ok, copy_ok, pv_ok, out_ok, turn_ok,
                    act_took, dve_took, vp_ok, set_ok, dve_own), \
                    nc.Block(no_gpsimd_drain=True) as block:

                def wait_turn_bank(eng, use):
                    n = turn_no[use]
                    if n:
                        prev = turns[n - 1]
                        if by_act[prev]:
                            eng.wait_ge(act_took, by_act[prev])
                        if by_dve[prev]:
                            eng.wait_ge(dve_took, by_dve[prev])

                @block.sync
                def _(sp):
                    for t in range(NT - 1):
                        sp.wait_ge(v_ok, 2 * (t + 1))
                        if t >= 1:
                            sp.wait_ge(pv_ok, 4 * t)
                            sp.wait_ge(vp_ok, 16 * t)
                        sp.dma_start(vp[:, (t + 1) % 2, :], vt[P - WIN:P, t % 2, :]).then_inc(vp_ok, 16)
                    sp.wait_ge(vp_ok, 16 * (NT - 1))

                @block.tensor
                def _(pe):
                    def J(t, j):
                        n = 6 * t + j
                        if j == 0:
                            pe.wait_ge(xl_ok, t + 1)
                        if n >= 2:
                            u, i = divmod(n - 2, 6)
                            if i < 4:
                                pe.wait_ge(sq_ok, 4 * u + i + 1)
                                pe.wait_ge(rot_ok, 4 * u + i + 1)
                            else:
                                pe.wait_ge(v_ok, 2 * u + i - 3)
                        first = PIECE[j] * 512
                        for c in range(C):
                            for k, (p, q) in enumerate(HILO):
                                last = nc.tensor.matmul(proj_ps[:, n % 2], xs[p][:, t % 2, c, :],
                                                        wq[q][:, c, first:first + 512],
                                                        start=(c == 0 and k == 0), stop=(c == C - 1 and k == 2))
                        last.then_inc(proj_ok, 1)

                    def TQ(t, half):
                        turn_rotated(("TQ", t, half), 0, t, half)

                    def TK(t, half):
                        turn_rotated(("TK", t, half), 1, t, half)

                    def turn_rotated(use, which, t, half):
                        if which:
                            pe.wait_ge(kmul_ok, 2 * t + half + 1)
                        else:
                            pe.wait_ge(sum_ok, 4 * t + 2 + half + 1)
                        wait_turn_bank(pe, use)
                        for i in range(4):
                            first = (half * 4 + i) * P
                            last = nc.tensor.transpose(t_ps[:, i, :], rot[:, which, first:first + P],
                                                       K.ident[:, :])
                        last.then_inc(turn_ok, 1)

                    def S(t, g):
                        if g % 2 == 0:
                            pe.wait_ge(act_took, by_act[("TQ", t, g // 2)])
                        lo = 0 if t else WIN
                        n = 4 * t + g
                        if n:
                            pe.wait_ge(less_ok, 2 * n)
                        for i in range(2):
                            for par in range(2):
                                rows = slice(par * LD, (par + 1) * LD)
                                last = nc.tensor.matmul(s_ps[:, par, i * KEYS + lo:(i + 1) * KEYS],
                                                        qT[rows, t % 2, 2 * g + i, :],
                                                        kT[rows, t % 2, 2 * g + i, lo:KEYS],
                                                        start=True, stop=True)
                        last.then_inc(scores_ok, 1)

                    def PT(t, g):
                        n = 4 * t + g
                        pe.wait_ge(exp_ok, 2 * n + 2)
                        if n >= 1:
                            pe.wait_ge(copy_ok, n)
                        for i in range(4):
                            if t:
                                nc.tensor.transpose(pTa_ps[0:WIN, i, :], pr[:, n % 2, i, 0:WIN],
                                                    K.ident[:, :])
                            last = nc.tensor.transpose(pTb_ps[:, i, :], pr[:, n % 2, i, WIN:KEYS],
                                                       K.ident[:, :])
                        last.then_inc(turned_ok, 1)

                    def PV(t, g):
                        n = 4 * t + g
                        pe.wait_ge(copy_ok, n + 1)
                        if g == 0:
                            pe.wait_ge(v_ok, 2 * (t + 1))
                            if t:
                                pe.wait_ge(vp_ok, 16 * t)
                        if g % 2 == 0 and n >= 2:
                            pe.wait_ge(out_ok, n // 2)
                        for i in range(4):
                            h = 4 * g + i
                            dst = o_ps[:, (h % 8) * LD:(h % 8 + 1) * LD]
                            if t:
                                nc.tensor.matmul(dst, pTa[:, n % 2, i, :], vp[:, t % 2, h * LD:(h + 1) * LD],
                                                 start=True, stop=False)
                            last = nc.tensor.matmul(dst, pTb[:, n % 2, i, :], vt[:, t % 2, h * LD:(h + 1) * LD],
                                                    start=not t, stop=True)
                        last.then_inc(pv_ok, 1)

                    def TO(t, half):
                        pe.wait_ge(out_ok, 2 * t + half + 1)
                        wait_turn_bank(pe, ("TO", t, half))
                        for i in range(4):
                            first = (half * 4 + i) * P
                            last = nc.tensor.transpose(t_ps[:, i, :], o_sb[:, first:first + P], K.ident[:, :])
                        last.then_inc(turn_ok, 1)

                    def Y(t, m):
                        wait_turn_bank(pe, ("Y", t, m))
                        for i in range(PAIRS):
                            for k, (p, q) in enumerate(HILO):
                                last = nc.tensor.matmul(
                                    t_ps[:, 2 * m:2 * m + 2, :].rearrange("p a n -> p (a n)"),
                                    wo[p][:, i, m * P:(m + 1) * P], oT[q][:, i, :],
                                    start=(i == 0 and k == 0), stop=(i == PAIRS - 1 and k == 2))
                        last.then_inc(turn_ok, 1)
                    follow({"J": J, "TQ": TQ, "TK": TK, "S": S, "PT": PT, "PV": PV, "TO": TO, "Y": Y})

                @block.scalar
                def _(act):
                    def xh(t, _=0):
                        if t >= 2:
                            act.wait_ge(proj_ok, 6 * (t - 1))
                        for c in range(C):
                            last = nc.scalar.activation(xs[0][:, t % 2, c, :], ztok(c, t * P, P, c), ACT.Copy)
                        last.then_inc(xh_ok, 1)

                    def square(t, j):
                        n = 6 * t + j
                        act.wait_ge(proj_ok, n + 1)
                        if 4 * t + j >= 2:
                            act.wait_ge(ssq_ok, 4 * t + j - 1)
                        nc.scalar.activation(sq[:, j % 2], proj_ps[:, n % 2], ACT.Square).then_inc(sq_ok, 1)

                    def values(t, j):
                        n = 6 * t + j
                        act.wait_ge(proj_ok, n + 1)
                        if j == 4 and t >= 2:
                            act.wait_ge(pv_ok, 4 * (t - 1))
                            act.wait_ge(vp_ok, 16 * (t - 1))
                        nc.scalar.activation(vt[:, t % 2, (j - 4) * 512:(j - 3) * 512], proj_ps[:, n % 2],
                                             ACT.Copy).then_inc(v_ok, 1)

                    def TQ(t, half):
                        act.wait_ge(turn_ok, turn_no[("TQ", t, half)] + 1)
                        if t >= 2:
                            act.wait_ge(scores_ok, 4 * (t - 1))
                        nc.scalar.activation(qT[:, t % 2, half * 4:half * 4 + 4, :], t_ps[:, :, :],
                                             ACT.Copy).then_inc(act_took, 1)

                    def TK(t, half):
                        act.wait_ge(turn_ok, turn_no[("TK", t, half)] + 1)
                        pairs = slice(half * 4, half * 4 + 4)
                        if t >= 1:
                            act.wait_ge(scores_ok, 4 * t)
                        if t + 1 < NT:
                            nc.scalar.activation(kT[:, (t + 1) % 2, pairs, 0:WIN], t_ps[:, :, P - WIN:P],
                                                 ACT.Copy)
                        nc.scalar.activation(kT[:, t % 2, pairs, WIN:KEYS], t_ps[:, :, :],
                                             ACT.Copy).then_inc(act_took, 1)

                    def exp(t, pair):
                        n, half = 4 * t + pair // 2, pair % 2
                        act.wait_ge(less_ok, 8 * t + pair + 1)
                        if n >= 2:
                            act.wait_ge(turned_ok, n - 1)
                        if pair == 0 and t >= 2:
                            act.wait_ge(out_ok, 2 * (t - 1))
                        lo = 0 if t else WIN
                        for i in (2 * half, 2 * half + 1):
                            h = 2 * pair + i % 2
                            last = nc.scalar.activation(pr[:, n % 2, i, lo:], sm[:, n % 2, i, lo:], ACT.Exp,
                                                        bias=nb[:, t % 2, h:h + 1],
                                                        scale=sc8[:, t % 2, h:h + 1],
                                                        accum_out=sums[:, t % 2, h:h + 1])
                        last.then_inc(exp_ok, 1)

                    def copy(t, g):
                        n = 4 * t + g
                        act.wait_ge(turned_ok, n + 1)
                        if n >= 2:
                            act.wait_ge(pv_ok, n - 1)
                        if t:
                            nc.scalar.activation(pTa[:, n % 2], pTa_ps[0:WIN], ACT.Copy)
                        nc.scalar.activation(pTb[:, n % 2], pTb_ps[:, :, :], ACT.Copy).then_inc(copy_ok, 1)

                    def TO(t, half):
                        use = ("TO", t, half)
                        act.wait_ge(turn_ok, turn_no[use] + 1)
                        if t >= 2 and t % 2 == 0 and half == 0:
                            act.wait_ge(turn_ok, turn_no[("Y", t - 1, 1)] + 1)
                        part = slice((t % 2) * P, (t % 2 + 1) * P)
                        nc.scalar.activation(oT[0][:, half * 4:half * 4 + 4, part], t_ps[:, :, :],
                                             ACT.Copy).then_inc(act_took, 1)
                    xh(0)
                    follow({"xh": xh, "sq": square, "v": values, "tq": TQ, "tk": TK, "exp": exp, "copy": copy,
                            "to": TO})

                @block.gpsimd
                def _(pool):
                    nc.gpsimd.memset(minus_half[:, :], -0.5).then_inc(set_ok, 1)
                    pool.wait_ge(set_ok, 1)
                    powers = 0
                    for t in range(NT):
                        for which in (1, 0):
                            for half in range(2):
                                j = 2 * (1 - which) + half
                                pool.wait_ge(rot_ok, 4 * t + j + 1)
                                if t:
                                    pool.wait_ge(turn_ok, turn_no[("TK" if which else "TQ", t - 1, half)] + 1)
                                part = rot[:, which, half * 512:(half + 1) * 512]
                                nc.gpsimd.tensor_tensor(part, ra[:, j % 2], rb[:, j % 2], ALU.add
                                                        ).then_inc(sum_ok, 1)
                            pool.wait_ge(norm_ok, powers + 1)
                            if not which and t >= 2:
                                pool.wait_ge(exp_ok, 8 * (t - 1))
                            dst = rn[:, t % 2, :] if which else sc8[:, t % 2, :]
                            mine = slice(0, LH) if which else slice(LH, 2 * LH)
                            nc.gpsimd.tensor_tensor(dst, ssq[:, t % 2, mine], minus_half[:, 0:LH], ALU.pow
                                                    ).then_inc(pow_ok, 1)
                            powers += 1
                            if which:
                                pool.wait_ge(pow_ok, powers)
                                pool.wait_ge(sum_ok, 4 * t + 2)
                                for half in range(2):
                                    part = rot[:, 1, half * 512:(half + 1) * 512].rearrange(
                                        "p (h d) -> p h d", d=LD)
                                    nc.gpsimd.tensor_tensor(
                                        part, part, bc(rn[:, t % 2, 8 * half:8 * half + 8], 2, [P, 8, LD]),
                                        ALU.mult).then_inc(kmul_ok, 1)

                @block.vector
                def _(dve):
                    own = Own(dve, dve_own)
                    tt = nc.vector.tensor_tensor

                    def xl(t, _=0):
                        dve.wait_ge(xh_ok, t + 1)
                        for c in range(C):
                            last = tt(xs[1][:, t % 2, c, :], ztok(c, t * P, P, c),
                                      xs[0][:, t % 2, c, :].bitcast(F32), ALU.subtract)
                        last.then_inc(xl_ok, 1)

                    def rotate(t, j):
                        n = 6 * t + j
                        table = 2 * (PIECE[j] // 2)
                        dve.wait_ge(sq_ok, 4 * t + j + 1)
                        if 4 * t + j >= 2:
                            dve.wait_ge(sum_ok, 4 * t + j - 1)
                        heads = lambda x: x.rearrange("p (h d) -> p h d", d=LD)
                        src, a, r = heads(proj_ps[:, n % 2]), heads(ra[:, j % 2]), heads(rb[:, j % 2])
                        cos, sin = tabs[:, table, t, :], tabs[:, table + 1, t, :]
                        lo, up = slice(0, LD // 2), slice(LD // 2, LD)
                        tt(a, src, bc(cos, 1, [P, 8, LD]), ALU.mult)
                        tt(r[:, :, lo], src[:, :, up], bc(sin[:, lo], 1, [P, 8, LD // 2]), ALU.mult)
                        tt(r[:, :, up], src[:, :, lo], bc(sin[:, up], 1, [P, 8, LD // 2]), ALU.mult
                           ).then_inc(rot_ok, 1)
                        if j == 0 and t >= 2:
                            dve.wait_ge(pow_ok, 2 * (t - 1))
                        nc.vector.tensor_reduce(ssq[:, t % 2, j * 8:(j + 1) * 8], heads(sq[:, j % 2]),
                                                AX.X, ALU.add).then_inc(ssq_ok, 1)
                        if j % 2:
                            dve.wait_ge(ssq_ok, 4 * t + j + 1)
                            part = ssq[:, t % 2, (j - 1) * 8:(j + 1) * 8]
                            scale = 1.0 if j == 1 else QK_SCALE ** -2
                            nc.vector.tensor_scalar(part, part, scale, LEAST * LEAST * scale, ALU.mult,
                                                    ALU.max).then_inc(norm_ok, 1)

                    def less(t, g):
                        n = 4 * t + g
                        if n >= 2:
                            dve.wait_ge(exp_ok, 2 * n - 2)
                        lo = 0 if t else WIN
                        for i in range(2):
                            h = 4 * g + 2 * i
                            dve.wait_ge(scores_ok, n + 1)
                            for par in range(2):
                                ins = nc.vector.tensor_tensor_reduce(
                                    sm[:, n % 2, 2 * i + par, lo:],
                                    s_ps[:, par, i * KEYS + lo:(i + 1) * KEYS], mask[:, lo:], 1.0,
                                    3.0 * MASKED, ALU.add, ALU.max, mx[:, t % 2, h + par:h + par + 1])
                            own(ins)
                            if g == 0 and i == 0:
                                dve.wait_ge(pow_ok, 2 * t + 2)
                            nc.vector.scalar_tensor_tensor(
                                out=nb[:, t % 2, h:h + 2], in0=mx[:, t % 2, h:h + 2], scalar=-1.0,
                                in1=sc8[:, t % 2, h:h + 2], op0=ALU.mult, op1=ALU.mult).then_inc(less_ok, 1)

                    def outputs(t, half):
                        heads = slice(8 * half, 8 * half + 8)
                        dve.wait_ge(pv_ok, 4 * t + 2 * half + 2)
                        own(nc.vector.reciprocal(rs[:, t % 2, heads], sums[:, t % 2, heads]))
                        if t:
                            dve.wait_ge(turn_ok, turn_no[("TO", t - 1, half)] + 1)
                        tt(o_sb[:, half * 512:(half + 1) * 512].rearrange("p (h d) -> p h d", d=LD),
                           o_ps[:, :].rearrange("p (h d) -> p h d", d=LD),
                           bc(rs[:, t % 2, heads], 2, [P, 8, LD]), ALU.mult).then_inc(out_ok, 1)

                    def TO(t, half):
                        use = ("TO", t, half)
                        dve.wait_ge(act_took, by_act[use])
                        part = slice((t % 2) * P, (t % 2 + 1) * P)
                        four = slice(half * 4, half * 4 + 4)
                        tt(oT[1][:, four, part], t_ps[:, :, :], oT[0][:, four, part].bitcast(F32),
                           ALU.subtract).then_inc(dve_took, 1)

                    def add(t, m):
                        dve.wait_ge(turn_ok, turn_no[("Y", t, m)] + 1)
                        view = ztok(m, (t - 1) * P, 2 * P)
                        tt(view, view, t_ps[:, 2 * m:2 * m + 2, :].rearrange("p a n -> p (a n)"), ALU.add
                           ).then_inc(dve_took, 1)
                    xl(0)
                    follow({"xl": xl, "rot": rotate, "less": less, "out": outputs, "to": TO, "yadd": add})


def layer_ffn(nc, K, Z, A, layer, tag):
    with ExitStack() as s:
        sb = lambda n, sh, dt=F32: s.enter_context(nc.sbuf_tensor(f"{tag}_{n}", sh, dt))
        w1 = [sb(f"w1{n}", [P, C, 2 * FIP], F32R) for n in range(2)]
        w2 = [sb(f"w2{n}", [P, FIC, D], F32R) for n in range(2)]
        vec = sb("vec", [P, 2 * C + 2 * FIC + C])
        LNG, LNB, B1, B2 = vec[:, 0:C], vec[:, C:2 * C], vec[:, 2 * C:2 * C + 2 * FIC], vec[:, 2 * C + 2 * FIC:]
        xh = sb("xh", [P, C, T], F32R)
        xl = sb("xl", [P, C, T], F32R)
        with ExitStack() as s2:
            raw = s2.enter_context(nc.sbuf_tensor(f"{tag}_raw", [P, W1 + W2], F32))
            dram = lambda a, lo, n: a[ds(layer, 1), :, lo:lo + n].rearrange("o p n -> p (o n)")
            flat = [w[:, :, :].rearrange("p c n -> p (c n)") for w in w1 + w2]
            jobs = [(raw[:, j * (W1 // 2):(j + 1) * (W1 // 2)], dram(A["l_w1"], j * (W1 // 2), W1 // 2),
                     flat[0][:, j * (W1 // 2):(j + 1) * (W1 // 2)],
                     flat[1][:, j * (W1 // 2):(j + 1) * (W1 // 2)]) for j in range(2)]
            jobs.append((raw[:, W1:], dram(A["l_w2"], 0, W2), flat[2], flat[3]))
            with semaphores(nc, f"{tag}_w", "loaded", "vec", "high") as (loaded, vec_ok, high), \
                    nc.Block(no_gpsimd_drain=True) as block:
                @block.sync
                def _(sp):
                    sp.dma_start(vec[:, :], dram(A["l_vec"], 0, vec.shape[1])).then_inc(vec_ok, 16)
                    for n, (dst, src, _h, _l) in enumerate(jobs):
                        if n:
                            sp.wait_ge(loaded, 16 * n)
                        sp.dma_start(dst, src).then_inc(loaded, 16)
                    sp.wait_ge(vec_ok, 16)

                @block.scalar
                def _(act):
                    for n, (src, _, hi, lo) in enumerate(jobs):
                        act.wait_ge(loaded, 16 * (n + 1))
                        nc.scalar.activation(hi, src, ACT.Copy).then_inc(high, 1)

                @block.vector
                def _(dve):
                    for n, (src, _, hi, lo) in enumerate(jobs):
                        dve.wait_ge(high, n + 1)
                        nc.vector.tensor_tensor(lo, src, hi.bitcast(F32), ALU.subtract)
        with ExitStack() as s2:
            XN = s2.enter_context(nc.sbuf_tensor(f"{tag}_xn", [P, C, T], F32))

            def shifted(c, g):
                first = (g // GB) * SP1 + 1 + (g % GB) * G - c
                return Z[:, c, first:first + G]
            layer_norm(nc, K, shifted, XN, f"{tag}_ln", affine=(LNG, LNB))
            split_tokens(nc, XN, xh, xl, f"{tag}_split")

        hg = sb("hg", [P, 2, G])
        hid = sb("hid", [P, 2, G])
        hh = sb("hh", [P, 2, G], F32R)
        hl = sb("hl", [P, 2, G], F32R)
        gu_ps = s.enter_context(nc.psum_tensor(f"{tag}_gu", [P, 2, 2, G], F32))
        y_ps = s.enter_context(nc.psum_tensor(f"{tag}_y", [P, 2, C, G], F32))
        N = NG * FIC
        with semaphores(nc, tag, "gu", "gelu", "prod", "high", "low", "down", "added") as (
                gu_ready, gelu_ready, prod, high, low, down_done, added), \
                nc.Block(no_gpsimd_drain=True) as block:

            @block.tensor
            def _(pe):
                def up(k):
                    g, i = divmod(k, FIC)
                    if k >= 2:
                        pe.wait_ge(prod, k - 1)
                    tok = slice(g * G, (g + 1) * G)
                    for u in range(2):
                        first = u * FIP + i * P
                        for c in range(C):
                            x = (xh[:, c, tok], xl[:, c, tok])
                            for n, (p, q) in enumerate(HILO):
                                last = nc.tensor.matmul(gu_ps[:, k % 2, u], w1[p][:, c, first:first + P], x[q],
                                                        start=(c == 0 and n == 0), stop=(c == C - 1 and n == 2))
                    last.then_inc(gu_ready, 1)

                def down(k):
                    g, i = divmod(k, FIC)
                    pe.wait_ge(low, k + 1)
                    if i == 0 and g >= 2:
                        pe.wait_ge(added, g - 1)
                    for m in range(C):
                        x = (hh[:, k % 2], hl[:, k % 2])
                        for n, (p, q) in enumerate(HILO):
                            last = nc.tensor.matmul(y_ps[:, g % 2, m], w2[p][:, i, m * P:(m + 1) * P], x[q],
                                                    start=(i == 0 and n == 0), stop=(i == FIC - 1 and n == 2))
                    last.then_inc(down_done, 1)
                for k in range(N + 2):
                    if k < N:
                        up(k)
                    if k >= 2:
                        down(k - 2)

            @block.scalar
            def _(act):
                for k in range(N + 1):
                    if k < N:
                        i = k % FIC
                        act.wait_ge(gu_ready, k + 1)
                        if k >= 2:
                            act.wait_ge(prod, k - 1)
                        nc.scalar.activation(hg[:, k % 2], gu_ps[:, k % 2, 1], ACT.Gelu,
                                             bias=B1[:, FIC + i:FIC + i + 1]).then_inc(gelu_ready, 1)
                    if k:
                        act.wait_ge(prod, k)
                        if k >= 3:
                            act.wait_ge(down_done, k - 2)
                        nc.scalar.activation(hh[:, (k - 1) % 2], hid[:, (k - 1) % 2], ACT.Copy
                                             ).then_inc(high, 1)

            @block.vector
            def _(dve):
                def product(k):
                    i = k % FIC
                    dve.wait_ge(gelu_ready, k + 1)
                    if k >= 2:
                        dve.wait_ge(low, k - 1)
                    nc.vector.scalar_tensor_tensor(out=hid[:, k % 2], in0=gu_ps[:, k % 2, 0],
                                                   scalar=B1[:, i:i + 1], in1=hg[:, k % 2], op0=ALU.add,
                                                   op1=ALU.mult).then_inc(prod, 1)

                def take_low(k):
                    dve.wait_ge(high, k + 1)
                    if k >= 2:
                        dve.wait_ge(down_done, k - 1)
                    nc.vector.tensor_tensor(hl[:, k % 2], hid[:, k % 2], hh[:, k % 2].bitcast(F32),
                                            ALU.subtract).then_inc(low, 1)

                def add(g):
                    dve.wait_ge(down_done, FIC * (g + 1))
                    for c in range(C):
                        first = (g // GB) * SP1 + 1 + (g % GB) * G
                        view = Z[:, c, first:first + G]
                        last = nc.vector.scalar_tensor_tensor(out=view, in0=y_ps[:, g % 2, c],
                                                              scalar=B2[:, c:c + 1], in1=view, op0=ALU.add,
                                                              op1=ALU.add)
                    last.then_inc(added, 1)
                for k in range(N + 3):
                    if k < N:
                        product(k)
                    if 1 <= k <= N:
                        take_low(k - 1)
                    if k >= 3 and (k - 3) % FIC == FIC - 1:
                        add((k - 3) // FIC)


def flamingo(nc, A, out_x):
    with ExitStack() as s:
        sb = lambda n, sh: s.enter_context(nc.sbuf_tensor(n, sh, F32))
        X = sb("X", [P, C, B * SP1])
        K = Constants(sb, A)
        gates = sb("gates", [P, 8])
        ctxT = sb("ctxT", [P, C, B * E])
        start_loaded = s.enter_context(nc.semaphore("start_loaded"))
        stored = s.enter_context(nc.semaphore("stored"))

        with semaphores(nc, "start", "filled") as (filled,), nc.Block() as block:
            @block.sync
            def _(sp):
                for b in range(B):
                    sp.dma_start(X[:, :, b * SP1 + 1:(b + 1) * SP1],
                                 A["xT"].rearrange("(c p) (b t) -> p c b t", p=P, b=B)[:, :, b]
                                 ).then_inc(start_loaded, 16)
                sp.dma_start(K.ident[:, :], A["ident"]).then_inc(start_loaded, 16)
                sp.dma_start(ctxT[:, :, :], A["ctxT"].rearrange("(c p) t -> p c t", p=P)
                             ).then_inc(start_loaded, 16)
                sp.dma_start(gates[:, 0:4], A["g_xattn"].partition_broadcast(P)).then_inc(start_loaded, 16)
                sp.dma_start(gates[:, 4:8], A["g_ffn"].partition_broadcast(P)).then_inc(start_loaded, 16)
                sp.dma_start(K.last_row[0:E + 1, :], A["last_row"]).then_inc(start_loaded, 16)
                sp.wait_ge(start_loaded, 16 * 7)

            @block.scalar
            def _(act):
                act.wait_ge(start_loaded, 16 * 7)
                nc.scalar.activation(gates[:, :], gates[:, :], ACT.Tanh)

            @block.vector
            def _(dve):
                for b in range(B):
                    nc.vector.memset(X[:, :, b * SP1:b * SP1 + 1], 0.0)
                nc.vector.memset(K.mean_w[:, :], 1.0 / D)
                nc.vector.memset(K.ones[:, :], 1.0)
                nc.vector.memset(K.eps[:, :], EPS)

        kept = nc.dram_tensor("kept", (P, C, B * SP1), F32).ap()

        def tokens(c, g):
            first = (g // GB) * SP1 + 1 + (g % GB) * G
            return X[:, c, first:first + G]

        def weights(prefix):
            return {n[len(prefix) + 1:]: a for n, a in A.items() if n.startswith(prefix + "_")}

        with ExitStack() as s1:
            XN = s1.enter_context(nc.sbuf_tensor("XN", [P, C, T], F32))
            layer_norm(nc, K, tokens, XN, "ln0a")
            wide_attention(nc, K, X, XN, ctxT, weights("a0"), gates[:, 0:1], "a0", True, 1.0)
            layer_norm(nc, K, tokens, XN, "ln0f")
            quantised_ffn(nc, K, X, XN, weights("f0"), gates[:, 4:5], "f0")
            layer_norm(nc, K, tokens, XN, "ln1a")
            wide_attention(nc, K, X, XN, ctxT, weights("a1"), gates[:, 1:2], "a1", False, D ** -0.5)
            w_dram = nc.dram_tensor("expert_weights", (NE + 1, T), F32).ap()
            layer_norm(nc, K, tokens, XN, "ln1f")
            with ExitStack() as s2:
                xh = s2.enter_context(nc.sbuf_tensor("moe_xh", [P, C, T], F32R))
                xl = s2.enter_context(nc.sbuf_tensor("moe_xl", [P, C, T], F32R))
                with ExitStack() as s3:
                    XN2 = s3.enter_context(nc.sbuf_tensor("XN2", [P, C, T], F32))
                    ln_g = s3.enter_context(nc.sbuf_tensor("moe_ln_g", [P, C], F32))
                    ln_b = s3.enter_context(nc.sbuf_tensor("moe_ln_b", [P, C], F32))
                    with semaphores(nc, "moe_ln", "loaded") as (loaded,), \
                            nc.Block(no_gpsimd_drain=True) as block:
                        @block.sync
                        def _(sp):
                            sp.dma_start(ln_g[:, :], A["moe_ln_scale"]).then_inc(loaded, 16)
                            sp.dma_start(ln_b[:, :], A["moe_ln_bias"]).then_inc(loaded, 16)
                            sp.wait_ge(loaded, 32)
                    layer_norm(nc, K, lambda c, g: XN[:, c, g * G:(g + 1) * G], XN2, "ln1r",
                               affine=(ln_g, ln_b))
                    router(nc, K, XN2, A["moe_gate_w"], w_dram, "rt")
                split_tokens(nc, XN, xh, xl, "moe_split")
                experts(nc, K, X, xh, xl, w_dram, A["moe_w"], gates[:, 5:6], "moe")
            for stage, tag, g, rel in ((5, "a2", 2, False), (7, "a3", 3, True)):
                layer_norm(nc, K, tokens, XN, f"ln{tag}")
                head_attention(nc, K, X, XN, ctxT, weights(tag), gates[:, g:g + 1], tag, rel)
                if stage == 5:
                    layer_norm(nc, K, tokens, XN, "ln2f")
                    bit_ffn(nc, K, X, XN, weights("f2"), gates[:, 6:7], "f2")
            layer_norm(nc, K, tokens, XN, "ln3f")
            with semaphores(nc, "swap", "away", "taken") as (away, taken), \
                    nc.Block(no_gpsimd_drain=True) as block:
                @block.sync
                def _(sp):
                    sp.dma_start(kept, X[:, :, :]).then_inc(away, 16)
                    sp.wait_ge(away, 16)

                @block.vector
                def _(dve):
                    dve.wait_ge(away, 16)
                    for g in range(NG):
                        for c in range(C):
                            nc.vector.tensor_copy(tokens(c, g), XN[:, c, g * G:(g + 1) * G])
        with nc.Fori(0, DEPTH) as layer:
            local_attention(nc, K, X, A, layer, "la")
            layer_ffn(nc, K, X, A, layer, "lf")
        with nc.sbuf_tensor("kept_x", [P, C, B * SP1], F32) as old, \
                semaphores(nc, "back", "back") as (back,), nc.Block(no_gpsimd_drain=True) as block:
            @block.sync
            def _(sp):
                sp.dma_start(old[:, :, :], kept).then_inc(back, 16)

            @block.vector
            def _(dve):
                dve.wait_ge(back, 16)
                nc.vector.scalar_tensor_tensor(out=X[:, :, :], in0=X[:, :, :], scalar=gates[:, 7:8],
                                               in1=old[:, :, :], op0=ALU.mult, op1=ALU.add)

        with nc.Block() as block:
            @block.sync
            def _(sp):
                for b in range(B):
                    sp.dma_start(out_x.rearrange("(c p) (b t) -> p c b t", p=P, b=B)[:, :, b],
                                 X[:, :, b * SP1 + 1:(b + 1) * SP1]).then_inc(stored, 16)
                sp.wait_ge(stored, 16 * B)


def kc(a):
    return a.reshape(a.shape[0] // P, P, a.shape[1]).transpose(1, 0, 2)


def cols(a):
    return a.reshape(-1, P).T


def rows(a):
    return np.broadcast_to(a, (P, a.shape[0]))


def layout(i):
    L = {"xT": i["x"].reshape(T, D).T, "ctxT": i["ctx_1024"].reshape(B * E, D).T,
         "g_xattn": i["g_xattn"], "g_ffn": i["g_ffn"],
         "ident": np.eye(P, dtype=np.float32)}
    last = np.zeros((E + 1, P), np.float32)
    last[E] = 1.0
    L["last_row"] = last
    for st, p, tr in (("a0", "L0_xattn_", False), ("a1", "L1_xattn_", True)):
        for n in "qkv":
            wt = i[f"{p}W{n}"]
            L[f"{st}_w{n}"] = kc(wt.T if tr else wt)
            L[f"{st}_b{n}"] = cols(i[f"{p}b{n}"])
        L[f"{st}_bv_row"] = rows(i[f"{p}bv"])
    for st, p in (("a2", "L2_xattn_"), ("a3", "L3_xattn_")):
        wk, wv = (i[p + "Wkv"][:, :D], i[p + "Wkv"][:, D:]) if st == "a2" else (i[p + "Wk"], i[p + "Wv"])
        bk, bv = (i[p + "bkv"][:D], i[p + "bkv"][D:]) if st == "a2" else (i[p + "bk"], i[p + "bv"])
        L[f"{st}_wq"], L[f"{st}_wk"], L[f"{st}_wv"], L[f"{st}_wo"] = kc(i[p + "Wq"]), kc(wk), kc(wv), kc(i[p + "Wo"])
        L[f"{st}_bq"], L[f"{st}_bk"], L[f"{st}_bo"] = cols(i[p + "bq"]), cols(bk), cols(i[p + "bo"])
        L[f"{st}_bv_row"] = rows(bv)
    L["a3_rel_k"] = np.tile(i["L3_xattn_rel_k"], (1, HC)).T
    L["a3_rel_v"] = np.tile(i["L3_xattn_rel_v"], (1, NH))
    L["a3_rel_v0"] = rows(L["a3_rel_v"][0])
    L["head_of"] = (np.arange(P)[:, None] // HD == np.arange(HC)[None, :]).astype(np.float32)
    L["head_cols"] = np.broadcast_to(L["head_of"].T, (P, HC, P))
    dist = np.arange(E)[None, :] - np.arange(P)[:, None]
    L["rel_mask"] = np.stack([np.clip(dist, -2, 2) + 2 == r for r in range(1, 1 + R)], axis=1).astype(np.float32)

    p = "L0_ffn_w_"
    L["f0_wg"], L["f0_wu"], L["f0_wd"] = (kc(i[p + n]).reshape(P, -1) for n in ("gate", "up", "down"))
    p = "L2_ffn_"
    L["f2_w1"], L["f2_w2"] = kc(i[p + "w1"].T).reshape(P, -1), kc(i[p + "w2"].T).reshape(P, -1)
    L["f2_conv_w"] = kc(i[p + "conv_w"][:, 0, :])
    L["f2_conv_b"] = cols(i[p + "conv_b"])

    p = "L3_ffn_"
    per = lambda f: np.stack([f(n) for n in range(DEPTH)])
    pad = lambda a: np.concatenate([a, np.zeros(a.shape[:-1] + (FIP - FI,), a.dtype)], axis=-1)
    two = lambda a: np.concatenate([pad(a[..., :FI]), pad(a[..., FI:])], axis=-1)
    L["l_wqkv"] = per(lambda n: kc(i[p + "Wqkv"][n]).reshape(P, -1))
    L["l_wo"] = per(lambda n: kc(i[p + "Wo"][n]).reshape(P, -1))
    L["l_w1"] = per(lambda n: kc(two(i[p + "W1"][n])).reshape(P, -1))
    L["l_w2"] = per(lambda n: kc(pad(i[p + "W2"][n].T).T).reshape(P, -1))
    L["l_vec"] = per(lambda n: np.concatenate([cols(i[p + "ln_g"][n]), cols(i[p + "ln_b"][n]),
                                               cols(two(i[p + "b1"][n])), cols(i[p + "b2"][n])], axis=1))
    partner = np.roll(np.arange(LD), LD // 2)
    L["l_qk_scale"] = per(lambda n: np.broadcast_to(np.stack(
        [i[p + "q_scale"][n], i[p + "q_scale"][n][partner], i[p + "k_scale"][n], i[p + "k_scale"][n][partner]]),
        (P, 4, LD)))
    f32 = np.float32
    half = np.arange(0, LD, 2, dtype=f32)
    freqs = np.arange(S, dtype=f32)[:, None] * (f32(1.0) / f32(10000.0) ** (half / f32(LD)))[None, :]
    base = (half + f32(0.4 * LD)) / f32(1.4 * LD)
    grow = base[None, :] ** ((np.arange(S, dtype=f32) - S // 2) / (WIN // 2))[:, None]
    twice = lambda a: np.concatenate([a, a], axis=1)
    cos, sin = twice(np.cos(freqs)), np.concatenate([-np.sin(freqs), np.sin(freqs)], axis=1)
    grow, fall = twice(grow), twice(f32(1.0) / grow)
    L["rotary"] = np.stack([cos * grow, sin * grow, cos * fall, sin * fall]).astype(f32).reshape(
        4, NT, P, LD).transpose(2, 0, 1, 3)
    key, query = np.arange(KEYS)[None, :], np.arange(P)[:, None]
    L["band_mask"] = np.where((key >= query) & (key <= query + WIN), 0.0, MASKED).astype(f32)

    def expert(wg, wu, wd):
        return np.concatenate([kc(w).reshape(P, -1) for w in (wg, wu, wd)], axis=1)
    p = "L1_ffn_"
    L["moe_w"] = np.stack([expert(i[p + "Wg"][e], i[p + "Wu"][e], i[p + "Wd"][e]) for e in range(NE)]
                          + [expert(i[p + "sWg"], i[p + "sWu"], i[p + "sWd"])])
    L["moe_gate_w"] = kc(i[p + "gate_w"].T)
    L["moe_ln_scale"], L["moe_ln_bias"] = cols(i[p + "ln_scale"]), cols(i[p + "ln_bias"])
    L["expert_iota"] = rows(np.arange(NE, dtype=np.float32) - NE)
    return L


def kernel(**inputs):
    import numpy as _np
    import concourse.bacc as _bacc
    from concourse import mybir as _mybir
    from concourse.bass_utils import run_bass_kernel_spmd as _run

    nc = _bacc.Bacc("TRN2", target_bir_lowering=False, num_devices=1)
    L = {k: _np.ascontiguousarray(v) for k, v in layout({k: _np.asarray(v) for k, v in inputs.items()}).items()}
    arrays, aps = {}, {}
    for name, a in L.items():
        arrays[f"in_{name}"] = a
        aps[name] = nc.dram_tensor(f"in_{name}", a.shape, _mybir.dt.from_np(a.dtype), kind="ExternalInput").ap()
    out = nc.dram_tensor("out_x", (D, T), _mybir.dt.float32, kind="ExternalOutput").ap()
    flamingo(nc, aps, out)
    r = _run(nc, [arrays], core_ids=[0])
    got = r.results[0]["out_x"]
    return _np.ascontiguousarray(got.T).reshape(B, S, D)
```

```python
from contextlib import ExitStack, contextmanager

import numpy as np
import concourse.bass as bass
from concourse import mybir

ALU = mybir.AluOpType
ACT = mybir.ActivationFunctionType
AX = mybir.AxisListType
F32 = mybir.dt.float32
BF16 = mybir.dt.bfloat16
F32R = mybir.dt.float32r
ABSMAX = bass.bass_isa.ReduceOp.absmax
RADD = bass.bass_isa.ReduceOp.add
ds = bass.ds

P = 128
B, S, D = 2, 1024, 256
C = D // P
T = B * S
G = 512
NG = T // G
GB = S // G
TG = G // P
E = 77
SP1 = S + 1
MAGIC = 12582912.0
EPS = 1e-5


@contextmanager
def semaphores(nc, stage, *names):
    with ExitStack() as s:
        sems = [s.enter_context(nc.semaphore(f"{stage}_{n}")) for n in names]
        yield sems
        with nc.Block(no_gpsimd_drain=True) as block:
            @block.sync
            def _(sp):
                for sem in sems:
                    sp.sem_clear(sem)


class Own:

    def __init__(self, eng, sem):
        self.eng, self.sem, self.n = eng, sem, 0

    def __call__(self, ins):
        self.n += 1
        ins.then_inc(self.sem, 1)
        self.eng.wait_ge(self.sem, self.n)


class Constants:

    def __init__(self, sb, early, A):
        self.ident, self.mean_w, self.eps = sb("ident", [P, P]), sb("mean_w", [P, P]), sb("eps", [P, 1])
        self.ones, self.last_row = early("ones", [P, P]), early("last_row", [P, P])
        self.head_of, self.head_cols, self.rel_mask = A["head_of"], A["head_cols"], A["rel_mask"]
        self.expert_iota = A["expert_iota"]


def bc(ap, axis, shape):
    return ap.unsqueeze(axis).to_broadcast(shape)


def layer_norm(nc, K, src, XN, tag, affine=None):
    with ExitStack() as s:
        sb = lambda n, sh: s.enter_context(nc.sbuf_tensor(f"{tag}_{n}", sh, F32))
        xsum = sb("xsum", [P, 2, G])
        sq = sb("sq", [P, 2, C, G])
        sqsum = sb("sqsum", [P, 2, G])
        lnv = sb("lnv", [P, 2, G])
        rstd = sb("rstd", [P, 2, G])
        mean_ps = s.enter_context(nc.psum_tensor(f"{tag}_mean", [P, 2, G], F32))
        var_ps = s.enter_context(nc.psum_tensor(f"{tag}_var", [P, 2, G], F32))
        with semaphores(nc, tag, "xsum", "mean", "centred", "squares", "sqsum", "var",
                        "lnv", "rstd", "scaled") as (
                xsum_ready, mean_ready, centred, squares, sqsum_ready, var_ready,
                lnv_ready, rstd_ready, scaled), nc.Block(no_gpsimd_drain=True) as block:

            @block.gpsimd
            def _(pool):
                for g in range(NG):
                    if g >= 2:
                        pool.wait_ge(mean_ready, g - 1)
                    nc.gpsimd.tensor_tensor(xsum[:, g % 2], src(0, g), src(1, g),
                                            ALU.add).then_inc(xsum_ready, 1)

            @block.tensor
            def _(pe):
                def mean(g):
                    pe.wait_ge(xsum_ready, g + 1)
                    if g >= 2:
                        pe.wait_ge(centred, g - 1)
                    nc.tensor.matmul(mean_ps[:, g % 2], K.mean_w[:, :], xsum[:, g % 2],
                                     start=True, stop=True).then_inc(mean_ready, 1)

                def var(g):
                    pe.wait_ge(sqsum_ready, g + 1)
                    if g >= 2:
                        pe.wait_ge(lnv_ready, g - 1)
                    nc.tensor.matmul(var_ps[:, g % 2], K.mean_w[:, :], sqsum[:, g % 2],
                                     start=True, stop=True).then_inc(var_ready, 1)
                for g in range(NG):
                    mean(g)
                    if g:
                        var(g - 1)
                var(NG - 1)

            @block.vector
            def _(dve):
                def centre(g):
                    dve.wait_ge(mean_ready, g + 1)
                    for c in range(C):
                        last = nc.vector.tensor_tensor(XN[:, c, g * G:(g + 1) * G], src(c, g),
                                                       mean_ps[:, g % 2], ALU.subtract)
                    last.then_inc(centred, 1)

                def sum_squares(g):
                    dve.wait_ge(squares, g + 1)
                    if g >= 2:
                        dve.wait_ge(var_ready, g - 1)
                    nc.vector.tensor_tensor(sqsum[:, g % 2], sq[:, g % 2, 0], sq[:, g % 2, 1],
                                            ALU.add).then_inc(sqsum_ready, 1)

                def scale(g):
                    dve.wait_ge(rstd_ready, g + 1)
                    for c in range(C):
                        view = XN[:, c, g * G:(g + 1) * G]
                        last = nc.vector.tensor_tensor(view, view, rstd[:, g % 2], ALU.mult)
                        last.then_inc(scaled, 1)
                    if affine is not None:
                        dve.wait_ge(scaled, C * (g + 1))
                        for c in range(C):
                            view = XN[:, c, g * G:(g + 1) * G]
                            nc.vector.tensor_scalar(view, view, affine[0][:, c:c + 1],
                                                    affine[1][:, c:c + 1], ALU.mult, ALU.add)
                for g in range(NG + 2):
                    if g < NG:
                        centre(g)
                    if 1 <= g <= NG:
                        sum_squares(g - 1)
                    if g >= 2:
                        scale(g - 2)

            @block.scalar
            def _(act):
                def square(g):
                    act.wait_ge(centred, g + 1)
                    if g >= 2:
                        act.wait_ge(sqsum_ready, g - 1)
                    nc.scalar.activation(sq[:, g % 2], XN[:, :, g * G:(g + 1) * G],
                                         ACT.Square).then_inc(squares, 1)

                def inverse_std(g):
                    act.wait_ge(var_ready, g + 1)
                    nc.scalar.activation(lnv[:, g % 2], var_ps[:, g % 2], ACT.Ln,
                                         bias=K.eps[:, 0:1]).then_inc(lnv_ready, 1)
                    act.wait_ge(lnv_ready, g + 1)
                    if g >= 2:
                        act.wait_ge(scaled, C * (g - 1))
                    nc.scalar.activation(rstd[:, g % 2], lnv[:, g % 2], ACT.Exp,
                                         scale=-0.5).then_inc(rstd_ready, 1)
                for g in range(NG + 1):
                    if g < NG:
                        square(g)
                    if g:
                        inverse_std(g - 1)


def wide_attention(nc, K, X, XN, ctxT, W, gate, tag, self_key, scale):
    M = E + 1 if self_key else E
    names = ("q", "k", "v")
    with ExitStack() as s:
        sb = lambda n, sh: s.enter_context(nc.sbuf_tensor(f"{tag}_{n}", sh, F32))
        w = {n: sb(f"w{n}", [P, C, D]) for n in names}
        b_col = {n: sb(f"b{n}", [P, C]) for n in names}
        bv_row = sb("bv_row", [P, D])
        kxT = sb("kxT", [P, C, B, E])
        vx = sb("vx", [P, B, D])

        with ExitStack() as s2:
            kx_ps = s2.enter_context(nc.psum_tensor(f"{tag}_kx_ps", [P, C, G], F32))
            vx_ps = s2.enter_context(nc.psum_tensor(f"{tag}_vx_ps", [P, B, G], F32))
            with semaphores(nc, f"{tag}_ctx", "loaded", "zeroed", "products") as (
                    loaded, zeroed, products), \
                    nc.Block(no_gpsimd_drain=True) as block:
                @block.sync
                def _(sp):
                    n = 0
                    for a in names:
                        sp.dma_start(w[a][:, :, :], W[f"w{a}"]).then_inc(loaded, 16)
                        sp.dma_start(b_col[a][:, :], W[f"b{a}"]).then_inc(loaded, 16)
                        n += 32
                    sp.dma_start(bv_row[:, :], W["bv_row"]).then_inc(loaded, 16)
                    sp.wait_ge(loaded, n + 16)

                @block.tensor
                def _(pe):
                    pe.wait_ge(loaded, 16 * 7)
                    for m in range(C):
                        for c in range(C):
                            nc.tensor.matmul(kx_ps[:, m, 0:B * E], w["k"][:, c, m * P:(m + 1) * P],
                                             ctxT[:, c, :], start=(c == 0), stop=(c == C - 1))
                    for b in range(B):
                        for c in range(C):
                            last = nc.tensor.matmul(vx_ps[0:E, b, 0:D], ctxT[:, c, b * E:(b + 1) * E],
                                                    w["v"][:, c, :], start=(c == 0), stop=(c == C - 1))
                    last.then_inc(products, 1)

                @block.vector
                def _(dve):
                    nc.vector.memset(vx[:, :, :], 0.0).then_inc(zeroed, 1)
                    dve.wait_ge(products, 1)
                    dve.wait_ge(zeroed, 1)
                    for m in range(C):
                        nc.vector.tensor_scalar(kxT[:, m].rearrange("p b e -> p (b e)"),
                                                kx_ps[:, m, 0:B * E], b_col["k"][:, m:m + 1], None,
                                                ALU.add)
                    for b in range(B):
                        nc.vector.tensor_tensor(vx[0:E, b], vx_ps[0:E, b, 0:D], bv_row[0:E, :],
                                                ALU.add)

        kg = sb("kg", [P, C, E])
        vg = sb("vg", [P, D])
        q_sb = sb("q", [P, C, G])
        qk_sb = sb("qk", [P, C, G])
        v_sb = sb("v", [P, C, G])
        t_sb = sb("t", [P, C, G])
        prob = sb("prob", [P, TG, M])
        stat = sb("stat", [P, 3, TG])
        pT = sb("pT", [P, G])
        proj_ps = s.enter_context(nc.psum_tensor(f"{tag}_proj", [P, 2, G], F32))
        s_ps = s.enter_context(nc.psum_tensor(f"{tag}_s", [P, TG, P], F32))
        pT_ps = s.enter_context(nc.psum_tensor(f"{tag}_pT_ps", [P, G], F32))
        o_ps = s.enter_context(nc.psum_tensor(f"{tag}_o", [P, C, G], F32))
        p0_ps = s.enter_context(nc.psum_tensor(f"{tag}_p0", [P, G], F32))
        which = [(n, m) for n in (names if self_key else ("q",)) for m in range(C)]

        with nc.Fori(0, B) as b, nc.Fori(0, GB) as h:
            cols = lambda c: X[:, c, ds(b * SP1 + h * G + 1, G)]
            xn = lambda c: XN[:, c, ds(b * S + h * G, G)]
            with semaphores(nc, tag, "staged", "proj", "taken", "scores", "maxed", "exped",
                            "prob", "probT", "pT", "out", "dve", "act") as (
                    staged, proj, taken, scores, maxed, exped, prob_ready, probT, pT_ready,
                    out_ready, dve_own, act_own), nc.Block(no_gpsimd_drain=True) as block:

                @block.tensor
                def _(pe):
                    for i, (n, m) in enumerate(which):
                        if i >= 2:
                            pe.wait_ge(taken, i - 1)
                        for c in range(C):
                            last = nc.tensor.matmul(proj_ps[:, i % 2], w[n][:, c, m * P:(m + 1) * P],
                                                    xn(c), start=(c == 0), stop=(c == C - 1))
                        last.then_inc(proj, 1)
                    pe.wait_ge(taken, len(which))
                    pe.wait_ge(staged, 2)
                    for t in range(TG):
                        tok = slice(t * P, (t + 1) * P)
                        for c in range(C):
                            last = nc.tensor.matmul(s_ps[:, t, 0:E], q_sb[:, c, tok], kg[:, c, :],
                                                    start=(c == 0), stop=(c == C - 1))
                        if self_key:
                            for c in range(C):
                                last = nc.tensor.matmul(s_ps[:, t, E:M], qk_sb[:, c, tok],
                                                        K.ones[:, 0:1], start=(c == 0), stop=(c == C - 1))
                    last.then_inc(scores, 1)
                    for t in range(TG):
                        pe.wait_ge(prob_ready, t + 1)
                        last = nc.tensor.transpose(pT_ps[0:M, t * P:(t + 1) * P], prob[:, t, :],
                                                   K.ident[:, :])
                    last.then_inc(probT, 1)
                    pe.wait_ge(pT_ready, 1)
                    if self_key:
                        nc.tensor.matmul(p0_ps[:, :], K.last_row[0:M, :], pT[0:M, :],
                                         start=True, stop=True)
                    for m in range(C):
                        last = nc.tensor.matmul(o_ps[:, m], vg[0:M, m * P:(m + 1) * P], pT[0:M, :],
                                                start=True, stop=True)
                    last.then_inc(out_ready, 1)

                @block.vector
                def _(dve):
                    own = Own(dve, dve_own)
                    nc.vector.tensor_copy(kg[:, :, :], kxT[:, :, ds(b, 1), :].rearrange(
                        "p c o e -> p (c o) e")).then_inc(staged, 1)
                    nc.vector.tensor_copy(vg[:, :], vx[:, ds(b, 1), :].rearrange(
                        "p o d -> p (o d)")).then_inc(staged, 1)
                    for i, (n, m) in enumerate(which):
                        dve.wait_ge(proj, i + 1)
                        src, bias = proj_ps[:, i % 2], b_col[n][:, m:m + 1]
                        if n == "q":
                            nc.vector.tensor_scalar(q_sb[:, m], src, bias, None, ALU.add).then_inc(taken, 1)
                            dve.wait_ge(taken, i + 1)
                        elif n == "k":
                            nc.vector.scalar_tensor_tensor(out=qk_sb[:, m], in0=src, scalar=bias,
                                                           in1=q_sb[:, m], op0=ALU.add,
                                                           op1=ALU.mult).then_inc(taken, 1)
                        else:
                            nc.vector.tensor_scalar(v_sb[:, m], src, bias, None, ALU.add).then_inc(taken, 1)
                    dve.wait_ge(scores, 1)
                    own(nc.vector.tensor_reduce(stat[:, 0, :], s_ps[:, :, 0:M], AX.X, ALU.max))
                    nc.vector.tensor_scalar(stat[:, 0, :], stat[:, 0, :], -scale, None,
                                            ALU.mult).then_inc(maxed, 1)
                    dve.wait_ge(exped, TG)
                    own(nc.vector.reciprocal(stat[:, 2, :], stat[:, 1, :]))
                    for t in range(TG):
                        nc.vector.tensor_scalar(prob[:, t, :], prob[:, t, :], stat[:, 2, t:t + 1], None,
                                                ALU.mult).then_inc(prob_ready, 1)
                    dve.wait_ge(probT, 1)
                    nc.vector.tensor_copy(pT[0:M, :], pT_ps[0:M, :]).then_inc(pT_ready, 1)
                    dve.wait_ge(out_ready, 1)
                    for m in range(C):
                        src = o_ps[:, m]
                        if self_key:
                            own(nc.vector.tensor_tensor(t_sb[:, m], v_sb[:, m], p0_ps[:, :], ALU.mult))
                            own(nc.vector.tensor_tensor(t_sb[:, m], t_sb[:, m], o_ps[:, m], ALU.add))
                            src = t_sb[:, m]
                        nc.vector.scalar_tensor_tensor(out=cols(m), in0=src, scalar=gate, in1=cols(m),
                                                       op0=ALU.mult, op1=ALU.add)

                @block.scalar
                def _(act):
                    act.wait_ge(maxed, 1)
                    for t in range(TG):
                        nc.scalar.activation(prob[:, t, :], s_ps[:, t, 0:M], ACT.Exp,
                                             bias=stat[:, 0, t:t + 1], scale=scale,
                                             accum_out=stat[:, 1, t:t + 1]).then_inc(exped, 1)


NE, TOPK, FE = 8, 2, 512
FC = FE // P
WE = 2 * C * FE + FC * D


def router(nc, K, XN2, gate_w, w_dram, tag):
    NT = T // P
    with ExitStack() as s:
        sb = lambda n, sh: s.enter_context(nc.sbuf_tensor(f"{tag}_{n}", sh, F32))
        gw = sb("gw", [P, C, NE])
        iota = sb("iota", [P, NE])
        prob = sb("prob", [P, NT, NE])
        rest = sb("rest", [P, NT, NE])
        pick = sb("pick", [P, 2, NT, NE])
        tmp = sb("tmp", [P, NT, NE])
        col = sb("col", [P, 6, NT])
        w9 = sb("w9", [P, NT, NE + 1])
        wT = sb("wT", [P, T])
        lg_ps = s.enter_context(nc.psum_tensor(f"{tag}_lg", [P, NT, NE], F32))
        wT_ps = s.enter_context(nc.psum_tensor(f"{tag}_wT_ps", [P, T], F32))
        full = [P, NT, NE]
        with semaphores(nc, tag, "loaded", "logits", "exped", "maxed", "weights", "turned", "copied",
                        "stored", "own") as (loaded, logits, exped, maxed, weighted, turned, copied,
                                             stored, dve_own), \
                nc.Block(no_gpsimd_drain=True) as block:
            @block.sync
            def _(sp):
                sp.dma_start(gw[:, :, :], gate_w).then_inc(loaded, 16)
                sp.dma_start(iota[:, :], K.expert_iota).then_inc(loaded, 16)
                sp.wait_ge(copied, 1)
                sp.dma_start(w_dram, wT[0:NE + 1, :]).then_inc(stored, 16)
                sp.wait_ge(stored, 16)

            @block.tensor
            def _(pe):
                pe.wait_ge(loaded, 32)
                for t in range(NT):
                    for c in range(C):
                        last = nc.tensor.matmul(lg_ps[:, t, :], XN2[:, c, t * P:(t + 1) * P], gw[:, c, :],
                                                start=(c == 0), stop=(c == C - 1))
                last.then_inc(logits, 1)
                pe.wait_ge(weighted, 1)
                for t in range(NT):
                    last = nc.tensor.transpose(wT_ps[0:NE + 1, t * P:(t + 1) * P], w9[:, t, :],
                                               K.ident[:, :])
                last.then_inc(turned, 1)

            @block.scalar
            def _(act):
                act.wait_ge(maxed, 1)
                nc.scalar.activation(prob[:, :, :], rest[:, :, :], ACT.Exp).then_inc(exped, 1)

            @block.vector
            def _(dve):
                own = Own(dve, dve_own)
                tt, tr, ts = nc.vector.tensor_tensor, nc.vector.tensor_reduce, nc.vector.tensor_scalar
                wide = lambda n: bc(col[:, n, :], 2, full)
                numbers = bc(iota[:, :], 1, full)
                dve.wait_ge(loaded, 32)
                dve.wait_ge(logits, 1)
                own(tr(col[:, 0, :], lg_ps[:, :, :], AX.X, ALU.max))
                tt(rest[:, :, :], lg_ps[:, :, :], wide(0), ALU.subtract).then_inc(maxed, 1)
                dve.wait_ge(exped, 1)
                own(tr(col[:, 1, :], prob[:, :, :], AX.X, ALU.add))
                own(nc.vector.reciprocal(col[:, 1, :], col[:, 1, :]))
                own(tt(prob[:, :, :], prob[:, :, :], wide(1), ALU.mult))
                left = prob
                for n in range(TOPK):
                    own(tr(col[:, 2 + n, :], left[:, :, :], AX.X, ALU.max))
                    own(tt(tmp[:, :, :], left[:, :, :], wide(2 + n), ALU.is_equal))
                    own(tt(tmp[:, :, :], tmp[:, :, :], numbers, ALU.mult))
                    own(tr(col[:, 4, :], tmp[:, :, :], AX.X, ALU.min))
                    own(tt(pick[:, n], numbers, wide(4), ALU.is_equal))
                    if n == 0:
                        own(nc.vector.scalar_tensor_tensor(
                            out=rest[:, :, :], in0=pick[:, 0], scalar=-2.0, in1=prob[:, :, :],
                            op0=ALU.mult, op1=ALU.add))
                        left = rest
                own(tt(col[:, 5, :], col[:, 2, :], col[:, 3, :], ALU.add))
                own(ts(col[:, 5, :], col[:, 5, :], EPS, None, ALU.add))
                own(nc.vector.reciprocal(col[:, 5, :], col[:, 5, :]))
                own(tt(tmp[:, :, :], pick[:, 0], pick[:, 1], ALU.add))
                own(tt(tmp[:, :, :], tmp[:, :, :], prob[:, :, :], ALU.mult))
                own(nc.vector.memset(w9[:, :, NE:NE + 1], 1.0))
                tt(w9[:, :, 0:NE], tmp[:, :, :], wide(5), ALU.mult).then_inc(weighted, 1)
                dve.wait_ge(turned, 1)
                nc.vector.tensor_copy(wT[0:NE + 1, :], wT_ps[0:NE + 1, :]).then_inc(copied, 1)


def split_tokens(nc, XN, XH, XL, tag, n=4):
    size = XN.shape[1] * XN.shape[2] // n
    flat = lambda x: x[:, :, :].rearrange("p c t -> p (c t)")
    with semaphores(nc, tag, "high") as (high,), nc.Block(no_gpsimd_drain=True) as block:
        @block.scalar
        def _(act):
            for i in range(n):
                part = slice(i * size, (i + 1) * size)
                nc.scalar.activation(flat(XH)[:, part], flat(XN)[:, part], ACT.Copy).then_inc(high, 1)

        @block.vector
        def _(dve):
            for i in range(n):
                part = slice(i * size, (i + 1) * size)
                dve.wait_ge(high, i + 1)
                nc.vector.tensor_tensor(flat(XL)[:, part], flat(XN)[:, part],
                                        flat(XH)[:, part].bitcast(F32), ALU.subtract)


def experts(nc, K, X, XH, XL, w_dram, we_dram, gate, tag):
    with ExitStack() as s:
        sb = lambda n, sh, dt=F32: s.enter_context(nc.sbuf_tensor(f"{tag}_{n}", sh, dt))
        raw = sb("raw", [P, 2, WE])
        wh = [sb(f"wh{j}", [P, WE], F32R) for j in range(2)]
        wl = [sb(f"wl{j}", [P, WE], F32R) for j in range(2)]
        share = sb("share", [P, 2, T])
        hg = sb("hg", [P, 2, G])
        hgw = sb("hgw", [P, 2, G])
        hid = sb("hid", [P, 2, G])
        hh = sb("hh", [P, 2, G], F32R)
        hl = sb("hl", [P, 2, G], F32R)
        gu_ps = s.enter_context(nc.psum_tensor(f"{tag}_gu", [P, 2, 2, G], F32))
        y_ps = s.enter_context(nc.psum_tensor(f"{tag}_y", [P, 2, C, G], F32))
        QW = 4
        piece = lambda q: slice(q * WE // QW, (q + 1) * WE // QW)

        def up_w(w, u, c, i):
            first = u * C * FE + c * FE + i * P
            return w[:, first:first + P]

        def down_w(w, i, m):
            first = 2 * C * FE + i * D + m * P
            return w[:, first:first + P]

        with semaphores(nc, f"{tag}_first", "loaded", "high") as (loaded, high), \
                nc.Block(no_gpsimd_drain=True) as block:
            @block.sync
            def _(sp):
                sp.dma_start(share[:, 0, :], w_dram[0:1, :].to_broadcast([P, T])).then_inc(loaded, 16)
                sp.dma_start(raw[:, 0, :], we_dram[0]).then_inc(loaded, 16)
                sp.wait_ge(loaded, 32)

            @block.scalar
            def _(act):
                act.wait_ge(loaded, 32)
                for q in range(QW):
                    nc.scalar.activation(wh[0][:, piece(q)], raw[:, 0, piece(q)], ACT.Copy).then_inc(high, 1)

            @block.vector
            def _(dve):
                for q in range(QW):
                    dve.wait_ge(high, q + 1)
                    nc.vector.tensor_tensor(wl[0][:, piece(q)], raw[:, 0, piece(q)],
                                            wh[0][:, piece(q)].bitcast(F32), ALU.subtract)

        def one_pass(e, both):
            half = NG * FC
            N = half * (2 if both else 1)
            where = lambda k: (k // half, (k % half) // FC, k % FC)
            second_at = {4 + q: q for q in range(QW)}
            next_at = {half + 4 + q: q for q in range(QW)}
            with semaphores(nc, tag, "raw1", "raw0", "share1", "share0", "gu", "silu", "shared", "prod",
                            "high", "low", "y", "added", "wh1", "wl1", "wh0", "down") as (
                    raw1, raw0, share1, share0, gu_ready, silu_ready, shared, prod, high, low,
                    y_ready, added, wh1, wl1, wh0, down_done), \
                    nc.Block(no_gpsimd_drain=True) as block:

                @block.sync
                def _(sp):
                    if not both:
                        return
                    sp.dma_start(raw[:, 1, :], we_dram[ds(e + 1, 1)].rearrange("o p w -> p (o w)")
                                 ).then_inc(raw1, 16)
                    sp.dma_start(share[:, 1, :], w_dram[ds(e + 1, 1), :].to_broadcast([P, T])
                                 ).then_inc(share1, 16)
                    sp.dma_start(raw[:, 0, :], we_dram[ds(e + 2, 1)].rearrange("o p w -> p (o w)")
                                 ).then_inc(raw0, 16)
                    sp.wait_ge(shared, half)
                    sp.dma_start(share[:, 0, :], w_dram[ds(e + 2, 1), :].to_broadcast([P, T])
                                 ).then_inc(share0, 16)
                    sp.wait_ge(share0, 16)
                    sp.wait_ge(raw0, 16)

                @block.tensor
                def _(pe):
                    def up(k):
                        j, g, i = where(k)
                        if k == half:
                            pe.wait_ge(wl1, QW)
                        if k >= 2:
                            pe.wait_ge(prod, k - 1)
                        tok = slice(g * G, (g + 1) * G)
                        for u in range(2):
                            for c in range(C):
                                a = (up_w(wh[j], u, c, i), up_w(wl[j], u, c, i))
                                x = (XH[:, c, tok], XL[:, c, tok])
                                for n, (p, q) in enumerate(((0, 0), (0, 1), (1, 0))):
                                    last = nc.tensor.matmul(gu_ps[:, k % 2, u], a[p], x[q],
                                                            start=(c == 0 and n == 0),
                                                            stop=(c == C - 1 and n == 2))
                        last.then_inc(gu_ready, 1)

                    def down(k):
                        j, g, i = where(k)
                        gg = j * NG + g
                        pe.wait_ge(low, k + 1)
                        if i == 0 and gg >= 2:
                            pe.wait_ge(added, gg - 1)
                        for m in range(C):
                            a = (down_w(wh[j], i, m), down_w(wl[j], i, m))
                            x = (hh[:, k % 2], hl[:, k % 2])
                            for n, (p, q) in enumerate(((0, 0), (0, 1), (1, 0))):
                                last = nc.tensor.matmul(y_ps[:, gg % 2, m], a[p], x[q],
                                                        start=(i == 0 and n == 0),
                                                        stop=(i == FC - 1 and n == 2))
                        last.then_inc(down_done, 1)
                    for k in range(N + 2):
                        if k < N:
                            up(k)
                        if k >= 2:
                            down(k - 2)

                @block.scalar
                def _(act):
                    def silu(k):
                        act.wait_ge(gu_ready, k + 1)
                        if k >= 2:
                            act.wait_ge(shared, k - 1)
                        nc.scalar.activation(hg[:, k % 2], gu_ps[:, k % 2, 0], ACT.Silu).then_inc(silu_ready, 1)

                    def take_high(k):
                        act.wait_ge(prod, k + 1)
                        if k >= 2:
                            act.wait_ge(down_done, k - 1)
                        nc.scalar.activation(hh[:, k % 2], hid[:, k % 2], ACT.Copy).then_inc(high, 1)
                    for k in range(N + 1):
                        if k < N:
                            silu(k)
                        if k:
                            take_high(k - 1)
                        if both and k in second_at:
                            act.wait_ge(raw1, 16)
                            q = piece(second_at[k])
                            nc.scalar.activation(wh[1][:, q], raw[:, 1, q], ACT.Copy).then_inc(wh1, 1)
                        if both and k in next_at:
                            act.wait_ge(raw0, 16)
                            act.wait_ge(down_done, half)
                            q = piece(next_at[k])
                            nc.scalar.activation(wh[0][:, q], raw[:, 0, q], ACT.Copy).then_inc(wh0, 1)

                @block.gpsimd
                def _(pool):
                    for k in range(N):
                        j, g, i = where(k)
                        if k == half:
                            pool.wait_ge(share1, 16)
                        pool.wait_ge(silu_ready, k + 1)
                        if k >= 2:
                            pool.wait_ge(prod, k - 1)
                        nc.gpsimd.tensor_tensor(hgw[:, k % 2], hg[:, k % 2],
                                                share[:, j, g * G:(g + 1) * G], ALU.mult
                                                ).then_inc(shared, 1)

                @block.vector
                def _(dve):
                    def product(k):
                        dve.wait_ge(shared, k + 1)
                        if k >= 2:
                            dve.wait_ge(low, k - 1)
                        nc.vector.tensor_tensor(hid[:, k % 2], gu_ps[:, k % 2, 1], hgw[:, k % 2],
                                                ALU.mult).then_inc(prod, 1)

                    def take_low(k):
                        dve.wait_ge(high, k + 1)
                        if k >= 2:
                            dve.wait_ge(down_done, k - 1)
                        nc.vector.tensor_tensor(hl[:, k % 2], hid[:, k % 2], hh[:, k % 2].bitcast(F32),
                                                ALU.subtract).then_inc(low, 1)

                    def add(gg):
                        dve.wait_ge(down_done, FC * (gg + 1))
                        if gg >= NG:
                            dve.wait_ge(added, gg - NG + 1)
                        g = gg % NG
                        for c in range(C):
                            view = X[:, c, (g // GB) * SP1 + 1 + (g % GB) * G:][:, 0:G]
                            last = nc.vector.scalar_tensor_tensor(out=view, in0=y_ps[:, gg % 2, c],
                                                                  scalar=gate, in1=view,
                                                                  op0=ALU.mult, op1=ALU.add)
                        last.then_inc(added, 1)
                    for k in range(N + 3):
                        if k < N:
                            product(k)
                        if 1 <= k <= N:
                            take_low(k - 1)
                        if k >= 3 and (k - 3) % FC == FC - 1:
                            add((k - 3) // FC)
                        if both and k in second_at:
                            dve.wait_ge(wh1, second_at[k] + 1)
                            q = piece(second_at[k])
                            nc.vector.tensor_tensor(wl[1][:, q], raw[:, 1, q], wh[1][:, q].bitcast(F32),
                                                    ALU.subtract).then_inc(wl1, 1)
                        if both and k in next_at:
                            dve.wait_ge(wh0, next_at[k] + 1)
                            q = piece(next_at[k])
                            nc.vector.tensor_tensor(wl[0][:, q], raw[:, 0, q], wh[0][:, q].bitcast(F32),
                                                    ALU.subtract)

        with nc.Fori(0, NE // 2) as pair:
            one_pass(pair * 2, True)
        one_pass(NE, False)


NH, HD = 16, 16
HC = NH // C
R = 4
MA = E + R
BANK_HEADS = G // E


def head_attention(nc, K, X, XN, ctxT, W, gate, tag, relative):
    with ExitStack() as s:
        sb = lambda n, sh: s.enter_context(nc.sbuf_tensor(f"{tag}_{n}", sh, F32))
        w = {n: sb(f"w{n}", [P, C, D]) for n in "qkvo"}
        b_col = {n: sb(f"b{n}", [P, C]) for n in "qko"}
        bv_row = sb("bv_row", [P, D])
        head_of = sb("head_of", [P, HC])
        head_cols = sb("head_cols", [P, HC, P])
        kT = sb("kT", [P, C, B * E])
        vx = sb("vx", [P, B, D])
        kblk = sb("kblk", [P, C, HC, E])
        vblk = sb("vblk", [P, NH, P])
        if relative:
            rel_k = sb("rel_k", [P, 1 + R])
            rel_v = sb("rel_v", [1 + R, D])
            rel_v0 = sb("rel_v0", [P, D])
            rel_mask = sb("rel_mask", [P, R, E])
            rblk = sb("rblk", [P, HC, R])
            corr = sb("corr", [P, NH, R])
            tmp = sb("tmp", [P, NH, E])

        loads = [(w[n][:, :, :], W[f"w{n}"]) for n in "qkvo"] + [(b_col[n][:, :], W[f"b{n}"]) for n in "qko"]
        loads += [(bv_row[:, :], W["bv_row"]), (head_of[:, :], K.head_of), (head_cols[:, :, :], K.head_cols)]
        if relative:
            loads += [(rel_k[:, :], W["rel_k"]), (rel_v[:, :], W["rel_v"]), (rel_v0[:, :], W["rel_v0"]),
                      (rel_mask[:, :, :], K.rel_mask)]

        with ExitStack() as s2:
            k_ps = s2.enter_context(nc.psum_tensor(f"{tag}_k_ps", [P, C, G], F32))
            v_ps = s2.enter_context(nc.psum_tensor(f"{tag}_v_ps", [P, B, G], F32))
            with semaphores(nc, f"{tag}_ctx", "loaded", "products", "own") as (
                    loaded, products, dve_own), \
                    nc.Block(no_gpsimd_drain=True) as block:
                @block.sync
                def _(sp):
                    for dst, src in loads:
                        sp.dma_start(dst, src).then_inc(loaded, 16)
                    sp.wait_ge(loaded, 16 * len(loads))

                @block.tensor
                def _(pe):
                    pe.wait_ge(loaded, 16 * len(loads))
                    for m in range(C):
                        for c in range(C):
                            nc.tensor.matmul(k_ps[:, m, 0:B * E], w["k"][:, c, m * P:(m + 1) * P],
                                             ctxT[:, c, :], start=(c == 0), stop=(c == C - 1))
                    for b in range(B):
                        for c in range(C):
                            last = nc.tensor.matmul(v_ps[0:E, b, 0:D], ctxT[:, c, b * E:(b + 1) * E],
                                                    w["v"][:, c, :], start=(c == 0), stop=(c == C - 1))
                    last.then_inc(products, 1)

                @block.vector
                def _(dve):
                    own = Own(dve, dve_own)
                    dve.wait_ge(loaded, 16 * len(loads))
                    if relative:
                        own(nc.vector.tensor_scalar(rel_k[:, 1:], rel_k[:, 1:], rel_k[:, 0:1], None,
                                                    ALU.subtract))
                        nc.vector.tensor_tensor(rblk[:, :, :], bc(rel_k[:, 1:], 1, [P, HC, R]),
                                                bc(head_of[:, :], 2, [P, HC, R]), ALU.mult)
                        own(nc.vector.tensor_tensor(rel_v[:, :], rel_v[:, :], rel_v0[0:1 + R, :],
                                                    ALU.subtract))
                        own(nc.vector.tensor_tensor(bv_row[:, :], bv_row[:, :], rel_v0[:, :], ALU.add))
                        for m in range(C):
                            own(nc.vector.tensor_scalar(b_col["k"][:, m:m + 1], b_col["k"][:, m:m + 1],
                                                        rel_k[:, 0:1], None, ALU.add))
                    dve.wait_ge(products, 1)
                    for m in range(C):
                        nc.vector.tensor_scalar(kT[:, m], k_ps[:, m, 0:B * E], b_col["k"][:, m:m + 1],
                                                None, ALU.add)
                    for b in range(B):
                        nc.vector.tensor_tensor(vx[0:E, b], v_ps[0:E, b, 0:D], bv_row[0:E, :], ALU.add)
            if relative:
                with semaphores(nc, f"{tag}_rel", "moved") as (moved,), \
                        nc.Block(no_gpsimd_drain=True) as block:
                    @block.sync
                    def _(sp):
                        for b in range(B):
                            sp.dma_start(vx[E:MA, b, :], rel_v[1:1 + R, :]).then_inc(moved, 16)
                        sp.wait_ge(moved, 16 * B)

        MK = MA if relative else E
        q_sb = sb("q", [P, C, G])
        ctx_sb = sb("ctx", [P, C, G])
        y_sb = sb("y", [P, C, G])
        ex = sb("ex", [P, 2, NH, E])
        prob = sb("prob", [P, 2, NH, MK])
        stat = sb("stat", [P, 2, 3, NH])
        pT = sb("pT", [P, NH, G])
        o_ps = s.enter_context(nc.psum_tensor(f"{tag}_o", [P, C, G], F32))
        s_ps = s.enter_context(nc.psum_tensor(f"{tag}_s", [P, 3, G], F32))
        pT_ps = s.enter_context(nc.psum_tensor(f"{tag}_pT_ps", [P, 2, TG, P], F32))
        pieces = []
        for h0 in range(0, NH, BANK_HEADS):
            h1 = min(h0 + BANK_HEADS, NH)
            for c in range(C):
                a, z = max(h0, c * HC), min(h1, (c + 1) * HC)
                if a < z:
                    pieces.append((h0 // BANK_HEADS, a - h0, a, z - a))
        banks = [(k, h0, min(BANK_HEADS, NH - h0)) for k, h0 in enumerate(range(0, NH, BANK_HEADS))]
        sview = lambda k, n: s_ps[:, k, 0:n * E].rearrange("p (h e) -> p h e", e=E)
        HB = TG
        NB = NH // HB

        with nc.Fori(0, B) as b:
            with nc.Block(no_gpsimd_drain=True) as block:
                @block.vector
                def _(dve):
                    for c in range(C):
                        nc.vector.tensor_tensor(
                            kblk[:, c], kT[:, c, ds(b * E, E)].unsqueeze(1).to_broadcast([P, HC, E]),
                            bc(head_of[:, :], 2, [P, HC, E]), ALU.mult)
                        nc.vector.tensor_tensor(
                            vblk[0:MK, c * HC:(c + 1) * HC, :],
                            vx[0:MK, ds(b, 1), c * P:(c + 1) * P].to_broadcast([MK, HC, P]),
                            head_cols[0:MK, :, :], ALU.mult)
            for h in range(GB):
                first = lambda t: relative and h == 0 and t == 0
                cols = lambda c: X[:, c, ds(b * SP1 + h * G + 1, G)]
                xn = lambda c: XN[:, c, ds(b * S + h * G, G)]
                with semaphores(nc, f"{tag}{h}", "q", "q_taken", "scores", "s_free", "less", "exped",
                                "prob", "zeroed", "turned", "copied", "mixed", "ctx", "y", "corr",
                                "own") as (
                        q_ready, q_taken, scores, s_free, less, exped, prob_ready, zeroed, turned,
                        copied, mixed, ctx_ready, y_ready, corr_ready, dve_own), \
                        nc.Block(no_gpsimd_drain=True) as block:

                    @block.tensor
                    def _(pe):
                        for m in range(C):
                            for c in range(C):
                                last = nc.tensor.matmul(o_ps[:, m], w["q"][:, c, m * P:(m + 1) * P], xn(c),
                                                        start=(c == 0), stop=(c == C - 1))
                            last.then_inc(q_ready, 1)
                        pe.wait_ge(q_taken, C)

                        def score(t):
                            if t:
                                pe.wait_ge(s_free, t)
                            tok = slice(t * P, (t + 1) * P)
                            if first(t):
                                for c in range(C):
                                    last = nc.tensor.matmul(
                                        pT_ps[:, 0, c, 0:HC * R], q_sb[:, c, tok],
                                        rblk[:, :, :].rearrange("p h r -> p (h r)"), start=True, stop=True)
                                last.then_inc(corr_ready, 1)
                            for k, off, h0, n in pieces:
                                c = h0 // HC
                                last = nc.tensor.matmul(
                                    s_ps[:, k, off * E:(off + n) * E], q_sb[:, c, tok],
                                    kblk[:, c, h0 - c * HC:h0 - c * HC + n, :].rearrange("p h e -> p (h e)"),
                                    start=True, stop=True)
                            last.then_inc(scores, 1)

                        def turn(t):
                            pe.wait_ge(prob_ready, t + 1)
                            for n in range(NB):
                                i = t * NB + n
                                if i >= 2:
                                    pe.wait_ge(copied, i - 1)
                                if first(t):
                                    pe.wait_ge(corr_ready, 2)
                                for j in range(HB):
                                    last = nc.tensor.transpose(pT_ps[0:MK, i % 2, j, :],
                                                               prob[:, t % 2, n * HB + j, :], K.ident[:, :])
                                last.then_inc(turned, 1)
                        score(0)
                        for t in range(TG):
                            if t + 1 < TG:
                                score(t + 1)
                            turn(t)
                        pe.wait_ge(copied, TG * NB)
                        for c in range(C):
                            for j in range(HC):
                                last = nc.tensor.matmul(o_ps[:, c], vblk[0:MK, c * HC + j, :],
                                                        pT[0:MK, c * HC + j, :],
                                                        start=(j == 0), stop=(j == HC - 1))
                            last.then_inc(mixed, 1)
                        pe.wait_ge(ctx_ready, C)
                        for m in range(C):
                            for c in range(C):
                                last = nc.tensor.matmul(s_ps[:, m], w["o"][:, c, m * P:(m + 1) * P],
                                                        ctx_sb[:, c], start=(c == 0), stop=(c == C - 1))
                            last.then_inc(y_ready, 1)

                    @block.vector
                    def _(dve):
                        own = Own(dve, dve_own)
                        for m in range(C):
                            dve.wait_ge(q_ready, m + 1)
                            nc.vector.tensor_scalar(q_sb[:, m], o_ps[:, m], b_col["q"][:, m:m + 1],
                                                    HD ** -0.5, ALU.add, ALU.mult).then_inc(q_taken, 1)

                        def less_max(t):
                            dve.wait_ge(scores, t + 1)
                            if first(t):
                                nc.vector.tensor_copy(
                                    corr[:, :, :].rearrange("p (c h) r -> p c (h r)", c=C),
                                    pT_ps[:, 0, 0:C, 0:HC * R]).then_inc(corr_ready, 1)
                                for k, h0, n in banks:
                                    last = nc.vector.tensor_copy(ex[:, 0, h0:h0 + n, :], sview(k, n))
                                last.then_inc(s_free, 1)
                                dve.wait_ge(corr_ready, 2)
                                dve.wait_ge(s_free, 1)
                                for r in range(R):
                                    own(nc.vector.tensor_tensor(
                                        tmp[:, :, :], bc(rel_mask[:, r, :], 1, [P, NH, E]),
                                        corr[:, :, r:r + 1].to_broadcast([P, NH, E]), ALU.mult))
                                    own(nc.vector.tensor_tensor(ex[:, 0], ex[:, 0], tmp[:, :, :], ALU.add))
                                own(nc.vector.tensor_reduce(stat[:, 0, 0, :], ex[:, 0], AX.X, ALU.max))
                                nc.vector.tensor_tensor(ex[:, 0], ex[:, 0],
                                                        bc(stat[:, 0, 0, :], 2, [P, NH, E]),
                                                        ALU.subtract).then_inc(less, 1)
                                return
                            for k, h0, n in banks:
                                last = nc.vector.tensor_reduce(stat[:, t % 2, 0, h0:h0 + n], sview(k, n),
                                                               AX.X, ALU.max)
                            own(last)
                            if t >= 2:
                                dve.wait_ge(exped, t - 1)
                            for k, h0, n in banks:
                                last = nc.vector.tensor_tensor(
                                    ex[:, t % 2, h0:h0 + n, :], sview(k, n),
                                    bc(stat[:, t % 2, 0, h0:h0 + n], 2, [P, n, E]), ALU.subtract)
                            last.then_inc(s_free, 1)
                            dve.wait_ge(s_free, t + 1)
                            nc.vector.nop().then_inc(less, 1)

                        def normalise(t):
                            dve.wait_ge(exped, t + 1)
                            own(nc.vector.tensor_reduce(stat[:, t % 2, 1, :], ex[:, t % 2], AX.X, ALU.add))
                            own(nc.vector.reciprocal(stat[:, t % 2, 2, :], stat[:, t % 2, 1, :]))
                            if t >= 2:
                                dve.wait_ge(turned, NB * (t - 1))
                            out = prob[:, t % 2, :, 0:E]
                            ins = nc.vector.tensor_tensor(out, ex[:, t % 2],
                                                          bc(stat[:, t % 2, 2, :], 2, [P, NH, E]), ALU.mult)
                            if first(t):
                                own(ins)
                                for r in range(R):
                                    own(nc.vector.tensor_tensor(
                                        tmp[:, :, :], bc(rel_mask[:, r, :], 1, [P, NH, E]), out, ALU.mult))
                                    ins = nc.vector.tensor_reduce(prob[:, 0, :, E + r:E + r + 1],
                                                                  tmp[:, :, :], AX.X, ALU.add)
                                    own(ins)
                                nc.vector.nop().then_inc(prob_ready, 1)
                            elif relative:
                                own(ins)
                                nc.vector.memset(prob[:, t % 2, :, E:MA], 0.0).then_inc(prob_ready, 1)
                            else:
                                ins.then_inc(prob_ready, 1)
                        less_max(0)
                        for t in range(TG):
                            if t + 1 < TG:
                                less_max(t + 1)
                            normalise(t)
                        for c in range(C):
                            dve.wait_ge(mixed, c + 1)
                            nc.vector.tensor_copy(ctx_sb[:, c], o_ps[:, c]).then_inc(ctx_ready, 1)
                        for m in range(C):
                            dve.wait_ge(y_ready, m + 1)
                            own(nc.vector.tensor_scalar(y_sb[:, m], s_ps[:, m], b_col["o"][:, m:m + 1],
                                                        gate, ALU.add, ALU.mult))
                            nc.vector.tensor_tensor(cols(m), y_sb[:, m], cols(m), ALU.add)

                    @block.scalar
                    def _(act):
                        def copies(t):
                            for n in range(NB):
                                i = t * NB + n
                                act.wait_ge(turned, i + 1)
                                nc.scalar.activation(
                                    pT[0:MK, n * HB:(n + 1) * HB, t * P:(t + 1) * P],
                                    pT_ps[0:MK, i % 2], ACT.Copy).then_inc(copied, 1)
                        for t in range(TG):
                            act.wait_ge(less, t + 1)
                            nc.scalar.activation(ex[:, t % 2], ex[:, t % 2], ACT.Exp).then_inc(exped, 1)
                            if t:
                                copies(t - 1)
                        copies(TG - 1)


FQ = 768
FQC = FQ // P
QB = 32
ACT_QMAX, ACT_QMIN = 32767.0, -32768.0
W_QMAX, W_QMIN = 7.0, -8.0
U16 = 65536.0
LEAST = 1e-12


def quantised_ffn(nc, K, X, XN, W, gate, tag):
    with ExitStack() as s:
        sb = lambda n, sh: s.enter_context(nc.sbuf_tensor(f"{tag}_{n}", sh, F32))
        wT = [sb("guT", [P, 2, C, FQ]), sb("dT", [P, FQC, D])]
        UP = sb("up", [P, FQC, T])
        GATE = sb("gate", [P, FQC, T])
        sig = sb("sig", [P, 2, T])
        peak = sb("peak", [P, 2, NG * FQC])
        peak_x = sb("peak_x", [P, 1])
        top = sb("top", [P, 4, 2])
        sc = sb("sc", [P, 12])
        SX, RX, SU, RU, SG, RG, SS, RS, SO, RO, SUS, SY = [sc[:, i:i + 1] for i in range(12)]

        with ExitStack() as s2:
            rows_of = (("g", FQC, D), ("u", FQC, D), ("d", C, FQ))
            t = lambda n, sh: s2.enter_context(nc.sbuf_tensor(f"{tag}_{n}", sh, F32))
            raw = [t(f"raw{n}", [P, k * m]) for n, k, m in rows_of]
            NBLK = FQC * D // QB
            wpeak = [t(f"wpeak{n}", [P, 2, NBLK]) for n, _, _ in rows_of]
            t_ps = s2.enter_context(nc.psum_tensor(f"{tag}_t_ps", [P, 4, TG, P], F32))
            turns = []
            for n, (name, k, m) in enumerate(rows_of):
                for j in range(k):
                    for c in range(m // P):
                        dst = (wT[0][:, n, c, j * P:(j + 1) * P] if n < 2 else
                               wT[1][:, c, j * P:(j + 1) * P])
                        turns.append((n, slice(j * m + c * P, j * m + (c + 1) * P), dst))
            with semaphores(nc, f"{tag}_w", "loaded", "quant", "turned", "own", "copied") as (
                    loaded, quant, turned, dve_own, copied), nc.Block(no_gpsimd_drain=True) as block:
                @block.sync
                def _(sp):
                    for n, (name, k, m) in enumerate(rows_of):
                        sp.dma_start(raw[n][:, :], W[f"w{name}"]).then_inc(loaded, 16)
                    sp.wait_ge(loaded, 16 * 3)

                @block.vector
                def _(dve):
                    own = Own(dve, dve_own)
                    dve.wait_ge(loaded, 16 * 3)
                    for n in range(3):
                        blocks = raw[n][:, :].rearrange("p (k w) -> p k w", w=QB)
                        scale, inv = wpeak[n][:, 0, :], wpeak[n][:, 1, :]
                        full = [P, NBLK, QB]
                        own(nc.vector.tensor_reduce(scale, blocks, AX.X, ALU.max, apply_absolute_value=True))
                        own(nc.vector.tensor_scalar(scale, scale, 1.0 / W_QMAX, LEAST, ALU.mult, ALU.max))
                        own(nc.vector.reciprocal(inv, scale))
                        own(nc.vector.tensor_tensor(blocks, blocks, bc(inv, 2, full), ALU.mult))
                        own(nc.vector.tensor_scalar(raw[n][:, :], raw[n][:, :], MAGIC, MAGIC, ALU.add,
                                                    ALU.subtract))
                        own(nc.vector.tensor_scalar(raw[n][:, :], raw[n][:, :], W_QMAX, W_QMIN, ALU.min,
                                                    ALU.max))
                        nc.vector.tensor_tensor(blocks, blocks, bc(scale, 2, full), ALU.mult
                                                ).then_inc(quant, 1)

                @block.tensor
                def _(pe):
                    for i, (n, src, dst) in enumerate(turns):
                        pe.wait_ge(quant, n + 1)
                        if i % TG == 0 and i // TG >= 4:
                            pe.wait_ge(copied, i - 4 * TG + TG)
                        nc.tensor.transpose(t_ps[:, (i // TG) % 4, i % TG, :], raw[n][:, src],
                                            K.ident[:, :]).then_inc(turned, 1)

                @block.scalar
                def _(act):
                    for i, (n, src, dst) in enumerate(turns):
                        act.wait_ge(turned, min((i // TG + 1) * TG, len(turns)))
                        nc.scalar.activation(dst, t_ps[:, (i // TG) % 4, i % TG, :], ACT.Copy
                                             ).then_inc(copied, 1)

        def scale_of(dve, own, dst, inv, peak_ap, least=LEAST):
            own(nc.vector.tensor_scalar(dst, peak_ap, 1.0 / ACT_QMAX, least, ALU.mult, ALU.max))
            own(nc.vector.reciprocal(inv, dst))

        with semaphores(nc, f"{tag}_x", "peaked", "reduced", "own") as (peaked, reduced, dve_own), \
                nc.Block(no_gpsimd_drain=True) as block:
            @block.gpsimd
            def _(pool):
                pool.wait_ge(peaked, 1)
                nc.gpsimd.partition_all_reduce(top[:, 0, 0:1], peak_x[:, :], P, ABSMAX).then_inc(reduced, 1)

            @block.vector
            def _(dve):
                own = Own(dve, dve_own)
                x = XN[:, :, :].rearrange("p c t -> p (c t)")
                nc.vector.tensor_reduce(peak_x[:, :], x, AX.X, ALU.max,
                                        apply_absolute_value=True).then_inc(peaked, 1)
                dve.wait_ge(reduced, 1)
                scale_of(dve, own, SX, RX, top[:, 0, 0:1])
                own(nc.vector.tensor_scalar(x, x, RX, ACT_QMAX, ALU.mult, ALU.min))
                own(nc.vector.tensor_scalar(x, x, ACT_QMIN, MAGIC, ALU.max, ALU.add))
                nc.vector.tensor_scalar(x, x, MAGIC, None, ALU.subtract)

        with ExitStack() as s2:
            gu_ps = s2.enter_context(nc.psum_tensor(f"{tag}_gu_ps", [P, 4, G], F32))
            with nc.Fori(0, NG) as g:
                with semaphores(nc, f"{tag}_gu", "ready", "scaled", "peaked") as (ready, scaled, peaked), \
                        nc.Block(no_gpsimd_drain=True) as block:
                    steps = [(u, i) for i in range(FQC) for u in range(2)]
                    dst = lambda u, i: (GATE, UP)[u][:, i, ds(g * G, G)]

                    @block.tensor
                    def _(pe):
                        for k, (u, i) in enumerate(steps):
                            if k >= 4:
                                pe.wait_ge(scaled, k - 3)
                            for c in range(C):
                                last = nc.tensor.matmul(gu_ps[:, k % 4], wT[0][:, u, c, i * P:(i + 1) * P],
                                                        XN[:, c, ds(g * G, G)], start=(c == 0),
                                                        stop=(c == C - 1))
                            last.then_inc(ready, 1)

                    @block.scalar
                    def _(act):
                        for k, (u, i) in enumerate(steps):
                            act.wait_ge(ready, k + 1)
                            nc.scalar.activation(dst(u, i), gu_ps[:, k % 4], ACT.Copy, scale=SX
                                                 ).then_inc(scaled, 1)

                    @block.vector
                    def _(dve):
                        for k, (u, i) in enumerate(steps):
                            dve.wait_ge(scaled, k + 1)
                            nc.vector.tensor_reduce(peak[:, 1 - u, ds(g * FQC + i, 1)], dst(u, i), AX.X,
                                                    ALU.max, apply_absolute_value=True)

        with semaphores(nc, f"{tag}_e", "peaked", "reduced", "own", "scales", "up", "gateq", "sig",
                        "gated", "pool") as (
                peaked, reduced, dve_own, scales, up_ready, gate_ready, sig_ready, gated, pool_own), \
                nc.Block(no_gpsimd_drain=True) as block:

            @block.gpsimd
            def _(pool):
                own = Own(pool, pool_own)
                for n, w in ((1, 2), (2, 1), (3, 1)):
                    pool.wait_ge(peaked, n)
                    nc.gpsimd.partition_all_reduce(top[:, n, 0:w], (peak[:, :, 0] if n == 1 else
                                                                    peak[:, 0, n:n + 1]),
                                                   P, ABSMAX).then_inc(reduced, 1)
                    if n == 1:
                        pool.wait_ge(scales, 1)
                        for i in range(FQC):
                            u = UP[:, i, :]
                            own(nc.gpsimd.tensor_scalar(u, u, RU, ACT_QMAX, ALU.mult, ALU.min))
                            own(nc.gpsimd.tensor_scalar(u, u, ACT_QMIN, MAGIC, ALU.max, ALU.add))
                            nc.gpsimd.tensor_scalar(u, u, MAGIC, None, ALU.subtract).then_inc(up_ready, 1)

            @block.scalar
            def _(act):
                for i in range(FQC):
                    act.wait_ge(gate_ready, i + 1)
                    if i >= 2:
                        act.wait_ge(gated, i - 1)
                    nc.scalar.activation(sig[:, i % 2], GATE[:, i, :], ACT.Sigmoid).then_inc(sig_ready, 1)

            @block.vector
            def _(dve):
                own = Own(dve, dve_own)
                ts = nc.vector.tensor_scalar
                own(nc.vector.tensor_reduce(sc[:, 0:2], peak[:, :, :], AX.X, ALU.max))
                nc.vector.tensor_copy(peak[:, :, 0], sc[:, 0:2]).then_inc(peaked, 1)
                dve.wait_ge(reduced, 1)
                scale_of(dve, own, SU, RU, top[:, 1, 0:1])
                scale_of(dve, own, SG, RG, top[:, 1, 1:2])
                nc.vector.nop().then_inc(scales, 1)

                def gate_numbers(i):
                    v = GATE[:, i, :]
                    own(ts(v, v, RG, ACT_QMAX, ALU.mult, ALU.min))
                    own(ts(v, v, ACT_QMIN, MAGIC, ALU.max, ALU.add))
                    ts(v, v, MAGIC, SG, ALU.subtract, ALU.mult).then_inc(gate_ready, 1)

                def times_sigmoid(i):
                    v = sig[:, i % 2]
                    dve.wait_ge(sig_ready, i + 1)
                    own(ts(v, v, U16, U16 - 1, ALU.mult, ALU.min))
                    own(ts(v, v, 0.0, MAGIC, ALU.max, ALU.add))
                    own(nc.vector.scalar_tensor_tensor(out=GATE[:, i, :], in0=v, scalar=MAGIC,
                                                       in1=GATE[:, i, :], op0=ALU.subtract, op1=ALU.mult))
                    nc.vector.tensor_reduce(peak[:, 1, 1 + i:2 + i], GATE[:, i, :], AX.X, ALU.max,
                                            apply_absolute_value=True).then_inc(gated, 1)
                gate_numbers(0)
                for i in range(FQC):
                    if i + 1 < FQC:
                        gate_numbers(i + 1)
                    times_sigmoid(i)
                dve.wait_ge(gated, FQC)
                nc.vector.tensor_reduce(peak[:, 0, 2:3], peak[:, 1, 1:1 + FQC], AX.X, ALU.max).then_inc(peaked, 1)
                dve.wait_ge(reduced, 2)
                scale_of(dve, own, SS, RS, top[:, 2, 0:1], LEAST * U16)
                for i in range(FQC):
                    v = GATE[:, i, :]
                    own(ts(v, v, RS, ACT_QMAX, ALU.mult, ALU.min))
                    own(ts(v, v, ACT_QMIN, MAGIC, ALU.max, ALU.add))
                    dve.wait_ge(up_ready, i + 1)
                    own(nc.vector.scalar_tensor_tensor(out=v, in0=v, scalar=MAGIC, in1=UP[:, i, :],
                                                       op0=ALU.subtract, op1=ALU.mult))
                    own(nc.vector.tensor_reduce(peak[:, 1, 1 + i:2 + i], v, AX.X, ALU.max,
                                                apply_absolute_value=True))
                nc.vector.tensor_reduce(peak[:, 0, 3:4], peak[:, 1, 1:1 + FQC], AX.X, ALU.max).then_inc(peaked, 1)
                own(ts(SUS, SS, SU, 1.0 / U16, ALU.mult, ALU.mult))
                dve.wait_ge(reduced, 3)
                own(ts(RO, top[:, 3, 0:1], SUS, None, ALU.mult))
                scale_of(dve, own, SO, RO, RO)
                own(ts(RO, RO, SUS, None, ALU.mult))
                ts(SY, SO, gate, None, ALU.mult)
                for i in range(FQC):
                    v = GATE[:, i, :]
                    own(ts(v, v, RO, ACT_QMAX, ALU.mult, ALU.min))
                    own(ts(v, v, ACT_QMIN, MAGIC, ALU.max, ALU.add))
                    ts(v, v, MAGIC, None, ALU.subtract)

        with ExitStack() as s2:
            y_ps = s2.enter_context(nc.psum_tensor(f"{tag}_y_ps", [P, C, G], F32))
            for b in range(B):
                with nc.Fori(0, GB) as h:
                    with semaphores(nc, f"{tag}_d{b}", "ready") as (ready,), \
                            nc.Block(no_gpsimd_drain=True) as block:
                        @block.tensor
                        def _(pe):
                            for m in range(C):
                                for i in range(FQC):
                                    last = nc.tensor.matmul(y_ps[:, m], wT[1][:, i, m * P:(m + 1) * P],
                                                            GATE[:, i, ds(h * G + b * S, G)],
                                                            start=(i == 0), stop=(i == FQC - 1))
                                last.then_inc(ready, 1)

                        @block.vector
                        def _(dve):
                            for m in range(C):
                                view = X[:, m, ds(h * G + (b * SP1 + 1), G)]
                                dve.wait_ge(ready, m + 1)
                                nc.vector.scalar_tensor_tensor(out=view, in0=y_ps[:, m], scalar=SY, in1=view,
                                                               op0=ALU.mult, op1=ALU.add)


FB = 1024
FBC = FB // P
SPAD = S + 2


def bit_ffn(nc, K, X, XN, W, gate, tag):
    with ExitStack() as s:
        sb = lambda n, sh, dt=F32: s.enter_context(nc.sbuf_tensor(f"{tag}_{n}", sh, dt))
        w_int = [sb("w1i", [P, C * FB], BF16), sb("w2i", [P, FBC * D], BF16)]
        wstat = sb("wstat", [P, 2, 4])
        sy = sb("sy", [P, 1])
        conv = sb("conv", [P, FBC, 3])
        conv_b = sb("conv_b", [P, FBC])
        H = sb("h", [P, FBC, B * SPAD])
        with ExitStack() as s2:
            raw = [s2.enter_context(nc.sbuf_tensor(f"{tag}_raw{n}", [P, C * FB], F32)) for n in range(2)]
            with semaphores(nc, f"{tag}_w", "loaded", "summed", "reduced", "own") as (
                    loaded, summed, reduced, dve_own), nc.Block(no_gpsimd_drain=True) as block:
                @block.sync
                def _(sp):
                    for dst, src in ((raw[0][:, :], W["w1"]), (raw[1][:, :], W["w2"]),
                                     (conv[:, :, :], W["conv_w"]), (conv_b[:, :], W["conv_b"])):
                        sp.dma_start(dst, src).then_inc(loaded, 16)
                    sp.wait_ge(loaded, 64)

                @block.gpsimd
                def _(pool):
                    for n in range(2):
                        pool.wait_ge(summed, n + 1)
                        nc.gpsimd.partition_all_reduce(wstat[:, n, 1:2], wstat[:, n, 0:1], P, RADD
                                                       ).then_inc(reduced, 1)

                @block.vector
                def _(dve):
                    own = Own(dve, dve_own)
                    ts = nc.vector.tensor_scalar
                    dve.wait_ge(loaded, 64)
                    for b in range(B):
                        for side in (0, SPAD - 1):
                            nc.vector.memset(H[:, :, b * SPAD + side:b * SPAD + side + 1], 0.0)
                    for n in range(2):
                        nc.vector.tensor_reduce(wstat[:, n, 0:1], raw[n][:, :], AX.X, ALU.add,
                                                apply_absolute_value=True).then_inc(summed, 1)
                    for n in range(2):
                        dve.wait_ge(reduced, n + 1)
                        own(ts(wstat[:, n, 2:3], wstat[:, n, 1:2], 1.0 / (FB * D), EPS, ALU.mult, ALU.max))
                        own(nc.vector.reciprocal(wstat[:, n, 3:4], wstat[:, n, 2:3]))
                        own(ts(raw[n][:, :], raw[n][:, :], wstat[:, n, 3:4], MAGIC, ALU.mult, ALU.add))
                        own(ts(raw[n][:, :], raw[n][:, :], MAGIC, 1.0, ALU.subtract, ALU.min))
                        own(ts(w_int[n][:, :], raw[n][:, :], -1.0, None, ALU.max))
                    ts(sy[:, :], wstat[:, 1, 2:3], gate, None, ALU.mult)

        peak = sb("peak", [P, G])
        top = sb("top", [P, G])
        scale = sb("scale", [P, G])
        back = sb("back", [P, G])

        def token_scales(own):
            own(nc.vector.tensor_scalar(top[:, :], top[:, :], EPS, None, ALU.max))
            own(nc.vector.reciprocal(scale[:, :], top[:, :]))
            own(nc.vector.tensor_scalar(scale[:, :], scale[:, :], 127.0, None, ALU.mult))
            own(nc.vector.tensor_scalar(back[:, :], top[:, :], 1.0 / 127.0, None, ALU.mult))

        def whole_numbers(own, dst, src, tmp):
            own(nc.vector.tensor_tensor(tmp, src, scale[:, :], ALU.mult))
            own(nc.vector.tensor_scalar(tmp, tmp, MAGIC, MAGIC, ALU.add, ALU.subtract))
            return nc.vector.tensor_scalar(dst, tmp, 127.0, -128.0, ALU.min, ALU.max)

        with ExitStack() as s2:
            x_int = s2.enter_context(nc.sbuf_tensor(f"{tag}_x_int", [P, C, G], BF16))
            tmp = s2.enter_context(nc.sbuf_tensor(f"{tag}_tmp", [P, C, G], F32))
            h_ps = s2.enter_context(nc.psum_tensor(f"{tag}_h_ps", [P, 4, G], F32))
            with nc.Fori(0, B) as b, nc.Fori(0, GB) as h:
                xn = lambda c: XN[:, c, ds(b * S + h * G, G)]
                with semaphores(nc, f"{tag}_1", "sizes", "peaked", "reduced", "x", "h", "taken", "own") as (
                        sizes, peaked, reduced, x_ready, h_ready, taken, dve_own), \
                        nc.Block(no_gpsimd_drain=True) as block:
                    @block.scalar
                    def _(act):
                        for c in range(C):
                            nc.scalar.activation(tmp[:, c], xn(c), ACT.Abs).then_inc(sizes, 1)

                    @block.gpsimd
                    def _(pool):
                        pool.wait_ge(peaked, 1)
                        nc.gpsimd.partition_all_reduce(top[:, :], peak[:, :], P, ABSMAX).then_inc(reduced, 1)

                    @block.vector
                    def _(dve):
                        own = Own(dve, dve_own)
                        dve.wait_ge(sizes, C)
                        nc.vector.tensor_tensor(peak[:, :], tmp[:, 0], tmp[:, 1], ALU.max).then_inc(peaked, 1)
                        dve.wait_ge(reduced, 1)
                        token_scales(own)
                        for c in range(C):
                            whole_numbers(own, x_int[:, c], xn(c), tmp[:, c]).then_inc(x_ready, 1)
                        for i in range(FBC):
                            dve.wait_ge(h_ready, i + 1)
                            nc.vector.scalar_tensor_tensor(out=H[:, i, ds(b * SPAD + h * G + 1, G)],
                                                           in0=h_ps[:, i % 4], scalar=wstat[:, 0, 2:3],
                                                           in1=back[:, :], op0=ALU.mult,
                                                           op1=ALU.mult).then_inc(taken, 1)

                    @block.tensor
                    def _(pe):
                        pe.wait_ge(x_ready, C)
                        for i in range(FBC):
                            if i >= 4:
                                pe.wait_ge(taken, i - 3)
                            for c in range(C):
                                last = nc.tensor.matmul(h_ps[:, i % 4],
                                                        w_int[0][:, c * FB + i * P:c * FB + (i + 1) * P],
                                                        x_int[:, c], start=(c == 0), stop=(c == C - 1))
                            last.then_inc(h_ready, 1)

        with ExitStack() as s2:
            act_sb = s2.enter_context(nc.sbuf_tensor(f"{tag}_act", [P, FBC, G], F32))
            size = s2.enter_context(nc.sbuf_tensor(f"{tag}_size", [P, 2, G], F32))
            a_int = s2.enter_context(nc.sbuf_tensor(f"{tag}_a_int", [P, FBC, G], BF16))
            y_sb = s2.enter_context(nc.sbuf_tensor(f"{tag}_y", [P, C, G], F32))
            y_ps = s2.enter_context(nc.psum_tensor(f"{tag}_y_ps", [P, C, G], F32))
            with nc.Fori(0, B) as b, nc.Fori(0, GB) as h:
                tap = lambda i, j: H[:, i, ds(b * SPAD + h * G + j, G)]
                with semaphores(nc, f"{tag}_2", "conv", "silu", "sizes", "peaked", "reduced", "a", "y", "own") as (
                        conv_ready, silu, sizes, peaked, reduced, a_ready, y_ready, dve_own), \
                        nc.Block(no_gpsimd_drain=True) as block:
                    @block.vector
                    def _(dve):
                        own = Own(dve, dve_own)

                        def widen(i):
                            dve.wait_ge(sizes, i + 1)
                            if i:
                                dve.wait_ge(peaked, i)
                                nc.vector.tensor_tensor(peak[:, :], peak[:, :], size[:, i % 2],
                                                        ALU.max).then_inc(peaked, 1)
                            else:
                                nc.vector.tensor_copy(peak[:, :], size[:, 0]).then_inc(peaked, 1)
                        for i in range(FBC):
                            v = act_sb[:, i]
                            own(nc.vector.tensor_scalar(v, tap(i, 1), conv[:, i, 1:2], conv_b[:, i:i + 1],
                                                        ALU.mult, ALU.add))
                            own(nc.vector.scalar_tensor_tensor(out=v, in0=tap(i, 0), scalar=conv[:, i, 0:1],
                                                               in1=v, op0=ALU.mult, op1=ALU.add))
                            nc.vector.scalar_tensor_tensor(out=v, in0=tap(i, 2), scalar=conv[:, i, 2:3],
                                                           in1=v, op0=ALU.mult, op1=ALU.add
                                                           ).then_inc(conv_ready, 1)
                            if i:
                                widen(i - 1)
                        widen(FBC - 1)
                        dve.wait_ge(reduced, 1)
                        token_scales(own)
                        for i in range(FBC):
                            whole_numbers(own, a_int[:, i], act_sb[:, i], act_sb[:, i]).then_inc(a_ready, 1)
                        for m in range(C):
                            dve.wait_ge(y_ready, m + 1)
                            own(nc.vector.scalar_tensor_tensor(out=y_sb[:, m], in0=y_ps[:, m],
                                                               scalar=sy[:, :], in1=back[:, :],
                                                               op0=ALU.mult, op1=ALU.mult))
                            view = X[:, m, ds(b * SP1 + h * G + 1, G)]
                            nc.vector.tensor_tensor(view, view, y_sb[:, m], ALU.add)

                    @block.scalar
                    def _(act):
                        for i in range(FBC):
                            act.wait_ge(conv_ready, i + 1)
                            nc.scalar.activation(act_sb[:, i], act_sb[:, i], ACT.Silu).then_inc(silu, 1)
                            act.wait_ge(silu, i + 1)
                            if i >= 2:
                                act.wait_ge(peaked, i - 1)
                            nc.scalar.activation(size[:, i % 2], act_sb[:, i], ACT.Abs).then_inc(sizes, 1)

                    @block.gpsimd
                    def _(pool):
                        pool.wait_ge(peaked, FBC)
                        nc.gpsimd.partition_all_reduce(top[:, :], peak[:, :], P, ABSMAX).then_inc(reduced, 1)

                    @block.tensor
                    def _(pe):
                        for m in range(C):
                            for i in range(FBC):
                                if m == 0:
                                    pe.wait_ge(a_ready, i + 1)
                                last = nc.tensor.matmul(y_ps[:, m],
                                                        w_int[1][:, i * D + m * P:i * D + (m + 1) * P],
                                                        a_int[:, i], start=(i == 0), stop=(i == FBC - 1))
                            last.then_inc(y_ready, 1)


DEPTH, LH, LD = 6, 16, 64
INNER = LH * LD
WIN = 64
KEYS = WIN + P
NT = S // P
PAIRS = LH // 2
QK_SCALE = 8.0
MASKED = -1e30
FI = 682
FIC = -(-FI // P)
FIP = FIC * P
WQKV, WO = C * 3 * INNER, PAIRS * D
W1, W2 = C * 2 * FIP, FIC * D
PIECE = (2, 3, 0, 1, 4, 5)
HILO = ((0, 0), (0, 1), (1, 0))


class LayerBuffers:

    def __init__(self, sb):
        self.wa = [sb(f"wa{n}", [P, WQKV + WO], F32R) for n in range(2)]
        self.wf = [sb(f"wf{n}", [P, W1 + W2], F32R) for n in range(2)]
        self.tabs = sb("tabs", [P, 4, NT, LD])
        self.qk = sb("qk", [P, 4, LD])
        self.mask = sb("mask", [P, KEYS])
        self.vec = sb("vec", [P, 2 * C + 2 * FIC + C])

    def wq(self, n, c, first, width):
        return self.wa[n][:, c * 3 * INNER + first:c * 3 * INNER + first + width]

    def wo(self, n, i, first):
        return self.wa[n][:, WQKV + i * D + first:WQKV + i * D + first + P]

    def w1(self, n, c, first):
        return self.wf[n][:, c * 2 * FIP + first:c * 2 * FIP + first + P]

    def w2(self, n, i, first):
        return self.wf[n][:, W1 + i * D + first:W1 + i * D + first + P]


def layer_rows(a, layer, lo=0, n=None):
    n = a.shape[2] if n is None else n
    return a[ds(layer, 1), :, lo:lo + n].rearrange("o p n -> p (o n)")


PIECE_COLS = 512
NWA, NWF = (WQKV + WO) // PIECE_COLS, (W1 + W2) // PIECE_COLS


def fetch_tables(sp, W, A, layer, tabled):
    sp.dma_start(W.tabs[:, :, :, :], A["rotary"]).then_inc(tabled, 16)
    sp.dma_start(W.qk[:, :, :], A["l_qk_scale"][ds(layer, 1)].rearrange("o p a d -> p (o a) d")
                 ).then_inc(tabled, 16)


def fetch_pieces(sp, ring, slots, matrices, layer, loaded, split):
    pieces = [(a, lo) for a in matrices for lo in range(0, a.shape[2], PIECE_COLS)]
    for n, (a, lo) in enumerate(pieces):
        if n >= slots:
            sp.wait_ge(split, n - slots + 1)
        if n:
            sp.wait_ge(loaded, 16 * n)
        sp.dma_start(ring[:, n % slots], layer_rows(a, layer, lo, PIECE_COLS)).then_inc(loaded, 16)
    sp.wait_ge(loaded, 16 * len(pieces))


def scale_tables(nc, pool, W, tabled, scaled):
    pool.wait_ge(tabled, 32)
    for n in range(4):
        nc.gpsimd.tensor_tensor(W.tabs[:, n], W.tabs[:, n], bc(W.qk[:, n, :], 1, [P, NT, LD]),
                                ALU.mult).then_inc(scaled, 1)
    pool.wait_ge(scaled, 4)


def take_high(nc, w, n, raw):
    return nc.scalar.activation(w[0][:, n * PIECE_COLS:(n + 1) * PIECE_COLS], raw, ACT.Copy)


def take_low(nc, w, n, raw):
    part = slice(n * PIECE_COLS, (n + 1) * PIECE_COLS)
    return nc.vector.tensor_tensor(w[1][:, part], raw, w[0][:, part].bitcast(F32), ALU.subtract)


def transformer(nc, K, Z, A):
    with ExitStack() as s:
        W = LayerBuffers(lambda n, sh, dt=F32: s.enter_context(nc.sbuf_tensor(f"layer_{n}", sh, dt)))
        with nc.sbuf_tensor("first_raw", [P, NWA, PIECE_COLS], F32) as raw, \
                semaphores(nc, "first", "tabled", "mask", "loaded", "high", "low", "scaled") as (
                    tabled, masked, loaded, high, low, scaled), nc.Block(no_gpsimd_drain=True) as block:
            @block.sync
            def _(sp):
                sp.dma_start(W.mask[:, :], A["band_mask"]).then_inc(masked, 16)
                fetch_tables(sp, W, A, 0, tabled)
                third = WQKV // 3
                for n in range(4):
                    if n:
                        sp.wait_ge(loaded, 16 * n)
                    src = layer_rows(A["l_wqkv"], 0, n * third, third) if n < 3 else layer_rows(A["l_wo"], 0)
                    sp.dma_start(raw[:, 4 * n:4 * n + 4].rearrange("p a n -> p (a n)"), src
                                 ).then_inc(loaded, 16)
                sp.wait_ge(masked, 16)

            @block.gpsimd
            def _(pool):
                scale_tables(nc, pool, W, tabled, scaled)

            @block.scalar
            def _(act):
                for n in range(NWA):
                    act.wait_ge(loaded, 16 * (n // 4 + 1))
                    take_high(nc, W.wa, n, raw[:, n]).then_inc(high, 1)

            @block.vector
            def _(dve):
                for n in range(NWA):
                    dve.wait_ge(high, n + 1)
                    take_low(nc, W.wa, n, raw[:, n])
        with nc.Fori(0, DEPTH) as layer:
            local_attention(nc, K, Z, A, W, layer, "la")
            layer_ffn(nc, K, Z, A, W, layer, "lf")


def local_attention(nc, K, Z, A, W, layer, tag):
    NA = B * NT
    FIRST_W = 2
    with ExitStack() as s:
        sb = lambda n, sh, dt=F32: s.enter_context(nc.sbuf_tensor(f"{tag}_{n}", sh, dt))
        xs = [sb(f"xs{n}", [P, 2, C, P], F32R) for n in range(2)]
        sq = sb("sq", [P, 2, 512])
        rb = sb("rb", [P, 2, 512])
        rot = sb("rot", [P, 2, INNER])
        ssq = sb("ssq", [P, 2, 2 * LH])
        rn = sb("rn", [P, 2, LH])
        minus_half = sb("minus_half", [P, 2 * LH])
        sc8 = sb("sc8", [P, 2, LH])
        qT = sb("qT", [P, PAIRS, P])
        kT = sb("kT", [P, PAIRS, KEYS])
        vt = sb("vt", [P, 3, INNER])
        pr = sb("pr", [P, 2, WIN + 4 * KEYS])
        mx = sb("mx", [P, 2, LH])
        nb = sb("nb", [P, 2, LH])
        sums = sb("sums", [P, 2, LH])
        rs = sb("rs", [P, 2, LH])
        pTa = sb("pTa", [P, 2, 4, P])
        pTb = sb("pTb", [P, 2, 4, P])
        raw = sb("raw", [P, 1, PIECE_COLS])
        o_sb = sb("o", [P, INNER])
        oT = [sb(f"oT{n}", [P, PAIRS, 2 * P], F32R) for n in range(2)]
        ps = lambda n, sh: s.enter_context(nc.psum_tensor(f"{tag}_{n}", sh, F32))
        proj_ps, s_ps = ps("proj_ps", [P, 2, 512]), ps("s_ps", [P, 2, 512])
        pTa_ps, pTb_ps = ps("pTa_ps", [P, 4, P]), ps("pTb_ps", [P, 4, P])
        o_ps, t_ps = ps("o_ps", [P, 512]), ps("t_ps", [P, 4, P])

        def pcols(n, i, lo, hi=KEYS):
            return pr[:, n % 2, WIN + i * KEYS + lo:WIN + i * KEYS + hi]

        def steps(t):
            p, n = t - 1, t + 1
            y = p % 2 == 1
            seq = [("S", t, 0), ("TQ", t, 1), ("less", t, 0), ("xh", n + 1, 0), ("tq", t, 1), ("PT", p, 3),
                   ("copy", p, 3), ("exp", t, 0), ("J", n, 0), ("sq", n, 0), ("PV", p, 3), ("exp", t, 1),
                   ("rot", n, 0), ("xl", n + 1, 0), ("J", n, 1), ("out", p, 1),
                   ("S", t, 1), ("TO", p, 0), ("sq", n, 1), ("less", t, 1), ("to", p, 0), ("PT", t, 0),
                   ("copy", t, 0), ("exp", t, 2), ("rot", n, 1), ("J", n, 2), ("TO", p, 1), ("to", p, 1),
                   ("sq", n, 2), ("PV", t, 0), ("exp", t, 3), ("rot", n, 2), ("J", n, 3),
                   ("S", t, 2), ("sq", n, 3), ("less", t, 2), ("PT", t, 1)]
            seq += [("Y", p, 0)] * y
            seq += [("copy", t, 1), ("exp", t, 4), ("rot", n, 3), ("J", n, 4), ("PV", t, 1)] \
                + [("yadd", p, 0)] * y
            seq += [("v", n, 4), ("exp", t, 5), ("out", t, 0)]
            seq += [("Y", p, 1)] * y
            seq += [("S", t, 3), ("TK", n, 0), ("halo", n, 0)] + [("yadd", p, 1)] * y
            seq += [("tk", n, 0), ("less", t, 3), ("PT", t, 2), ("halo", n, 1), ("copy", t, 2), ("TK", n, 1),
                    ("tk", n, 1), ("J", n, 5), ("exp", t, 6), ("TQ", n, 0), ("tq", n, 0), ("PV", t, 2),
                    ("v", n, 5), ("exp", t, 7)]
            if FIRST_W <= t < FIRST_W + NWF:
                seq += [("wh", t, 0), ("wl", t, 0)]
            return seq
        z, p = NA - 1, NA - 2
        last_steps = [
            ("S", z, 0), ("TQ", z, 1), ("less", z, 0), ("tq", z, 1), ("PT", p, 3), ("copy", p, 3),
            ("exp", z, 0), ("exp", z, 1), ("S", z, 1), ("PV", p, 3), ("less", z, 1), ("out", p, 1),
            ("TO", p, 0), ("to", p, 0), ("PT", z, 0), ("copy", z, 0), ("exp", z, 2), ("exp", z, 3),
            ("S", z, 2), ("PV", z, 0), ("less", z, 2), ("TO", p, 1), ("to", p, 1), ("PT", z, 1),
            ("copy", z, 1), ("exp", z, 4), ("exp", z, 5), ("S", z, 3), ("PV", z, 1), ("less", z, 3),
            ("out", z, 0), ("PT", z, 2), ("copy", z, 2), ("exp", z, 6), ("exp", z, 7), ("TO", z, 0),
            ("to", z, 0), ("PV", z, 2), ("PT", z, 3), ("copy", z, 3), ("PV", z, 3), ("out", z, 1),
            ("TO", z, 1), ("to", z, 1), ("Y", z, 0), ("yadd", z, 0), ("Y", z, 1), ("yadd", z, 1)]
        order = [x for t in range(-1, z) for x in steps(t) if 0 <= x[1] < NA] + last_steps
        turns = [x for x in order if x[0] in ("TQ", "TK", "TO", "Y")]
        turn_no = {x: n for n, x in enumerate(turns)}
        by_act = {x: sum(y[0] != "Y" for y in turns[:n + 1]) for x, n in turn_no.items()}
        by_dve = {x: sum(y[0] in ("TO", "Y") for y in turns[:n + 1]) for x, n in turn_no.items()}

        def follow(do):
            for name, t, i in order:
                if name in do:
                    do[name](t, i)

        def ztok(c, t, n, shift=0):
            first = (t // NT) * SP1 + (t % NT) * P + 1 - shift
            return Z[:, c, first:first + n]
        with semaphores(nc, tag, "xh", "xl", "proj", "sq", "rot", "v", "ssq", "norm", "pow", "rsum",
                        "kmul", "scores", "less", "exped", "turned", "copied", "pv", "out", "turn",
                        "t_act", "t_dve", "set", "own", "loaded", "vec", "high", "low", "halo") as (
                xh_ok, xl_ok, proj_ok, sq_ok, rot_ok, v_ok, ssq_ok, norm_ok, pow_ok, sum_ok,
                kmul_ok, scores_ok, less_ok, exp_ok, turned_ok, copy_ok, pv_ok, out_ok, turn_ok,
                act_took, dve_took, set_ok, dve_own, loaded, vec_ok, high, low, halo_ok), \
                nc.Block(no_gpsimd_drain=True) as block:

            def wait_turn_bank(eng, use):
                n = turn_no[use]
                if n:
                    prev = turns[n - 1]
                    if by_act[prev]:
                        eng.wait_ge(act_took, by_act[prev])
                    if by_dve[prev]:
                        eng.wait_ge(dve_took, by_dve[prev])

            @block.sync
            def _(sp):
                sp.dma_start(W.vec[:, :], layer_rows(A["l_vec"], layer)).then_inc(vec_ok, 16)
                fetch_pieces(sp, raw, 1, (A["l_w1"], A["l_w2"]), layer, loaded, low)
                sp.wait_ge(vec_ok, 16)

            @block.tensor
            def _(pe):
                def J(t, j):
                    n = 6 * t + j
                    if j == 0:
                        pe.wait_ge(xl_ok, t + 1)
                    if n >= 2:
                        u, i = divmod(n - 2, 6)
                        if i < 4:
                            pe.wait_ge(sq_ok, 4 * u + i + 1)
                            pe.wait_ge(rot_ok, 4 * u + i + 1)
                        else:
                            pe.wait_ge(v_ok, 2 * u + i - 3)
                    first = PIECE[j] * 512
                    for c in range(C):
                        for k, (p, q) in enumerate(HILO):
                            last = nc.tensor.matmul(proj_ps[:, n % 2], xs[p][:, t % 2, c, :],
                                                    W.wq(q, c, first, 512),
                                                    start=(c == 0 and k == 0), stop=(c == C - 1 and k == 2))
                    last.then_inc(proj_ok, 1)

                def TQ(t, half):
                    turn_rotated(("TQ", t, half), 0, t, half)

                def TK(t, half):
                    turn_rotated(("TK", t, half), 1, t, half)

                def turn_rotated(use, which, t, half):
                    if which:
                        pe.wait_ge(kmul_ok, 2 * t + half + 1)
                    else:
                        pe.wait_ge(sum_ok, 4 * t + 2 + half + 1)
                    wait_turn_bank(pe, use)
                    for i in range(4):
                        first = (half * 4 + i) * P
                        last = nc.tensor.transpose(t_ps[:, i, :], rot[:, which, first:first + P],
                                                   K.ident[:, :])
                    last.then_inc(turn_ok, 1)

                def S(t, g):
                    if g % 2 == 0:
                        pe.wait_ge(act_took, by_act[("TQ", t, g // 2)])
                    lo = 0 if t % NT else WIN
                    n = 4 * t + g
                    if n:
                        pe.wait_ge(less_ok, 2 * n)
                    for i in range(2):
                        for par in range(2):
                            rows = slice(par * LD, (par + 1) * LD)
                            last = nc.tensor.matmul(s_ps[:, par, i * KEYS + lo:(i + 1) * KEYS],
                                                    qT[rows, 2 * g + i, :],
                                                    kT[rows, 2 * g + i, lo:KEYS],
                                                    start=True, stop=True)
                    last.then_inc(scores_ok, 1)

                def PT(t, g):
                    n = 4 * t + g
                    pe.wait_ge(exp_ok, 2 * n + 2)
                    if n >= 1:
                        pe.wait_ge(copy_ok, n)
                    for i in range(4):
                        if t % NT:
                            nc.tensor.transpose(pTa_ps[:, i, :], pcols(n, i, -WIN, WIN), K.ident[:, :])
                        last = nc.tensor.transpose(pTb_ps[:, i, :], pcols(n, i, WIN), K.ident[:, :])
                    last.then_inc(turned_ok, 1)

                def PV(t, g):
                    n = 4 * t + g
                    pe.wait_ge(copy_ok, n + 1)
                    if g == 0:
                        pe.wait_ge(v_ok, 2 * (t + 1))
                    if g % 2 == 0 and n >= 2:
                        pe.wait_ge(out_ok, n // 2)
                    for i in range(4):
                        h = 4 * g + i
                        dst = o_ps[:, (h % 8) * LD:(h % 8 + 1) * LD]
                        if t % NT:
                            nc.tensor.matmul(dst, pTa[P - WIN:, n % 2, i, :],
                                             vt[P - WIN:, (t - 1) % 3, h * LD:(h + 1) * LD],
                                             start=True, stop=False)
                        last = nc.tensor.matmul(dst, pTb[:, n % 2, i, :], vt[:, t % 3, h * LD:(h + 1) * LD],
                                                start=t % NT == 0, stop=True)
                    last.then_inc(pv_ok, 1)

                def TO(t, half):
                    pe.wait_ge(out_ok, 2 * t + half + 1)
                    wait_turn_bank(pe, ("TO", t, half))
                    for i in range(4):
                        first = (half * 4 + i) * P
                        last = nc.tensor.transpose(t_ps[:, i, :], o_sb[:, first:first + P], K.ident[:, :])
                    last.then_inc(turn_ok, 1)

                def Y(t, m):
                    wait_turn_bank(pe, ("Y", t, m))
                    for i in range(PAIRS):
                        for k, (p, q) in enumerate(HILO):
                            last = nc.tensor.matmul(
                                t_ps[:, 2 * m:2 * m + 2, :].rearrange("p a n -> p (a n)"),
                                W.wo(p, i, m * P), oT[q][:, i, :],
                                start=(i == 0 and k == 0), stop=(i == PAIRS - 1 and k == 2))
                    last.then_inc(turn_ok, 1)
                follow({"J": J, "TQ": TQ, "TK": TK, "S": S, "PT": PT, "PV": PV, "TO": TO, "Y": Y})

            @block.scalar
            def _(act):
                def xh(t, _=0):
                    if t >= 2:
                        act.wait_ge(proj_ok, 6 * (t - 1))
                    for c in range(C):
                        last = nc.scalar.activation(xs[0][:, t % 2, c, :], ztok(c, t, P, c), ACT.Copy)
                    last.then_inc(xh_ok, 1)

                def square(t, j):
                    n = 6 * t + j
                    act.wait_ge(proj_ok, n + 1)
                    if 4 * t + j >= 2:
                        act.wait_ge(ssq_ok, 4 * t + j - 1)
                    nc.scalar.activation(sq[:, j % 2], proj_ps[:, n % 2], ACT.Square).then_inc(sq_ok, 1)

                def values(t, j):
                    n = 6 * t + j
                    act.wait_ge(proj_ok, n + 1)
                    if j == 4 and t >= 3:
                        act.wait_ge(pv_ok, 4 * (t - 1))
                    nc.scalar.activation(vt[:, t % 3, (j - 4) * 512:(j - 3) * 512], proj_ps[:, n % 2],
                                         ACT.Copy).then_inc(v_ok, 1)

                def TQ(t, half):
                    act.wait_ge(turn_ok, turn_no[("TQ", t, half)] + 1)
                    if t >= 1:
                        act.wait_ge(scores_ok, 4 * (t - 1) + 2 * half + 2)
                    nc.scalar.activation(qT[:, half * 4:half * 4 + 4, :], t_ps[:, :, :],
                                         ACT.Copy).then_inc(act_took, 1)

                def halo(t, half):
                    pairs = slice(half * 4, half * 4 + 4)
                    if t % NT:
                        act.wait_ge(scores_ok, 4 * (t - 1) + 2 * half + 2)
                        nc.scalar.activation(kT[:, pairs, 0:WIN], kT[:, pairs, P:KEYS], ACT.Copy
                                             ).then_inc(halo_ok, 1)

                def TK(t, half):
                    act.wait_ge(turn_ok, turn_no[("TK", t, half)] + 1)
                    if t % NT:
                        act.wait_ge(halo_ok, (t - t // NT - 1) * 2 + half + 1)
                    elif t:
                        act.wait_ge(scores_ok, 4 * (t - 1) + 2 * half + 2)
                    nc.scalar.activation(kT[:, half * 4:half * 4 + 4, WIN:KEYS], t_ps[:, :, :],
                                         ACT.Copy).then_inc(act_took, 1)

                def exp(t, pair):
                    n, half = 4 * t + pair // 2, pair % 2
                    act.wait_ge(less_ok, 8 * t + pair + 1)
                    if pair == 0 and t >= 2:
                        act.wait_ge(out_ok, 2 * (t - 1))
                    lo = 0 if t % NT else WIN
                    for i in (2 * half, 2 * half + 1):
                        h = 2 * pair + i % 2
                        last = nc.scalar.activation(pcols(n, i, lo), pcols(n, i, lo), ACT.Exp,
                                                    bias=nb[:, t % 2, h:h + 1],
                                                    scale=sc8[:, t % 2, h:h + 1],
                                                    accum_out=sums[:, t % 2, h:h + 1])
                    last.then_inc(exp_ok, 1)

                def copy(t, g):
                    n = 4 * t + g
                    act.wait_ge(turned_ok, n + 1)
                    if n >= 2:
                        act.wait_ge(pv_ok, n - 1)
                    if t % NT:
                        nc.scalar.activation(pTa[P - WIN:, n % 2], pTa_ps[P - WIN:], ACT.Copy)
                    nc.scalar.activation(pTb[:, n % 2], pTb_ps[:, :, :], ACT.Copy).then_inc(copy_ok, 1)

                def TO(t, half):
                    use = ("TO", t, half)
                    act.wait_ge(turn_ok, turn_no[use] + 1)
                    if t >= 2 and t % 2 == 0 and half == 0:
                        act.wait_ge(turn_ok, turn_no[("Y", t - 1, 1)] + 1)
                    part = slice((t % 2) * P, (t % 2 + 1) * P)
                    nc.scalar.activation(oT[0][:, half * 4:half * 4 + 4, part], t_ps[:, :, :],
                                         ACT.Copy).then_inc(act_took, 1)

                def weight_high(t, _):
                    act.wait_ge(loaded, 16 * (t - FIRST_W + 1))
                    take_high(nc, W.wf, t - FIRST_W, raw[:, 0]).then_inc(high, 1)
                xh(0)
                follow({"halo": halo, "wh": weight_high, "xh": xh, "sq": square, "v": values, "tq": TQ,
                        "tk": TK, "exp": exp, "copy": copy, "to": TO})

            @block.gpsimd
            def _(pool):
                nc.gpsimd.memset(minus_half[:, :], -0.5).then_inc(set_ok, 1)
                pool.wait_ge(set_ok, 1)
                powers = 0
                for t in range(NA):
                    for which in (1, 0):
                        for half in range(2):
                            j = 2 * (1 - which) + half
                            pool.wait_ge(rot_ok, 4 * t + j + 1)
                            part = rot[:, which, half * 512:(half + 1) * 512]
                            nc.gpsimd.tensor_tensor(part, part, rb[:, j % 2], ALU.add
                                                    ).then_inc(sum_ok, 1)
                        pool.wait_ge(norm_ok, powers + 1)
                        if not which and t >= 2:
                            pool.wait_ge(exp_ok, 8 * (t - 1))
                        dst = rn[:, t % 2, :] if which else sc8[:, t % 2, :]
                        mine = slice(0, LH) if which else slice(LH, 2 * LH)
                        nc.gpsimd.tensor_tensor(dst, ssq[:, t % 2, mine], minus_half[:, 0:LH], ALU.pow
                                                ).then_inc(pow_ok, 1)
                        powers += 1
                        if which:
                            pool.wait_ge(pow_ok, powers)
                            pool.wait_ge(sum_ok, 4 * t + 2)
                            for half in range(2):
                                part = rot[:, 1, half * 512:(half + 1) * 512].rearrange(
                                    "p (h d) -> p h d", d=LD)
                                nc.gpsimd.tensor_tensor(
                                    part, part, bc(rn[:, t % 2, 8 * half:8 * half + 8], 2, [P, 8, LD]),
                                    ALU.mult).then_inc(kmul_ok, 1)

            @block.vector
            def _(dve):
                own = Own(dve, dve_own)
                tt = nc.vector.tensor_tensor

                def xl(t, _=0):
                    dve.wait_ge(xh_ok, t + 1)
                    for c in range(C):
                        last = tt(xs[1][:, t % 2, c, :], ztok(c, t, P, c),
                                  xs[0][:, t % 2, c, :].bitcast(F32), ALU.subtract)
                    last.then_inc(xl_ok, 1)

                def rotate(t, j):
                    n = 6 * t + j
                    table = 2 * (PIECE[j] // 2)
                    dve.wait_ge(sq_ok, 4 * t + j + 1)
                    if 4 * t + j >= 2:
                        dve.wait_ge(sum_ok, 4 * t + j - 1)
                    heads = lambda x: x.rearrange("p (h d) -> p h d", d=LD)
                    which, half = PIECE[j] // 2, j % 2
                    if t:
                        dve.wait_ge(turn_ok, turn_no[("TK" if which else "TQ", t - 1, half)] + 1)
                    src, r = heads(proj_ps[:, n % 2]), heads(rb[:, j % 2])
                    a = heads(rot[:, which, half * 512:(half + 1) * 512])
                    cos, sin = W.tabs[:, table, t % NT, :], W.tabs[:, table + 1, t % NT, :]
                    lo, up = slice(0, LD // 2), slice(LD // 2, LD)
                    tt(a, src, bc(cos, 1, [P, 8, LD]), ALU.mult)
                    tt(r[:, :, lo], src[:, :, up], bc(sin[:, lo], 1, [P, 8, LD // 2]), ALU.mult)
                    tt(r[:, :, up], src[:, :, lo], bc(sin[:, up], 1, [P, 8, LD // 2]), ALU.mult
                       ).then_inc(rot_ok, 1)
                    if j == 0 and t >= 2:
                        dve.wait_ge(pow_ok, 2 * (t - 1))
                    nc.vector.tensor_reduce(ssq[:, t % 2, j * 8:(j + 1) * 8], heads(sq[:, j % 2]),
                                            AX.X, ALU.add).then_inc(ssq_ok, 1)
                    if j % 2:
                        dve.wait_ge(ssq_ok, 4 * t + j + 1)
                        part = ssq[:, t % 2, (j - 1) * 8:(j + 1) * 8]
                        scale = 1.0 if j == 1 else QK_SCALE ** -2
                        nc.vector.tensor_scalar(part, part, scale, LEAST * LEAST * scale, ALU.mult,
                                                ALU.max).then_inc(norm_ok, 1)

                def less(t, g):
                    n = 4 * t + g
                    if n >= 2:
                        dve.wait_ge(turned_ok, n - 1)
                    lo = 0 if t % NT else WIN
                    for i in range(2):
                        h = 4 * g + 2 * i
                        dve.wait_ge(scores_ok, n + 1)
                        for par in range(2):
                            ins = nc.vector.tensor_tensor_reduce(
                                pcols(n, 2 * i + par, lo),
                                s_ps[:, par, i * KEYS + lo:(i + 1) * KEYS], W.mask[:, lo:], 1.0,
                                3.0 * MASKED, ALU.add, ALU.max, mx[:, t % 2, h + par:h + par + 1])
                        own(ins)
                        if g == 0 and i == 0:
                            dve.wait_ge(pow_ok, 2 * t + 2)
                        nc.vector.scalar_tensor_tensor(
                            out=nb[:, t % 2, h:h + 2], in0=mx[:, t % 2, h:h + 2], scalar=-1.0,
                            in1=sc8[:, t % 2, h:h + 2], op0=ALU.mult, op1=ALU.mult).then_inc(less_ok, 1)

                def outputs(t, half):
                    heads = slice(8 * half, 8 * half + 8)
                    dve.wait_ge(pv_ok, 4 * t + 2 * half + 2)
                    own(nc.vector.reciprocal(rs[:, t % 2, heads], sums[:, t % 2, heads]))
                    if t:
                        dve.wait_ge(turn_ok, turn_no[("TO", t - 1, half)] + 1)
                    tt(o_sb[:, half * 512:(half + 1) * 512].rearrange("p (h d) -> p h d", d=LD),
                       o_ps[:, :].rearrange("p (h d) -> p h d", d=LD),
                       bc(rs[:, t % 2, heads], 2, [P, 8, LD]), ALU.mult).then_inc(out_ok, 1)

                def TO(t, half):
                    use = ("TO", t, half)
                    dve.wait_ge(act_took, by_act[use])
                    part = slice((t % 2) * P, (t % 2 + 1) * P)
                    four = slice(half * 4, half * 4 + 4)
                    tt(oT[1][:, four, part], t_ps[:, :, :], oT[0][:, four, part].bitcast(F32),
                       ALU.subtract).then_inc(dve_took, 1)

                def add(t, m):
                    dve.wait_ge(turn_ok, turn_no[("Y", t, m)] + 1)
                    view = ztok(m, t - 1, 2 * P)
                    tt(view, view, t_ps[:, 2 * m:2 * m + 2, :].rearrange("p a n -> p (a n)"), ALU.add
                       ).then_inc(dve_took, 1)

                def weight_low(t, _):
                    dve.wait_ge(high, t - FIRST_W + 1)
                    take_low(nc, W.wf, t - FIRST_W, raw[:, 0]).then_inc(low, 1)
                nc.vector.memset(pr[:, :, 0:WIN], 0.0)
                xl(0)
                follow({"wl": weight_low, "xl": xl, "rot": rotate, "less": less, "out": outputs, "to": TO, "yadd": add})


def layer_ffn(nc, K, Z, A, W, layer, tag):
    vec = W.vec
    LNG, LNB, B1, B2 = vec[:, 0:C], vec[:, C:2 * C], vec[:, 2 * C:2 * C + 2 * FIC], vec[:, 2 * C + 2 * FIC:]
    N = NG * FIC
    SLOTS = 4
    FIRST_W = 4
    with ExitStack() as s:
        sb = lambda n, sh, dt=F32: s.enter_context(nc.sbuf_tensor(f"{tag}_{n}", sh, dt))
        xsum, sqsum, lnv, rstd = (sb(n, [P, G]) for n in ("xsum", "sqsum", "lnv", "rstd"))
        sq = sb("sq", [P, C, G])
        xn = sb("xn", [P, C, G])
        xh = sb("xh", [P, 2, C, G], F32R)
        xl = sb("xl", [P, 2, C, G], F32R)
        raw = sb("raw", [P, SLOTS, PIECE_COLS])
        hg = sb("hg", [P, 2, G])
        hid = sb("hid", [P, 2, G])
        hh = sb("hh", [P, 2, G], F32R)
        hl = sb("hl", [P, 2, G], F32R)
        gu_ps = s.enter_context(nc.psum_tensor(f"{tag}_gu", [P, 2, 2, G], F32))
        y_ps = s.enter_context(nc.psum_tensor(f"{tag}_y", [P, C, G], F32))
        mean_ps = s.enter_context(nc.psum_tensor(f"{tag}_mean", [P, G], F32))
        var_ps = s.enter_context(nc.psum_tensor(f"{tag}_var", [P, G], F32))

        def tokens(c, g, shift=0):
            first = (g // GB) * SP1 + 1 + (g % GB) * G - shift
            return Z[:, c, first:first + G]

        def at(g, chunk):
            return (g - 1) * FIC + chunk
        with semaphores(nc, tag, "xsum", "mean", "centred", "squares", "sqsum", "var", "lnv", "rstd",
                        "scaled", "xn", "xh", "xl", "gu", "gelu", "prod", "high", "low", "down", "added",
                        "tabled", "loaded", "w_high", "w_low", "tab_scaled") as (
                xsum_ready, mean_ready, centred, squares, sqsum_ready, var_ready, lnv_ready, rstd_ready,
                scaled, xn_ready, xh_ready, xl_ready, gu_ready, gelu_ready, prod, high, low, down_done,
                added, tabled, loaded, w_high, w_low, tab_scaled), \
                nc.Block(no_gpsimd_drain=True) as block:

            @block.sync
            def _(sp):
                fetch_tables(sp, W, A, layer + 1, tabled)
                fetch_pieces(sp, raw, SLOTS, (A["l_wqkv"], A["l_wo"]), layer + 1, loaded, w_low)

            @block.gpsimd
            def _(pool):
                for g in range(NG):
                    if g:
                        pool.wait_ge(mean_ready, g)
                    nc.gpsimd.tensor_tensor(xsum[:, :], tokens(0, g), tokens(1, g, 1), ALU.add
                                            ).then_inc(xsum_ready, 1)
                    if g == 0:
                        scale_tables(nc, pool, W, tabled, tab_scaled)

            @block.tensor
            def _(pe):
                def mean(g):
                    pe.wait_ge(xsum_ready, g + 1)
                    if g:
                        pe.wait_ge(centred, g)
                    nc.tensor.matmul(mean_ps[:, :], K.mean_w[:, :], xsum[:, :], start=True, stop=True
                                     ).then_inc(mean_ready, 1)

                def var(g):
                    pe.wait_ge(sqsum_ready, g + 1)
                    if g:
                        pe.wait_ge(lnv_ready, g)
                    nc.tensor.matmul(var_ps[:, :], K.mean_w[:, :], sqsum[:, :], start=True, stop=True
                                     ).then_inc(var_ready, 1)

                def up(k):
                    g, i = divmod(k, FIC)
                    if i == 0:
                        pe.wait_ge(xl_ready, g + 1)
                    if k >= 2:
                        pe.wait_ge(prod, k - 1)
                    for u in range(2):
                        first = u * FIP + i * P
                        for c in range(C):
                            x = (xh[:, g % 2, c], xl[:, g % 2, c])
                            for n, (p, q) in enumerate(HILO):
                                last = nc.tensor.matmul(gu_ps[:, k % 2, u], W.w1(p, c, first), x[q],
                                                        start=(c == 0 and n == 0), stop=(c == C - 1 and n == 2))
                    last.then_inc(gu_ready, 1)

                def down(k):
                    g, i = divmod(k, FIC)
                    pe.wait_ge(low, k + 1)
                    if i == 0 and g:
                        pe.wait_ge(added, g)
                    for m in range(C):
                        x = (hh[:, k % 2], hl[:, k % 2])
                        for n, (p, q) in enumerate(HILO):
                            last = nc.tensor.matmul(y_ps[:, m], W.w2(p, i, m * P), x[q],
                                                    start=(i == 0 and n == 0), stop=(i == FIC - 1 and n == 2))
                    last.then_inc(down_done, 1)
                mean(0)
                var(0)
                for k in range(N + 2):
                    if k < N:
                        up(k)
                    if k >= 2:
                        down(k - 2)
                    for g in range(1, NG):
                        if k == at(g, 0):
                            mean(g)
                        if k == at(g, 2):
                            var(g)

            @block.scalar
            def _(act):
                def square(g):
                    act.wait_ge(centred, g + 1)
                    if g:
                        act.wait_ge(sqsum_ready, g)
                    nc.scalar.activation(sq[:, :, :], xn[:, :, :], ACT.Square).then_inc(squares, 1)

                def inverse_std(g):
                    act.wait_ge(var_ready, g + 1)
                    nc.scalar.activation(lnv[:, :], var_ps[:, :], ACT.Ln, bias=K.eps[:, 0:1]
                                         ).then_inc(lnv_ready, 1)
                    act.wait_ge(lnv_ready, g + 1)
                    if g:
                        act.wait_ge(scaled, g)
                    nc.scalar.activation(rstd[:, :], lnv[:, :], ACT.Exp, scale=-0.5).then_inc(rstd_ready, 1)

                def x_high(g):
                    act.wait_ge(xn_ready, g + 1)
                    if g >= 2:
                        act.wait_ge(gu_ready, FIC * (g - 1))
                    nc.scalar.activation(xh[:, g % 2], xn[:, :, :], ACT.Copy).then_inc(xh_ready, 1)

                def gelu(k):
                    i = k % FIC
                    act.wait_ge(gu_ready, k + 1)
                    if k >= 2:
                        act.wait_ge(prod, k - 1)
                    nc.scalar.activation(hg[:, k % 2], gu_ps[:, k % 2, 1], ACT.Gelu,
                                         bias=B1[:, FIC + i:FIC + i + 1]).then_inc(gelu_ready, 1)

                def hidden_high(k):
                    act.wait_ge(prod, k + 1)
                    if k >= 2:
                        act.wait_ge(down_done, k - 1)
                    nc.scalar.activation(hh[:, k % 2], hid[:, k % 2], ACT.Copy).then_inc(high, 1)
                square(0)
                inverse_std(0)
                x_high(0)
                for k in range(N + 1):
                    if k < N:
                        gelu(k)
                    if k:
                        hidden_high(k - 1)
                    for g in range(1, NG):
                        if k == at(g, 0):
                            square(g)
                        if k == at(g, 2):
                            inverse_std(g)
                        if k == at(g, 4):
                            x_high(g)
                    n = k - FIRST_W
                    if 0 <= n < NWA:
                        act.wait_ge(loaded, 16 * (n + 1))
                        take_high(nc, W.wa, n, raw[:, n % SLOTS]).then_inc(w_high, 1)

            @block.vector
            def _(dve):
                tt = nc.vector.tensor_tensor

                def centre(g):
                    dve.wait_ge(mean_ready, g + 1)
                    if g:
                        dve.wait_ge(xl_ready, g)
                    for c in range(C):
                        last = tt(xn[:, c], tokens(c, g, c), mean_ps[:, :], ALU.subtract)
                    last.then_inc(centred, 1)

                def sum_squares(g):
                    dve.wait_ge(squares, g + 1)
                    if g:
                        dve.wait_ge(var_ready, g)
                    tt(sqsum[:, :], sq[:, 0], sq[:, 1], ALU.add).then_inc(sqsum_ready, 1)

                def scale(g):
                    dve.wait_ge(rstd_ready, g + 1)
                    tt(xn[:, :, :], xn[:, :, :], bc(rstd[:, :], 1, [P, C, G]), ALU.mult).then_inc(scaled, 1)
                    dve.wait_ge(scaled, g + 1)
                    for c in range(C):
                        last = nc.vector.tensor_scalar(xn[:, c], xn[:, c], LNG[:, c:c + 1], LNB[:, c:c + 1],
                                                       ALU.mult, ALU.add)
                    last.then_inc(xn_ready, 1)

                def x_low(g):
                    dve.wait_ge(xh_ready, g + 1)
                    if g >= 2:
                        dve.wait_ge(gu_ready, FIC * (g - 1))
                    tt(xl[:, g % 2], xn[:, :, :], xh[:, g % 2].bitcast(F32), ALU.subtract
                       ).then_inc(xl_ready, 1)

                def product(k):
                    i = k % FIC
                    dve.wait_ge(gelu_ready, k + 1)
                    if k >= 2:
                        dve.wait_ge(low, k - 1)
                    nc.vector.scalar_tensor_tensor(out=hid[:, k % 2], in0=gu_ps[:, k % 2, 0],
                                                   scalar=B1[:, i:i + 1], in1=hg[:, k % 2], op0=ALU.add,
                                                   op1=ALU.mult).then_inc(prod, 1)

                def hidden_low(k):
                    dve.wait_ge(high, k + 1)
                    if k >= 2:
                        dve.wait_ge(down_done, k - 1)
                    tt(hl[:, k % 2], hid[:, k % 2], hh[:, k % 2].bitcast(F32), ALU.subtract
                       ).then_inc(low, 1)

                def add(g):
                    dve.wait_ge(down_done, FIC * (g + 1))
                    for c in range(C):
                        last = nc.vector.scalar_tensor_tensor(out=tokens(c, g), in0=y_ps[:, c],
                                                              scalar=B2[:, c:c + 1], in1=tokens(c, g),
                                                              op0=ALU.add, op1=ALU.add)
                    last.then_inc(added, 1)
                centre(0)
                sum_squares(0)
                scale(0)
                x_low(0)
                for k in range(N + 3):
                    if k >= 3 and (k - 2) % FIC == 0:
                        add((k - 2) // FIC - 1)
                    if k < N:
                        product(k)
                    if 1 <= k <= N:
                        hidden_low(k - 1)
                    for g in range(1, NG):
                        if k == at(g, 0):
                            centre(g)
                        if k == at(g, 1):
                            sum_squares(g)
                        if k == at(g, 3):
                            scale(g)
                        if k == at(g, 4):
                            x_low(g)
                    n = k - FIRST_W - 1
                    if 0 <= n < NWA:
                        dve.wait_ge(w_high, n + 1)
                        take_low(nc, W.wa, n, raw[:, n % SLOTS]).then_inc(w_low, 1)


def flamingo(nc, A, out_x):
    with ExitStack() as s:
        sb = lambda n, sh: s.enter_context(nc.sbuf_tensor(n, sh, F32))
        X = sb("X", [P, C, B * SP1])
        gates = sb("gates", [P, 8])
        before_transformer = s.enter_context(ExitStack())
        early = lambda n, sh: before_transformer.enter_context(nc.sbuf_tensor(n, sh, F32))
        K = Constants(sb, early, A)
        ctxT = early("ctxT", [P, C, B * E])
        start_loaded = s.enter_context(nc.semaphore("start_loaded"))
        stored = s.enter_context(nc.semaphore("stored"))

        with semaphores(nc, "start", "filled") as (filled,), nc.Block() as block:
            @block.sync
            def _(sp):
                for b in range(B):
                    sp.dma_start(X[:, :, b * SP1 + 1:(b + 1) * SP1],
                                 A["xT"].rearrange("(c p) (b t) -> p c b t", p=P, b=B)[:, :, b]
                                 ).then_inc(start_loaded, 16)
                sp.dma_start(K.ident[:, :], A["ident"]).then_inc(start_loaded, 16)
                sp.dma_start(ctxT[:, :, :], A["ctxT"].rearrange("(c p) t -> p c t", p=P)
                             ).then_inc(start_loaded, 16)
                sp.dma_start(gates[:, 0:4], A["g_xattn"].partition_broadcast(P)).then_inc(start_loaded, 16)
                sp.dma_start(gates[:, 4:8], A["g_ffn"].partition_broadcast(P)).then_inc(start_loaded, 16)
                sp.dma_start(K.last_row[0:E + 1, :], A["last_row"]).then_inc(start_loaded, 16)
                sp.wait_ge(start_loaded, 16 * 7)

            @block.scalar
            def _(act):
                act.wait_ge(start_loaded, 16 * 7)
                nc.scalar.activation(gates[:, :], gates[:, :], ACT.Tanh)

            @block.vector
            def _(dve):
                for b in range(B):
                    nc.vector.memset(X[:, :, b * SP1:b * SP1 + 1], 0.0)
                nc.vector.memset(K.mean_w[:, :], 1.0 / D)
                nc.vector.memset(K.ones[:, :], 1.0)
                nc.vector.memset(K.eps[:, :], EPS)

        kept = nc.dram_tensor("kept", (P, C, B * SP1), F32).ap()

        def tokens(c, g):
            first = (g // GB) * SP1 + 1 + (g % GB) * G
            return X[:, c, first:first + G]

        def weights(prefix):
            return {n[len(prefix) + 1:]: a for n, a in A.items() if n.startswith(prefix + "_")}

        with ExitStack() as s1:
            XN = s1.enter_context(nc.sbuf_tensor("XN", [P, C, T], F32))
            layer_norm(nc, K, tokens, XN, "ln0a")
            wide_attention(nc, K, X, XN, ctxT, weights("a0"), gates[:, 0:1], "a0", True, 1.0)
            layer_norm(nc, K, tokens, XN, "ln0f")
            quantised_ffn(nc, K, X, XN, weights("f0"), gates[:, 4:5], "f0")
            layer_norm(nc, K, tokens, XN, "ln1a")
            wide_attention(nc, K, X, XN, ctxT, weights("a1"), gates[:, 1:2], "a1", False, D ** -0.5)
            w_dram = nc.dram_tensor("expert_weights", (NE + 1, T), F32).ap()
            layer_norm(nc, K, tokens, XN, "ln1f")
            with ExitStack() as s2:
                xh = s2.enter_context(nc.sbuf_tensor("moe_xh", [P, C, T], F32R))
                xl = s2.enter_context(nc.sbuf_tensor("moe_xl", [P, C, T], F32R))
                with ExitStack() as s3:
                    XN2 = s3.enter_context(nc.sbuf_tensor("XN2", [P, C, T], F32))
                    ln_g = s3.enter_context(nc.sbuf_tensor("moe_ln_g", [P, C], F32))
                    ln_b = s3.enter_context(nc.sbuf_tensor("moe_ln_b", [P, C], F32))
                    with semaphores(nc, "moe_ln", "loaded") as (loaded,), \
                            nc.Block(no_gpsimd_drain=True) as block:
                        @block.sync
                        def _(sp):
                            sp.dma_start(ln_g[:, :], A["moe_ln_scale"]).then_inc(loaded, 16)
                            sp.dma_start(ln_b[:, :], A["moe_ln_bias"]).then_inc(loaded, 16)
                            sp.wait_ge(loaded, 32)
                    layer_norm(nc, K, lambda c, g: XN[:, c, g * G:(g + 1) * G], XN2, "ln1r",
                               affine=(ln_g, ln_b))
                    router(nc, K, XN2, A["moe_gate_w"], w_dram, "rt")
                split_tokens(nc, XN, xh, xl, "moe_split")
                experts(nc, K, X, xh, xl, w_dram, A["moe_w"], gates[:, 5:6], "moe")
            for stage, tag, g, rel in ((5, "a2", 2, False), (7, "a3", 3, True)):
                layer_norm(nc, K, tokens, XN, f"ln{tag}")
                head_attention(nc, K, X, XN, ctxT, weights(tag), gates[:, g:g + 1], tag, rel)
                if stage == 5:
                    layer_norm(nc, K, tokens, XN, "ln2f")
                    bit_ffn(nc, K, X, XN, weights("f2"), gates[:, 6:7], "f2")
            layer_norm(nc, K, tokens, XN, "ln3f")
            with semaphores(nc, "swap", "away", "taken") as (away, taken), \
                    nc.Block(no_gpsimd_drain=True) as block:
                @block.sync
                def _(sp):
                    sp.dma_start(kept, X[:, :, :]).then_inc(away, 16)
                    sp.wait_ge(away, 16)

                @block.vector
                def _(dve):
                    dve.wait_ge(away, 16)
                    for g in range(NG):
                        for c in range(C):
                            nc.vector.tensor_copy(tokens(c, g), XN[:, c, g * G:(g + 1) * G])
        before_transformer.close()
        transformer(nc, K, X, A)
        with nc.sbuf_tensor("kept_x", [P, C, B * SP1], F32) as old, \
                semaphores(nc, "back", "back") as (back,), nc.Block(no_gpsimd_drain=True) as block:
            @block.sync
            def _(sp):
                sp.dma_start(old[:, :, :], kept).then_inc(back, 16)

            @block.vector
            def _(dve):
                dve.wait_ge(back, 16)
                nc.vector.scalar_tensor_tensor(out=X[:, :, :], in0=X[:, :, :], scalar=gates[:, 7:8],
                                               in1=old[:, :, :], op0=ALU.mult, op1=ALU.add)

        with nc.Block() as block:
            @block.sync
            def _(sp):
                for b in range(B):
                    sp.dma_start(out_x.rearrange("(c p) (b t) -> p c b t", p=P, b=B)[:, :, b],
                                 X[:, :, b * SP1 + 1:(b + 1) * SP1]).then_inc(stored, 16)
                sp.wait_ge(stored, 16 * B)


def kc(a):
    return a.reshape(a.shape[0] // P, P, a.shape[1]).transpose(1, 0, 2)


def cols(a):
    return a.reshape(-1, P).T


def rows(a):
    return np.broadcast_to(a, (P, a.shape[0]))


def layout(i):
    L = {"xT": i["x"].reshape(T, D).T, "ctxT": i["ctx_1024"].reshape(B * E, D).T,
         "g_xattn": i["g_xattn"], "g_ffn": i["g_ffn"],
         "ident": np.eye(P, dtype=np.float32)}
    last = np.zeros((E + 1, P), np.float32)
    last[E] = 1.0
    L["last_row"] = last
    for st, p, tr in (("a0", "L0_xattn_", False), ("a1", "L1_xattn_", True)):
        for n in "qkv":
            wt = i[f"{p}W{n}"]
            L[f"{st}_w{n}"] = kc(wt.T if tr else wt)
            L[f"{st}_b{n}"] = cols(i[f"{p}b{n}"])
        L[f"{st}_bv_row"] = rows(i[f"{p}bv"])
    for st, p in (("a2", "L2_xattn_"), ("a3", "L3_xattn_")):
        wk, wv = (i[p + "Wkv"][:, :D], i[p + "Wkv"][:, D:]) if st == "a2" else (i[p + "Wk"], i[p + "Wv"])
        bk, bv = (i[p + "bkv"][:D], i[p + "bkv"][D:]) if st == "a2" else (i[p + "bk"], i[p + "bv"])
        L[f"{st}_wq"], L[f"{st}_wk"], L[f"{st}_wv"], L[f"{st}_wo"] = kc(i[p + "Wq"]), kc(wk), kc(wv), kc(i[p + "Wo"])
        L[f"{st}_bq"], L[f"{st}_bk"], L[f"{st}_bo"] = cols(i[p + "bq"]), cols(bk), cols(i[p + "bo"])
        L[f"{st}_bv_row"] = rows(bv)
    L["a3_rel_k"] = np.tile(i["L3_xattn_rel_k"], (1, HC)).T
    L["a3_rel_v"] = np.tile(i["L3_xattn_rel_v"], (1, NH))
    L["a3_rel_v0"] = rows(L["a3_rel_v"][0])
    L["head_of"] = (np.arange(P)[:, None] // HD == np.arange(HC)[None, :]).astype(np.float32)
    L["head_cols"] = np.broadcast_to(L["head_of"].T, (P, HC, P))
    dist = np.arange(E)[None, :] - np.arange(P)[:, None]
    L["rel_mask"] = np.stack([np.clip(dist, -2, 2) + 2 == r for r in range(1, 1 + R)], axis=1).astype(np.float32)

    p = "L0_ffn_w_"
    L["f0_wg"], L["f0_wu"], L["f0_wd"] = (kc(i[p + n]).reshape(P, -1) for n in ("gate", "up", "down"))
    p = "L2_ffn_"
    L["f2_w1"], L["f2_w2"] = kc(i[p + "w1"].T).reshape(P, -1), kc(i[p + "w2"].T).reshape(P, -1)
    L["f2_conv_w"] = kc(i[p + "conv_w"][:, 0, :])
    L["f2_conv_b"] = cols(i[p + "conv_b"])

    p = "L3_ffn_"
    per = lambda f: np.stack([f(min(n, DEPTH - 1)) for n in range(DEPTH + 1)])
    pad = lambda a: np.concatenate([a, np.zeros(a.shape[:-1] + (FIP - FI,), a.dtype)], axis=-1)
    two = lambda a: np.concatenate([pad(a[..., :FI]), pad(a[..., FI:])], axis=-1)
    L["l_wqkv"] = per(lambda n: kc(i[p + "Wqkv"][n]).reshape(P, -1))
    L["l_wo"] = per(lambda n: kc(i[p + "Wo"][n]).reshape(P, -1))
    L["l_w1"] = per(lambda n: kc(two(i[p + "W1"][n])).reshape(P, -1))
    L["l_w2"] = per(lambda n: kc(pad(i[p + "W2"][n].T).T).reshape(P, -1))
    L["l_vec"] = per(lambda n: np.concatenate([cols(i[p + "ln_g"][n]), cols(i[p + "ln_b"][n]),
                                               cols(two(i[p + "b1"][n])), cols(i[p + "b2"][n])], axis=1))
    partner = np.roll(np.arange(LD), LD // 2)
    L["l_qk_scale"] = per(lambda n: np.broadcast_to(np.stack(
        [i[p + "q_scale"][n], i[p + "q_scale"][n][partner], i[p + "k_scale"][n], i[p + "k_scale"][n][partner]]),
        (P, 4, LD)))
    f32 = np.float32
    half = np.arange(0, LD, 2, dtype=f32)
    freqs = np.arange(S, dtype=f32)[:, None] * (f32(1.0) / f32(10000.0) ** (half / f32(LD)))[None, :]
    base = (half + f32(0.4 * LD)) / f32(1.4 * LD)
    grow = base[None, :] ** ((np.arange(S, dtype=f32) - S // 2) / (WIN // 2))[:, None]
    twice = lambda a: np.concatenate([a, a], axis=1)
    cos, sin = twice(np.cos(freqs)), np.concatenate([-np.sin(freqs), np.sin(freqs)], axis=1)
    grow, fall = twice(grow), twice(f32(1.0) / grow)
    L["rotary"] = np.stack([cos * grow, sin * grow, cos * fall, sin * fall]).astype(f32).reshape(
        4, NT, P, LD).transpose(2, 0, 1, 3)
    key, query = np.arange(KEYS)[None, :], np.arange(P)[:, None]
    L["band_mask"] = np.where((key >= query) & (key <= query + WIN), 0.0, MASKED).astype(f32)

    def expert(wg, wu, wd):
        return np.concatenate([kc(w).reshape(P, -1) for w in (wg, wu, wd)], axis=1)
    p = "L1_ffn_"
    L["moe_w"] = np.stack([expert(i[p + "Wg"][e], i[p + "Wu"][e], i[p + "Wd"][e]) for e in range(NE)]
                          + [expert(i[p + "sWg"], i[p + "sWu"], i[p + "sWd"])])
    L["moe_gate_w"] = kc(i[p + "gate_w"].T)
    L["moe_ln_scale"], L["moe_ln_bias"] = cols(i[p + "ln_scale"]), cols(i[p + "ln_bias"])
    L["expert_iota"] = rows(np.arange(NE, dtype=np.float32) - NE)
    return L


def kernel(**inputs):
    import numpy as _np
    import concourse.bacc as _bacc
    from concourse import mybir as _mybir
    from concourse.bass_utils import run_bass_kernel_spmd as _run

    nc = _bacc.Bacc("TRN2", target_bir_lowering=False, num_devices=1)
    L = {k: _np.ascontiguousarray(v) for k, v in layout({k: _np.asarray(v) for k, v in inputs.items()}).items()}
    arrays, aps = {}, {}
    for name, a in L.items():
        arrays[f"in_{name}"] = a
        aps[name] = nc.dram_tensor(f"in_{name}", a.shape, _mybir.dt.from_np(a.dtype), kind="ExternalInput").ap()
    out = nc.dram_tensor("out_x", (D, T), _mybir.dt.float32, kind="ExternalOutput").ap()
    flamingo(nc, aps, out)
    r = _run(nc, [arrays], core_ids=[0])
    got = r.results[0]["out_x"]
    return _np.ascontiguousarray(got.T).reshape(B, S, D)
```

```python
from contextlib import ExitStack, contextmanager

import numpy as np
import concourse.bass as bass
from concourse import mybir

ALU = mybir.AluOpType
ACT = mybir.ActivationFunctionType
AX = mybir.AxisListType
F32 = mybir.dt.float32
BF16 = mybir.dt.bfloat16
F32R = mybir.dt.float32r
ABSMAX = bass.bass_isa.ReduceOp.absmax
RADD = bass.bass_isa.ReduceOp.add
ds = bass.ds

P = 128
B, S, D = 2, 1024, 256
C = D // P
T = B * S
G = 512
NG = T // G
GB = S // G
TG = G // P
E = 77
SP1 = S + 1
MAGIC = 12582912.0
EPS = 1e-5


@contextmanager
def semaphores(nc, stage, *names):
    with ExitStack() as s:
        sems = [s.enter_context(nc.semaphore(f"{stage}_{n}")) for n in names]
        yield sems
        with nc.Block(no_gpsimd_drain=True) as block:
            @block.sync
            def _(sp):
                for sem in sems:
                    sp.sem_clear(sem)


class Own:

    def __init__(self, eng, sem):
        self.eng, self.sem, self.n = eng, sem, 0

    def __call__(self, ins):
        self.n += 1
        ins.then_inc(self.sem, 1)
        self.eng.wait_ge(self.sem, self.n)


class Constants:

    def __init__(self, sb, A):
        self.ident, self.mean_w, self.eps = sb("ident", [P, P]), sb("mean_w", [P, P]), sb("eps", [P, 1])
        self.head_of, self.head_cols, self.rel_mask = A["head_of"], A["head_cols"], A["rel_mask"]
        self.expert_iota = A["expert_iota"]


def bc(ap, axis, shape):
    return ap.unsqueeze(axis).to_broadcast(shape)


def layer_norm(nc, K, src, XN, tag, loads=(), affine=None):
    with ExitStack() as s:
        sb = lambda n, sh: s.enter_context(nc.sbuf_tensor(f"{tag}_{n}", sh, F32))
        xsum = sb("xsum", [P, 2, G])
        sq = sb("sq", [P, 2, C, G])
        sqsum = sb("sqsum", [P, 2, G])
        rstd = sb("rstd", [P, NG, G])
        mean_ps = s.enter_context(nc.psum_tensor(f"{tag}_mean", [P, 2, G], F32))
        var_ps = s.enter_context(nc.psum_tensor(f"{tag}_var", [P, NG, G], F32))
        with semaphores(nc, tag, "xsum", "mean", "centred", "squares", "sqsum", "var",
                        "lnv", "rstd", "scaled", "loaded") as (
                xsum_ready, mean_ready, centred, squares, sqsum_ready, var_ready,
                lnv_ready, rstd_ready, scaled, loaded), nc.Block(no_gpsimd_drain=True) as block:

            @block.sync
            def _(sp):
                for to, source in loads:
                    sp.dma_start(to, source).then_inc(loaded, 16)
                if loads:
                    sp.wait_ge(loaded, 16 * len(loads))

            @block.gpsimd
            def _(pool):
                for g in range(NG):
                    if g >= 2:
                        pool.wait_ge(mean_ready, g - 1)
                    nc.gpsimd.tensor_tensor(xsum[:, g % 2], src(0, g), src(1, g),
                                            ALU.add).then_inc(xsum_ready, 1)

            @block.tensor
            def _(pe):
                def mean(g):
                    pe.wait_ge(xsum_ready, g + 1)
                    if g >= 2:
                        pe.wait_ge(centred, g - 1)
                    nc.tensor.matmul(mean_ps[:, g % 2], K.mean_w[:, :], xsum[:, g % 2],
                                     start=True, stop=True).then_inc(mean_ready, 1)

                def var(g):
                    pe.wait_ge(sqsum_ready, g + 1)
                    nc.tensor.matmul(var_ps[:, g], K.mean_w[:, :], sqsum[:, g % 2],
                                     start=True, stop=True).then_inc(var_ready, 1)
                for g in range(NG):
                    mean(g)
                    if g:
                        var(g - 1)
                var(NG - 1)

            @block.vector
            def _(dve):
                def centre(g):
                    dve.wait_ge(mean_ready, g + 1)
                    for c in range(C):
                        last = nc.vector.tensor_tensor(XN[:, c, g * G:(g + 1) * G], src(c, g),
                                                       mean_ps[:, g % 2], ALU.subtract)
                    last.then_inc(centred, 1)

                def sum_squares(g):
                    dve.wait_ge(squares, g + 1)
                    if g >= 2:
                        dve.wait_ge(var_ready, g - 1)
                    nc.vector.tensor_tensor(sqsum[:, g % 2], sq[:, g % 2, 0], sq[:, g % 2, 1],
                                            ALU.add).then_inc(sqsum_ready, 1)

                def scale(g):
                    dve.wait_ge(rstd_ready, g + 1)
                    for c in range(C):
                        view = XN[:, c, g * G:(g + 1) * G]
                        last = nc.vector.tensor_tensor(view, view, rstd[:, g], ALU.mult)
                        last.then_inc(scaled, 1)
                    if affine is not None:
                        dve.wait_ge(scaled, C * (g + 1))
                        for c in range(C):
                            view = XN[:, c, g * G:(g + 1) * G]
                            nc.vector.tensor_scalar(view, view, affine[0][:, c:c + 1],
                                                    affine[1][:, c:c + 1], ALU.mult, ALU.add)
                for g in range(NG + 1):
                    if g < NG:
                        centre(g)
                    if g:
                        sum_squares(g - 1)
                for g in range(NG):
                    scale(g)

            @block.scalar
            def _(act):
                def square(g):
                    act.wait_ge(centred, g + 1)
                    if g >= 2:
                        act.wait_ge(sqsum_ready, g - 1)
                    nc.scalar.activation(sq[:, g % 2], XN[:, :, g * G:(g + 1) * G],
                                         ACT.Square).then_inc(squares, 1)

                def logarithm(g):
                    act.wait_ge(var_ready, g + 1)
                    nc.scalar.activation(rstd[:, g], var_ps[:, g], ACT.Ln, bias=K.eps[:, 0:1]
                                         ).then_inc(lnv_ready, 1)

                def inverse_std(g):
                    act.wait_ge(lnv_ready, g + 1)
                    nc.scalar.activation(rstd[:, g], rstd[:, g], ACT.Exp, scale=-0.5).then_inc(rstd_ready, 1)
                for g in range(NG):
                    square(g)
                    if g == NG - 1 or g % 2 == 0 and g:
                        first = g - g % 2 - (0 if g == NG - 1 else 2)
                        for n in range(first, first + 2):
                            logarithm(n)
                        for n in range(first, first + 2):
                            inverse_std(n)


def wide_attention(nc, K, X, XN, norm, ctxT, W, gate, tag, self_key, scale):
    M = E + 1 if self_key else E
    names = ("q", "k", "v")
    with ExitStack() as s:
        sb = lambda n, sh: s.enter_context(nc.sbuf_tensor(f"{tag}_{n}", sh, F32))
        w = {n: sb(f"w{n}", [P, C, D]) for n in names}
        b_col = {n: sb(f"b{n}", [P, C]) for n in names}
        bv_row = sb("bv_row", [P, D])
        kxT = sb("kxT", [P, C, B, E])
        vx = sb("vx", [P, B, D])

        norm([(w[n][:, :, :], W[f"w{n}"]) for n in names] + [(b_col[n][:, :], W[f"b{n}"]) for n in names]
             + [(bv_row[:, :], W["bv_row"])])

        with ExitStack() as s2:
            kx_ps = s2.enter_context(nc.psum_tensor(f"{tag}_kx_ps", [P, C, G], F32))
            vx_ps = s2.enter_context(nc.psum_tensor(f"{tag}_vx_ps", [P, B, G], F32))
            with semaphores(nc, f"{tag}_ctx", "zeroed", "products") as (zeroed, products), \
                    nc.Block(no_gpsimd_drain=True) as block:
                @block.tensor
                def _(pe):
                    for m in range(C):
                        for c in range(C):
                            nc.tensor.matmul(kx_ps[:, m, 0:B * E], w["k"][:, c, m * P:(m + 1) * P],
                                             ctxT[:, c, :], start=(c == 0), stop=(c == C - 1))
                    for b in range(B):
                        for c in range(C):
                            last = nc.tensor.matmul(vx_ps[0:E, b, 0:D], ctxT[:, c, b * E:(b + 1) * E],
                                                    w["v"][:, c, :], start=(c == 0), stop=(c == C - 1))
                    last.then_inc(products, 1)

                @block.vector
                def _(dve):
                    nc.vector.memset(vx[:, :, :], 0.0).then_inc(zeroed, 1)
                    dve.wait_ge(products, 1)
                    dve.wait_ge(zeroed, 1)
                    for m in range(C):
                        nc.vector.tensor_scalar(kxT[:, m].rearrange("p b e -> p (b e)"),
                                                kx_ps[:, m, 0:B * E], b_col["k"][:, m:m + 1], None,
                                                ALU.add)
                    for b in range(B):
                        nc.vector.tensor_tensor(vx[0:E, b], vx_ps[0:E, b, 0:D], bv_row[0:E, :],
                                                ALU.add)

        q_sb = sb("q", [P, 2, C, G])
        qk_sb = sb("qk", [P, 2, C, G])
        v_sb = sb("v", [P, 2, C, G])
        t_sb = sb("t", [P, C, G])
        prob = sb("prob", [P, 2, TG, M])
        stat = sb("stat", [P, 2, 3, TG])
        pT = sb("pT", [P, 2, G])
        proj_ps = s.enter_context(nc.psum_tensor(f"{tag}_proj", [P, 2, G], F32))
        s_ps = s.enter_context(nc.psum_tensor(f"{tag}_s", [P, TG, P], F32))
        pT_ps = s.enter_context(nc.psum_tensor(f"{tag}_pT_ps", [P, G], F32))
        o_ps = s.enter_context(nc.psum_tensor(f"{tag}_o", [P, C, G], F32))
        p0_ps = s.enter_context(nc.psum_tensor(f"{tag}_p0", [P, G], F32))
        which = [(n, m) for n in (names if self_key else ("q",)) for m in range(C)]
        NP = len(which)

        def cols(g, c):
            first = (g // GB) * SP1 + 1 + (g % GB) * G
            return X[:, c, first:first + G]
        with semaphores(nc, tag, "proj", "taken", "scores", "maxed", "exped", "prob", "probT", "pT", "out",
                        "added", "own") as (
                proj, taken, scores, maxed, exped, prob_ready, probT, pT_ready, out_ready, added,
                dve_own), nc.Block(no_gpsimd_drain=True) as block:

            @block.tensor
            def _(pe):
                def project(g):
                    for i, (n, m) in enumerate(which):
                        k = NP * g + i
                        if k >= 2:
                            pe.wait_ge(taken, k - 1)
                        for c in range(C):
                            last = nc.tensor.matmul(proj_ps[:, k % 2], w[n][:, c, m * P:(m + 1) * P],
                                                    XN[:, c, g * G:(g + 1) * G],
                                                    start=(c == 0), stop=(c == C - 1))
                        last.then_inc(proj, 1)

                def score(g):
                    pe.wait_ge(taken, NP * (g + 1))
                    if g:
                        pe.wait_ge(exped, TG * g)
                    for t in range(TG):
                        tok = slice(t * P, (t + 1) * P)
                        for c in range(C):
                            last = nc.tensor.matmul(s_ps[:, t, 0:E], q_sb[:, g % 2, c, tok],
                                                    kxT[:, c, g // GB, :], start=(c == 0), stop=(c == C - 1))
                        if self_key:
                            for c in range(C):
                                last = nc.tensor.matmul(s_ps[:, t, E:M], qk_sb[:, g % 2, c, tok],
                                                        K.ones[:, 0:1], start=(c == 0), stop=(c == C - 1))
                    last.then_inc(scores, 1)

                def mix(g):
                    if g:
                        pe.wait_ge(pT_ready, g)
                    for t in range(TG):
                        pe.wait_ge(prob_ready, TG * g + t + 1)
                        last = nc.tensor.transpose(pT_ps[0:M, t * P:(t + 1) * P], prob[:, g % 2, t, :],
                                                   K.ident[:, :])
                    last.then_inc(probT, 1)
                    pe.wait_ge(pT_ready, g + 1)
                    if g:
                        pe.wait_ge(added, C * g)
                    if self_key:
                        nc.tensor.matmul(p0_ps[:, :], K.last_row[0:M, :], pT[0:M, g % 2], start=True, stop=True)
                    for m in range(C):
                        last = nc.tensor.matmul(o_ps[:, m], vx[0:M, g // GB, m * P:(m + 1) * P],
                                                pT[0:M, g % 2], start=True, stop=True)
                    last.then_inc(out_ready, 1)
                project(0)
                for g in range(NG):
                    score(g)
                    if g + 1 < NG:
                        project(g + 1)
                    mix(g)

            @block.vector
            def _(dve):
                own = Own(dve, dve_own)

                def take(g):
                    if g >= 2:
                        dve.wait_ge(scores, g - 1)
                    for i, (n, m) in enumerate(which):
                        k = NP * g + i
                        dve.wait_ge(proj, k + 1)
                        src, bias = proj_ps[:, k % 2], b_col[n][:, m:m + 1]
                        if n == "k":
                            dve.wait_ge(taken, NP * g + m + 1)
                            nc.vector.scalar_tensor_tensor(out=qk_sb[:, g % 2, m], in0=src, scalar=bias,
                                                           in1=q_sb[:, g % 2, m], op0=ALU.add,
                                                           op1=ALU.mult).then_inc(taken, 1)
                        else:
                            dst = (q_sb if n == "q" else v_sb)[:, g % 2, m]
                            nc.vector.tensor_scalar(dst, src, bias, None, ALU.add).then_inc(taken, 1)

                def maxima(g):
                    st = stat[:, g % 2, 0, :]
                    dve.wait_ge(scores, g + 1)
                    own(nc.vector.tensor_reduce(st, s_ps[:, :, 0:M], AX.X, ALU.max))
                    nc.vector.tensor_scalar(st, st, -scale, None, ALU.mult).then_inc(maxed, 1)

                def normalise(g):
                    dve.wait_ge(exped, TG * (g + 1))
                    own(nc.vector.reciprocal(stat[:, g % 2, 2, :], stat[:, g % 2, 1, :]))
                    for t in range(TG):
                        nc.vector.tensor_scalar(prob[:, g % 2, t, :], prob[:, g % 2, t, :],
                                                stat[:, g % 2, 2, t:t + 1], None, ALU.mult
                                                ).then_inc(prob_ready, 1)

                def add(g):
                    dve.wait_ge(out_ready, g + 1)
                    for m in range(C):
                        src = o_ps[:, m]
                        if self_key:
                            own(nc.vector.tensor_tensor(t_sb[:, m], v_sb[:, g % 2, m], p0_ps[:, :], ALU.mult))
                            own(nc.vector.tensor_tensor(t_sb[:, m], t_sb[:, m], o_ps[:, m], ALU.add))
                            src = t_sb[:, m]
                        nc.vector.scalar_tensor_tensor(out=cols(g, m), in0=src, scalar=gate, in1=cols(g, m),
                                                       op0=ALU.mult, op1=ALU.add).then_inc(added, 1)
                take(0)
                for g in range(NG):
                    maxima(g)
                    if g + 1 < NG:
                        take(g + 1)
                    normalise(g)
                    add(g)

            @block.scalar
            def _(act):
                for g in range(NG):
                    act.wait_ge(maxed, g + 1)
                    if g >= 2:
                        act.wait_ge(probT, g - 1)
                    for t in range(TG):
                        nc.scalar.activation(prob[:, g % 2, t, :], s_ps[:, t, 0:M], ACT.Exp,
                                             bias=stat[:, g % 2, 0, t:t + 1], scale=scale,
                                             accum_out=stat[:, g % 2, 1, t:t + 1]).then_inc(exped, 1)
                    act.wait_ge(probT, g + 1)
                    if g >= 2:
                        act.wait_ge(out_ready, g - 1)
                    nc.scalar.activation(pT[0:M, g % 2], pT_ps[0:M, :], ACT.Copy).then_inc(pT_ready, 1)


NE, TOPK, FE = 8, 2, 512
FC = FE // P
WE = 2 * C * FE + FC * D


def router(nc, K, XN2, gw, iota, w_dram, tag):
    NT = T // P
    with ExitStack() as s:
        sb = lambda n, sh: s.enter_context(nc.sbuf_tensor(f"{tag}_{n}", sh, F32))
        prob = sb("prob", [P, NT, NE])
        rest = sb("rest", [P, NT, NE])
        pick = sb("pick", [P, 2, NT, NE])
        tmp = sb("tmp", [P, NT, NE])
        col = sb("col", [P, 6, NT])
        w9 = sb("w9", [P, NT, NE + 1])
        wT = sb("wT", [P, T])
        lg_ps = s.enter_context(nc.psum_tensor(f"{tag}_lg", [P, NT, NE], F32))
        wT_ps = s.enter_context(nc.psum_tensor(f"{tag}_wT_ps", [P, T], F32))
        full = [P, NT, NE]
        with semaphores(nc, tag, "logits", "exped", "maxed", "weights", "turned", "copied",
                        "stored", "own") as (logits, exped, maxed, weighted, turned, copied,
                                             stored, dve_own), \
                nc.Block(no_gpsimd_drain=True) as block:
            @block.sync
            def _(sp):
                sp.wait_ge(copied, 1)
                sp.dma_start(w_dram, wT[0:NE + 1, :]).then_inc(stored, 16)
                sp.wait_ge(stored, 16)

            @block.tensor
            def _(pe):
                for t in range(NT):
                    for c in range(C):
                        last = nc.tensor.matmul(lg_ps[:, t, :], XN2[:, c, t * P:(t + 1) * P], gw[:, c, :],
                                                start=(c == 0), stop=(c == C - 1))
                last.then_inc(logits, 1)
                pe.wait_ge(weighted, 1)
                for t in range(NT):
                    last = nc.tensor.transpose(wT_ps[0:NE + 1, t * P:(t + 1) * P], w9[:, t, :],
                                               K.ident[:, :])
                last.then_inc(turned, 1)

            @block.scalar
            def _(act):
                act.wait_ge(maxed, 1)
                nc.scalar.activation(prob[:, :, :], rest[:, :, :], ACT.Exp).then_inc(exped, 1)

            @block.vector
            def _(dve):
                own = Own(dve, dve_own)
                tt, tr, ts = nc.vector.tensor_tensor, nc.vector.tensor_reduce, nc.vector.tensor_scalar
                wide = lambda n: bc(col[:, n, :], 2, full)
                numbers = bc(iota[:, :], 1, full)
                dve.wait_ge(logits, 1)
                own(tr(col[:, 0, :], lg_ps[:, :, :], AX.X, ALU.max))
                tt(rest[:, :, :], lg_ps[:, :, :], wide(0), ALU.subtract).then_inc(maxed, 1)
                dve.wait_ge(exped, 1)
                own(tr(col[:, 1, :], prob[:, :, :], AX.X, ALU.add))
                own(nc.vector.reciprocal(col[:, 1, :], col[:, 1, :]))
                own(tt(prob[:, :, :], prob[:, :, :], wide(1), ALU.mult))
                left = prob
                for n in range(TOPK):
                    own(tr(col[:, 2 + n, :], left[:, :, :], AX.X, ALU.max))
                    own(tt(tmp[:, :, :], left[:, :, :], wide(2 + n), ALU.is_equal))
                    own(tt(tmp[:, :, :], tmp[:, :, :], numbers, ALU.mult))
                    own(tr(col[:, 4, :], tmp[:, :, :], AX.X, ALU.min))
                    own(tt(pick[:, n], numbers, wide(4), ALU.is_equal))
                    if n == 0:
                        own(nc.vector.scalar_tensor_tensor(
                            out=rest[:, :, :], in0=pick[:, 0], scalar=-2.0, in1=prob[:, :, :],
                            op0=ALU.mult, op1=ALU.add))
                        left = rest
                own(tt(col[:, 5, :], col[:, 2, :], col[:, 3, :], ALU.add))
                own(ts(col[:, 5, :], col[:, 5, :], EPS, None, ALU.add))
                own(nc.vector.reciprocal(col[:, 5, :], col[:, 5, :]))
                own(tt(tmp[:, :, :], pick[:, 0], pick[:, 1], ALU.add))
                own(tt(tmp[:, :, :], tmp[:, :, :], prob[:, :, :], ALU.mult))
                own(nc.vector.memset(w9[:, :, NE:NE + 1], 1.0))
                tt(w9[:, :, 0:NE], tmp[:, :, :], wide(5), ALU.mult).then_inc(weighted, 1)
                dve.wait_ge(turned, 1)
                nc.vector.tensor_copy(wT[0:NE + 1, :], wT_ps[0:NE + 1, :]).then_inc(copied, 1)


def experts(nc, K, X, XN, XH, XL, raw, w_dram, we_dram, gate, tag):
    with ExitStack() as s:
        sb = lambda n, sh, dt=F32: s.enter_context(nc.sbuf_tensor(f"{tag}_{n}", sh, dt))
        wh = [sb(f"wh{j}", [P, WE], F32R) for j in range(2)]
        wl = [sb(f"wl{j}", [P, WE], F32R) for j in range(2)]
        share = sb("share", [P, 2, T])
        hg = sb("hg", [P, 2, G])
        hgw = sb("hgw", [P, 2, G])
        hid = sb("hid", [P, 2, G])
        hh = sb("hh", [P, 2, G], F32R)
        hl = sb("hl", [P, 2, G], F32R)
        gu_ps = s.enter_context(nc.psum_tensor(f"{tag}_gu", [P, 2, 2, G], F32))
        y_ps = s.enter_context(nc.psum_tensor(f"{tag}_y", [P, 2, C, G], F32))
        QW = 4
        piece = lambda q: slice(q * WE // QW, (q + 1) * WE // QW)

        def up_w(w, u, c, i):
            first = u * C * FE + c * FE + i * P
            return w[:, first:first + P]

        def down_w(w, i, m):
            first = 2 * C * FE + i * D + m * P
            return w[:, first:first + P]

        TP = 4
        flat = lambda x: x[:, :, :].rearrange("p c t -> p (c t)")
        jobs = [(wh[0][:, piece(q)], wl[0][:, piece(q)], raw[:, 0, piece(q)]) for q in range(QW)]
        for n in range(TP):
            part = slice(n * C * T // TP, (n + 1) * C * T // TP)
            jobs.append((flat(XH)[:, part], flat(XL)[:, part], flat(XN)[:, part]))
        with semaphores(nc, f"{tag}_first", "loaded", "high") as (loaded, high), \
                nc.Block(no_gpsimd_drain=True) as block:
            @block.sync
            def _(sp):
                sp.dma_start(share[:, 0, :], w_dram[0:1, :].to_broadcast([P, T])).then_inc(loaded, 16)
                sp.wait_ge(loaded, 16)

            @block.scalar
            def _(act):
                for hi, lo, src in jobs:
                    nc.scalar.activation(hi, src, ACT.Copy).then_inc(high, 1)

            @block.vector
            def _(dve):
                for n, (hi, lo, src) in enumerate(jobs):
                    dve.wait_ge(high, n + 1)
                    nc.vector.tensor_tensor(lo, src, hi.bitcast(F32), ALU.subtract)

        def one_pass(e, both):
            half = NG * FC
            N = half * (2 if both else 1)
            where = lambda k: (k // half, (k % half) // FC, k % FC)
            second_at = {4 + q: q for q in range(QW)}
            next_at = {half + 4 + q: q for q in range(QW)}
            with semaphores(nc, tag, "raw1", "raw0", "share1", "share0", "gu", "silu", "shared", "prod",
                            "high", "low", "y", "added", "wh1", "wl1", "wh0", "down") as (
                    raw1, raw0, share1, share0, gu_ready, silu_ready, shared, prod, high, low,
                    y_ready, added, wh1, wl1, wh0, down_done), \
                    nc.Block(no_gpsimd_drain=True) as block:

                @block.sync
                def _(sp):
                    if not both:
                        return
                    sp.dma_start(raw[:, 1, :], we_dram[ds(e + 1, 1)].rearrange("o p w -> p (o w)")
                                 ).then_inc(raw1, 16)
                    sp.dma_start(share[:, 1, :], w_dram[ds(e + 1, 1), :].to_broadcast([P, T])
                                 ).then_inc(share1, 16)
                    sp.dma_start(raw[:, 0, :], we_dram[ds(e + 2, 1)].rearrange("o p w -> p (o w)")
                                 ).then_inc(raw0, 16)
                    sp.wait_ge(shared, half)
                    sp.dma_start(share[:, 0, :], w_dram[ds(e + 2, 1), :].to_broadcast([P, T])
                                 ).then_inc(share0, 16)
                    sp.wait_ge(share0, 16)
                    sp.wait_ge(raw0, 16)

                @block.tensor
                def _(pe):
                    def up(k):
                        j, g, i = where(k)
                        if k == half:
                            pe.wait_ge(wl1, QW)
                        if k >= 2:
                            pe.wait_ge(prod, k - 1)
                        tok = slice(g * G, (g + 1) * G)
                        for u in range(2):
                            for c in range(C):
                                a = (up_w(wh[j], u, c, i), up_w(wl[j], u, c, i))
                                x = (XH[:, c, tok], XL[:, c, tok])
                                for n, (p, q) in enumerate(((0, 0), (0, 1), (1, 0))):
                                    last = nc.tensor.matmul(gu_ps[:, k % 2, u], a[p], x[q],
                                                            start=(c == 0 and n == 0),
                                                            stop=(c == C - 1 and n == 2))
                        last.then_inc(gu_ready, 1)

                    def down(k):
                        j, g, i = where(k)
                        gg = j * NG + g
                        pe.wait_ge(low, k + 1)
                        if i == 0 and gg >= 2:
                            pe.wait_ge(added, gg - 1)
                        for m in range(C):
                            a = (down_w(wh[j], i, m), down_w(wl[j], i, m))
                            x = (hh[:, k % 2], hl[:, k % 2])
                            for n, (p, q) in enumerate(((0, 0), (0, 1), (1, 0))):
                                last = nc.tensor.matmul(y_ps[:, gg % 2, m], a[p], x[q],
                                                        start=(i == 0 and n == 0),
                                                        stop=(i == FC - 1 and n == 2))
                        last.then_inc(down_done, 1)
                    for k in range(N + 2):
                        if k < N:
                            up(k)
                        if k >= 2:
                            down(k - 2)

                @block.scalar
                def _(act):
                    def silu(k):
                        act.wait_ge(gu_ready, k + 1)
                        if k >= 2:
                            act.wait_ge(shared, k - 1)
                        nc.scalar.activation(hg[:, k % 2], gu_ps[:, k % 2, 0], ACT.Silu).then_inc(silu_ready, 1)

                    def take_high(k):
                        act.wait_ge(prod, k + 1)
                        if k >= 2:
                            act.wait_ge(down_done, k - 1)
                        nc.scalar.activation(hh[:, k % 2], hid[:, k % 2], ACT.Copy).then_inc(high, 1)
                    for k in range(N + 1):
                        if k < N:
                            silu(k)
                        if k:
                            take_high(k - 1)
                        if both and k in second_at:
                            act.wait_ge(raw1, 16)
                            q = piece(second_at[k])
                            nc.scalar.activation(wh[1][:, q], raw[:, 1, q], ACT.Copy).then_inc(wh1, 1)
                        if both and k in next_at:
                            act.wait_ge(raw0, 16)
                            act.wait_ge(down_done, half)
                            q = piece(next_at[k])
                            nc.scalar.activation(wh[0][:, q], raw[:, 0, q], ACT.Copy).then_inc(wh0, 1)

                @block.gpsimd
                def _(pool):
                    for k in range(N):
                        j, g, i = where(k)
                        if k == half:
                            pool.wait_ge(share1, 16)
                        pool.wait_ge(silu_ready, k + 1)
                        if k >= 2:
                            pool.wait_ge(prod, k - 1)
                        nc.gpsimd.tensor_tensor(hgw[:, k % 2], hg[:, k % 2],
                                                share[:, j, g * G:(g + 1) * G], ALU.mult
                                                ).then_inc(shared, 1)

                @block.vector
                def _(dve):
                    def product(k):
                        dve.wait_ge(shared, k + 1)
                        if k >= 2:
                            dve.wait_ge(low, k - 1)
                        nc.vector.tensor_tensor(hid[:, k % 2], gu_ps[:, k % 2, 1], hgw[:, k % 2],
                                                ALU.mult).then_inc(prod, 1)

                    def take_low(k):
                        dve.wait_ge(high, k + 1)
                        if k >= 2:
                            dve.wait_ge(down_done, k - 1)
                        nc.vector.tensor_tensor(hl[:, k % 2], hid[:, k % 2], hh[:, k % 2].bitcast(F32),
                                                ALU.subtract).then_inc(low, 1)

                    def add(gg):
                        dve.wait_ge(down_done, FC * (gg + 1))
                        if gg >= NG:
                            dve.wait_ge(added, gg - NG + 1)
                        g = gg % NG
                        for c in range(C):
                            view = X[:, c, (g // GB) * SP1 + 1 + (g % GB) * G:][:, 0:G]
                            last = nc.vector.scalar_tensor_tensor(out=view, in0=y_ps[:, gg % 2, c],
                                                                  scalar=gate, in1=view,
                                                                  op0=ALU.mult, op1=ALU.add)
                        last.then_inc(added, 1)
                    for k in range(N + 3):
                        if k < N:
                            product(k)
                        if 1 <= k <= N:
                            take_low(k - 1)
                        if k >= 3 and (k - 3) % FC == FC - 1:
                            add((k - 3) // FC)
                        if both and k in second_at:
                            dve.wait_ge(wh1, second_at[k] + 1)
                            q = piece(second_at[k])
                            nc.vector.tensor_tensor(wl[1][:, q], raw[:, 1, q], wh[1][:, q].bitcast(F32),
                                                    ALU.subtract).then_inc(wl1, 1)
                        if both and k in next_at:
                            dve.wait_ge(wh0, next_at[k] + 1)
                            q = piece(next_at[k])
                            nc.vector.tensor_tensor(wl[0][:, q], raw[:, 0, q], wh[0][:, q].bitcast(F32),
                                                    ALU.subtract)

        with nc.Fori(0, NE // 2) as pair:
            one_pass(pair * 2, True)
        one_pass(NE, False)


NH, HD = 16, 16
HC = NH // C
R = 4
MA = E + R
BANK_HEADS = G // E


def head_attention(nc, K, X, XN, norm, ctxT, W, gate, tag, relative):
    with ExitStack() as s:
        sb = lambda n, sh: s.enter_context(nc.sbuf_tensor(f"{tag}_{n}", sh, F32))
        w = {n: sb(f"w{n}", [P, C, D]) for n in "qkvo"}
        b_col = {n: sb(f"b{n}", [P, C]) for n in "qko"}
        bv_row = sb("bv_row", [P, D])
        head_of = sb("head_of", [P, HC])
        head_cols = sb("head_cols", [P, HC, P])
        kT = sb("kT", [P, C, B * E])
        vx = sb("vx", [P, B, D])
        kblk = sb("kblk", [P, B, C, HC, E])
        vblk = sb("vblk", [P, B, NH, P])
        bo_gate = sb("bo_gate", [P, C])
        if relative:
            rel_k = sb("rel_k", [P, 1 + R])
            rel_v = sb("rel_v", [1 + R, D])
            rel_v0 = sb("rel_v0", [P, D])
            rel_mask = sb("rel_mask", [P, R, E])
            rblk = sb("rblk", [P, HC, R])
            corr = sb("corr", [P, NH, R])
            tmp = sb("tmp", [P, NH, E])

        loads = [(w[n][:, :, :], W[f"w{n}"]) for n in "qkvo"] + [(b_col[n][:, :], W[f"b{n}"]) for n in "qko"]
        loads += [(bv_row[:, :], W["bv_row"]), (head_of[:, :], K.head_of), (head_cols[:, :, :], K.head_cols)]
        if relative:
            loads += [(rel_k[:, :], W["rel_k"]), (rel_v[:, :], W["rel_v"]), (rel_v0[:, :], W["rel_v0"]),
                      (rel_mask[:, :, :], K.rel_mask)]

        norm(loads)

        with ExitStack() as s2:
            k_ps = s2.enter_context(nc.psum_tensor(f"{tag}_k_ps", [P, C, G], F32))
            v_ps = s2.enter_context(nc.psum_tensor(f"{tag}_v_ps", [P, B, G], F32))
            with semaphores(nc, f"{tag}_ctx", "products", "own") as (products, dve_own), \
                    nc.Block(no_gpsimd_drain=True) as block:
                @block.tensor
                def _(pe):
                    for m in range(C):
                        for c in range(C):
                            nc.tensor.matmul(k_ps[:, m, 0:B * E], w["k"][:, c, m * P:(m + 1) * P],
                                             ctxT[:, c, :], start=(c == 0), stop=(c == C - 1))
                    for b in range(B):
                        for c in range(C):
                            last = nc.tensor.matmul(v_ps[0:E, b, 0:D], ctxT[:, c, b * E:(b + 1) * E],
                                                    w["v"][:, c, :], start=(c == 0), stop=(c == C - 1))
                    last.then_inc(products, 1)

                @block.vector
                def _(dve):
                    own = Own(dve, dve_own)
                    if relative:
                        own(nc.vector.tensor_scalar(rel_k[:, 1:], rel_k[:, 1:], rel_k[:, 0:1], None,
                                                    ALU.subtract))
                        nc.vector.tensor_tensor(rblk[:, :, :], bc(rel_k[:, 1:], 1, [P, HC, R]),
                                                bc(head_of[:, :], 2, [P, HC, R]), ALU.mult)
                        own(nc.vector.tensor_tensor(rel_v[:, :], rel_v[:, :], rel_v0[0:1 + R, :],
                                                    ALU.subtract))
                        own(nc.vector.tensor_tensor(bv_row[:, :], bv_row[:, :], rel_v0[:, :], ALU.add))
                        for m in range(C):
                            own(nc.vector.tensor_scalar(b_col["k"][:, m:m + 1], b_col["k"][:, m:m + 1],
                                                        rel_k[:, 0:1], None, ALU.add))
                    nc.vector.tensor_scalar(bo_gate[:, :], b_col["o"][:, :], gate, None, ALU.mult)
                    dve.wait_ge(products, 1)
                    for m in range(C):
                        nc.vector.tensor_scalar(kT[:, m], k_ps[:, m, 0:B * E], b_col["k"][:, m:m + 1],
                                                None, ALU.add)
                    for b in range(B):
                        nc.vector.tensor_tensor(vx[0:E, b], v_ps[0:E, b, 0:D], bv_row[0:E, :], ALU.add)

        MK = MA if relative else E
        NTILES = NG * TG
        q_sb = sb("q", [P, 2, C, G])
        ctx_sb = sb("ctx", [P, C, G])
        y_sb = sb("y", [P, C, G])
        ex = sb("ex", [P, 2, NH, E])
        prob = sb("prob", [P, 2, NH, MK])
        stat = sb("stat", [P, 2, 3, NH])
        pT = sb("pT", [P, 2, NH, G])
        o_ps = s.enter_context(nc.psum_tensor(f"{tag}_o", [P, C, G], F32))
        s_ps = s.enter_context(nc.psum_tensor(f"{tag}_s", [P, 3, G], F32))
        pT_ps = s.enter_context(nc.psum_tensor(f"{tag}_pT_ps", [P, 2, TG, P], F32))
        qy_ps = s.enter_context(nc.psum_tensor(f"{tag}_qy", [P, G], F32))
        pieces = []
        for h0 in range(0, NH, BANK_HEADS):
            h1 = min(h0 + BANK_HEADS, NH)
            for c in range(C):
                a, z = max(h0, c * HC), min(h1, (c + 1) * HC)
                if a < z:
                    pieces.append((h0 // BANK_HEADS, a - h0, a, z - a))
        banks = [(k, h0, min(BANK_HEADS, NH - h0)) for k, h0 in enumerate(range(0, NH, BANK_HEADS))]
        sview = lambda k, n: s_ps[:, k, 0:n * E].rearrange("p (h e) -> p h e", e=E)
        HB = TG
        NB = NH // HB
        first = lambda i: relative and i % (GB * TG) == 0

        order = [("kblk", 0, 0), ("q", 0, 0), ("q", 0, 1), ("corr", 0, 0), ("score", 0, 0), ("less", 0, 0),
                 ("exp", 0, 0), ("corr", 1, 0), ("score", 1, 0), ("less", 1, 0), ("norm", 0, 0),
                 ("exp", 1, 0)]
        for i in range(NTILES + TG):
            g, t = divmod(i, TG)
            fill = [[("q", g + 1, 0), ("mix", g - 1, 0), ("q", g + 1, 1), ("mix", g - 1, 1)],
                    [("mix", g - 1, 2), ("mix", g - 1, 3), ("ctx", g - 1, 0), ("mix", g - 1, 4)],
                    [("mix", g - 1, 5), ("mix", g - 1, 6), ("mix", g - 1, 7), ("ctx", g - 1, 1)],
                    [("y", g - 1, 0), ("y", g - 1, 1)]][t]
            fill = [x for x in fill if 0 <= x[1] < NG]
            turn = [("turn", i, n) for n in range(NB)] if i < NTILES else []
            score = [("corr", i + 2, 0), ("score", i + 2, 0), ("less", i + 2, 0)] if i + 2 < NTILES else []
            order += turn[:1] + ([("norm", i + 1, 0)] if i + 1 < NTILES else []) + fill[:1] + turn[1:2]
            order += score + fill[1:2] + turn[2:3] + fill[2:] + turn[3:]
            if i + 2 < NTILES:
                order.append(("exp", i + 2, 0))
            order += {0: [("vblk", 0, 0)], 1: [("kblk", 1, 0)], 2: [("vblk", 1, 0)]}.get(i, [])
        uses = [x for x in order if x[0] in ("q", "y") or x[0] == "corr" and first(x[1])]
        use_no = {x: n for n, x in enumerate(uses)}
        by_act = {x: sum(y[0] == "y" for y in uses[:n + 1]) for x, n in use_no.items()}
        by_dve = {x: sum(y[0] != "y" for y in uses[:n + 1]) for x, n in use_no.items()}

        BLOCKS = {("kblk", 0): 1, ("vblk", 0): 2, ("kblk", 1): 3, ("vblk", 1): 4}

        def follow(do):
            for name, i, n in order:
                if name in do:
                    do[name](i, n)

        def cols(g, c):
            start = (g // GB) * SP1 + 1 + (g % GB) * G
            return X[:, c, start:start + G]
        with semaphores(nc, tag, "moved", "blocks", "qy", "t_dve", "t_act", "scores", "s_free", "less",
                        "exped", "prob", "turned", "copied", "mixed", "ctx", "added", "own") as (
                moved, blocks, qy_ready, dve_took, act_took, scores, s_free, less, exped, prob_ready,
                turned, copied, mixed, ctx_ready, added, dve_own), \
                nc.Block(no_gpsimd_drain=True) as block:

            if relative:
                @block.sync
                def _(sp):
                    for b in range(B):
                        sp.dma_start(vx[E:MA, b, :], rel_v[1:1 + R, :]).then_inc(moved, 16)
                    sp.wait_ge(moved, 16 * B)

            @block.tensor
            def _(pe):
                def wait_bank(use):
                    n = use_no[use]
                    if n and by_dve[uses[n - 1]]:
                        pe.wait_ge(dve_took, by_dve[uses[n - 1]])
                    if n and by_act[uses[n - 1]]:
                        pe.wait_ge(act_took, by_act[uses[n - 1]])

                def q(g, m):
                    wait_bank(("q", g, m))
                    for c in range(C):
                        last = nc.tensor.matmul(qy_ps[:, :], w["q"][:, c, m * P:(m + 1) * P],
                                                XN[:, c, g * G:(g + 1) * G], start=(c == 0), stop=(c == C - 1))
                    last.then_inc(qy_ready, 1)

                def corr_scores(i, _):
                    if not first(i):
                        return
                    g, t = divmod(i, TG)
                    wait_bank(("corr", i, 0))
                    for c in range(C):
                        last = nc.tensor.matmul(qy_ps[:, c * HC * R:(c + 1) * HC * R],
                                                q_sb[:, g % 2, c, t * P:(t + 1) * P],
                                                rblk[:, :, :].rearrange("p h r -> p (h r)"),
                                                start=True, stop=True)
                    last.then_inc(qy_ready, 1)

                def score(i, _):
                    g, t = divmod(i, TG)
                    if t == 0:
                        pe.wait_ge(dve_took, by_dve[("q", g, C - 1)])
                    if i % (GB * TG) == 0:
                        pe.wait_ge(blocks, BLOCKS[("kblk", g // GB)])
                    if i:
                        pe.wait_ge(s_free, i)
                    for k, off, h0, n in pieces:
                        c = h0 // HC
                        last = nc.tensor.matmul(
                            s_ps[:, k, off * E:(off + n) * E], q_sb[:, g % 2, c, t * P:(t + 1) * P],
                            kblk[:, g // GB, c, h0 - c * HC:h0 - c * HC + n, :].rearrange("p h e -> p (h e)"),
                            start=True, stop=True)
                    last.then_inc(scores, 1)

                def turn(i, n):
                    if n == 0:
                        pe.wait_ge(prob_ready, i + 1)
                    k = i * NB + n
                    if k >= 2:
                        pe.wait_ge(copied, k - 1)
                    for j in range(HB):
                        last = nc.tensor.transpose(pT_ps[0:MK, k % 2, j, :], prob[:, i % 2, n * HB + j, :],
                                                   K.ident[:, :])
                    last.then_inc(turned, 1)

                def mix(g, part):
                    c, first_j = part // 4, 2 * (part % 4)
                    if part == 0:
                        pe.wait_ge(copied, TG * NB * (g + 1))
                        if g % GB == 0:
                            pe.wait_ge(blocks, BLOCKS[("vblk", g // GB)])
                    if first_j == 0 and g:
                        pe.wait_ge(ctx_ready, C * (g - 1) + c + 1)
                    for j in (first_j, first_j + 1):
                        last = nc.tensor.matmul(o_ps[:, c], vblk[0:MK, g // GB, c * HC + j, :],
                                                pT[0:MK, g % 2, c * HC + j, :],
                                                start=(j == 0), stop=(j == HC - 1))
                    if j == HC - 1:
                        last.then_inc(mixed, 1)

                def y(g, m):
                    wait_bank(("y", g, m))
                    pe.wait_ge(ctx_ready, C * (g + 1))
                    for c in range(C):
                        last = nc.tensor.matmul(qy_ps[:, :], w["o"][:, c, m * P:(m + 1) * P], ctx_sb[:, c],
                                                start=(c == 0), stop=(c == C - 1))
                    last.then_inc(qy_ready, 1)
                follow({"q": q, "corr": corr_scores, "score": score, "turn": turn, "mix": mix, "y": y})

            @block.vector
            def _(dve):
                own = Own(dve, dve_own)
                tt = nc.vector.tensor_tensor

                def key_block(b, _):
                    for c in range(C):
                        last = tt(kblk[:, b, c], bc(kT[:, c, b * E:(b + 1) * E], 1, [P, HC, E]),
                                  bc(head_of[:, :], 2, [P, HC, E]), ALU.mult)
                    last.then_inc(blocks, 1)

                def value_block(b, _):
                    if relative:
                        dve.wait_ge(moved, 16 * B)
                    for c in range(C):
                        last = tt(vblk[0:MK, b, c * HC:(c + 1) * HC, :],
                                  bc(vx[0:MK, b, c * P:(c + 1) * P], 1, [MK, HC, P]),
                                  head_cols[0:MK, :, :], ALU.mult)
                    last.then_inc(blocks, 1)

                def take_q(g, m):
                    dve.wait_ge(qy_ready, use_no[("q", g, m)] + 1)
                    if g >= 2:
                        dve.wait_ge(scores, TG * (g - 1))
                    nc.vector.tensor_scalar(q_sb[:, g % 2, m], qy_ps[:, :], b_col["q"][:, m:m + 1],
                                            HD ** -0.5, ALU.add, ALU.mult).then_inc(dve_took, 1)

                def less_max(i, _):
                    e, st = ex[:, i % 2], stat[:, i % 2, 0, :]
                    if first(i):
                        dve.wait_ge(qy_ready, use_no[("corr", i, 0)] + 1)
                        nc.vector.tensor_copy(corr[:, :, :].rearrange("p h r -> p (h r)"),
                                              qy_ps[:, 0:NH * R]).then_inc(dve_took, 1)
                    dve.wait_ge(scores, i + 1)
                    if first(i):
                        for k, h0, n in banks:
                            last = nc.vector.tensor_copy(e[:, h0:h0 + n, :], sview(k, n))
                        last.then_inc(s_free, 1)
                        dve.wait_ge(dve_took, by_dve[("corr", i, 0)])
                        dve.wait_ge(s_free, i + 1)
                        for r in range(R):
                            own(tt(tmp[:, :, :], bc(rel_mask[:, r, :], 1, [P, NH, E]),
                                   corr[:, :, r:r + 1].to_broadcast([P, NH, E]), ALU.mult))
                            own(tt(e, e, tmp[:, :, :], ALU.add))
                        own(nc.vector.tensor_reduce(st, e, AX.X, ALU.max))
                        tt(e, e, bc(st, 2, [P, NH, E]), ALU.subtract).then_inc(less, 1)
                        return
                    for k, h0, n in banks:
                        last = nc.vector.tensor_reduce(st[:, h0:h0 + n], sview(k, n), AX.X, ALU.max)
                    own(last)
                    for k, h0, n in banks:
                        last = tt(e[:, h0:h0 + n, :], sview(k, n), bc(st[:, h0:h0 + n], 2, [P, n, E]),
                                  ALU.subtract)
                    last.then_inc(s_free, 1)
                    dve.wait_ge(s_free, i + 1)
                    nc.vector.nop().then_inc(less, 1)

                def normalise(i, _):
                    total, inverse = stat[:, i % 2, 1, :], stat[:, i % 2, 2, :]
                    dve.wait_ge(exped, i + 1)
                    own(nc.vector.tensor_reduce(total, ex[:, i % 2], AX.X, ALU.add))
                    own(nc.vector.reciprocal(inverse, total))
                    if i >= 2:
                        dve.wait_ge(turned, NB * (i - 1))
                    if relative and not first(i) and (i == 1 or first(i - 2)):
                        nc.vector.memset(prob[:, i % 2, :, E:MA], 0.0)
                    out = prob[:, i % 2, :, 0:E]
                    ins = tt(out, ex[:, i % 2], bc(inverse, 2, [P, NH, E]), ALU.mult)
                    if first(i):
                        own(ins)
                        for r in range(R):
                            own(tt(tmp[:, :, :], bc(rel_mask[:, r, :], 1, [P, NH, E]), out, ALU.mult))
                            ins = nc.vector.tensor_reduce(prob[:, i % 2, :, E + r:E + r + 1],
                                                          tmp[:, :, :], AX.X, ALU.add)
                            own(ins)
                        ins = nc.vector.nop()
                    ins.then_inc(prob_ready, 1)

                def add(g, m):
                    dve.wait_ge(act_took, by_act[("y", g, m)])
                    tt(cols(g, m), y_sb[:, m], cols(g, m), ALU.add).then_inc(added, 1)
                follow({"kblk": key_block, "vblk": value_block, "q": take_q, "less": less_max,
                        "norm": normalise, "y": add})

            @block.scalar
            def _(act):
                def exp(i, _):
                    act.wait_ge(less, i + 1)
                    nc.scalar.activation(ex[:, i % 2], ex[:, i % 2], ACT.Exp).then_inc(exped, 1)

                def copy(i, n):
                    k, g, t = i * NB + n, i // TG, i % TG
                    act.wait_ge(turned, k + 1)
                    if g >= 2:
                        act.wait_ge(mixed, C * (g - 1))
                    nc.scalar.activation(pT[0:MK, g % 2, n * HB:(n + 1) * HB, t * P:(t + 1) * P],
                                         pT_ps[0:MK, k % 2], ACT.Copy).then_inc(copied, 1)

                def context(g, c):
                    act.wait_ge(mixed, C * g + c + 1)
                    if g:
                        act.wait_ge(qy_ready, use_no[("y", g - 1, C - 1)] + 1)
                    nc.scalar.activation(ctx_sb[:, c], o_ps[:, c], ACT.Copy).then_inc(ctx_ready, 1)

                def take_y(g, m):
                    act.wait_ge(qy_ready, use_no[("y", g, m)] + 1)
                    if g:
                        act.wait_ge(added, C * (g - 1) + m + 1)
                    nc.scalar.activation(y_sb[:, m], qy_ps[:, :], ACT.Identity, bias=bo_gate[:, m:m + 1],
                                         scale=gate).then_inc(act_took, 1)
                follow({"exp": exp, "turn": copy, "ctx": context, "y": take_y})


FQ = 768
FQC = FQ // P
QB = 32
ACT_QMAX, ACT_QMIN = 32767.0, -32768.0
W_QMAX, W_QMIN = 7.0, -8.0
U16 = 65536.0
LEAST = 1e-12


def quantised_ffn(nc, K, X, XN, norm, W, gate, tag):
    with ExitStack() as s:
        sb = lambda n, sh: s.enter_context(nc.sbuf_tensor(f"{tag}_{n}", sh, F32))
        wT = [sb("guT", [P, 2, C, FQ]), sb("dT", [P, FQC, D])]
        peak = sb("peak", [P, 2, NG * FQC])
        peak_x = sb("peak_x", [P, 1])
        top = sb("top", [P, 4, 2])
        sc = sb("sc", [P, 12])
        SX, RX, SU, RU, SG, RG, SS, RS, SO, RO, SUS, SY = [sc[:, i:i + 1] for i in range(12)]

        with ExitStack() as s2:
            rows_of = (("g", FQC, D), ("u", FQC, D), ("d", C, FQ))
            t = lambda n, sh: s2.enter_context(nc.sbuf_tensor(f"{tag}_{n}", sh, F32))
            raw = [t(f"raw{n}", [P, k * m]) for n, k, m in rows_of]
            NBLK = FQC * D // QB
            wpeak = [t(f"wpeak{n}", [P, 2, NBLK]) for n, _, _ in rows_of]
            turns = []
            for n, (name, k, m) in enumerate(rows_of):
                for j in range(k):
                    for c in range(m // P):
                        dst = (wT[0][:, n, c, j * P:(j + 1) * P] if n < 2 else
                               wT[1][:, c, j * P:(j + 1) * P])
                        turns.append((n, slice(j * m + c * P, j * m + (c + 1) * P), dst))
            norm([(raw[n][:, :], W[f"w{name}"]) for n, (name, k, m) in enumerate(rows_of)])
            t_ps = s2.enter_context(nc.psum_tensor(f"{tag}_t_ps", [P, 4, TG, P], F32))
            with semaphores(nc, f"{tag}_w", "quant", "turned", "own", "copied") as (
                    quant, turned, dve_own, copied), nc.Block(no_gpsimd_drain=True) as block:
                @block.vector
                def _(dve):
                    own = Own(dve, dve_own)
                    for n in range(3):
                        blocks = raw[n][:, :].rearrange("p (k w) -> p k w", w=QB)
                        scale, inv = wpeak[n][:, 0, :], wpeak[n][:, 1, :]
                        full = [P, NBLK, QB]
                        own(nc.vector.tensor_reduce(scale, blocks, AX.X, ALU.max, apply_absolute_value=True))
                        own(nc.vector.tensor_scalar(scale, scale, 1.0 / W_QMAX, LEAST, ALU.mult, ALU.max))
                        own(nc.vector.reciprocal(inv, scale))
                        own(nc.vector.tensor_tensor(blocks, blocks, bc(inv, 2, full), ALU.mult))
                        own(nc.vector.tensor_scalar(raw[n][:, :], raw[n][:, :], MAGIC, MAGIC, ALU.add,
                                                    ALU.subtract))
                        own(nc.vector.tensor_scalar(raw[n][:, :], raw[n][:, :], W_QMAX, W_QMIN, ALU.min,
                                                    ALU.max))
                        nc.vector.tensor_tensor(blocks, blocks, bc(scale, 2, full), ALU.mult
                                                ).then_inc(quant, 1)

                @block.tensor
                def _(pe):
                    for i, (n, src, dst) in enumerate(turns):
                        pe.wait_ge(quant, n + 1)
                        if i % TG == 0 and i // TG >= 4:
                            pe.wait_ge(copied, i - 4 * TG + TG)
                        nc.tensor.transpose(t_ps[:, (i // TG) % 4, i % TG, :], raw[n][:, src],
                                            K.ident[:, :]).then_inc(turned, 1)

                @block.scalar
                def _(act):
                    for i, (n, src, dst) in enumerate(turns):
                        act.wait_ge(turned, min((i // TG + 1) * TG, len(turns)))
                        nc.scalar.activation(dst, t_ps[:, (i // TG) % 4, i % TG, :], ACT.Copy
                                             ).then_inc(copied, 1)

        UP = sb("up", [P, FQC, T])
        GATE = sb("gate", [P, FQC, T])
        sig = sb("sig", [P, 2, T])
        magic = sb("magic", [P, 1])

        def scale_of(dve, own, dst, inv, peak_ap, least=LEAST):
            own(nc.vector.tensor_scalar(dst, peak_ap, 1.0 / ACT_QMAX, least, ALU.mult, ALU.max))
            own(nc.vector.reciprocal(inv, dst))

        with semaphores(nc, f"{tag}_x", "peaked", "reduced", "own") as (peaked, reduced, dve_own), \
                nc.Block(no_gpsimd_drain=True) as block:
            @block.gpsimd
            def _(pool):
                pool.wait_ge(peaked, 1)
                nc.gpsimd.partition_all_reduce(top[:, 0, 0:1], peak_x[:, :], P, ABSMAX).then_inc(reduced, 1)

            @block.vector
            def _(dve):
                own = Own(dve, dve_own)
                nc.vector.memset(magic[:, :], MAGIC)
                x = XN[:, :, :].rearrange("p c t -> p (c t)")
                nc.vector.tensor_reduce(peak_x[:, :], x, AX.X, ALU.max,
                                        apply_absolute_value=True).then_inc(peaked, 1)
                dve.wait_ge(reduced, 1)
                scale_of(dve, own, SX, RX, top[:, 0, 0:1])
                own(nc.vector.tensor_scalar(x, x, RX, MAGIC, ALU.mult, ALU.add))
                nc.vector.tensor_scalar(x, x, MAGIC + ACT_QMAX, MAGIC, ALU.min, ALU.subtract)

        with ExitStack() as s2:
            gu_ps = s2.enter_context(nc.psum_tensor(f"{tag}_gu_ps", [P, 4, G], F32))
            with nc.Fori(0, NG) as g:
                with semaphores(nc, f"{tag}_gu", "ready", "scaled", "peaked") as (ready, scaled, peaked), \
                        nc.Block(no_gpsimd_drain=True) as block:
                    steps = [(u, i) for i in range(FQC) for u in range(2)]
                    dst = lambda u, i: (GATE, UP)[u][:, i, ds(g * G, G)]

                    @block.tensor
                    def _(pe):
                        for k, (u, i) in enumerate(steps):
                            if k >= 4:
                                pe.wait_ge(scaled, k - 3)
                            for c in range(C):
                                last = nc.tensor.matmul(gu_ps[:, k % 4], wT[0][:, u, c, i * P:(i + 1) * P],
                                                        XN[:, c, ds(g * G, G)], start=(c == 0),
                                                        stop=(c == C - 1))
                            last.then_inc(ready, 1)

                    @block.scalar
                    def _(act):
                        for k, (u, i) in enumerate(steps):
                            act.wait_ge(ready, k + 1)
                            nc.scalar.activation(dst(u, i), gu_ps[:, k % 4], ACT.Copy, scale=SX
                                                 ).then_inc(scaled, 1)

                    @block.vector
                    def _(dve):
                        for k, (u, i) in enumerate(steps):
                            dve.wait_ge(scaled, k + 1)
                            nc.vector.tensor_reduce(peak[:, 1 - u, ds(g * FQC + i, 1)], dst(u, i), AX.X,
                                                    ALU.max, apply_absolute_value=True)

        with semaphores(nc, f"{tag}_s", "peaked", "reduced", "own") as (peaked, reduced, dve_own), \
                nc.Block(no_gpsimd_drain=True) as block:
            @block.gpsimd
            def _(pool):
                pool.wait_ge(peaked, 1)
                nc.gpsimd.partition_all_reduce(top[:, 1, :], peak[:, :, 0], P, ABSMAX).then_inc(reduced, 1)

            @block.vector
            def _(dve):
                own = Own(dve, dve_own)
                own(nc.vector.tensor_reduce(sc[:, 0:2], peak[:, :, :], AX.X, ALU.max))
                nc.vector.tensor_copy(peak[:, :, 0], sc[:, 0:2]).then_inc(peaked, 1)
                dve.wait_ge(reduced, 1)
                scale_of(dve, own, SU, RU, top[:, 1, 0:1])
                scale_of(dve, own, SG, RG, top[:, 1, 1:2])

        def round_by(src, factor, dst=None):
            return nc.scalar.activation(src if dst is None else dst, src, ACT.Identity, bias=magic[:, 0:1],
                                        scale=factor)

        def take_magic(v):
            return nc.vector.tensor_scalar(v, v, MAGIC + ACT_QMAX, MAGIC, ALU.min, ALU.subtract)

        y_ps = s.enter_context(nc.psum_tensor(f"{tag}_y_ps", [P, NG, C, G], F32))
        with semaphores(nc, f"{tag}_e", "gate_r", "gate_n", "sig", "up_r", "gated", "peak_s", "top_s",
                        "scale_s", "s_r", "peak_o", "top_o", "scale_o", "o_r", "o_n", "ready", "own") as (
                gate_round, gate_ready, sig_ready, up_round, gated, gated_peak, gated_top, gated_scale,
                gated_round, product_peak, product_top, product_scale, product_round, numbers, ready,
                dve_own), nc.Block(no_gpsimd_drain=True) as block:

            @block.gpsimd
            def _(pool):
                pool.wait_ge(gated_peak, 1)
                nc.gpsimd.partition_all_reduce(top[:, 2, 0:1], peak[:, 0, 2:3], P, ABSMAX
                                               ).then_inc(gated_top, 1)
                pool.wait_ge(product_peak, 1)
                nc.gpsimd.partition_all_reduce(top[:, 3, 0:1], peak[:, 0, 3:4], P, ABSMAX
                                               ).then_inc(product_top, 1)

            @block.scalar
            def _(act):
                def gate_numbers(i):
                    round_by(GATE[:, i, :], RG).then_inc(gate_round, 1)

                def sigmoid(i):
                    v = sig[:, i % 2]
                    act.wait_ge(gate_ready, i + 1)
                    if i >= 2:
                        act.wait_ge(gated, i - 1)
                    nc.scalar.activation(v, GATE[:, i, :], ACT.Sigmoid, scale=SG).then_inc(sig_ready, 1)
                    act.wait_ge(sig_ready, 2 * i + 1)
                    round_by(v, U16).then_inc(sig_ready, 1)
                gate_numbers(0)
                gate_numbers(1)
                for i in range(FQC):
                    sigmoid(i)
                    if i + 2 < FQC:
                        gate_numbers(i + 2)
                    round_by(UP[:, i, :], RU).then_inc(up_round, 1)
                act.wait_ge(gated_scale, 1)
                for i in range(FQC):
                    round_by(GATE[:, i, :], RS).then_inc(gated_round, 1)
                act.wait_ge(product_scale, 1)
                for g in range(NG):
                    for i in range(FQC):
                        round_by(GATE[:, i, g * G:(g + 1) * G], RO).then_inc(product_round, 1)

            @block.vector
            def _(dve):
                own = Own(dve, dve_own)
                ts = nc.vector.tensor_scalar

                def gate_numbers(i):
                    dve.wait_ge(gate_round, i + 1)
                    take_magic(GATE[:, i, :]).then_inc(gate_ready, 1)

                def times_sigmoid(i):
                    v = sig[:, i % 2]
                    dve.wait_ge(sig_ready, 2 * i + 2)
                    own(ts(v, v, MAGIC + U16 - 1, MAGIC, ALU.min, ALU.max))
                    own(nc.vector.scalar_tensor_tensor(out=GATE[:, i, :], in0=v, scalar=MAGIC,
                                                       in1=GATE[:, i, :], op0=ALU.subtract, op1=ALU.mult))
                    nc.vector.tensor_reduce(peak[:, 1, 1 + i:2 + i], GATE[:, i, :], AX.X, ALU.max,
                                            apply_absolute_value=True).then_inc(gated, 1)
                gate_numbers(0)
                for i in range(FQC):
                    if i + 1 < FQC:
                        gate_numbers(i + 1)
                    times_sigmoid(i)
                dve.wait_ge(gated, FQC)
                nc.vector.tensor_reduce(peak[:, 0, 2:3], peak[:, 1, 1:1 + FQC], AX.X, ALU.max
                                        ).then_inc(gated_peak, 1)
                dve.wait_ge(gated_top, 1)
                own(ts(SUS, SG, 1.0 / U16, None, ALU.mult))
                own(ts(SS, top[:, 2, 0:1], SUS, None, ALU.mult))
                scale_of(dve, own, SS, RS, SS)
                ts(RS, RS, SUS, None, ALU.mult).then_inc(gated_scale, 1)
                for i in range(FQC):
                    v = GATE[:, i, :]
                    dve.wait_ge(gated_round, i + 1)
                    dve.wait_ge(up_round, i + 1)
                    own(take_magic(v))
                    own(nc.vector.scalar_tensor_tensor(out=v, in0=UP[:, i, :], scalar=MAGIC, in1=v,
                                                       op0=ALU.subtract, op1=ALU.mult))
                    own(nc.vector.tensor_reduce(peak[:, 1, 1 + i:2 + i], v, AX.X, ALU.max,
                                                apply_absolute_value=True))
                nc.vector.tensor_reduce(peak[:, 0, 3:4], peak[:, 1, 1:1 + FQC], AX.X, ALU.max
                                        ).then_inc(product_peak, 1)
                own(ts(SUS, SS, SU, None, ALU.mult))
                dve.wait_ge(product_top, 1)
                own(ts(RO, top[:, 3, 0:1], SUS, None, ALU.mult))
                scale_of(dve, own, SO, RO, RO)
                ts(RO, RO, SUS, None, ALU.mult).then_inc(product_scale, 1)
                own(ts(SY, SO, gate, None, ALU.mult))

                def add(g):
                    for m in range(C):
                        first = (g // GB) * SP1 + 1 + (g % GB) * G
                        view = X[:, m, first:first + G]
                        dve.wait_ge(ready, C * g + m + 1)
                        nc.vector.scalar_tensor_tensor(out=view, in0=y_ps[:, g, m], scalar=SY, in1=view,
                                                       op0=ALU.mult, op1=ALU.add)
                for g in range(NG):
                    for i in range(FQC):
                        dve.wait_ge(product_round, FQC * g + i + 1)
                        take_magic(GATE[:, i, g * G:(g + 1) * G]).then_inc(numbers, 1)
                for g in range(NG):
                    add(g)

            @block.tensor
            def _(pe):
                for g in range(NG):
                    for m in range(C):
                        for i in range(FQC):
                            pe.wait_ge(numbers, FQC * g + i + 1)
                            last = nc.tensor.matmul(y_ps[:, g, m], wT[1][:, i, m * P:(m + 1) * P],
                                                    GATE[:, i, g * G:(g + 1) * G],
                                                    start=(i == 0), stop=(i == FQC - 1))
                        last.then_inc(ready, 1)


FB = 1024
FBC = FB // P
SPAD = S + 2


def bit_ffn(nc, K, X, XN, norm, W, gate, tag):
    with ExitStack() as s:
        sb = lambda n, sh, dt=F32: s.enter_context(nc.sbuf_tensor(f"{tag}_{n}", sh, dt))
        w_int = [sb("w1i", [P, C * FB], BF16), sb("w2i", [P, FBC * D], BF16)]
        wstat = sb("wstat", [P, 2, 4])
        sy = sb("sy", [P, 1])
        conv = sb("conv", [P, FBC, 3])
        conv_b = sb("conv_b", [P, FBC])
        with ExitStack() as s2:
            raw = [s2.enter_context(nc.sbuf_tensor(f"{tag}_raw{n}", [P, C * FB], F32)) for n in range(2)]
            norm([(raw[0][:, :], W["w1"]), (raw[1][:, :], W["w2"]), (conv[:, :, :], W["conv_w"]),
                  (conv_b[:, :], W["conv_b"])])
            with semaphores(nc, f"{tag}_w", "summed", "reduced", "own") as (summed, reduced, dve_own), \
                    nc.Block(no_gpsimd_drain=True) as block:
                @block.gpsimd
                def _(pool):
                    for n in range(2):
                        pool.wait_ge(summed, n + 1)
                        nc.gpsimd.partition_all_reduce(wstat[:, n, 1:2], wstat[:, n, 0:1], P, RADD
                                                       ).then_inc(reduced, 1)

                @block.vector
                def _(dve):
                    own = Own(dve, dve_own)
                    ts = nc.vector.tensor_scalar
                    for n in range(2):
                        nc.vector.tensor_reduce(wstat[:, n, 0:1], raw[n][:, :], AX.X, ALU.add,
                                                apply_absolute_value=True).then_inc(summed, 1)
                    for n in range(2):
                        dve.wait_ge(reduced, n + 1)
                        own(ts(wstat[:, n, 2:3], wstat[:, n, 1:2], 1.0 / (FB * D), EPS, ALU.mult, ALU.max))
                        own(nc.vector.reciprocal(wstat[:, n, 3:4], wstat[:, n, 2:3]))
                        own(ts(raw[n][:, :], raw[n][:, :], wstat[:, n, 3:4], MAGIC, ALU.mult, ALU.add))
                        own(ts(raw[n][:, :], raw[n][:, :], MAGIC, 1.0, ALU.subtract, ALU.min))
                        own(ts(w_int[n][:, :], raw[n][:, :], -1.0, None, ALU.max))
                    ts(sy[:, :], wstat[:, 1, 2:3], gate, None, ALU.mult)

        H = sb("h", [P, FBC, B * SPAD])
        with nc.Block(no_gpsimd_drain=True) as block:
            @block.vector
            def _(dve):
                for b in range(B):
                    for side in (0, SPAD - 1):
                        nc.vector.memset(H[:, :, b * SPAD + side:b * SPAD + side + 1], 0.0)
        minus_magic = sb("minus_magic", [P, 1])
        peak = sb("peak", [P, 2, G])
        top = sb("top", [P, 2, G])
        scale = sb("scale", [P, 2, G])
        back = sb("back", [P, 2, G])

        def token_scales(own, g):
            t, sc = top[:, g % 2], scale[:, g % 2]
            own(nc.vector.tensor_scalar(t, t, EPS, None, ALU.max))
            own(nc.vector.reciprocal(sc, t))
            nc.vector.tensor_scalar(back[:, g % 2], t, 1.0 / 127.0, None, ALU.mult)
            own(nc.vector.tensor_scalar(sc, sc, 127.0, None, ALU.mult))

        def whole_numbers(own, dst, src, tmp, g):
            own(nc.vector.tensor_tensor(tmp, src, scale[:, g % 2], ALU.mult))
            own(nc.vector.tensor_scalar(tmp, tmp, MAGIC, MAGIC, ALU.add, ALU.subtract))
            return nc.vector.tensor_scalar(dst, tmp, 127.0, -128.0, ALU.min, ALU.max)

        def hidden(i, g, shift=1):
            first = (g // GB) * SPAD + (g % GB) * G + shift
            return H[:, i, first:first + G]

        with ExitStack() as s2:
            x_int = s2.enter_context(nc.sbuf_tensor(f"{tag}_x_int", [P, 2, C, G], BF16))
            size = s2.enter_context(nc.sbuf_tensor(f"{tag}_xsize", [P, 2, C, G], F32))
            tmp = s2.enter_context(nc.sbuf_tensor(f"{tag}_tmp", [P, C, G], F32))
            h_ps = s2.enter_context(nc.psum_tensor(f"{tag}_h_ps", [P, 4, G], F32))
            xn = lambda c, g: XN[:, c, g * G:(g + 1) * G]
            with semaphores(nc, f"{tag}_1", "sizes", "peaked", "reduced", "x", "h", "taken", "own") as (
                    sizes, peaked, reduced, x_ready, h_ready, taken, dve_own), \
                    nc.Block(no_gpsimd_drain=True) as block:
                @block.scalar
                def _(act):
                    for g in range(NG):
                        if g >= 2:
                            act.wait_ge(peaked, g - 1)
                        nc.scalar.activation(size[:, g % 2], XN[:, :, g * G:(g + 1) * G], ACT.Abs
                                             ).then_inc(sizes, 1)

                @block.gpsimd
                def _(pool):
                    for g in range(NG):
                        pool.wait_ge(peaked, g + 1)
                        if g >= 2:
                            pool.wait_ge(x_ready, C * (g - 1))
                        nc.gpsimd.partition_all_reduce(top[:, g % 2], peak[:, g % 2], P, ABSMAX
                                                       ).then_inc(reduced, 1)

                @block.vector
                def _(dve):
                    own = Own(dve, dve_own)
                    nc.vector.memset(minus_magic[:, :], -MAGIC)

                    def find_peak(g):
                        dve.wait_ge(sizes, g + 1)
                        if g >= 2:
                            dve.wait_ge(reduced, g - 1)
                        nc.vector.tensor_tensor(peak[:, g % 2], size[:, g % 2, 0], size[:, g % 2, 1], ALU.max
                                                ).then_inc(peaked, 1)

                    def take(g):
                        for i in range(FBC):
                            dve.wait_ge(h_ready, FBC * g + i + 1)
                            nc.vector.scalar_tensor_tensor(out=hidden(i, g), in0=h_ps[:, i % 4],
                                                           scalar=wstat[:, 0, 2:3], in1=back[:, g % 2],
                                                           op0=ALU.mult, op1=ALU.mult).then_inc(taken, 1)
                    find_peak(0)
                    find_peak(1)
                    for g in range(NG):
                        dve.wait_ge(reduced, g + 1)
                        token_scales(own, g)
                        if g >= 2:
                            dve.wait_ge(h_ready, FBC * (g - 1))
                        for c in range(C):
                            whole_numbers(own, x_int[:, g % 2, c], xn(c, g), tmp[:, c], g
                                          ).then_inc(x_ready, 1)
                        if g + 2 < NG:
                            find_peak(g + 2)
                        if g:
                            take(g - 1)
                    take(NG - 1)

                @block.tensor
                def _(pe):
                    for g in range(NG):
                        pe.wait_ge(x_ready, C * (g + 1))
                        for i in range(FBC):
                            if FBC * g + i >= 4:
                                pe.wait_ge(taken, FBC * g + i - 3)
                            for c in range(C):
                                last = nc.tensor.matmul(h_ps[:, i % 4],
                                                        w_int[0][:, c * FB + i * P:c * FB + (i + 1) * P],
                                                        x_int[:, g % 2, c], start=(c == 0), stop=(c == C - 1))
                            last.then_inc(h_ready, 1)

        with ExitStack() as s2:
            act_sb = s2.enter_context(nc.sbuf_tensor(f"{tag}_act", [P, 2, FBC, G], F32))
            a_int = s2.enter_context(nc.sbuf_tensor(f"{tag}_a_int", [P, 2, FBC, G], BF16))
            y_sb = s2.enter_context(nc.sbuf_tensor(f"{tag}_y", [P, C, G], F32))
            y_ps = s2.enter_context(nc.psum_tensor(f"{tag}_y_ps", [P, 2, C, G], F32))
            with semaphores(nc, f"{tag}_2", "centre", "conv", "silu", "peaked", "reduced", "rounded", "a",
                            "y", "y_taken", "own") as (
                    centre_ready, conv_ready, silu, peaked, reduced, rounded, a_ready, y_ready, y_taken,
                    dve_own), nc.Block(no_gpsimd_drain=True) as block:
                @block.vector
                def _(dve):
                    own = Own(dve, dve_own)

                    def convolve(g):
                        for i in range(FBC):
                            v = act_sb[:, g % 2, i]
                            dve.wait_ge(centre_ready, FBC * g + i + 1)
                            own(nc.vector.scalar_tensor_tensor(out=v, in0=hidden(i, g, 0),
                                                               scalar=conv[:, i, 0:1], in1=v, op0=ALU.mult,
                                                               op1=ALU.add))
                            nc.vector.scalar_tensor_tensor(out=v, in0=hidden(i, g, 2),
                                                           scalar=conv[:, i, 2:3], in1=v, op0=ALU.mult,
                                                           op1=ALU.add).then_inc(conv_ready, 1)

                    def find_peak(g):
                        dve.wait_ge(silu, FBC * (g + 1))
                        if g >= 2:
                            dve.wait_ge(reduced, g - 1)
                        nc.vector.tensor_reduce(peak[:, g % 2], act_sb[:, g % 2].rearrange("p i t -> p t i"),
                                                AX.X, ALU.max, apply_absolute_value=True).then_inc(peaked, 1)

                    def quantise(g):
                        dve.wait_ge(reduced, g + 1)
                        token_scales(own, g)
                        for i in range(FBC):
                            v = act_sb[:, g % 2, i]
                            own(nc.vector.tensor_tensor(v, v, scale[:, g % 2], ALU.mult))
                            nc.vector.tensor_scalar(v, v, MAGIC, MAGIC + 127.0, ALU.add, ALU.min
                                                    ).then_inc(rounded, 1)

                    def add(g):
                        for m in range(C):
                            dve.wait_ge(y_ready, C * g + m + 1)
                            own(nc.vector.scalar_tensor_tensor(out=y_sb[:, m], in0=y_ps[:, g % 2, m],
                                                               scalar=sy[:, :], in1=back[:, g % 2],
                                                               op0=ALU.mult, op1=ALU.mult))
                            first = (g // GB) * SP1 + 1 + (g % GB) * G
                            view = X[:, m, first:first + G]
                            nc.vector.tensor_tensor(view, view, y_sb[:, m], ALU.add).then_inc(y_taken, 1)
                    convolve(0)
                    for g in range(NG):
                        find_peak(g)
                        if g + 1 < NG:
                            convolve(g + 1)
                        quantise(g)
                        if g:
                            add(g - 1)
                    add(NG - 1)

                @block.scalar
                def _(act):
                    def centre(k):
                        g, i = divmod(k, FBC)
                        if g >= 2:
                            act.wait_ge(a_ready, k - 2 * FBC + 1)
                        nc.scalar.activation(act_sb[:, g % 2, i], hidden(i, g), ACT.Identity,
                                             bias=conv_b[:, i:i + 1], scale=conv[:, i, 1:2]
                                             ).then_inc(centre_ready, 1)

                    def apply_silu(k):
                        g, i = divmod(k, FBC)
                        v = act_sb[:, g % 2, i]
                        act.wait_ge(conv_ready, k + 1)
                        nc.scalar.activation(v, v, ACT.Silu).then_inc(silu, 1)

                    def less_magic(g):
                        if g >= 2:
                            act.wait_ge(y_ready, C * (g - 1))
                        for i in range(FBC):
                            act.wait_ge(rounded, FBC * g + i + 1)
                            nc.scalar.activation(a_int[:, g % 2, i], act_sb[:, g % 2, i], ACT.Identity,
                                                 bias=minus_magic[:, 0:1]).then_inc(a_ready, 1)
                            if g + 2 < NG:
                                centre(FBC * (g + 2) + i)
                    for k in range(FBC):
                        centre(k)
                    for g in range(NG + 1):
                        if g < NG:
                            for i in range(FBC):
                                if g == 0:
                                    centre(FBC + i)
                                apply_silu(FBC * g + i)
                        if g:
                            less_magic(g - 1)

                @block.gpsimd
                def _(pool):
                    for g in range(NG):
                        pool.wait_ge(peaked, g + 1)
                        if g >= 2:
                            pool.wait_ge(rounded, FBC * (g - 1))
                        nc.gpsimd.partition_all_reduce(top[:, g % 2], peak[:, g % 2], P, ABSMAX
                                                       ).then_inc(reduced, 1)

                @block.tensor
                def _(pe):
                    for g in range(NG):
                        if g >= 2:
                            pe.wait_ge(y_taken, C * (g - 1))
                        for m in range(C):
                            for i in range(FBC):
                                if m == 0:
                                    pe.wait_ge(a_ready, FBC * g + i + 1)
                                last = nc.tensor.matmul(y_ps[:, g % 2, m],
                                                        w_int[1][:, i * D + m * P:i * D + (m + 1) * P],
                                                        a_int[:, g % 2, i], start=(i == 0), stop=(i == FBC - 1))
                            last.then_inc(y_ready, 1)


DEPTH, LH, LD = 6, 16, 64
INNER = LH * LD
WIN = 64
KEYS = WIN + P
NT = S // P
PAIRS = LH // 2
QK_SCALE = 8.0
MASKED = -1e30
FI = 682
FIC = -(-FI // P)
FIP = FIC * P
WQKV, WO = C * 3 * INNER, PAIRS * D
W1, W2 = C * 2 * FIP, FIC * D
PIECE = (2, 4, 3, 5, 0, 1)
ROTATED = (0, 2, 4, 5)
VALUES = (1, 3)
HILO = ((0, 0), (0, 1), (1, 0))


class LayerBuffers:

    def __init__(self, sb):
        self.wa = [sb(f"wa{n}", [P, WQKV + WO], F32R) for n in range(2)]
        self.wf = [sb(f"wf{n}", [P, W1 + W2], F32R) for n in range(2)]
        self.tabs = sb("tabs", [P, 4, NT, LD])
        self.qk = sb("qk", [P, 4, LD])
        self.mask = sb("mask", [P, KEYS])
        self.vec = sb("vec", [P, 2 * C + 2 * FIC + C])

    def wq(self, n, c, first, width):
        return self.wa[n][:, c * 3 * INNER + first:c * 3 * INNER + first + width]

    def wo(self, n, i, first):
        return self.wa[n][:, WQKV + i * D + first:WQKV + i * D + first + P]

    def w1(self, n, c, first):
        return self.wf[n][:, c * 2 * FIP + first:c * 2 * FIP + first + P]

    def w2(self, n, i, first):
        return self.wf[n][:, W1 + i * D + first:W1 + i * D + first + P]


def layer_rows(a, layer, lo=0, n=None):
    n = a.shape[2] if n is None else n
    return a[ds(layer, 1), :, lo:lo + n].rearrange("o p n -> p (o n)")


PIECE_COLS = 512
NWA, NWF = (WQKV + WO) // PIECE_COLS, (W1 + W2) // PIECE_COLS


def fetch_tables(sp, W, A, layer, tabled):
    sp.dma_start(W.tabs[:, :, :, :], A["rotary"]).then_inc(tabled, 16)
    sp.dma_start(W.qk[:, :, :], A["l_qk_scale"][ds(layer, 1)].rearrange("o p a d -> p (o a) d")
                 ).then_inc(tabled, 16)


def fetch_pieces(sp, ring, slots, matrices, layer, loaded, split):
    pieces = [(a, lo) for a in matrices for lo in range(0, a.shape[2], PIECE_COLS)]
    for n, (a, lo) in enumerate(pieces):
        if n >= slots:
            sp.wait_ge(split, n - slots + 1)
        if n:
            sp.wait_ge(loaded, 16 * n)
        sp.dma_start(ring[:, n % slots], layer_rows(a, layer, lo, PIECE_COLS)).then_inc(loaded, 16)
    sp.wait_ge(loaded, 16 * len(pieces))


def scale_tables(nc, pool, W, tabled, scaled):
    pool.wait_ge(tabled, 32)
    for n in range(4):
        nc.gpsimd.tensor_tensor(W.tabs[:, n], W.tabs[:, n], bc(W.qk[:, n, :], 1, [P, NT, LD]),
                                ALU.mult).then_inc(scaled, 1)
    pool.wait_ge(scaled, 4)


def take_high(nc, w, n, raw):
    return nc.scalar.activation(w[0][:, n * PIECE_COLS:(n + 1) * PIECE_COLS], raw, ACT.Copy)


def take_low(nc, w, n, raw):
    part = slice(n * PIECE_COLS, (n + 1) * PIECE_COLS)
    return nc.vector.tensor_tensor(w[1][:, part], raw, w[0][:, part].bitcast(F32), ALU.subtract)


def transformer(nc, K, Z, A):
    with ExitStack() as s:
        W = LayerBuffers(lambda n, sh, dt=F32: s.enter_context(nc.sbuf_tensor(f"layer_{n}", sh, dt)))
        with nc.sbuf_tensor("first_raw", [P, NWA, PIECE_COLS], F32) as raw, \
                semaphores(nc, "first", "tabled", "mask", "loaded", "high", "low", "scaled") as (
                    tabled, masked, loaded, high, low, scaled), nc.Block(no_gpsimd_drain=True) as block:
            @block.sync
            def _(sp):
                sp.dma_start(W.mask[:, :], A["band_mask"]).then_inc(masked, 16)
                fetch_tables(sp, W, A, 0, tabled)
                third = WQKV // 3
                for n in range(4):
                    if n:
                        sp.wait_ge(loaded, 16 * n)
                    src = layer_rows(A["l_wqkv"], 0, n * third, third) if n < 3 else layer_rows(A["l_wo"], 0)
                    sp.dma_start(raw[:, 4 * n:4 * n + 4].rearrange("p a n -> p (a n)"), src
                                 ).then_inc(loaded, 16)
                sp.wait_ge(masked, 16)

            @block.gpsimd
            def _(pool):
                scale_tables(nc, pool, W, tabled, scaled)

            @block.scalar
            def _(act):
                for n in range(NWA):
                    act.wait_ge(loaded, 16 * (n // 4 + 1))
                    take_high(nc, W.wa, n, raw[:, n]).then_inc(high, 1)

            @block.vector
            def _(dve):
                for n in range(NWA):
                    dve.wait_ge(high, n + 1)
                    take_low(nc, W.wa, n, raw[:, n])
        with nc.Fori(0, DEPTH) as layer:
            local_attention(nc, K, Z, A, W, layer, "la")
            layer_ffn(nc, K, Z, A, W, layer, "lf")


def local_attention(nc, K, Z, A, W, layer, tag):
    NA = B * NT
    FIRST_W = 2
    with ExitStack() as s:
        sb = lambda n, sh, dt=F32: s.enter_context(nc.sbuf_tensor(f"{tag}_{n}", sh, dt))
        xs = [sb(f"xs{n}", [P, 2, C, P], F32R) for n in range(2)]
        sq = sb("sq", [P, 2, 512])
        rb = sb("rb", [P, 2, 512])
        rot = sb("rot", [P, 2, INNER])
        ssq = sb("ssq", [P, 2, 2 * LH])
        rn = sb("rn", [P, 2, LH])
        minus_half = sb("minus_half", [P, 2 * LH])
        sc8 = sb("sc8", [P, 2, LH])
        qT = sb("qT", [P, PAIRS, P])
        kT = sb("kT", [P, PAIRS, KEYS])
        vt = sb("vt", [P, 3, INNER])
        pr = sb("pr", [P, 2, WIN + 4 * KEYS])
        mx = sb("mx", [P, 2, LH])
        nb = sb("nb", [P, 2, LH])
        sums = sb("sums", [P, 2, LH])
        rs = sb("rs", [P, 2, LH])
        pTa = sb("pTa", [P, 2, 4, P])
        pTb = sb("pTb", [P, 2, 4, P])
        raw = sb("raw", [P, 1, PIECE_COLS])
        oT = [sb(f"oT{n}", [P, PAIRS, 2 * P], F32R) for n in range(2)]
        ps = lambda n, sh: s.enter_context(nc.psum_tensor(f"{tag}_{n}", sh, F32))
        proj_ps, s_ps = ps("proj_ps", [P, 2, 512]), ps("s_ps", [P, 2, 512])
        pTa_ps, pTb_ps = ps("pTa_ps", [P, 4, P]), ps("pTb_ps", [P, 4, P])
        o_ps, t_ps = ps("o_ps", [P, 4, P]), ps("t_ps", [P, 4, P])

        def pcols(n, i, lo, hi=KEYS):
            return pr[:, n % 2, WIN + i * KEYS + lo:WIN + i * KEYS + hi]

        def steps(t):
            p, n = t - 1, t + 1
            y = p % 2 == 1
            seq = [("S", t, 0), ("norm", p, 3), ("less", t, 0), ("PV", p, 2), ("TQ", t, 1), ("tq", t, 1),
                   ("xh", n + 1, 0), ("J", n, 0), ("exp", t, 0), ("sq", n, 0), ("xl", n + 1, 0), ("PT", p, 3),
                   ("copy", p, 3), ("exp", t, 1), ("rot", n, 0), ("J", n, 1), ("v", n, 0), ("S", t, 1),
                   ("norm", t, 0), ("less", t, 1), ("PV", p, 3), ("out", p, 1), ("J", n, 2), ("exp", t, 2),
                   ("sq", n, 1), ("low", p, 1), ("PT", t, 0), ("copy", t, 0), ("exp", t, 3), ("S", t, 2),
                   ("rot", n, 1), ("J", n, 3), ("v", n, 1), ("norm", t, 1), ("halo", n, 0), ("less", t, 2),
                   ("PV", t, 0), ("TK", n, 0), ("tk", n, 0), ("J", n, 4), ("exp", t, 4), ("sq", n, 2),
                   ("PT", t, 1), ("copy", t, 1), ("exp", t, 5), ("rot", n, 2)]
            seq += [("Y", p, 0)] * y + [("S", t, 3), ("norm", t, 2)] + [("yadd", p, 0)] * y
            seq += [("less", t, 3)] + [("Y", p, 1)] * y
            seq += [("PV", t, 1), ("out", t, 0), ("halo", n, 1)] + [("yadd", p, 1)] * y
            seq += [("TK", n, 1), ("tk", n, 1), ("J", n, 5), ("exp", t, 6), ("low", t, 0), ("TQ", n, 0),
                    ("sq", n, 3), ("tq", n, 0), ("PT", t, 2), ("copy", t, 2), ("exp", t, 7), ("rot", n, 3)]
            if FIRST_W <= t < FIRST_W + NWF:
                seq += [("wh", t, 0), ("wl", t, 0)]
            return seq
        z, p = NA - 1, NA - 2
        last_steps = [
            ("S", z, 0), ("PV", p, 2), ("TQ", z, 1), ("norm", p, 3), ("less", z, 0), ("tq", z, 1), ("PT", p, 3),
            ("copy", p, 3), ("exp", z, 0), ("exp", z, 1), ("S", z, 1), ("PV", p, 3), ("norm", z, 0),
            ("less", z, 1), ("out", p, 1), ("low", p, 1), ("PT", z, 0), ("copy", z, 0), ("exp", z, 2),
            ("exp", z, 3), ("S", z, 2), ("PV", z, 0), ("norm", z, 1), ("less", z, 2), ("PT", z, 1),
            ("copy", z, 1), ("exp", z, 4), ("exp", z, 5), ("S", z, 3), ("PV", z, 1), ("norm", z, 2),
            ("less", z, 3), ("out", z, 0), ("low", z, 0), ("PT", z, 2), ("copy", z, 2), ("exp", z, 6),
            ("exp", z, 7), ("PV", z, 2), ("norm", z, 3), ("PT", z, 3), ("copy", z, 3), ("PV", z, 3),
            ("out", z, 1), ("low", z, 1), ("Y", z, 0), ("yadd", z, 0), ("Y", z, 1), ("yadd", z, 1)]
        order = [x for t in range(-1, z) for x in steps(t) if 0 <= x[1] < NA] + last_steps
        turns = [x for x in order if x[0] in ("TQ", "TK", "Y")]
        turn_no = {x: n for n, x in enumerate(turns)}
        by_act = {x: sum(y[0] != "Y" for y in turns[:n + 1]) for x, n in turn_no.items()}
        by_dve = {x: sum(y[0] == "Y" for y in turns[:n + 1]) for x, n in turn_no.items()}

        def follow(do):
            for name, t, i in order:
                if name in do:
                    do[name](t, i)

        def ztok(c, t, n, shift=0):
            first = (t // NT) * SP1 + (t % NT) * P + 1 - shift
            return Z[:, c, first:first + n]
        with semaphores(nc, tag, "xh", "xl", "proj", "sq", "rot", "v", "ssq", "norm", "pow", "rsum",
                        "kmul", "scores", "less", "exped", "turned", "copied", "pv", "out", "turn",
                        "t_act", "t_dve", "pnorm", "out_high", "set", "own", "loaded", "vec", "high", "low", "halo") as (
                xh_ok, xl_ok, proj_ok, sq_ok, rot_ok, v_ok, ssq_ok, norm_ok, pow_ok, sum_ok,
                kmul_ok, scores_ok, less_ok, exp_ok, turned_ok, copy_ok, pv_ok, out_ok, turn_ok,
                act_took, dve_took, norm_p, high_ok, set_ok, dve_own, loaded, vec_ok, high, low, halo_ok), \
                nc.Block(no_gpsimd_drain=True) as block:

            def wait_turn_bank(eng, use):
                n = turn_no[use]
                if n:
                    prev = turns[n - 1]
                    if by_act[prev]:
                        eng.wait_ge(act_took, by_act[prev])
                    if by_dve[prev]:
                        eng.wait_ge(dve_took, by_dve[prev])

            @block.sync
            def _(sp):
                sp.dma_start(W.vec[:, :], layer_rows(A["l_vec"], layer)).then_inc(vec_ok, 16)
                fetch_pieces(sp, raw, 1, (A["l_w1"], A["l_w2"]), layer, loaded, low)
                sp.wait_ge(vec_ok, 16)

            @block.tensor
            def _(pe):
                def J(t, j):
                    n = 6 * t + j
                    if j == 0:
                        pe.wait_ge(xl_ok, t + 1)
                    if n >= 2:
                        u, i = divmod(n - 2, 6)
                        if i in ROTATED:
                            pe.wait_ge(sq_ok, 4 * u + ROTATED.index(i) + 1)
                            pe.wait_ge(rot_ok, 4 * u + ROTATED.index(i) + 1)
                        else:
                            pe.wait_ge(v_ok, 2 * u + VALUES.index(i) + 1)
                    first = PIECE[j] * 512
                    for c in range(C):
                        for k, (p, q) in enumerate(HILO):
                            last = nc.tensor.matmul(proj_ps[:, n % 2], xs[p][:, t % 2, c, :],
                                                    W.wq(q, c, first, 512),
                                                    start=(c == 0 and k == 0), stop=(c == C - 1 and k == 2))
                    last.then_inc(proj_ok, 1)

                def TQ(t, half):
                    turn_rotated(("TQ", t, half), 0, t, half)

                def TK(t, half):
                    turn_rotated(("TK", t, half), 1, t, half)

                def turn_rotated(use, which, t, half):
                    if which:
                        pe.wait_ge(kmul_ok, 2 * t + half + 1)
                    else:
                        pe.wait_ge(sum_ok, 4 * t + 2 + half + 1)
                    wait_turn_bank(pe, use)
                    for i in range(4):
                        first = (half * 4 + i) * P
                        last = nc.tensor.transpose(t_ps[:, i, :], rot[:, which, first:first + P],
                                                   K.ident[:, :])
                    last.then_inc(turn_ok, 1)

                def S(t, g):
                    if g % 2 == 0:
                        pe.wait_ge(act_took, by_act[("TQ", t, g // 2)])
                    lo = 0 if t % NT else WIN
                    n = 4 * t + g
                    if n:
                        pe.wait_ge(less_ok, 2 * n)
                    for i in range(2):
                        for par in range(2):
                            rows = slice(par * LD, (par + 1) * LD)
                            last = nc.tensor.matmul(s_ps[:, par, i * KEYS + lo:(i + 1) * KEYS],
                                                    qT[rows, 2 * g + i, :],
                                                    kT[rows, 2 * g + i, lo:KEYS],
                                                    start=True, stop=True)
                    last.then_inc(scores_ok, 1)

                def PT(t, g):
                    n = 4 * t + g
                    pe.wait_ge(norm_p, n + 1)
                    if n >= 1:
                        pe.wait_ge(copy_ok, n)
                    for i in range(4):
                        if t % NT:
                            nc.tensor.transpose(pTa_ps[:, i, :], pcols(n, i, -WIN, WIN), K.ident[:, :])
                        last = nc.tensor.transpose(pTb_ps[:, i, :], pcols(n, i, WIN), K.ident[:, :])
                    last.then_inc(turned_ok, 1)

                def PV(t, g):
                    n = 4 * t + g
                    pe.wait_ge(copy_ok, n + 1)
                    if g == 0:
                        pe.wait_ge(v_ok, 2 * (t + 1))
                    if g % 2 == 0 and n >= 2:
                        pe.wait_ge(out_ok, n // 2)
                    for i in range(4):
                        h = 4 * g + i
                        dst = o_ps[(h % 2) * LD:(h % 2 + 1) * LD, (h // 2) % 4, :]
                        if t % NT:
                            nc.tensor.matmul(dst, vt[P - WIN:, (t - 1) % 3, h * LD:(h + 1) * LD],
                                             pTa[P - WIN:, n % 2, i, :], start=True, stop=False)
                        last = nc.tensor.matmul(dst, vt[:, t % 3, h * LD:(h + 1) * LD], pTb[:, n % 2, i, :],
                                                start=t % NT == 0, stop=True)
                    last.then_inc(pv_ok, 1)

                def Y(t, m):
                    pe.wait_ge(out_ok, 2 * t + 2)
                    wait_turn_bank(pe, ("Y", t, m))
                    for i in range(PAIRS):
                        for k, (p, q) in enumerate(HILO):
                            last = nc.tensor.matmul(
                                t_ps[:, 2 * m:2 * m + 2, :].rearrange("p a n -> p (a n)"),
                                W.wo(p, i, m * P), oT[q][:, i, :],
                                start=(i == 0 and k == 0), stop=(i == PAIRS - 1 and k == 2))
                    last.then_inc(turn_ok, 1)
                follow({"J": J, "TQ": TQ, "TK": TK, "S": S, "PT": PT, "PV": PV, "Y": Y})

            @block.scalar
            def _(act):
                def xh(t, _=0):
                    if t >= 2:
                        act.wait_ge(proj_ok, 6 * (t - 1))
                    for c in range(C):
                        last = nc.scalar.activation(xs[0][:, t % 2, c, :], ztok(c, t, P, c), ACT.Copy)
                    last.then_inc(xh_ok, 1)

                def square(t, j):
                    n = 6 * t + ROTATED[j]
                    act.wait_ge(proj_ok, n + 1)
                    if 4 * t + j >= 2:
                        act.wait_ge(ssq_ok, 4 * t + j - 1)
                    nc.scalar.activation(sq[:, j % 2], proj_ps[:, n % 2], ACT.Square).then_inc(sq_ok, 1)

                def values(t, j):
                    n = 6 * t + VALUES[j]
                    act.wait_ge(proj_ok, n + 1)
                    if t >= 3:
                        act.wait_ge(pv_ok, 4 * (t - 2) + 2 * j + 2)
                    nc.scalar.activation(vt[:, t % 3, j * 512:(j + 1) * 512], proj_ps[:, n % 2],
                                         ACT.Copy).then_inc(v_ok, 1)

                def TQ(t, half):
                    act.wait_ge(turn_ok, turn_no[("TQ", t, half)] + 1)
                    if t >= 1:
                        act.wait_ge(scores_ok, 4 * (t - 1) + 2 * half + 2)
                    nc.scalar.activation(qT[:, half * 4:half * 4 + 4, :], t_ps[:, :, :],
                                         ACT.Copy).then_inc(act_took, 1)

                def halo(t, half):
                    pairs = slice(half * 4, half * 4 + 4)
                    if t % NT:
                        act.wait_ge(scores_ok, 4 * (t - 1) + 2 * half + 2)
                        nc.scalar.activation(kT[:, pairs, 0:WIN], kT[:, pairs, P:KEYS], ACT.Copy
                                             ).then_inc(halo_ok, 1)

                def TK(t, half):
                    act.wait_ge(turn_ok, turn_no[("TK", t, half)] + 1)
                    if t % NT:
                        act.wait_ge(halo_ok, (t - t // NT - 1) * 2 + half + 1)
                    elif t:
                        act.wait_ge(scores_ok, 4 * (t - 1) + 2 * half + 2)
                    nc.scalar.activation(kT[:, half * 4:half * 4 + 4, WIN:KEYS], t_ps[:, :, :],
                                         ACT.Copy).then_inc(act_took, 1)

                def exp(t, pair):
                    n, half = 4 * t + pair // 2, pair % 2
                    act.wait_ge(less_ok, 8 * t + pair + 1)
                    if pair == 0 and t >= 2:
                        act.wait_ge(norm_p, 4 * (t - 1))
                    lo = 0 if t % NT else WIN
                    for i in (2 * half, 2 * half + 1):
                        h = 2 * pair + i % 2
                        last = nc.scalar.activation(pcols(n, i, lo), pcols(n, i, lo), ACT.Exp,
                                                    bias=nb[:, t % 2, h:h + 1],
                                                    scale=sc8[:, t % 2, h:h + 1],
                                                    accum_out=sums[:, t % 2, h:h + 1])
                    last.then_inc(exp_ok, 1)

                def copy(t, g):
                    n = 4 * t + g
                    act.wait_ge(turned_ok, n + 1)
                    if n >= 2:
                        act.wait_ge(pv_ok, n - 1)
                    if t % NT:
                        nc.scalar.activation(pTa[P - WIN:, n % 2], pTa_ps[P - WIN:], ACT.Copy)
                    nc.scalar.activation(pTb[:, n % 2], pTb_ps[:, :, :], ACT.Copy).then_inc(copy_ok, 1)

                def outputs_high(t, half):
                    act.wait_ge(pv_ok, 4 * t + 2 * half + 2)
                    if t >= 2 and t % 2 == 0 and half == 0:
                        act.wait_ge(turn_ok, turn_no[("Y", t - 1, 1)] + 1)
                    part = slice((t % 2) * P, (t % 2 + 1) * P)
                    nc.scalar.activation(oT[0][:, half * 4:half * 4 + 4, part], o_ps[:, :, :],
                                         ACT.Copy).then_inc(high_ok, 1)

                def weight_high(t, _):
                    act.wait_ge(loaded, 16 * (t - FIRST_W + 1))
                    take_high(nc, W.wf, t - FIRST_W, raw[:, 0]).then_inc(high, 1)
                xh(0)
                follow({"halo": halo, "wh": weight_high, "xh": xh, "sq": square, "v": values, "tq": TQ,
                        "tk": TK, "exp": exp, "copy": copy, "out": outputs_high})

            @block.gpsimd
            def _(pool):
                nc.gpsimd.memset(minus_half[:, :], -0.5).then_inc(set_ok, 1)
                pool.wait_ge(set_ok, 1)
                for t in range(NA):
                    for j in range(4):
                        which, half = divmod(PIECE[ROTATED[j]], 2)
                        part = rot[:, which, half * 512:(half + 1) * 512]
                        pool.wait_ge(rot_ok, 4 * t + j + 1)
                        nc.gpsimd.tensor_tensor(part, part, rb[:, j % 2], ALU.add).then_inc(sum_ok, 1)
                        pool.wait_ge(norm_ok, 4 * t + j + 1)
                        if not which and t >= 2:
                            pool.wait_ge(exp_ok, 8 * (t - 2) + 4 * half + 4)
                        dst = (rn if which else sc8)[:, t % 2, 8 * half:8 * half + 8]
                        nc.gpsimd.tensor_tensor(dst, ssq[:, t % 2, 8 * j:8 * j + 8], minus_half[:, 0:8], ALU.pow
                                                ).then_inc(pow_ok, 1)
                        if which:
                            pool.wait_ge(pow_ok, 4 * t + j + 1)
                            pool.wait_ge(sum_ok, 4 * t + j + 1)
                            part = part.rearrange("p (h d) -> p h d", d=LD)
                            nc.gpsimd.tensor_tensor(part, part, bc(dst, 2, [P, 8, LD]), ALU.mult
                                                    ).then_inc(kmul_ok, 1)

            @block.vector
            def _(dve):
                own = Own(dve, dve_own)
                tt = nc.vector.tensor_tensor

                def xl(t, _=0):
                    dve.wait_ge(xh_ok, t + 1)
                    for c in range(C):
                        last = tt(xs[1][:, t % 2, c, :], ztok(c, t, P, c),
                                  xs[0][:, t % 2, c, :].bitcast(F32), ALU.subtract)
                    last.then_inc(xl_ok, 1)

                def rotate(t, j):
                    n = 6 * t + ROTATED[j]
                    which, half = divmod(PIECE[ROTATED[j]], 2)
                    table = 2 * which
                    dve.wait_ge(sq_ok, 4 * t + j + 1)
                    if 4 * t + j >= 2:
                        dve.wait_ge(sum_ok, 4 * t + j - 1)
                    heads = lambda x: x.rearrange("p (h d) -> p h d", d=LD)
                    if t:
                        dve.wait_ge(turn_ok, turn_no[("TK" if which else "TQ", t - 1, half)] + 1)
                    src, r = heads(proj_ps[:, n % 2]), heads(rb[:, j % 2])
                    a = heads(rot[:, which, half * 512:(half + 1) * 512])
                    cos, sin = W.tabs[:, table, t % NT, :], W.tabs[:, table + 1, t % NT, :]
                    lo, up = slice(0, LD // 2), slice(LD // 2, LD)
                    tt(a, src, bc(cos, 1, [P, 8, LD]), ALU.mult)
                    tt(r[:, :, lo], src[:, :, up], bc(sin[:, lo], 1, [P, 8, LD // 2]), ALU.mult)
                    tt(r[:, :, up], src[:, :, lo], bc(sin[:, up], 1, [P, 8, LD // 2]), ALU.mult
                       ).then_inc(rot_ok, 1)
                    part = ssq[:, t % 2, j * 8:(j + 1) * 8]
                    if t >= 2:
                        dve.wait_ge(pow_ok, 4 * (t - 2) + j + 1)
                    nc.vector.tensor_reduce(part, heads(sq[:, j % 2]), AX.X, ALU.add).then_inc(ssq_ok, 1)
                    dve.wait_ge(ssq_ok, 4 * t + j + 1)
                    scale = 1.0 if j < 2 else QK_SCALE ** -2
                    nc.vector.tensor_scalar(part, part, scale, LEAST * LEAST * scale, ALU.mult,
                                            ALU.max).then_inc(norm_ok, 1)

                def less(t, g):
                    n = 4 * t + g
                    if n >= 2:
                        dve.wait_ge(turned_ok, n - 1)
                    lo = 0 if t % NT else WIN
                    for i in range(2):
                        h = 4 * g + 2 * i
                        dve.wait_ge(scores_ok, n + 1)
                        for par in range(2):
                            ins = nc.vector.tensor_tensor_reduce(
                                pcols(n, 2 * i + par, lo),
                                s_ps[:, par, i * KEYS + lo:(i + 1) * KEYS], W.mask[:, lo:], 1.0,
                                3.0 * MASKED, ALU.add, ALU.max, mx[:, t % 2, h + par:h + par + 1])
                        own(ins)
                        if g % 2 == 0 and i == 0:
                            dve.wait_ge(pow_ok, 4 * t + 2 + g // 2 + 1)
                        nc.vector.scalar_tensor_tensor(
                            out=nb[:, t % 2, h:h + 2], in0=mx[:, t % 2, h:h + 2], scalar=-1.0,
                            in1=sc8[:, t % 2, h:h + 2], op0=ALU.mult, op1=ALU.mult).then_inc(less_ok, 1)

                def normalise(t, g):
                    n, four = 4 * t + g, slice(4 * g, 4 * g + 4)
                    dve.wait_ge(exp_ok, 2 * n + 2)
                    own(nc.vector.reciprocal(rs[:, t % 2, four], sums[:, t % 2, four]))
                    lo = 0 if t % NT else WIN
                    for i in range(4):
                        h = 4 * g + i
                        last = nc.vector.tensor_scalar(pcols(n, i, lo), pcols(n, i, lo),
                                                       rs[:, t % 2, h:h + 1], None, ALU.mult)
                    last.then_inc(norm_p, 1)

                def outputs_low(t, half):
                    dve.wait_ge(high_ok, 2 * t + half + 1)
                    part = slice((t % 2) * P, (t % 2 + 1) * P)
                    four = slice(half * 4, half * 4 + 4)
                    tt(oT[1][:, four, part], o_ps[:, :, :], oT[0][:, four, part].bitcast(F32),
                       ALU.subtract).then_inc(out_ok, 1)

                def add(t, m):
                    dve.wait_ge(turn_ok, turn_no[("Y", t, m)] + 1)
                    view = ztok(m, t - 1, 2 * P)
                    tt(view, view, t_ps[:, 2 * m:2 * m + 2, :].rearrange("p a n -> p (a n)"), ALU.add
                       ).then_inc(dve_took, 1)

                def weight_low(t, _):
                    dve.wait_ge(high, t - FIRST_W + 1)
                    take_low(nc, W.wf, t - FIRST_W, raw[:, 0]).then_inc(low, 1)
                nc.vector.memset(pr[:, :, 0:WIN], 0.0)
                xl(0)
                follow({"wl": weight_low, "xl": xl, "rot": rotate, "less": less, "norm": normalise,
                        "low": outputs_low, "yadd": add})


def layer_ffn(nc, K, Z, A, W, layer, tag):
    vec = W.vec
    LNG, LNB, B1, B2 = vec[:, 0:C], vec[:, C:2 * C], vec[:, 2 * C:2 * C + 2 * FIC], vec[:, 2 * C + 2 * FIC:]
    N = NG * FIC
    SLOTS = 4
    FIRST_W = 4
    with ExitStack() as s:
        sb = lambda n, sh, dt=F32: s.enter_context(nc.sbuf_tensor(f"{tag}_{n}", sh, dt))
        xsum, sqsum, lnv, rstd = (sb(n, [P, G]) for n in ("xsum", "sqsum", "lnv", "rstd"))
        sq = sb("sq", [P, C, G])
        xn = sb("xn", [P, C, G])
        xh = sb("xh", [P, 2, C, G], F32R)
        xl = sb("xl", [P, 2, C, G], F32R)
        raw = sb("raw", [P, SLOTS, PIECE_COLS])
        hg = sb("hg", [P, 2, G])
        hid = sb("hid", [P, 2, G])
        hh = sb("hh", [P, 2, G], F32R)
        hl = sb("hl", [P, 2, G], F32R)
        gu_ps = s.enter_context(nc.psum_tensor(f"{tag}_gu", [P, 2, 2, G], F32))
        y_ps = s.enter_context(nc.psum_tensor(f"{tag}_y", [P, C, G], F32))
        mean_ps = s.enter_context(nc.psum_tensor(f"{tag}_mean", [P, G], F32))
        var_ps = s.enter_context(nc.psum_tensor(f"{tag}_var", [P, G], F32))

        def tokens(c, g, shift=0):
            first = (g // GB) * SP1 + 1 + (g % GB) * G - shift
            return Z[:, c, first:first + G]

        def at(g, chunk):
            return (g - 1) * FIC + chunk
        with semaphores(nc, tag, "xsum", "mean", "centred", "squares", "sqsum", "var", "lnv", "rstd",
                        "scaled", "xn", "xh", "xl", "gu", "gelu", "prod", "high", "low", "down", "added",
                        "tabled", "loaded", "w_high", "w_low", "tab_scaled") as (
                xsum_ready, mean_ready, centred, squares, sqsum_ready, var_ready, lnv_ready, rstd_ready,
                scaled, xn_ready, xh_ready, xl_ready, gu_ready, gelu_ready, prod, high, low, down_done,
                added, tabled, loaded, w_high, w_low, tab_scaled), \
                nc.Block(no_gpsimd_drain=True) as block:

            @block.sync
            def _(sp):
                fetch_tables(sp, W, A, layer + 1, tabled)
                fetch_pieces(sp, raw, SLOTS, (A["l_wqkv"], A["l_wo"]), layer + 1, loaded, w_low)

            @block.gpsimd
            def _(pool):
                for g in range(NG):
                    if g:
                        pool.wait_ge(mean_ready, g)
                    nc.gpsimd.tensor_tensor(xsum[:, :], tokens(0, g), tokens(1, g, 1), ALU.add
                                            ).then_inc(xsum_ready, 1)
                    if g == 0:
                        scale_tables(nc, pool, W, tabled, tab_scaled)

            @block.tensor
            def _(pe):
                def mean(g):
                    pe.wait_ge(xsum_ready, g + 1)
                    if g:
                        pe.wait_ge(centred, g)
                    nc.tensor.matmul(mean_ps[:, :], K.mean_w[:, :], xsum[:, :], start=True, stop=True
                                     ).then_inc(mean_ready, 1)

                def var(g):
                    pe.wait_ge(sqsum_ready, g + 1)
                    if g:
                        pe.wait_ge(lnv_ready, g)
                    nc.tensor.matmul(var_ps[:, :], K.mean_w[:, :], sqsum[:, :], start=True, stop=True
                                     ).then_inc(var_ready, 1)

                def up(k):
                    g, i = divmod(k, FIC)
                    if i == 0:
                        pe.wait_ge(xl_ready, g + 1)
                    if k >= 2:
                        pe.wait_ge(prod, k - 1)
                    for u in range(2):
                        first = u * FIP + i * P
                        for c in range(C):
                            x = (xh[:, g % 2, c], xl[:, g % 2, c])
                            for n, (p, q) in enumerate(HILO):
                                last = nc.tensor.matmul(gu_ps[:, k % 2, u], W.w1(p, c, first), x[q],
                                                        start=(c == 0 and n == 0), stop=(c == C - 1 and n == 2))
                    last.then_inc(gu_ready, 1)

                def down(k):
                    g, i = divmod(k, FIC)
                    pe.wait_ge(low, k + 1)
                    if i == 0 and g:
                        pe.wait_ge(added, g)
                    for m in range(C):
                        x = (hh[:, k % 2], hl[:, k % 2])
                        for n, (p, q) in enumerate(HILO):
                            last = nc.tensor.matmul(y_ps[:, m], W.w2(p, i, m * P), x[q],
                                                    start=(i == 0 and n == 0), stop=(i == FIC - 1 and n == 2))
                    last.then_inc(down_done, 1)
                mean(0)
                var(0)
                for k in range(N + 2):
                    if k < N:
                        up(k)
                    if k >= 2:
                        down(k - 2)
                    for g in range(1, NG):
                        if k == at(g, 0):
                            mean(g)
                        if k == at(g, 2):
                            var(g)

            @block.scalar
            def _(act):
                def square(g):
                    act.wait_ge(centred, g + 1)
                    if g:
                        act.wait_ge(sqsum_ready, g)
                    nc.scalar.activation(sq[:, :, :], xn[:, :, :], ACT.Square).then_inc(squares, 1)

                def inverse_std(g):
                    act.wait_ge(var_ready, g + 1)
                    nc.scalar.activation(lnv[:, :], var_ps[:, :], ACT.Ln, bias=K.eps[:, 0:1]
                                         ).then_inc(lnv_ready, 1)
                    act.wait_ge(lnv_ready, g + 1)
                    if g:
                        act.wait_ge(scaled, g)
                    nc.scalar.activation(rstd[:, :], lnv[:, :], ACT.Exp, scale=-0.5).then_inc(rstd_ready, 1)

                def x_high(g):
                    act.wait_ge(xn_ready, g + 1)
                    if g >= 2:
                        act.wait_ge(gu_ready, FIC * (g - 1))
                    nc.scalar.activation(xh[:, g % 2], xn[:, :, :], ACT.Copy).then_inc(xh_ready, 1)

                def gelu(k):
                    i = k % FIC
                    act.wait_ge(gu_ready, k + 1)
                    if k >= 2:
                        act.wait_ge(prod, k - 1)
                    nc.scalar.activation(hg[:, k % 2], gu_ps[:, k % 2, 1], ACT.Gelu,
                                         bias=B1[:, FIC + i:FIC + i + 1]).then_inc(gelu_ready, 1)

                def hidden_high(k):
                    act.wait_ge(prod, k + 1)
                    if k >= 2:
                        act.wait_ge(down_done, k - 1)
                    nc.scalar.activation(hh[:, k % 2], hid[:, k % 2], ACT.Copy).then_inc(high, 1)
                square(0)
                inverse_std(0)
                x_high(0)
                for k in range(N + 1):
                    if k < N:
                        gelu(k)
                    if k:
                        hidden_high(k - 1)
                    for g in range(1, NG):
                        if k == at(g, 0):
                            square(g)
                        if k == at(g, 2):
                            inverse_std(g)
                        if k == at(g, 4):
                            x_high(g)
                    n = k - FIRST_W
                    if 0 <= n < NWA:
                        act.wait_ge(loaded, 16 * (n + 1))
                        take_high(nc, W.wa, n, raw[:, n % SLOTS]).then_inc(w_high, 1)

            @block.vector
            def _(dve):
                tt = nc.vector.tensor_tensor

                def centre(g):
                    dve.wait_ge(mean_ready, g + 1)
                    if g:
                        dve.wait_ge(xl_ready, g)
                    for c in range(C):
                        last = tt(xn[:, c], tokens(c, g, c), mean_ps[:, :], ALU.subtract)
                    last.then_inc(centred, 1)

                def sum_squares(g):
                    dve.wait_ge(squares, g + 1)
                    if g:
                        dve.wait_ge(var_ready, g)
                    tt(sqsum[:, :], sq[:, 0], sq[:, 1], ALU.add).then_inc(sqsum_ready, 1)

                def scale(g):
                    dve.wait_ge(rstd_ready, g + 1)
                    tt(xn[:, :, :], xn[:, :, :], bc(rstd[:, :], 1, [P, C, G]), ALU.mult).then_inc(scaled, 1)
                    dve.wait_ge(scaled, g + 1)
                    for c in range(C):
                        last = nc.vector.tensor_scalar(xn[:, c], xn[:, c], LNG[:, c:c + 1], LNB[:, c:c + 1],
                                                       ALU.mult, ALU.add)
                    last.then_inc(xn_ready, 1)

                def x_low(g):
                    dve.wait_ge(xh_ready, g + 1)
                    if g >= 2:
                        dve.wait_ge(gu_ready, FIC * (g - 1))
                    tt(xl[:, g % 2], xn[:, :, :], xh[:, g % 2].bitcast(F32), ALU.subtract
                       ).then_inc(xl_ready, 1)

                def product(k):
                    i = k % FIC
                    dve.wait_ge(gelu_ready, k + 1)
                    if k >= 2:
                        dve.wait_ge(low, k - 1)
                    nc.vector.scalar_tensor_tensor(out=hid[:, k % 2], in0=gu_ps[:, k % 2, 0],
                                                   scalar=B1[:, i:i + 1], in1=hg[:, k % 2], op0=ALU.add,
                                                   op1=ALU.mult).then_inc(prod, 1)

                def hidden_low(k):
                    dve.wait_ge(high, k + 1)
                    if k >= 2:
                        dve.wait_ge(down_done, k - 1)
                    tt(hl[:, k % 2], hid[:, k % 2], hh[:, k % 2].bitcast(F32), ALU.subtract
                       ).then_inc(low, 1)

                def add(g):
                    dve.wait_ge(down_done, FIC * (g + 1))
                    for c in range(C):
                        last = nc.vector.scalar_tensor_tensor(out=tokens(c, g), in0=y_ps[:, c],
                                                              scalar=B2[:, c:c + 1], in1=tokens(c, g),
                                                              op0=ALU.add, op1=ALU.add)
                    last.then_inc(added, 1)
                centre(0)
                sum_squares(0)
                scale(0)
                x_low(0)
                for k in range(N + 3):
                    if k >= 3 and (k - 2) % FIC == 0:
                        add((k - 2) // FIC - 1)
                    if k < N:
                        product(k)
                    if 1 <= k <= N:
                        hidden_low(k - 1)
                    for g in range(1, NG):
                        if k == at(g, 0):
                            centre(g)
                        if k == at(g, 1):
                            sum_squares(g)
                        if k == at(g, 3):
                            scale(g)
                        if k == at(g, 4):
                            x_low(g)
                    n = k - FIRST_W - 1
                    if 0 <= n < NWA:
                        dve.wait_ge(w_high, n + 1)
                        take_low(nc, W.wa, n, raw[:, n % SLOTS]).then_inc(w_low, 1)


def flamingo(nc, A, out_x):
    with ExitStack() as s:
        sb = lambda n, sh: s.enter_context(nc.sbuf_tensor(n, sh, F32))
        X = sb("X", [P, C, B * SP1])
        gates = sb("gates", [P, 8])
        K = Constants(sb, A)
        before_transformer = s.enter_context(ExitStack())
        early = lambda n, sh: before_transformer.enter_context(nc.sbuf_tensor(n, sh, F32))
        K.ones, K.last_row = early("ones", [P, P]), early("last_row", [P, P])
        ctxT = early("ctxT", [P, C, B * E])
        start_loaded = s.enter_context(nc.semaphore("start_loaded"))
        stored = s.enter_context(nc.semaphore("stored"))

        with semaphores(nc, "start", "filled") as (filled,), nc.Block() as block:
            @block.sync
            def _(sp):
                for b in range(B):
                    sp.dma_start(X[:, :, b * SP1 + 1:(b + 1) * SP1],
                                 A["xT"].rearrange("(c p) (b t) -> p c b t", p=P, b=B)[:, :, b]
                                 ).then_inc(start_loaded, 16)
                sp.dma_start(K.ident[:, :], A["ident"]).then_inc(start_loaded, 16)
                sp.dma_start(ctxT[:, :, :], A["ctxT"].rearrange("(c p) t -> p c t", p=P)
                             ).then_inc(start_loaded, 16)
                sp.dma_start(gates[:, 0:4], A["g_xattn"].partition_broadcast(P)).then_inc(start_loaded, 16)
                sp.dma_start(gates[:, 4:8], A["g_ffn"].partition_broadcast(P)).then_inc(start_loaded, 16)
                sp.dma_start(K.last_row[0:E + 1, :], A["last_row"]).then_inc(start_loaded, 16)
                sp.wait_ge(start_loaded, 16 * 7)

            @block.scalar
            def _(act):
                act.wait_ge(start_loaded, 16 * 7)
                nc.scalar.activation(gates[:, :], gates[:, :], ACT.Tanh)

            @block.vector
            def _(dve):
                for b in range(B):
                    nc.vector.memset(X[:, :, b * SP1:b * SP1 + 1], 0.0)
                nc.vector.memset(K.mean_w[:, :], 1.0 / D)
                nc.vector.memset(K.ones[:, :], 1.0)
                nc.vector.memset(K.eps[:, :], EPS)

        kept = nc.dram_tensor("kept", (P, C, B * SP1), F32).ap()

        def tokens(c, g):
            first = (g // GB) * SP1 + 1 + (g % GB) * G
            return X[:, c, first:first + G]

        def weights(prefix):
            return {n[len(prefix) + 1:]: a for n, a in A.items() if n.startswith(prefix + "_")}

        with ExitStack() as s1:
            XN = s1.enter_context(nc.sbuf_tensor("XN", [P, C, T], F32))

            def norm(tag):
                return lambda loads: layer_norm(nc, K, tokens, XN, tag, loads)
            wide_attention(nc, K, X, XN, norm("ln0a"), ctxT, weights("a0"), gates[:, 0:1], "a0", True, 1.0)
            quantised_ffn(nc, K, X, XN, norm("ln0f"), weights("f0"), gates[:, 4:5], "f0")
            wide_attention(nc, K, X, XN, norm("ln1a"), ctxT, weights("a1"), gates[:, 1:2], "a1", False, D ** -0.5)
            w_dram = nc.dram_tensor("expert_weights", (NE + 1, T), F32).ap()
            with ExitStack() as s2:
                sb2 = lambda n, sh, dt=F32: s2.enter_context(nc.sbuf_tensor(f"moe_{n}", sh, dt))
                xh, xl = sb2("xh", [P, C, T], F32R), sb2("xl", [P, C, T], F32R)
                raw = sb2("raw", [P, 2, WE])
                with ExitStack() as s3:
                    sb3 = lambda n, sh: s3.enter_context(nc.sbuf_tensor(f"moe_{n}", sh, F32))
                    XN2, ln_g, ln_b = sb3("xn2", [P, C, T]), sb3("ln_g", [P, C]), sb3("ln_b", [P, C])
                    gw, iota = sb3("gw", [P, C, NE]), sb3("iota", [P, NE])
                    norm("ln1f")([(ln_g[:, :], A["moe_ln_scale"]), (ln_b[:, :], A["moe_ln_bias"]),
                                  (gw[:, :, :], A["moe_gate_w"]), (iota[:, :], K.expert_iota),
                                  (raw[:, 0, :], A["moe_w"][0])])
                    layer_norm(nc, K, lambda c, g: XN[:, c, g * G:(g + 1) * G], XN2, "ln1r",
                               affine=(ln_g, ln_b))
                    router(nc, K, XN2, gw, iota, w_dram, "rt")
                experts(nc, K, X, XN, xh, xl, raw, w_dram, A["moe_w"], gates[:, 5:6], "moe")
            for stage, tag, g, rel in ((5, "a2", 2, False), (7, "a3", 3, True)):
                head_attention(nc, K, X, XN, norm(f"ln{tag}"), ctxT, weights(tag), gates[:, g:g + 1], tag, rel)
                if stage == 5:
                    bit_ffn(nc, K, X, XN, norm("ln2f"), weights("f2"), gates[:, 6:7], "f2")
            layer_norm(nc, K, tokens, XN, "ln3f")
            with semaphores(nc, "swap", "away", "taken") as (away, taken), \
                    nc.Block(no_gpsimd_drain=True) as block:
                @block.sync
                def _(sp):
                    sp.dma_start(kept, X[:, :, :]).then_inc(away, 16)
                    sp.wait_ge(away, 16)

                @block.vector
                def _(dve):
                    dve.wait_ge(away, 16)
                    for g in range(NG):
                        for c in range(C):
                            nc.vector.tensor_copy(tokens(c, g), XN[:, c, g * G:(g + 1) * G])
        before_transformer.close()
        transformer(nc, K, X, A)
        with nc.sbuf_tensor("kept_x", [P, C, B * SP1], F32) as old, \
                semaphores(nc, "back", "back") as (back,), nc.Block(no_gpsimd_drain=True) as block:
            @block.sync
            def _(sp):
                sp.dma_start(old[:, :, :], kept).then_inc(back, 16)

            @block.vector
            def _(dve):
                dve.wait_ge(back, 16)
                nc.vector.scalar_tensor_tensor(out=X[:, :, :], in0=X[:, :, :], scalar=gates[:, 7:8],
                                               in1=old[:, :, :], op0=ALU.mult, op1=ALU.add)

        with nc.Block() as block:
            @block.sync
            def _(sp):
                for b in range(B):
                    sp.dma_start(out_x.rearrange("(c p) (b t) -> p c b t", p=P, b=B)[:, :, b],
                                 X[:, :, b * SP1 + 1:(b + 1) * SP1]).then_inc(stored, 16)
                sp.wait_ge(stored, 16 * B)


def kc(a):
    return a.reshape(a.shape[0] // P, P, a.shape[1]).transpose(1, 0, 2)


def cols(a):
    return a.reshape(-1, P).T


def rows(a):
    return np.broadcast_to(a, (P, a.shape[0]))


def layout(i):
    L = {"xT": i["x"].reshape(T, D).T, "ctxT": i["ctx_1024"].reshape(B * E, D).T,
         "g_xattn": i["g_xattn"], "g_ffn": i["g_ffn"],
         "ident": np.eye(P, dtype=np.float32)}
    last = np.zeros((E + 1, P), np.float32)
    last[E] = 1.0
    L["last_row"] = last
    for st, p, tr in (("a0", "L0_xattn_", False), ("a1", "L1_xattn_", True)):
        for n in "qkv":
            wt = i[f"{p}W{n}"]
            L[f"{st}_w{n}"] = kc(wt.T if tr else wt)
            L[f"{st}_b{n}"] = cols(i[f"{p}b{n}"])
        L[f"{st}_bv_row"] = rows(i[f"{p}bv"])
    for st, p in (("a2", "L2_xattn_"), ("a3", "L3_xattn_")):
        wk, wv = (i[p + "Wkv"][:, :D], i[p + "Wkv"][:, D:]) if st == "a2" else (i[p + "Wk"], i[p + "Wv"])
        bk, bv = (i[p + "bkv"][:D], i[p + "bkv"][D:]) if st == "a2" else (i[p + "bk"], i[p + "bv"])
        L[f"{st}_wq"], L[f"{st}_wk"], L[f"{st}_wv"], L[f"{st}_wo"] = kc(i[p + "Wq"]), kc(wk), kc(wv), kc(i[p + "Wo"])
        L[f"{st}_bq"], L[f"{st}_bk"], L[f"{st}_bo"] = cols(i[p + "bq"]), cols(bk), cols(i[p + "bo"])
        L[f"{st}_bv_row"] = rows(bv)
    L["a3_rel_k"] = np.tile(i["L3_xattn_rel_k"], (1, HC)).T
    L["a3_rel_v"] = np.tile(i["L3_xattn_rel_v"], (1, NH))
    L["a3_rel_v0"] = rows(L["a3_rel_v"][0])
    L["head_of"] = (np.arange(P)[:, None] // HD == np.arange(HC)[None, :]).astype(np.float32)
    L["head_cols"] = np.broadcast_to(L["head_of"].T, (P, HC, P))
    dist = np.arange(E)[None, :] - np.arange(P)[:, None]
    L["rel_mask"] = np.stack([np.clip(dist, -2, 2) + 2 == r for r in range(1, 1 + R)], axis=1).astype(np.float32)

    p = "L0_ffn_w_"
    L["f0_wg"], L["f0_wu"], L["f0_wd"] = (kc(i[p + n]).reshape(P, -1) for n in ("gate", "up", "down"))
    p = "L2_ffn_"
    L["f2_w1"], L["f2_w2"] = kc(i[p + "w1"].T).reshape(P, -1), kc(i[p + "w2"].T).reshape(P, -1)
    L["f2_conv_w"] = kc(i[p + "conv_w"][:, 0, :])
    L["f2_conv_b"] = cols(i[p + "conv_b"])

    p = "L3_ffn_"
    per = lambda f: np.stack([f(min(n, DEPTH - 1)) for n in range(DEPTH + 1)])
    pad = lambda a: np.concatenate([a, np.zeros(a.shape[:-1] + (FIP - FI,), a.dtype)], axis=-1)
    two = lambda a: np.concatenate([pad(a[..., :FI]), pad(a[..., FI:])], axis=-1)
    L["l_wqkv"] = per(lambda n: kc(i[p + "Wqkv"][n]).reshape(P, -1))
    L["l_wo"] = per(lambda n: kc(i[p + "Wo"][n]).reshape(P, -1))
    L["l_w1"] = per(lambda n: kc(two(i[p + "W1"][n])).reshape(P, -1))
    L["l_w2"] = per(lambda n: kc(pad(i[p + "W2"][n].T).T).reshape(P, -1))
    L["l_vec"] = per(lambda n: np.concatenate([cols(i[p + "ln_g"][n]), cols(i[p + "ln_b"][n]),
                                               cols(two(i[p + "b1"][n])), cols(i[p + "b2"][n])], axis=1))
    partner = np.roll(np.arange(LD), LD // 2)
    L["l_qk_scale"] = per(lambda n: np.broadcast_to(np.stack(
        [i[p + "q_scale"][n], i[p + "q_scale"][n][partner], i[p + "k_scale"][n], i[p + "k_scale"][n][partner]]),
        (P, 4, LD)))
    f32 = np.float32
    half = np.arange(0, LD, 2, dtype=f32)
    freqs = np.arange(S, dtype=f32)[:, None] * (f32(1.0) / f32(10000.0) ** (half / f32(LD)))[None, :]
    base = (half + f32(0.4 * LD)) / f32(1.4 * LD)
    grow = base[None, :] ** ((np.arange(S, dtype=f32) - S // 2) / (WIN // 2))[:, None]
    twice = lambda a: np.concatenate([a, a], axis=1)
    cos, sin = twice(np.cos(freqs)), np.concatenate([-np.sin(freqs), np.sin(freqs)], axis=1)
    grow, fall = twice(grow), twice(f32(1.0) / grow)
    L["rotary"] = np.stack([cos * grow, sin * grow, cos * fall, sin * fall]).astype(f32).reshape(
        4, NT, P, LD).transpose(2, 0, 1, 3)
    key, query = np.arange(KEYS)[None, :], np.arange(P)[:, None]
    L["band_mask"] = np.where((key >= query) & (key <= query + WIN), 0.0, MASKED).astype(f32)

    def expert(wg, wu, wd):
        return np.concatenate([kc(w).reshape(P, -1) for w in (wg, wu, wd)], axis=1)
    p = "L1_ffn_"
    L["moe_w"] = np.stack([expert(i[p + "Wg"][e], i[p + "Wu"][e], i[p + "Wd"][e]) for e in range(NE)]
                          + [expert(i[p + "sWg"], i[p + "sWu"], i[p + "sWd"])])
    L["moe_gate_w"] = kc(i[p + "gate_w"].T)
    L["moe_ln_scale"], L["moe_ln_bias"] = cols(i[p + "ln_scale"]), cols(i[p + "ln_bias"])
    L["expert_iota"] = rows(np.arange(NE, dtype=np.float32) - NE)
    return L


def kernel(**inputs):
    import numpy as _np
    import concourse.bacc as _bacc
    from concourse import mybir as _mybir
    from concourse.bass_utils import run_bass_kernel_spmd as _run

    nc = _bacc.Bacc("TRN2", target_bir_lowering=False, num_devices=1)
    L = {k: _np.ascontiguousarray(v) for k, v in layout({k: _np.asarray(v) for k, v in inputs.items()}).items()}
    arrays, aps = {}, {}
    for name, a in L.items():
        arrays[f"in_{name}"] = a
        aps[name] = nc.dram_tensor(f"in_{name}", a.shape, _mybir.dt.from_np(a.dtype), kind="ExternalInput").ap()
    out = nc.dram_tensor("out_x", (D, T), _mybir.dt.float32, kind="ExternalOutput").ap()
    flamingo(nc, aps, out)
    r = _run(nc, [arrays], core_ids=[0])
    got = r.results[0]["out_x"]
    return _np.ascontiguousarray(got.T).reshape(B, S, D)
```
